# Optimizing a Trainium2 kernel written in Bass

```python
import numpy as np
import jax
import jax.numpy as jnp

def _softmax(x, axis=-1):
    return jax.nn.softmax(x, axis=axis)

def _gelu(x):
    return jax.nn.gelu(x, approximate=True)

def _silu(x):
    return jax.nn.silu(x)

def _sigmoid(x):
    return jax.nn.sigmoid(x)

def _layernorm(x, axis=-1, eps=1e-05):
    m = jnp.mean(x, axis=axis, keepdims=True)
    v = jnp.var(x, axis=axis, keepdims=True)
    return (x - m) / jnp.sqrt(v + eps)

def _scatter_add(tgt, idx, src, axis=0):
    return tgt.at[idx].add(src)

def _segment_sum(src, seg, n):
    return jax.ops.segment_sum(src, seg, n)
kernel_name = 'mk_early_fusion_d4_tok_img768_r4_fd0838'

def setup_inputs(seed: int=0):
    np.random.seed(seed)
    _w = jnp.asarray

    def _rec_inputs():
        import jax
        import jax.numpy as jnp
        _rk = jax.random.key(seed)
        x = -1.80045e-05 + 0.999906 * jax.random.normal(jax.random.fold_in(_rk, 1), (16, 3, 96, 96), jnp.float32)
        txt = 0.261128 + 1.19657 * jax.random.normal(jax.random.fold_in(_rk, 2), (16, 77, 192), jnp.float32)
        return (x, txt)
    x, txt = _rec_inputs()

    def _L0_tok_setup():
        import jax, jax.numpy as jnp
        import numpy as np
        IMAGE_SIZE = 96
        PATCH = 16
        CHANNELS = 3
        TOKEN_DIM = 192
        NUM_PATCHES = (IMAGE_SIZE // PATCH) ** 2
        PATCH_DIM = CHANNELS * PATCH * PATCH
        N_TOKENS = NUM_PATCHES + 1

        def _fixed_pos_embedding(n_tokens, dim):
            i = np.arange(n_tokens, dtype=np.float32)[:, None]
            j = np.arange(dim, dtype=np.float32)[None, :]
            j_even = np.where(j % 2 == 0, j, j - 1)
            angle = i / np.power(10000.0, j_even / dim)
            tab = np.where(j % 2 == 0, np.sin(angle), np.cos(angle)).astype(np.float32)
            return jnp.asarray(tab)

        def _make_patches(image):
            B, C, H, Wd = image.shape
            p = PATCH
            hp, wp = (H // p, Wd // p)
            x = image.reshape(B, C, hp, p, wp, p)
            x = x.transpose(0, 1, 2, 4, 3, 5)
            return x.reshape(B, hp * wp, C * p * p)
        key = jax.random.key(seed)
        k_img, k_w, k_b, k_cls = jax.random.split(key, 4)
        image = jax.random.normal(k_img, (128, CHANNELS, IMAGE_SIZE, IMAGE_SIZE), dtype=jnp.float32)
        W = jax.random.normal(k_w, (TOKEN_DIM, PATCH_DIM), dtype=jnp.float32) / np.sqrt(PATCH_DIM)
        b = jax.random.normal(k_b, (TOKEN_DIM,), dtype=jnp.float32) * 0.01
        class_token = jax.random.normal(k_cls, (1, TOKEN_DIM), dtype=jnp.float32)
        pos_embedding = _fixed_pos_embedding(N_TOKENS, TOKEN_DIM)
        return {'image': image, 'W': W, 'b': b, 'class_token': class_token, 'pos_embedding': pos_embedding}
    _L0_tok_all = _L0_tok_setup()
    _L0_tok_in = {k: v for k, v in _L0_tok_all.items() if k in ('W', 'b', 'class_token', 'pos_embedding')}
    del _L0_tok_all

    def _L0_attn_setup():
        import math
        import jax, jax.numpy as jnp
        import numpy as np
        B, N, D_IN, D_OUT = (8, 512, 192, 192)
        key = jax.random.key(seed)
        k1, k2, k3 = jax.random.split(key, 3)
        x = jax.random.normal(k1, (B, N, D_IN), dtype=jnp.float32)
        W_qkv = jax.random.normal(k2, (D_IN, 3 * D_OUT), dtype=jnp.float32) * (1.0 / math.sqrt(D_IN))
        b_qkv = jax.random.normal(k3, (3 * D_OUT,), dtype=jnp.float32) * 0.02
        return {'x': x, 'W_qkv': W_qkv, 'b_qkv': b_qkv}
    _L0_attn_all = _L0_attn_setup()
    _L0_attn_in = {k: v for k, v in _L0_attn_all.items() if k in ('W_qkv', 'b_qkv')}
    del _L0_attn_all

    def _L0_ffn_setup():
        import jax, jax.numpy as jnp
        import numpy as np
        DIM = 192
        FF = 768
        E = 8
        K = 2
        H = 12
        HD = DIM // H
        LN_EPS = 1e-05

        def _layernorm(x, g, b):
            m = jnp.mean(x, axis=-1, keepdims=True)
            v = jnp.var(x, axis=-1, keepdims=True)
            return (x - m) * jax.lax.rsqrt(v + LN_EPS) * g + b

        def _attention(x, Wqkv, Wproj):
            B, T, D = x.shape
            qkv = (x @ Wqkv).reshape(B, T, 3, H, HD)
            q, k, v = (qkv[:, :, 0], qkv[:, :, 1], qkv[:, :, 2])
            scores = jnp.einsum('bqhd,bkhd->bhqk', q, k) * jnp.float32(HD) ** (-0.5)
            attn = jax.nn.softmax(scores, axis=-1)
            out = jnp.einsum('bhqk,bkhd->bqhd', attn, v).reshape(B, T, D)
            return out @ Wproj

        def _moe(x, Wrouter, W1, W2):
            B, T, D = x.shape
            xf = x.reshape(-1, D)
            N = xf.shape[0]
            logits = xf @ Wrouter
            topk_w, topk_idx = jax.lax.top_k(logits, K)
            topk_w = jax.nn.softmax(topk_w.astype(jnp.float32), axis=-1).astype(x.dtype)
            we = jnp.zeros((N, E), x.dtype).at[jnp.arange(N)[:, None], topk_idx].add(topk_w)

            def body(acc, expert):
                W1e, W2e, we_e = expert
                h = jax.nn.gelu(xf @ W1e, approximate=False)
                return (acc + we_e[:, None] * (h @ W2e), None)
            out, _ = jax.lax.scan(body, jnp.zeros_like(xf), (W1, W2, we.T))
            return out.reshape(B, T, D)
        key = jax.random.key(seed)
        ks = jax.random.split(key, 7)
        B, T = (4, 256)
        init = lambda k, shape, fan: jax.random.normal(k, shape, jnp.float32) * fan ** (-0.5)
        return {'x': jax.random.normal(ks[0], (B, T, DIM), jnp.float32), 'Wqkv': init(ks[1], (DIM, 3 * DIM), DIM), 'Wproj': init(ks[2], (DIM, DIM), DIM), 'Wrouter': init(ks[3], (DIM, E), DIM), 'W1': init(ks[4], (E, DIM, FF), DIM), 'W2': init(ks[5], (E, FF, DIM), FF), 'ln1_g': jnp.ones((DIM,), jnp.float32), 'ln1_b': jnp.zeros((DIM,), jnp.float32), 'ln2_g': jnp.ones((DIM,), jnp.float32), 'ln2_b': jnp.zeros((DIM,), jnp.float32)}
    _L0_ffn_all = _L0_ffn_setup()
    _L0_ffn_in = {k: v for k, v in _L0_ffn_all.items() if k in ('Wqkv', 'Wproj', 'Wrouter', 'W1', 'W2', 'ln1_g', 'ln1_b', 'ln2_g', 'ln2_b')}
    del _L0_ffn_all

    def _L1_attn_setup():
        import jax, jax.numpy as jnp
        import numpy as np
        D_MODEL = 192
        D_STATE = 16
        K_CONV = 4
        BATCH = 2
        SEQ = 512

        def _forward(x, Wi, bi, Wconv, bconv, Wdt, bdt, WB, bB, WC, bC, A_log, D, Wo, bo):
            B, L, dm = x.shape
            ds = A_log.shape[1]
            K = Wconv.shape[1]
            uv = x @ Wi + bi
            u, v = (uv[..., :dm], uv[..., dm:])
            u_pad = jnp.pad(u, ((0, 0), (K - 1, 0), (0, 0)))
            u_conv = bconv + sum((u_pad[:, k:k + L, :] * Wconv[:, k] for k in range(K)))
            dt = jax.nn.softplus(u_conv @ Wdt + bdt)
            Bt = (u_conv @ WB + bB).reshape(B, L, dm, ds)
            Ct = (u_conv @ WC + bC).reshape(B, L, dm, ds)
            A = -jnp.exp(A_log)

            def step(s, inputs):
                dt_t, u_t, B_tt, C_tt = inputs
                dt_e = dt_t[..., None]
                s = s * jnp.exp(dt_e * A) + dt_e * B_tt * u_t[..., None]
                y = jnp.sum(C_tt * s, axis=-1) + D * u_t
                return (s, y)
            s0 = jnp.zeros((B, dm, ds), x.dtype)
            xs = (dt.transpose(1, 0, 2), u_conv.transpose(1, 0, 2), Bt.transpose(1, 0, 2, 3), Ct.transpose(1, 0, 2, 3))
            _, ys = jax.lax.scan(step, s0, xs)
            y = ys.transpose(1, 0, 2)
            y = y * jax.nn.sigmoid(v)
            return y @ Wo + bo
        key = jax.random.key(seed)
        ks = jax.random.split(key, 16)
        dm, ds, K = (D_MODEL, D_STATE, K_CONV)
        s = 0.02
        inp = {'x': jax.random.normal(ks[0], (BATCH, SEQ, dm), dtype=jnp.float32), 'Wi': jax.random.normal(ks[1], (dm, 2 * dm), dtype=jnp.float32) * s, 'bi': jnp.zeros((2 * dm,), jnp.float32), 'Wconv': jax.random.normal(ks[2], (dm, K), dtype=jnp.float32) * s, 'bconv': jnp.zeros((dm,), jnp.float32), 'Wdt': jax.random.normal(ks[3], (dm, dm), dtype=jnp.float32) * s, 'bdt': jnp.zeros((dm,), jnp.float32), 'WB': jax.random.normal(ks[4], (dm, dm * ds), dtype=jnp.float32) * s, 'bB': jnp.zeros((dm * ds,), jnp.float32), 'WC': jax.random.normal(ks[5], (dm, dm * ds), dtype=jnp.float32) * s, 'bC': jnp.zeros((dm * ds,), jnp.float32), 'A_log': jnp.zeros((dm, ds), jnp.float32), 'D': jnp.ones((dm,), jnp.float32), 'Wo': jax.random.normal(ks[6], (dm, dm), dtype=jnp.float32) * s, 'bo': jnp.zeros((dm,), jnp.float32)}
        return inp
    _L1_attn_all = _L1_attn_setup()
    _L1_attn_in = {k: v for k, v in _L1_attn_all.items() if k in ('Wi', 'bi', 'Wconv', 'bconv', 'Wdt', 'bdt', 'WB', 'bB', 'WC', 'bC', 'A_log', 'D', 'Wo', 'bo')}
    del _L1_attn_all

    def _L1_ffn_setup():
        import jax, jax.numpy as jnp
        import numpy as np
        DIM = 192
        H = 12
        HD = 64
        SHARED = 2
        ROUTED = 2
        E_ROUTED = H - SHARED
        LN_EPS = 1e-05

        def _layernorm(x, w, b):
            m = x.mean(-1, keepdims=True)
            v = ((x - m) ** 2).mean(-1, keepdims=True)
            return (x - m) * jax.lax.rsqrt(v + LN_EPS) * w + b
        key = jax.random.key(seed)
        ks = jax.random.split(key, 12)
        B, N = (4, 512)
        s = 0.02
        return {'x': jax.random.normal(ks[0], (B, N, DIM), jnp.float32), 'qkv_w': jax.random.normal(ks[1], (DIM, 3 * H * HD), jnp.float32) * s, 'qkv_b': jnp.zeros((3 * H * HD,), jnp.float32), 'q_norm_w': jnp.ones((HD,), jnp.float32), 'q_norm_b': jnp.zeros((HD,), jnp.float32), 'k_norm_w': jnp.ones((HD,), jnp.float32), 'k_norm_b': jnp.zeros((HD,), jnp.float32), 'wg_w': jax.random.normal(ks[2], (DIM, E_ROUTED), jnp.float32) * s, 'wg0_w': jax.random.normal(ks[3], (DIM, 2), jnp.float32) * s, 'wg1_w': jax.random.normal(ks[4], (DIM, SHARED), jnp.float32) * s, 'proj_w': jax.random.normal(ks[5], (H * HD, DIM), jnp.float32) * s, 'proj_b': jnp.zeros((DIM,), jnp.float32)}
    _L1_ffn_all = _L1_ffn_setup()
    _L1_ffn_in = {k: v for k, v in _L1_ffn_all.items() if k in ('qkv_w', 'qkv_b', 'q_norm_w', 'q_norm_b', 'k_norm_w', 'k_norm_b', 'wg_w', 'wg0_w', 'wg1_w', 'proj_w', 'proj_b')}
    del _L1_ffn_all

    def _L2_attn_setup():
        import jax, jax.numpy as jnp
        import numpy as np
        HIDDEN = 192
        KV_DIM = HIDDEN // 3
        BATCH, SEQ = (2, 2048)
        THETA = 10000.0

        def rope_table(seq_len, dim):
            pos = jnp.arange(seq_len, dtype=jnp.float32)
            freqs = THETA ** (-jnp.arange(0, dim, 2, dtype=jnp.float32) / dim)
            ang = pos[:, None] * freqs[None, :]
            return jnp.concatenate([jnp.sin(ang), jnp.cos(ang)], axis=-1)[None]
        key = jax.random.key(seed)
        kx, kq, kk, kv, ko = jax.random.split(key, 5)
        s = 1.0 / np.sqrt(HIDDEN)
        return {'x': jax.random.normal(kx, (BATCH, SEQ, HIDDEN), dtype=jnp.float32), 'Wq': jax.random.uniform(kq, (HIDDEN, HIDDEN), jnp.float32, -s, s), 'Wk': jax.random.uniform(kk, (KV_DIM, HIDDEN), jnp.float32, -s, s), 'Wv': jax.random.uniform(kv, (KV_DIM, HIDDEN), jnp.float32, -s, s), 'Wo': jax.random.uniform(ko, (HIDDEN, KV_DIM), jnp.float32, -s, s)}
    _L2_attn_all = _L2_attn_setup()
    _L2_attn_in = {k: v for k, v in _L2_attn_all.items() if k in ('Wq', 'Wk', 'Wv', 'Wo')}
    del _L2_attn_all

    def _L2_ffn_setup():
        import jax, jax.numpy as jnp
        import numpy as np
        ACT_SCALE = 0.02
        W_SCALE = 0.01
        EFF_SCALE = ACT_SCALE * W_SCALE
        B, S, D, M = (8, 1024, 192, 192)
        key = jax.random.key(seed)
        kx, kw, kb = jax.random.split(key, 3)
        x = jax.random.normal(kx, (B, S, D), dtype=jnp.float32)
        weight_t = jax.random.randint(kw, (D, M), -128, 128, dtype=jnp.int32).astype(jnp.int8)
        bias = jax.random.normal(kb, (M,), dtype=jnp.float32)
        return {'x': x, 'weight_t': weight_t, 'bias': bias}
    _L2_ffn_all = _L2_ffn_setup()
    _L2_ffn_in = {k: v for k, v in _L2_ffn_all.items() if k in ('weight_t', 'bias')}
    del _L2_ffn_all

    def _L3_attn_setup():
        import jax, jax.numpy as jnp
        import numpy as np
        EMBED_DIM = 192
        NUM_HEADS = 12
        HEAD_DIM = EMBED_DIM // NUM_HEADS
        MAX_WAVELENGTH = 10000.0
        ROPE_PERCENT = 0.5

        def p_rope(x, positions):
            rope_angles = int(ROPE_PERCENT * HEAD_DIM) // 2
            nope_angles = HEAD_DIM // 2 - rope_angles
            fraction = 2.0 * jnp.arange(rope_angles, dtype=x.dtype) / HEAD_DIM
            timescale = MAX_WAVELENGTH ** fraction
            timescale = jnp.concatenate([timescale, jnp.full((nope_angles,), jnp.inf, dtype=x.dtype)])
            sinusoid = positions[:, None] / timescale[None, :]
            sin, cos = (jnp.sin(sinusoid), jnp.cos(sinusoid))
            x1, x2 = jnp.split(x, 2, axis=-1)
            return jnp.concatenate([x1 * cos - x2 * sin, x2 * cos + x1 * sin], axis=-1)

        def _shape(x, B, S):
            return x.reshape(B, S, NUM_HEADS, HEAD_DIM).transpose(0, 2, 1, 3).reshape(B * NUM_HEADS, S, HEAD_DIM)
        key = jax.random.key(seed)
        ks = jax.random.split(key, 9)
        B, T, E = (16, 256, EMBED_DIM)
        s = 0.02
        return {'hidden_states': jax.random.normal(ks[0], (B, T, E), jnp.float32), 'wq': jax.random.normal(ks[1], (E, E), jnp.float32) * s, 'bq': jax.random.normal(ks[2], (E,), jnp.float32) * s, 'wk': jax.random.normal(ks[3], (E, E), jnp.float32) * s, 'bk': jax.random.normal(ks[4], (E,), jnp.float32) * s, 'wv': jax.random.normal(ks[5], (E, E), jnp.float32) * s, 'bv': jax.random.normal(ks[6], (E,), jnp.float32) * s, 'wo': jax.random.normal(ks[7], (E, E), jnp.float32) * s, 'bo': jax.random.normal(ks[8], (E,), jnp.float32) * s}
    _L3_attn_all = _L3_attn_setup()
    _L3_attn_in = {k: v for k, v in _L3_attn_all.items() if k in ('wq', 'bq', 'wk', 'bk', 'wv', 'bv', 'wo', 'bo')}
    del _L3_attn_all

    def _L3_ffn_setup():
        import jax, jax.numpy as jnp
        import numpy as np
        B, T, C, H, E, TOPK, DR = (2, 512, 192, 768, 8, 2, 24)

        def _normalize(v, axis=-1, eps=1e-12):
            return v / jnp.maximum(jnp.linalg.norm(v, axis=axis, keepdims=True), eps)
        key = jax.random.key(seed)
        ks = jax.random.split(key, 16)
        std = 0.02
        n = lambda k, shape, s=std: (s * jax.random.normal(k, shape)).astype(jnp.float32)
        emb = jax.random.normal(ks[3], (E, DR), dtype=jnp.float32)
        emb = emb / (jnp.linalg.norm(emb, axis=-1, keepdims=True) + 1e-08)
        return {'x': jax.random.normal(ks[0], (B, T, C), dtype=jnp.float32), 'router_w': n(ks[1], (E, C)), 'probe_w': n(ks[2], (DR, C)), 'router_emb': emb, 'fatigue': jnp.zeros((E,), jnp.float32), 'energy': jnp.ones((E,), jnp.float32), 'w_fast1': n(ks[4], (E, C, H)), 'w_slow1': n(ks[5], (E, C, H)), 'h_fast1': n(ks[6], (E, C, H), 0.005), 'm_gate1': jax.random.uniform(ks[7], (E,), dtype=jnp.float32), 'b1': jnp.zeros((E, H), jnp.float32), 'w_fast2': n(ks[8], (E, H, C)), 'w_slow2': n(ks[9], (E, H, C)), 'h_fast2': n(ks[10], (E, H, C), 0.005), 'm_gate2': jax.random.uniform(ks[11], (E,), dtype=jnp.float32), 'b2': jnp.zeros((E, C), jnp.float32)}
    _L3_ffn_all = _L3_ffn_setup()
    _L3_ffn_in = {k: v for k, v in _L3_ffn_all.items() if k in ('router_w', 'probe_w', 'router_emb', 'fatigue', 'energy', 'w_fast1', 'w_slow1', 'h_fast1', 'm_gate1', 'b1', 'w_fast2', 'w_slow2', 'h_fast2', 'm_gate2', 'b2')}
    del _L3_ffn_all
    return {'x': x, 'txt': txt, 'L0_tok_W': _L0_tok_in['W'], 'L0_tok_b': _L0_tok_in['b'], 'L0_tok_class_token': _L0_tok_in['class_token'], 'L0_tok_pos_embedding': _L0_tok_in['pos_embedding'], 'L0_attn_W_qkv': _L0_attn_in['W_qkv'], 'L0_attn_b_qkv': _L0_attn_in['b_qkv'], 'L0_ffn_Wqkv': _L0_ffn_in['Wqkv'], 'L0_ffn_Wproj': _L0_ffn_in['Wproj'], 'L0_ffn_Wrouter': _L0_ffn_in['Wrouter'], 'L0_ffn_W1': _L0_ffn_in['W1'], 'L0_ffn_W2': _L0_ffn_in['W2'], 'L0_ffn_ln1_g': _L0_ffn_in['ln1_g'], 'L0_ffn_ln1_b': _L0_ffn_in['ln1_b'], 'L0_ffn_ln2_g': _L0_ffn_in['ln2_g'], 'L0_ffn_ln2_b': _L0_ffn_in['ln2_b'], 'L1_attn_Wi': _L1_attn_in['Wi'], 'L1_attn_bi': _L1_attn_in['bi'], 'L1_attn_Wconv': _L1_attn_in['Wconv'], 'L1_attn_bconv': _L1_attn_in['bconv'], 'L1_attn_Wdt': _L1_attn_in['Wdt'], 'L1_attn_bdt': _L1_attn_in['bdt'], 'L1_attn_WB': _L1_attn_in['WB'], 'L1_attn_bB': _L1_attn_in['bB'], 'L1_attn_WC': _L1_attn_in['WC'], 'L1_attn_bC': _L1_attn_in['bC'], 'L1_attn_A_log': _L1_attn_in['A_log'], 'L1_attn_D': _L1_attn_in['D'], 'L1_attn_Wo': _L1_attn_in['Wo'], 'L1_attn_bo': _L1_attn_in['bo'], 'L1_ffn_qkv_w': _L1_ffn_in['qkv_w'], 'L1_ffn_qkv_b': _L1_ffn_in['qkv_b'], 'L1_ffn_q_norm_w': _L1_ffn_in['q_norm_w'], 'L1_ffn_q_norm_b': _L1_ffn_in['q_norm_b'], 'L1_ffn_k_norm_w': _L1_ffn_in['k_norm_w'], 'L1_ffn_k_norm_b': _L1_ffn_in['k_norm_b'], 'L1_ffn_wg_w': _L1_ffn_in['wg_w'], 'L1_ffn_wg0_w': _L1_ffn_in['wg0_w'], 'L1_ffn_wg1_w': _L1_ffn_in['wg1_w'], 'L1_ffn_proj_w': _L1_ffn_in['proj_w'], 'L1_ffn_proj_b': _L1_ffn_in['proj_b'], 'L2_attn_Wq': _L2_attn_in['Wq'], 'L2_attn_Wk': _L2_attn_in['Wk'], 'L2_attn_Wv': _L2_attn_in['Wv'], 'L2_attn_Wo': _L2_attn_in['Wo'], 'L2_ffn_weight_t': _L2_ffn_in['weight_t'], 'L2_ffn_bias': _L2_ffn_in['bias'], 'L3_attn_wq': _L3_attn_in['wq'], 'L3_attn_bq': _L3_attn_in['bq'], 'L3_attn_wk': _L3_attn_in['wk'], 'L3_attn_bk': _L3_attn_in['bk'], 'L3_attn_wv': _L3_attn_in['wv'], 'L3_attn_bv': _L3_attn_in['bv'], 'L3_attn_wo': _L3_attn_in['wo'], 'L3_attn_bo': _L3_attn_in['bo'], 'L3_ffn_router_w': _L3_ffn_in['router_w'], 'L3_ffn_probe_w': _L3_ffn_in['probe_w'], 'L3_ffn_router_emb': _L3_ffn_in['router_emb'], 'L3_ffn_fatigue': _L3_ffn_in['fatigue'], 'L3_ffn_energy': _L3_ffn_in['energy'], 'L3_ffn_w_fast1': _L3_ffn_in['w_fast1'], 'L3_ffn_w_slow1': _L3_ffn_in['w_slow1'], 'L3_ffn_h_fast1': _L3_ffn_in['h_fast1'], 'L3_ffn_m_gate1': _L3_ffn_in['m_gate1'], 'L3_ffn_b1': _L3_ffn_in['b1'], 'L3_ffn_w_fast2': _L3_ffn_in['w_fast2'], 'L3_ffn_w_slow2': _L3_ffn_in['w_slow2'], 'L3_ffn_h_fast2': _L3_ffn_in['h_fast2'], 'L3_ffn_m_gate2': _L3_ffn_in['m_gate2'], 'L3_ffn_b2': _L3_ffn_in['b2']}

def reference(x, txt, L0_tok_W, L0_tok_b, L0_tok_class_token, L0_tok_pos_embedding, L0_attn_W_qkv, L0_attn_b_qkv, L0_ffn_Wqkv, L0_ffn_Wproj, L0_ffn_Wrouter, L0_ffn_W1, L0_ffn_W2, L0_ffn_ln1_g, L0_ffn_ln1_b, L0_ffn_ln2_g, L0_ffn_ln2_b, L1_attn_Wi, L1_attn_bi, L1_attn_Wconv, L1_attn_bconv, L1_attn_Wdt, L1_attn_bdt, L1_attn_WB, L1_attn_bB, L1_attn_WC, L1_attn_bC, L1_attn_A_log, L1_attn_D, L1_attn_Wo, L1_attn_bo, L1_ffn_qkv_w, L1_ffn_qkv_b, L1_ffn_q_norm_w, L1_ffn_q_norm_b, L1_ffn_k_norm_w, L1_ffn_k_norm_b, L1_ffn_wg_w, L1_ffn_wg0_w, L1_ffn_wg1_w, L1_ffn_proj_w, L1_ffn_proj_b, L2_attn_Wq, L2_attn_Wk, L2_attn_Wv, L2_attn_Wo, L2_ffn_weight_t, L2_ffn_bias, L3_attn_wq, L3_attn_bq, L3_attn_wk, L3_attn_bk, L3_attn_wv, L3_attn_bv, L3_attn_wo, L3_attn_bo, L3_ffn_router_w, L3_ffn_probe_w, L3_ffn_router_emb, L3_ffn_fatigue, L3_ffn_energy, L3_ffn_w_fast1, L3_ffn_w_slow1, L3_ffn_h_fast1, L3_ffn_m_gate1, L3_ffn_b1, L3_ffn_w_fast2, L3_ffn_w_slow2, L3_ffn_h_fast2, L3_ffn_m_gate2, L3_ffn_b2):
    import jax
    import jax.numpy as jnp

    def _L0_tok_ref(image, W, b, class_token, pos_embedding):
        import jax, jax.numpy as jnp
        import numpy as np
        IMAGE_SIZE = 96
        PATCH = 16
        CHANNELS = 3
        TOKEN_DIM = 192
        NUM_PATCHES = (IMAGE_SIZE // PATCH) ** 2
        PATCH_DIM = CHANNELS * PATCH * PATCH
        N_TOKENS = NUM_PATCHES + 1

        def _fixed_pos_embedding(n_tokens, dim):
            i = np.arange(n_tokens, dtype=np.float32)[:, None]
            j = np.arange(dim, dtype=np.float32)[None, :]
            j_even = np.where(j % 2 == 0, j, j - 1)
            angle = i / np.power(10000.0, j_even / dim)
            tab = np.where(j % 2 == 0, np.sin(angle), np.cos(angle)).astype(np.float32)
            return jnp.asarray(tab)

        def _make_patches(image):
            B, C, H, Wd = image.shape
            p = PATCH
            hp, wp = (H // p, Wd // p)
            x = image.reshape(B, C, hp, p, wp, p)
            x = x.transpose(0, 1, 2, 4, 3, 5)
            return x.reshape(B, hp * wp, C * p * p)
        patches = _make_patches(image)
        tokens = jnp.einsum('bnd,td->bnt', patches, W) + b
        B = tokens.shape[0]
        cls = jnp.broadcast_to(class_token[None, :, :], (B, 1, TOKEN_DIM))
        tokens = jnp.concatenate([cls, tokens], axis=1)
        return tokens + pos_embedding[None, :, :]

    def _L0_attn_ref(x, W_qkv, b_qkv):
        import math
        import jax, jax.numpy as jnp
        import numpy as np
        B, N, D_IN, D_OUT = (8, 512, 192, 192)
        d_out = D_OUT
        qkv = jnp.einsum('bnd,de->bne', x, W_qkv) + b_qkv
        q = qkv[:, :, :d_out]
        k = qkv[:, :, d_out:2 * d_out]
        v = qkv[:, :, 2 * d_out:3 * d_out]
        scale = 1.0 / math.sqrt(d_out)
        scores = jnp.einsum('bqd,bkd->bqk', q, k) * scale
        attn = jax.nn.softmax(scores, axis=-1)
        context = jnp.einsum('bqk,bkd->bqd', attn, v)
        return context

    def _L0_ffn_ref(x, Wqkv, Wproj, Wrouter, W1, W2, ln1_g, ln1_b, ln2_g, ln2_b):
        import jax, jax.numpy as jnp
        import numpy as np
        DIM = 192
        FF = 768
        E = 8
        K = 2
        H = 12
        HD = DIM // H
        LN_EPS = 1e-05

        def _layernorm(x, g, b):
            m = jnp.mean(x, axis=-1, keepdims=True)
            v = jnp.var(x, axis=-1, keepdims=True)
            return (x - m) * jax.lax.rsqrt(v + LN_EPS) * g + b

        def _attention(x, Wqkv, Wproj):
            B, T, D = x.shape
            qkv = (x @ Wqkv).reshape(B, T, 3, H, HD)
            q, k, v = (qkv[:, :, 0], qkv[:, :, 1], qkv[:, :, 2])
            scores = jnp.einsum('bqhd,bkhd->bhqk', q, k) * jnp.float32(HD) ** (-0.5)
            attn = jax.nn.softmax(scores, axis=-1)
            out = jnp.einsum('bhqk,bkhd->bqhd', attn, v).reshape(B, T, D)
            return out @ Wproj

        def _moe(x, Wrouter, W1, W2):
            B, T, D = x.shape
            xf = x.reshape(-1, D)
            N = xf.shape[0]
            logits = xf @ Wrouter
            topk_w, topk_idx = jax.lax.top_k(logits, K)
            topk_w = jax.nn.softmax(topk_w.astype(jnp.float32), axis=-1).astype(x.dtype)
            we = jnp.zeros((N, E), x.dtype).at[jnp.arange(N)[:, None], topk_idx].add(topk_w)

            def body(acc, expert):
                W1e, W2e, we_e = expert
                h = jax.nn.gelu(xf @ W1e, approximate=False)
                return (acc + we_e[:, None] * (h @ W2e), None)
            out, _ = jax.lax.scan(body, jnp.zeros_like(xf), (W1, W2, we.T))
            return out.reshape(B, T, D)
        x = x + _attention(_layernorm(x, ln1_g, ln1_b), Wqkv, Wproj)
        x = x + _moe(_layernorm(x, ln2_g, ln2_b), Wrouter, W1, W2)
        return x

    def _L1_attn_ref(x, Wi, bi, Wconv, bconv, Wdt, bdt, WB, bB, WC, bC, A_log, D, Wo, bo):
        import jax, jax.numpy as jnp
        import numpy as np
        D_MODEL = 192
        D_STATE = 16
        K_CONV = 4
        BATCH = 2
        SEQ = 512

        def _forward(x, Wi, bi, Wconv, bconv, Wdt, bdt, WB, bB, WC, bC, A_log, D, Wo, bo):
            B, L, dm = x.shape
            ds = A_log.shape[1]
            K = Wconv.shape[1]
            uv = x @ Wi + bi
            u, v = (uv[..., :dm], uv[..., dm:])
            u_pad = jnp.pad(u, ((0, 0), (K - 1, 0), (0, 0)))
            u_conv = bconv + sum((u_pad[:, k:k + L, :] * Wconv[:, k] for k in range(K)))
            dt = jax.nn.softplus(u_conv @ Wdt + bdt)
            Bt = (u_conv @ WB + bB).reshape(B, L, dm, ds)
            Ct = (u_conv @ WC + bC).reshape(B, L, dm, ds)
            A = -jnp.exp(A_log)

            def step(s, inputs):
                dt_t, u_t, B_tt, C_tt = inputs
                dt_e = dt_t[..., None]
                s = s * jnp.exp(dt_e * A) + dt_e * B_tt * u_t[..., None]
                y = jnp.sum(C_tt * s, axis=-1) + D * u_t
                return (s, y)
            s0 = jnp.zeros((B, dm, ds), x.dtype)
            xs = (dt.transpose(1, 0, 2), u_conv.transpose(1, 0, 2), Bt.transpose(1, 0, 2, 3), Ct.transpose(1, 0, 2, 3))
            _, ys = jax.lax.scan(step, s0, xs)
            y = ys.transpose(1, 0, 2)
            y = y * jax.nn.sigmoid(v)
            return y @ Wo + bo
        return _forward(x, Wi, bi, Wconv, bconv, Wdt, bdt, WB, bB, WC, bC, A_log, D, Wo, bo)

    def _L1_ffn_ref(x, qkv_w, qkv_b, q_norm_w, q_norm_b, k_norm_w, k_norm_b, wg_w, wg0_w, wg1_w, proj_w, proj_b):
        import jax, jax.numpy as jnp
        import numpy as np
        DIM = 192
        H = 12
        HD = 64
        SHARED = 2
        ROUTED = 2
        E_ROUTED = H - SHARED
        LN_EPS = 1e-05

        def _layernorm(x, w, b):
            m = x.mean(-1, keepdims=True)
            v = ((x - m) ** 2).mean(-1, keepdims=True)
            return (x - m) * jax.lax.rsqrt(v + LN_EPS) * w + b
        B, N, C = x.shape
        scale = HD ** (-0.5)
        gates = jax.nn.softmax(x @ wg_w, axis=-1)
        _, idx = jax.lax.top_k(gates, ROUTED)
        mask = jax.nn.one_hot(idx, E_ROUTED, dtype=gates.dtype).sum(-2)
        rg = gates * mask
        denom = jnp.clip(rg.sum(-1, keepdims=True), jnp.finfo(rg.dtype).eps, None)
        routed_gates = rg / denom * ROUTED
        qkv = (x @ qkv_w + qkv_b).reshape(B, N, 3, H, HD)
        qkv = jnp.transpose(qkv, (2, 0, 3, 1, 4))
        q, k, v = (qkv[0], qkv[1], qkv[2])
        q = _layernorm(q, q_norm_w, q_norm_b)
        k = _layernorm(k, k_norm_w, k_norm_b)
        attn = jax.nn.softmax(jnp.einsum('bhqd,bhkd->bhqk', q * scale, k), axis=-1)
        o = jnp.einsum('bhqk,bhkd->bhqd', attn, v)
        o = jnp.transpose(o, (0, 2, 1, 3))
        shared_gates = jax.nn.softmax(x @ wg1_w, axis=-1) * SHARED
        w0 = jax.nn.softmax(x @ wg0_w, axis=-1) * 2.0
        shared_gates = w0[..., 0:1] * shared_gates
        routed_gates = w0[..., 1:2] * routed_gates
        masked_gates = jnp.concatenate([shared_gates, routed_gates], axis=-1)
        o = (masked_gates[..., None] * o).reshape(B, N, H * HD)
        return o @ proj_w + proj_b

    def _L2_attn_ref(x, Wq, Wk, Wv, Wo):
        import jax, jax.numpy as jnp
        import numpy as np
        HIDDEN = 192
        KV_DIM = HIDDEN // 3
        BATCH, SEQ = (2, 2048)
        THETA = 10000.0

        def rope_table(seq_len, dim):
            pos = jnp.arange(seq_len, dtype=jnp.float32)
            freqs = THETA ** (-jnp.arange(0, dim, 2, dtype=jnp.float32) / dim)
            ang = pos[:, None] * freqs[None, :]
            return jnp.concatenate([jnp.sin(ang), jnp.cos(ang)], axis=-1)[None]
        B, S, H = x.shape
        q = jnp.einsum('bsh,oh->bso', x, Wq)
        k = jnp.einsum('bsh,oh->bso', x, Wk)
        v = jnp.einsum('bsh,oh->bso', x, Wv)
        r = rope_table(S, H)
        attn_weights = jnp.matmul(r, jnp.swapaxes(r, -2, -1))
        attn_probs = jax.nn.softmax(attn_weights, axis=-1)
        attn_output = jnp.matmul(attn_probs, v)
        out = jnp.einsum('bsk,ok->bso', attn_output, Wo)
        return out

    def _L2_ffn_ref(x, weight_t, bias):
        import jax, jax.numpy as jnp
        import numpy as np
        ACT_SCALE = 0.02
        W_SCALE = 0.01
        EFF_SCALE = ACT_SCALE * W_SCALE
        B, S, D, M = (8, 1024, 192, 192)
        orig_shape = x.shape
        x_flat = x.reshape(-1, orig_shape[-1])
        x_int8 = jnp.clip(jnp.round(x_flat / ACT_SCALE), -128, 127).astype(jnp.int8)
        acc_i32 = jnp.matmul(x_int8, weight_t, preferred_element_type=jnp.int32)
        out = acc_i32.astype(jnp.float32) * jnp.float32(EFF_SCALE) + bias
        return out.reshape(orig_shape[:-1] + (M,))

    def _L3_attn_ref(hidden_states, wq, bq, wk, bk, wv, bv, wo, bo):
        import jax, jax.numpy as jnp
        import numpy as np
        EMBED_DIM = 192
        NUM_HEADS = 12
        HEAD_DIM = EMBED_DIM // NUM_HEADS
        MAX_WAVELENGTH = 10000.0
        ROPE_PERCENT = 0.5

        def p_rope(x, positions):
            rope_angles = int(ROPE_PERCENT * HEAD_DIM) // 2
            nope_angles = HEAD_DIM // 2 - rope_angles
            fraction = 2.0 * jnp.arange(rope_angles, dtype=x.dtype) / HEAD_DIM
            timescale = MAX_WAVELENGTH ** fraction
            timescale = jnp.concatenate([timescale, jnp.full((nope_angles,), jnp.inf, dtype=x.dtype)])
            sinusoid = positions[:, None] / timescale[None, :]
            sin, cos = (jnp.sin(sinusoid), jnp.cos(sinusoid))
            x1, x2 = jnp.split(x, 2, axis=-1)
            return jnp.concatenate([x1 * cos - x2 * sin, x2 * cos + x1 * sin], axis=-1)

        def _shape(x, B, S):
            return x.reshape(B, S, NUM_HEADS, HEAD_DIM).transpose(0, 2, 1, 3).reshape(B * NUM_HEADS, S, HEAD_DIM)
        B, T, E = hidden_states.shape
        scaling = HEAD_DIM ** (-0.5)
        q = (hidden_states @ wq.T + bq) * scaling
        k = hidden_states @ wk.T + bk
        v = hidden_states @ wv.T + bv
        q = _shape(q, B, T)
        k = _shape(k, B, T)
        v = _shape(v, B, T)
        positions = jnp.arange(T, dtype=hidden_states.dtype)
        k = p_rope(k, positions)
        q = p_rope(q, positions)
        attn = jnp.einsum('bqd,bkd->bqk', q, k)
        attn = jax.nn.softmax(attn, axis=-1)
        out = jnp.einsum('bqk,bkd->bqd', attn, v)
        out = out.reshape(B, NUM_HEADS, T, HEAD_DIM).transpose(0, 2, 1, 3).reshape(B, T, E)
        return out @ wo.T + bo

    def _L3_ffn_ref(x, router_w, probe_w, router_emb, fatigue, energy, w_fast1, w_slow1, h_fast1, m_gate1, b1, w_fast2, w_slow2, h_fast2, m_gate2, b2):
        import jax, jax.numpy as jnp
        import numpy as np
        B, T, C, H, E, TOPK, DR = (2, 512, 192, 768, 8, 2, 24)

        def _normalize(v, axis=-1, eps=1e-12):
            return v / jnp.maximum(jnp.linalg.norm(v, axis=axis, keepdims=True), eps)
        Bd, Td, Cd = x.shape
        logits = jnp.einsum('btc,ec->bte', x, router_w)
        tok_proxy = x.mean(axis=-1, keepdims=True)
        router_gain = jnp.linalg.norm(router_emb, axis=-1)
        base_bias = 0.02 * tok_proxy
        gain_bias = 0.02 * tok_proxy * router_gain
        tok_unit = _normalize(jnp.einsum('btc,dc->btd', x, probe_w))
        align_bias = 0.02 * jnp.einsum('btd,ed->bte', tok_unit, _normalize(router_emb))
        logits = logits + base_bias + gain_bias + align_bias + 0.1 * energy - 0.1 * fatigue
        g, idx = jax.lax.top_k(logits, TOPK)
        gates = jax.nn.softmax(g, axis=-1)
        N = Bd * Td
        gates_full = jnp.zeros((N, E), x.dtype).at[jnp.arange(N)[:, None], idx.reshape(N, TOPK)].set(gates.reshape(N, TOPK))
        flat_x = x.reshape(N, Cd)

        def body(acc, p):
            wf1, ws1, hf1, mg1, bb1, wf2, ws2, hf2, mg2, bb2, ge = p
            W1 = wf1 + mg1 * ws1 + hf1
            h = jnp.square(jnp.maximum(flat_x @ W1 + bb1, 0.0))
            W2 = wf2 + mg2 * ws2 + hf2
            y = h @ W2 + bb2
            return (acc + ge[:, None] * y, None)
        out, _ = jax.lax.scan(body, jnp.zeros((N, Cd), x.dtype), (w_fast1, w_slow1, h_fast1, m_gate1, b1, w_fast2, w_slow2, h_fast2, m_gate2, b2, gates_full.T))
        return out.reshape(Bd, Td, Cd)
    h = _L0_tok_ref(x, L0_tok_W, L0_tok_b, L0_tok_class_token, L0_tok_pos_embedding)
    h = jnp.concatenate([h, txt], axis=1)
    h = h + _L0_attn_ref(_layernorm(h, axis=-1), L0_attn_W_qkv, L0_attn_b_qkv)
    h = h + _L0_ffn_ref(_layernorm(h, axis=-1), L0_ffn_Wqkv, L0_ffn_Wproj, L0_ffn_Wrouter, L0_ffn_W1, L0_ffn_W2, L0_ffn_ln1_g, L0_ffn_ln1_b, L0_ffn_ln2_g, L0_ffn_ln2_b)
    h = h + _L1_attn_ref(_layernorm(h, axis=-1), L1_attn_Wi, L1_attn_bi, L1_attn_Wconv, L1_attn_bconv, L1_attn_Wdt, L1_attn_bdt, L1_attn_WB, L1_attn_bB, L1_attn_WC, L1_attn_bC, L1_attn_A_log, L1_attn_D, L1_attn_Wo, L1_attn_bo)
    h = h + _L1_ffn_ref(_layernorm(h, axis=-1), L1_ffn_qkv_w, L1_ffn_qkv_b, L1_ffn_q_norm_w, L1_ffn_q_norm_b, L1_ffn_k_norm_w, L1_ffn_k_norm_b, L1_ffn_wg_w, L1_ffn_wg0_w, L1_ffn_wg1_w, L1_ffn_proj_w, L1_ffn_proj_b)
    h = h + _L2_attn_ref(_layernorm(h, axis=-1), L2_attn_Wq, L2_attn_Wk, L2_attn_Wv, L2_attn_Wo)
    h = h + _L2_ffn_ref(_layernorm(h, axis=-1), L2_ffn_weight_t, L2_ffn_bias)
    h = h + _L3_attn_ref(_layernorm(h, axis=-1), L3_attn_wq, L3_attn_bq, L3_attn_wk, L3_attn_bk, L3_attn_wv, L3_attn_bv, L3_attn_wo, L3_attn_bo)
    h = h + _L3_ffn_ref(_layernorm(h, axis=-1), L3_ffn_router_w, L3_ffn_probe_w, L3_ffn_router_emb, L3_ffn_fatigue, L3_ffn_energy, L3_ffn_w_fast1, L3_ffn_w_slow1, L3_ffn_h_fast1, L3_ffn_m_gate1, L3_ffn_b1, L3_ffn_w_fast2, L3_ffn_w_slow2, L3_ffn_h_fast2, L3_ffn_m_gate2, L3_ffn_b2)
    return h

_drawn_inputs = setup_inputs


def setup_inputs(seed=0):
    import zlib

    import numpy as np

    out = dict(_drawn_inputs(seed))
    spreads = {'L0_ffn_ln1_g': (1.0, 0.2),
     'L0_ffn_ln1_b': (0.0, 0.1),
     'L0_ffn_ln2_g': (1.0, 0.2),
     'L0_ffn_ln2_b': (0.0, 0.1),
     'L1_attn_bi': (0.0, 0.8),
     'L1_attn_bconv': (0.0, 0.773),
     'L1_attn_bdt': (0.0, 0.8),
     'L1_attn_bB': (0.0, 0.8),
     'L1_attn_bC': (0.0, 0.8),
     'L1_attn_A_log': (0.0, 0.8),
     'L1_attn_D': (1.0, 0.6),
     'L1_attn_bo': (0.0, 0.1),
     'L1_ffn_qkv_b': (0.0, 0.512),
     'L1_ffn_q_norm_w': (1.0, 0.6),
     'L1_ffn_q_norm_b': (0.0, 0.8),
     'L1_ffn_k_norm_w': (1.0, 0.6),
     'L1_ffn_k_norm_b': (0.0, 2.0),
     'L1_ffn_proj_b': (0.0, 0.337),
     'L3_ffn_fatigue': (0.0, 0.8),
     'L3_ffn_energy': (1.0, 0.6),
     'L3_ffn_b1': (0.0, 0.8),
     'L3_ffn_b2': (0.0, 2.0)}
    factors = {'L0_tok_b': 5.616,
     'L1_attn_Wi': 8.0,
     'L1_attn_Wconv': 8.0,
     'L1_attn_Wdt': 8.0,
     'L1_attn_WB': 8.0,
     'L1_attn_WC': 8.0,
     'L1_attn_Wo': 6.739,
     'L1_ffn_qkv_w': 4.755,
     'L1_ffn_wg_w': 4.529,
     'L1_ffn_wg0_w': 8.0,
     'L1_ffn_wg1_w': 8.0,
     'L1_ffn_proj_w': 3.052,
     'L3_attn_wq': 8.0,
     'L3_attn_bq': 8.0,
     'L3_attn_wk': 8.0,
     'L3_attn_bk': 8.0,
     'L3_attn_wv': 8.0,
     'L3_attn_bv': 8.0,
     'L3_attn_wo': 8.0,
     'L3_attn_bo': 8.0,
     'L3_ffn_router_w': 7.11,
     'L3_ffn_probe_w': 8.0,
     'L3_ffn_router_emb': 8.0,
     'L3_ffn_w_fast1': 8.0,
     'L3_ffn_w_slow1': 8.0,
     'L3_ffn_h_fast1': 8.0,
     'L3_ffn_m_gate1': 8.0,
     'L3_ffn_w_fast2': 8.0,
     'L3_ffn_w_slow2': 8.0,
     'L3_ffn_h_fast2': 8.0,
     'L3_ffn_m_gate2': 8.0,
     'L2_attn_Wo': 2.843}
    for name, (base, spread) in spreads.items():
        noise = np.random.default_rng([zlib.crc32(name.encode()), seed]).standard_normal(out[name].shape)
        drawn = base * np.exp(spread * noise) if base else spread * noise
        out[name] = jnp.asarray(drawn.astype(out[name].dtype))
    for name, factor in factors.items():
        out[name] = (out[name] * factor).astype(out[name].dtype)
    return out
```

```python
from contextlib import ExitStack

import concourse.bass as bass
from concourse import mybir

F32 = mybir.dt.float32
BF16 = mybir.dt.bfloat16
U32 = mybir.dt.uint32
I8 = mybir.dt.int8
I32 = mybir.dt.int32
ALU = mybir.AluOpType
ACT = mybir.ActivationFunctionType
AX = mybir.AxisListType

SAMPLES = 16
IMG = 36
FRONT = IMG + 1
TXT = 77
T = FRONT + TXT
D = 192
C = D // 2
GROUP = 4
TURNS = SAMPLES // GROUP
N = GROUP * T
PATCH_K = 768 // 128
EPS = 1e-5
HEADS = 12
EXPERTS = 8
FF = 768
FC = FF // 128


START = 5


def turn(i, n=1, per=1):
    return i * per + n + START


def cols(b, width=T):
    return slice(b * width, (b + 1) * width)


class Core:
    pass


def stage_tools(core, ctx):
    nc = core.nc

    def sb(name, shape, dtype=F32):
        core.made += 1
        return ctx.enter_context(nc.sbuf_tensor(f"{name}_{core.made}", shape, dtype))

    raised, every = [], []
    ctx.callback(lambda: (nc.clear_and_free_semaphores(every), nc.all_engine_barrier()))

    def load_sem(name):
        core.made += 1
        every.append(nc.alloc_semaphore(f"{name}_{core.made}"))
        return every[-1]

    def sem(name):
        raised.append(load_sem(name))
        return raised[-1]

    return sb, sem, load_sem, raised


def raise_to_start(sp, raised):
    for s in raised:
        sp.sem_inc(s, START)


def sample_of(h, i, b):
    return h[:, bass.ds(i * (GROUP * D) + b * D, D)]



class Norm:

    def __init__(self, sb, sem, tag):
        self.stats = sb(f"{tag}_stats", [T, GROUP, 6])
        self.mean_var = sb(f"{tag}_mean_var", [T, GROUP, 2])
        self.var_eps = sb(f"{tag}_var_eps", [T, GROUP])
        self.rstd = sb(f"{tag}_rstd", [T, GROUP])
        self.var_ready = sem(f"{tag}_var_ready")
        self.rstd_ready = sem(f"{tag}_rstd_ready")


def norm_statistics(v, norm, source):
    for b in range(GROUP):
        v.bn_stats(norm.stats[:, b, :], source(b))
    v.drain()
    for b in range(GROUP):
        v.bn_aggr(norm.mean_var[:, b, :], norm.stats[:, b, :])
    v.drain()
    v.tensor_scalar(norm.var_eps[:, :], norm.mean_var[:, :, 1], EPS, None, ALU.add).then_inc(norm.var_ready, 1)


def norm_rstd(pool, core, norm, i):
    pool.wait_ge(norm.var_ready, turn(i))
    pool.tensor_tensor(norm.rstd[:, :], norm.var_eps[:, :], core.minus_half[0:T, 0:GROUP],
                       ALU.pow).then_inc(norm.rstd_ready, 1)


def norm_apply(v, norm, source, target, b):
    return v.tensor_scalar(target(b), source(b), norm.mean_var[:, b, 0:1], norm.rstd[:, b:b + 1],
                           ALU.subtract, ALU.mult)


def transpose_group(pe, core, banks, source, done):
    for c in range(2):
        for b in range(GROUP):
            mm = pe.transpose(banks[c][0:C, cols(b)], source[:, b, c * C:(c + 1) * C], core.ident[0:T, 0:T])
    mm.then_inc(done, 1)



def tokens_stage(core, a):
    nc = core.nc
    with ExitStack() as ctx:
        sb, sem, load_sem, raised = stage_tools(core, ctx)
        patches = sb("patches", [128, PATCH_K, GROUP, FRONT])
        w = sb("w_patch", [128, PATCH_K, D])
        front = sb("front", [FRONT, D])
        pos = sb("pos", [FRONT, D])
        front_pos = sb("front_pos", [FRONT, D])
        const_loaded, text_loaded, w_loaded, patch_loaded = (
            load_sem(n) for n in ("const_loaded", "text_loaded", "w_loaded", "patch_loaded"))
        cleared = load_sem("cleared")
        tokens_psum, tokens_added = sem("tokens_psum"), sem("tokens_added")

        with nc.Block() as block:
            @block.sync
            def _(sp):
                raise_to_start(sp, raised)
                sp.dma_start(w[:, :, :], a["tok_w"]).then_inc(w_loaded, 16)
                sp.dma_start(front[1:FRONT, :], a["tok_b"].to_broadcast([IMG, D])).then_inc(w_loaded, 16)
                sp.dma_start(front[0:1, :], a["cls"]).then_inc(w_loaded, 16)
                sp.dma_start(pos[:, :], a["pos"]).then_inc(w_loaded, 16)
                sp.wait_ge(cleared, 1)
                with sp.Fori(0, TURNS) as i:
                    sp.wait_ge(tokens_psum, turn(i, 0))
                    for k in range(PATCH_K):
                        sp.dma_start(patches[:, k, :, 1:FRONT],
                                     a["patches"][:, k, bass.ds(i * GROUP, GROUP), :]).then_inc(patch_loaded, 16)

            @block.scalar
            def _(act):
                act.dma_start(core.h[FRONT:T, :].rearrange("t (s d) -> t s d", d=D),
                              a["txt"].rearrange("s t d -> t s d")).then_inc(text_loaded, 16)
                for name, tile in core.constants.items():
                    act.dma_start(tile[tuple(slice(None) for _ in tile.shape)], a[name]).then_inc(const_loaded, 16)
                act.wait_ge(text_loaded, 16)
                act.wait_ge(const_loaded, 16 * len(core.constants))

            @block.gpsimd
            def _(pool):
                pool.memset(core.minus_half[:, :], -0.5)
                pool.memset(core.plus_half[:, :], 0.5)
                pool.memset(core.ones[:, :], 1.0)
                pool.memset(patches[:, :, :, 0:1], 0.0).then_inc(cleared, 1)

            @block.tensor
            def _(pe):
                pe.wait_ge(w_loaded, 64)
                pe.wait_ge(cleared, 1)
                with pe.Fori(0, TURNS) as i:
                    pe.wait_ge(patch_loaded, i * (16 * PATCH_K) + 16 * PATCH_K)
                    pe.wait_ge(tokens_added, turn(i, 0))
                    for b in range(GROUP):
                        for k in range(PATCH_K):
                            mm = pe.matmul(core.bank[b][0:FRONT, 0:D], patches[:, k, b, :], w[:, k, :],
                                           start=(k == 0), stop=(k == PATCH_K - 1))
                    mm.then_inc(tokens_psum, 1)

            @block.vector
            def _(v):
                v.wait_ge(w_loaded, 64)
                v.tensor_tensor(front_pos[:, :], front[:, :], pos[:, :], ALU.add)
                v.drain()
                with v.Fori(0, TURNS) as i:
                    v.wait_ge(tokens_psum, turn(i))
                    for b in range(GROUP):
                        add = v.tensor_tensor(core.h[0:FRONT, bass.ds(i * (GROUP * D) + b * D, D)],
                                              core.bank[b][0:FRONT, 0:D], front_pos[:, :], ALU.add)
                    add.then_inc(tokens_added, 1)



def wide_attention_stage(core, a):
    nc, bank, h = core.nc, core.bank, core.h
    scale = D ** -0.5
    with ExitStack() as ctx:
        sb, sem, load_sem, raised = stage_tools(core, ctx)
        norm = Norm(sb, sem, "norm")
        w = sb("w_qkv", [C, 2, 3 * D])
        bqk = sb("b_qk", [C, 4])
        bqk_s = sb("b_qk_scaled", [C, 4])
        bv = sb("b_v", [1, D])
        xn = sb("xn", [T, GROUP, D])
        xT = sb("xT", [C, 2, N])
        qkT = sb("qkT", [C, 4, N])
        vals = sb("vals", [T, GROUP, D])
        probs = sb("probs", [T, GROUP, T])
        probsT = sb("probsT", [T, GROUP, T])
        negmax = sb("negmax", [T, GROUP])
        total = sb("total", [T, GROUP])
        inv = sb("inv", [T, GROUP])
        w_loaded = load_sem("w_loaded")
        bias_scaled = load_sem("bias_scaled")
        names = ("xn_ready", "xT_psum", "xT_ready", "qk_psum", "qk_ready", "v_psum", "v_ready", "scores_psum",
                 "max_ready", "probs_ready", "probsT_psum", "probsT_ready", "context_psum", "h_done")
        s = {n: sem(n) for n in names}

        with nc.Block() as block:
            @block.sync
            def _(sp):
                raise_to_start(sp, raised)
                sp.dma_start(w[:, :, :], a["a_wqkv"]).then_inc(w_loaded, 16)
                sp.dma_start(bqk[:, :], a["a_bqk"]).then_inc(w_loaded, 16)
                sp.dma_start(bv[:, :], a["a_bv"]).then_inc(w_loaded, 16)

            @block.gpsimd
            def _(pool):
                with pool.Fori(0, TURNS) as i:
                    norm_rstd(pool, core, norm, i)

            @block.tensor
            def _(pe):
                pe.wait_ge(w_loaded, 48)
                with pe.Fori(0, TURNS) as i:
                    pe.wait_ge(s["probs_ready"], turn(i, 0))
                    pe.wait_ge(s["probsT_ready"], turn(i, 0))
                    pe.wait_ge(s["xn_ready"], turn(i))
                    transpose_group(pe, core, bank[0:2], xn, s["xT_psum"])
                    pe.wait_ge(s["h_done"], turn(i, 0))
                    pe.wait_ge(s["xT_ready"], turn(i))
                    for j in range(4):
                        for c in range(2):
                            mm = pe.matmul(bank[2 + j][0:C, 0:N], w[:, c, j * C:(j + 1) * C], xT[:, c, :],
                                           start=(c == 0), stop=(c == 1))
                    mm.then_inc(s["qk_psum"], 1)
                    pe.wait_ge(s["v_ready"], turn(i, 0))
                    for b in range(GROUP):
                        out = bank[6 + b // 2][0:T, (b % 2) * D:(b % 2 + 1) * D]
                        for c in range(2):
                            pe.matmul(out, xT[:, c, cols(b)], w[:, c, 2 * D:3 * D], start=(c == 0), stop=False)
                        mm = pe.matmul(out, core.ones[0:1, 0:T], bv[:, :], start=False, stop=True)
                    mm.then_inc(s["v_psum"], 1)
                    pe.wait_ge(s["qk_ready"], turn(i))
                    for b in range(GROUP):
                        for c in range(2):
                            mm = pe.matmul(bank[0][0:T, cols(b)], qkT[:, c, cols(b)], qkT[:, 2 + c, cols(b)],
                                           start=(c == 0), stop=(c == 1))
                    mm.then_inc(s["scores_psum"], 1)
                    pe.wait_ge(s["probs_ready"], turn(i))
                    for b in range(GROUP):
                        mm = pe.transpose(bank[1][0:T, cols(b)], probs[:, b, :], core.ident[0:T, 0:T])
                    mm.then_inc(s["probsT_psum"], 1)
                    pe.wait_ge(s["v_ready"], turn(i))
                    pe.wait_ge(s["probsT_ready"], turn(i))
                    for b in range(GROUP):
                        mm = pe.matmul(bank[2 + b // 2][0:T, (b % 2) * D:(b % 2 + 1) * D], probsT[:, b, :],
                                       vals[:, b, :], start=True, stop=True)
                    mm.then_inc(s["context_psum"], 1)

            @block.scalar
            def _(act):
                act.wait_ge(w_loaded, 48)
                act.wait_ge(bias_scaled, 1)
                with act.Fori(0, TURNS) as i:
                    act.wait_ge(s["v_psum"], turn(i, 0))
                    act.wait_ge(s["xT_psum"], turn(i))
                    for c in range(2):
                        ins = act.activation(xT[:, c, :], bank[c][0:C, 0:N], ACT.Copy)
                    ins.then_inc(s["xT_ready"], 1)
                    act.wait_ge(s["scores_psum"], turn(i, 0))
                    act.wait_ge(s["qk_psum"], turn(i))
                    for j in range(4):
                        ins = act.activation(qkT[:, j, :], bank[2 + j][0:C, 0:N], ACT.Identity,
                                             bias=bqk_s[:, j:j + 1], scale=scale if j < 2 else 1.0)
                    ins.then_inc(s["qk_ready"], 1)
                    act.wait_ge(s["probsT_psum"], turn(i, 0))
                    act.wait_ge(s["h_done"], turn(i, 0))
                    act.wait_ge(s["max_ready"], turn(i))
                    for b in range(GROUP):
                        ins = act.activation(probs[:, b, :], bank[0][0:T, cols(b)], ACT.Exp,
                                             bias=negmax[:, b:b + 1], accum_out=total[:, b:b + 1])
                    ins.then_inc(s["probs_ready"], 1)
                    act.wait_ge(s["context_psum"], turn(i, 0))
                    act.wait_ge(s["probsT_psum"], turn(i))
                    act.activation(probsT[:, :, :], bank[1][0:T, 0:N], ACT.Copy).then_inc(s["probsT_ready"], 1)

            @block.vector
            def _(v):
                v.wait_ge(w_loaded, 48)
                v.tensor_scalar(bqk_s[:, 0:2], bqk[:, 0:2], scale, None, ALU.mult)
                v.tensor_copy(bqk_s[:, 2:4], bqk[:, 2:4]).then_inc(bias_scaled, 1)
                with v.Fori(0, TURNS) as i:
                    norm_statistics(v, norm, lambda b: sample_of(h, i, b))
                    v.wait_ge(s["xT_psum"], turn(i, 0))
                    v.wait_ge(norm.rstd_ready, turn(i))
                    for b in range(GROUP):
                        ins = norm_apply(v, norm, lambda b: sample_of(h, i, b), lambda b: xn[:, b, :], b)
                    ins.then_inc(s["xn_ready"], 1)
                    v.wait_ge(s["context_psum"], turn(i, 0))
                    v.wait_ge(s["v_psum"], turn(i))
                    for p in range(2):
                        ins = v.tensor_copy(vals[:, 2 * p:2 * p + 2, :], bank[6 + p][0:T, 0:2 * D])
                    ins.then_inc(s["v_ready"], 1)
                    v.wait_ge(s["probs_ready"], turn(i, 0))
                    v.wait_ge(s["scores_psum"], turn(i))
                    v.tensor_reduce(negmax[:, :], bank[0][0:T, 0:N].rearrange("q (b k) -> q b k", b=GROUP),
                                    AX.X, ALU.max, negate=True).then_inc(s["max_ready"], 1)
                    v.wait_ge(s["probs_ready"], turn(i))
                    v.reciprocal(inv[:, :], total[:, :])
                    v.drain()
                    v.wait_ge(s["context_psum"], turn(i))
                    for b in range(GROUP):
                        ins = v.scalar_tensor_tensor(out=sample_of(h, i, b),
                                                     in0=bank[2 + b // 2][0:T, (b % 2) * D:(b % 2 + 1) * D],
                                                     scalar=inv[:, b:b + 1], in1=sample_of(h, i, b),
                                                     op0=ALU.mult, op1=ALU.add)
                    ins.then_inc(s["h_done"], 1)



class Heads:

    def __init__(self, core, sb, sem, head_dim, mask):
        self.core, self.head_dim, self.mask = core, head_dim, mask
        self.rows = mask.shape[0]
        self.per_chunk = self.rows // head_dim
        self.chunks = HEADS // self.per_chunk
        self.kblock = sb("kblock", [self.rows, GROUP, self.chunks, self.per_chunk, T])
        self.probs = sb("probs", [T, HEADS, T])
        self.probsT = sb("probsT", [T, HEADS, T])
        self.negmax = sb("negmax", [T, HEADS])
        self.total = sb("total", [T, HEADS])
        self.inv = sb("inv", [T, 2, HEADS])
        self.kblock_ready = sem("kblock_ready")
        self.scores_psum = sem("scores_psum")
        self.max_ready = sem("max_ready")
        self.probs_ready = sem("probs_ready")
        self.probsT_psum = sem("probsT_psum")
        self.probsT_ready = sem("probsT_ready")
        self.context_psum = sem("context_psum")
        self.context_done = sem("context_done")

    def scores_bank(self, m):
        return self.core.bank[m][0:T, 0:4 * T]

    def probsT_bank(self, m):
        return self.core.bank[3 + m][0:T, 0:4 * T]


def heads_pool(pool, att, i, kT, b):
    for c in range(att.chunks):
        shape = [att.rows, att.per_chunk, T]
        ins = pool.tensor_tensor(att.kblock[:, b, c, :, :],
                                 kT[:, c, cols(b)].unsqueeze(1).to_broadcast(shape),
                                 att.mask[:, :].unsqueeze(2).to_broadcast(shape), ALU.mult)
    ins.then_inc(att.kblock_ready, 1)


def heads_tensor(pe, att, i, qT, vals):
    core, hd = att.core, att.head_dim

    def scores(b):
        pe.wait_ge(att.probs_ready, turn(i, b, GROUP))
        pe.wait_ge(att.kblock_ready, turn(i, b + 1, GROUP))
        for c in range(att.chunks):
            first = c * att.per_chunk
            while first < (c + 1) * att.per_chunk:
                last = min((c + 1) * att.per_chunk, (first // 4 + 1) * 4)
                mm = pe.matmul(core.bank[first // 4][0:T, first % 4 * T:((last - 1) % 4 + 1) * T],
                               qT[:, c, cols(b)],
                               att.kblock[:, b, c, first - c * att.per_chunk:last - c * att.per_chunk, :],
                               start=True, stop=True)
                first = last
        mm.then_inc(att.scores_psum, 1)

    def transposes(b):
        pe.wait_ge(att.probsT_ready, turn(i, b, GROUP))
        pe.wait_ge(att.probs_ready, turn(i, b + 1, GROUP))
        for n in range(HEADS):
            mm = pe.transpose(core.bank[3 + n // 4][0:T, cols(n % 4)], att.probs[:, n, :], core.ident[0:T, 0:T])
        mm.then_inc(att.probsT_psum, 1)

    def context(b):
        pe.wait_ge(att.context_done, turn(i, b, GROUP))
        pe.wait_ge(att.probsT_ready, turn(i, b + 1, GROUP))
        for n in range(HEADS):
            if hd == 16:
                out = core.bank[6][0:T, cols(n, hd)]
            else:
                out = core.bank[6 + n // 6][0:T, cols(n % 6, hd)]
            mm = pe.matmul(out, att.probsT[:, n, :], vals[:, b, cols(n, hd)], start=True, stop=True)
        mm.then_inc(att.context_psum, 1)

    scores(0)
    for b in range(GROUP):
        transposes(b)
        if b + 1 < GROUP:
            scores(b + 1)
        context(b)


def heads_scalar(act, att, i):
    for b in range(GROUP):
        act.wait_ge(att.probsT_psum, turn(i, b, GROUP))
        act.wait_ge(att.max_ready, turn(i, b + 1, GROUP))
        for n in range(HEADS):
            ins = act.activation(att.probs[:, n, :], att.core.bank[n // 4][0:T, cols(n % 4)], ACT.Exp,
                                 bias=att.negmax[:, n:n + 1], accum_out=att.total[:, n:n + 1])
        ins.then_inc(att.probs_ready, 1)


def heads_vector(v, att, i, rescale):
    def maxima(b):
        v.wait_ge(att.scores_psum, turn(i, b + 1, GROUP))
        for m in range(3):
            ins = v.tensor_reduce(att.negmax[:, 4 * m:4 * m + 4],
                                  att.scores_bank(m).rearrange("q (n k) -> q n k", n=4),
                                  AX.X, ALU.max, negate=True)
        ins.then_inc(att.max_ready, 1)

    maxima(0)
    for b in range(GROUP):
        v.wait_ge(att.probs_ready, turn(i, b + 1, GROUP))
        v.reciprocal(att.inv[:, b % 2, :], att.total[:, :])
        v.wait_ge(att.probsT_psum, turn(i, b + 1, GROUP))
        for m in range(3):
            ins = v.tensor_copy(att.probsT[:, 4 * m:4 * m + 4, :], att.probsT_bank(m))
        ins.then_inc(att.probsT_ready, 1)
        if b + 1 < GROUP:
            maxima(b + 1)
        v.wait_ge(att.context_psum, turn(i, b + 1, GROUP))
        rescale(b, att.inv[:, b % 2, :]).then_inc(att.context_done, 1)



class TopTwo:
    def __init__(self, sb, width, tag):
        self.width = width
        self.best = sb(f"{tag}_best", [T, GROUP, 8])
        self.where = sb(f"{tag}_where", [T, GROUP, 8], U32)
        self.index = sb(f"{tag}_index", [T, GROUP, 8])
        self.hot = sb(f"{tag}_hot", [T, 2, GROUP, width])


def top_two_hot(v, core, top, logits):
    shape = [T, GROUP, top.width]
    for b in range(GROUP):
        v.max(top.best[:, b, :], logits[:, b, :])
    v.drain()
    for b in range(GROUP):
        v.max_index(top.where[:, b, :], top.best[:, b, :], logits[:, b, :])
    v.drain()
    v.tensor_copy(top.index[:, :, :], top.where[:, :, :])
    v.drain()
    for k in range(2):
        v.tensor_tensor(top.hot[:, k, :, :],
                        core.iota[0:T, 0:top.width].unsqueeze(1).to_broadcast(shape),
                        top.index[:, :, k:k + 1].to_broadcast(shape), ALU.is_equal)
    v.drain()


class Router:
    def __init__(self, sb, sem, tag):
        self.top = TopTwo(sb, EXPERTS, tag)
        self.logits = sb(f"{tag}_logits", [T, GROUP, EXPERTS])
        self.gap = sb(f"{tag}_gap", [T, GROUP])
        self.ratio = sb(f"{tag}_ratio", [T, GROUP])
        self.weight = sb(f"{tag}_weight", [T, 2, GROUP])
        self.gates = sb(f"{tag}_gates", [T, GROUP, EXPERTS])
        self.gap_ready = sem(f"{tag}_gap_ready")
        self.ratio_ready = sem(f"{tag}_ratio_ready")


def router_vector(v, core, r, i):
    shape = [T, GROUP, EXPERTS]
    top_two_hot(v, core, r.top, r.logits)
    v.tensor_tensor(r.gap[:, :], r.top.best[:, :, 1], r.top.best[:, :, 0], ALU.subtract).then_inc(r.gap_ready, 1)
    v.wait_ge(r.ratio_ready, turn(i))
    v.tensor_scalar(r.gap[:, :], r.ratio[:, :], 1.0, None, ALU.add)
    v.drain()
    v.reciprocal(r.weight[:, 0, :], r.gap[:, :])
    v.drain()
    v.tensor_tensor(r.weight[:, 1, :], r.weight[:, 0, :], r.ratio[:, :], ALU.mult)
    v.drain()
    for k in range(2):
        v.tensor_tensor(r.top.hot[:, k, :, :], r.top.hot[:, k, :, :],
                        r.weight[:, k, :].unsqueeze(2).to_broadcast(shape), ALU.mult)
    v.drain()
    v.tensor_tensor(core.gates[:, bass.ds(i * (GROUP * EXPERTS), GROUP * EXPERTS)],
                    r.top.hot[:, 0, :, :].rearrange("t b e -> t (b e)"),
                    r.top.hot[:, 1, :, :].rearrange("t b e -> t (b e)"), ALU.add)
    return v.tensor_tensor(r.gates[:, :, :], r.top.hot[:, 0, :, :], r.top.hot[:, 1, :, :], ALU.add)


def router_scalar(act, r, i):
    act.wait_ge(r.gap_ready, turn(i))
    act.activation(r.ratio[:, :], r.gap[:, :], ACT.Exp).then_inc(r.ratio_ready, 1)



def first_heads_stage(core, a):
    nc, bank, h = core.nc, core.bank, core.h
    with ExitStack() as ctx:
        sb, sem, load_sem, raised = stage_tools(core, ctx)
        outer, inner, second = (Norm(sb, sem, n) for n in ("outer", "inner", "second"))
        w = sb("w_qkv", [C, 2, 3 * D])
        w_out = sb("w_out", [C, 2, D])
        w_router = sb("w_router", [C, 2, EXPERTS])
        affine = sb("affine", [C, 8])
        xn = sb("xn", [T, GROUP, D])
        xnn = sb("xnn", [T, GROUP, D])
        xT = sb("xT", [C, 2, N])
        qT = sb("qT", [C, 2, N])
        kT = sb("kT", [C, 2, N])
        vals = sb("vals", [T, GROUP, D])
        o = sb("o", [T, GROUP, D])
        oT = sb("oT", [C, 2, N])
        zT = sb("zT", [C, 2, N])
        att = Heads(core, sb, sem, 16, core.mask16)
        router = Router(sb, sem, "router")
        w_loaded = load_sem("w_loaded")
        names = ("xnn_ready", "xT_psum", "xT_ready", "q_psum", "k_psum", "v_psum", "q_ready", "k_ready", "v_ready",
                 "oT_psum", "oT_ready", "out_psum", "zn_ready", "zT_psum", "zT_ready", "zT_kept", "logits_psum",
                 "logits_read", "gates_done")
        s = {n: sem(n) for n in names}

        with nc.Block() as block:
            @block.sync
            def _(sp):
                raise_to_start(sp, raised)
                sp.dma_start(w[:, :, :], a["b_wqkv"]).then_inc(w_loaded, 16)
                sp.dma_start(w_out[:, :, :], a["b_wproj"]).then_inc(w_loaded, 16)
                sp.dma_start(w_router[:, :, :], a["b_wrouter"]).then_inc(w_loaded, 16)
                sp.dma_start(affine[:, :], a["b_affine"]).then_inc(w_loaded, 16)

            @block.gpsimd
            def _(pool):
                with pool.Fori(0, TURNS) as i:
                    norm_rstd(pool, core, outer, i)
                    norm_rstd(pool, core, inner, i)
                    pool.wait_ge(att.scores_psum, turn(i, 0, GROUP))
                    pool.wait_ge(s["k_ready"], turn(i))
                    for b in range(GROUP):
                        heads_pool(pool, att, i, kT, b)
                    norm_rstd(pool, core, second, i)

            @block.tensor
            def _(pe):
                pe.wait_ge(w_loaded, 64)
                with pe.Fori(0, TURNS) as i:
                    pe.wait_ge(s["oT_ready"], turn(i, 0))
                    pe.wait_ge(s["xnn_ready"], turn(i))
                    transpose_group(pe, core, bank[0:2], xnn, s["xT_psum"])
                    pe.wait_ge(s["zn_ready"], turn(i, 0))
                    pe.wait_ge(s["zT_ready"], turn(i, 0))
                    pe.wait_ge(s["logits_read"], turn(i, 0))
                    pe.wait_ge(s["xT_ready"], turn(i))
                    for j, done in enumerate(("q_psum", "q_psum", "k_psum", "k_psum")):
                        for c in range(2):
                            mm = pe.matmul(bank[2 + j][0:C, 0:N], w[:, c, j * C:(j + 1) * C], xT[:, c, :],
                                           start=(c == 0), stop=(c == 1))
                        if j % 2:
                            mm.then_inc(s[done], 1)
                    for b in range(GROUP):
                        for c in range(2):
                            mm = pe.matmul(bank[6 + b // 2][0:T, cols(b % 2, D)], xT[:, c, cols(b)],
                                           w[:, c, 2 * D:3 * D], start=(c == 0), stop=(c == 1))
                    mm.then_inc(s["v_psum"], 1)
                    pe.wait_ge(s["q_ready"], turn(i))
                    pe.wait_ge(s["k_ready"], turn(i))
                    pe.wait_ge(s["v_ready"], turn(i))
                    heads_tensor(pe, att, i, qT, vals)
                    pe.wait_ge(att.context_done, turn(i, GROUP, GROUP))
                    transpose_group(pe, core, bank[0:2], o, s["oT_psum"])
                    pe.wait_ge(s["oT_ready"], turn(i))
                    for b in range(GROUP):
                        for c in range(2):
                            mm = pe.matmul(bank[2 + b // 2][0:T, cols(b % 2, D)], oT[:, c, cols(b)], w_out[:, c, :],
                                           start=(c == 0), stop=(c == 1))
                    mm.then_inc(s["out_psum"], 1)
                    pe.wait_ge(s["zn_ready"], turn(i))
                    transpose_group(pe, core, bank[4:6], xnn, s["zT_psum"])
                    pe.wait_ge(s["zT_ready"], turn(i))
                    for b in range(GROUP):
                        for c in range(2):
                            mm = pe.matmul(bank[6][0:T, cols(b, EXPERTS)], zT[:, c, cols(b)], w_router[:, c, :],
                                           start=(c == 0), stop=(c == 1))
                    mm.then_inc(s["logits_psum"], 1)

            @block.scalar
            def _(act):
                act.wait_ge(w_loaded, 64)
                with act.Fori(0, TURNS) as i:
                    act.wait_ge(s["v_psum"], turn(i, 0))
                    act.wait_ge(s["xT_psum"], turn(i))
                    for c in range(2):
                        ins = act.activation(xT[:, c, :], bank[c][0:C, 0:N], ACT.Identity,
                                             bias=affine[:, 2 + c:3 + c], scale=affine[:, c:c + 1])
                    ins.then_inc(s["xT_ready"], 1)
                    act.wait_ge(att.kblock_ready, turn(i, 0, GROUP))
                    act.wait_ge(s["k_psum"], turn(i))
                    for c in range(2):
                        ins = act.activation(kT[:, c, :], bank[4 + c][0:C, 0:N], ACT.Copy)
                    ins.then_inc(s["k_ready"], 1)
                    act.wait_ge(att.scores_psum, turn(i, 0, GROUP))
                    for c in range(2):
                        ins = act.activation(qT[:, c, :], bank[2 + c][0:C, 0:N], ACT.Copy, scale=0.25)
                    ins.then_inc(s["q_ready"], 1)
                    heads_scalar(act, att, i)
                    act.wait_ge(s["logits_psum"], turn(i, 0))
                    act.wait_ge(s["zT_kept"], turn(i, 0))
                    act.wait_ge(s["zT_psum"], turn(i))
                    for c in range(2):
                        ins = act.activation(zT[:, c, :], bank[4 + c][0:C, 0:N], ACT.Identity,
                                             bias=affine[:, 6 + c:7 + c], scale=affine[:, 4 + c:5 + c])
                    ins.then_inc(s["zT_ready"], 1)
                    router_scalar(act, router, i)

            @block.vector
            def _(v):
                v.wait_ge(w_loaded, 64)
                with v.Fori(0, TURNS) as i:
                    norm_statistics(v, outer, lambda b: sample_of(h, i, b))
                    v.wait_ge(outer.rstd_ready, turn(i))
                    for b in range(GROUP):
                        norm_apply(v, outer, lambda b: sample_of(h, i, b), lambda b: xn[:, b, :], b)
                    v.drain()
                    norm_statistics(v, inner, lambda b: xn[:, b, :])
                    v.wait_ge(inner.rstd_ready, turn(i))
                    for b in range(GROUP):
                        ins = norm_apply(v, inner, lambda b: xn[:, b, :], lambda b: xnn[:, b, :], b)
                    ins.then_inc(s["xnn_ready"], 1)
                    v.wait_ge(s["v_psum"], turn(i))
                    for p in range(2):
                        ins = v.tensor_copy(vals[:, 2 * p:2 * p + 2, :], bank[6 + p][0:T, 0:2 * D])
                    ins.then_inc(s["v_ready"], 1)

                    def rescale(b, inv):
                        return v.tensor_tensor(o[:, b, :].rearrange("t (n d) -> t n d", n=HEADS),
                                               bank[6][0:T, 0:D].rearrange("t (n d) -> t n d", n=HEADS),
                                               inv.unsqueeze(2).to_broadcast([T, HEADS, 16]), ALU.mult)
                    heads_vector(v, att, i, rescale)
                    v.wait_ge(s["oT_psum"], turn(i))
                    for c in range(2):
                        ins = v.tensor_copy(oT[:, c, :], bank[c][0:C, 0:N])
                    ins.then_inc(s["oT_ready"], 1)
                    v.wait_ge(s["out_psum"], turn(i))
                    for p in range(2):
                        v.tensor_tensor(xn[:, 2 * p:2 * p + 2, :], xn[:, 2 * p:2 * p + 2, :],
                                        bank[2 + p][0:T, 0:2 * D].rearrange("t (b d) -> t b d", b=2), ALU.add)
                    v.drain()
                    rows = h[:, bass.ds(i * (GROUP * D), GROUP * D)]
                    v.tensor_tensor(rows, rows, xn[:, :, :].rearrange("t b d -> t (b d)"), ALU.add)
                    norm_statistics(v, second, lambda b: xn[:, b, :])
                    v.wait_ge(second.rstd_ready, turn(i))
                    for b in range(GROUP):
                        ins = norm_apply(v, second, lambda b: xn[:, b, :], lambda b: xnn[:, b, :], b)
                    ins.then_inc(s["zn_ready"], 1)
                    v.wait_ge(s["zT_ready"], turn(i))
                    for c in range(2):
                        ins = v.tensor_scalar(core.zT_all[:, c, bass.ds(i * N, N)], zT[:, c, :], 1.0, None, ALU.mult)
                    ins.then_inc(s["zT_kept"], 1)
                    v.wait_ge(s["logits_psum"], turn(i))
                    v.tensor_copy(router.logits[:, :, :], bank[6][0:T, 0:GROUP * EXPERTS]).then_inc(s["logits_read"], 1)
                    v.drain()
                    router_vector(v, core, router, i).then_inc(s["gates_done"], 1)



def experts_stage(core, a, second):
    nc, bank, h = core.nc, core.bank, core.h
    tiles = EXPERTS * TURNS
    RING = 3
    with ExitStack() as ctx:
        sb, sem, load_sem, raised = stage_tools(core, ctx)
        w1 = [sb("w1", [C, 2, FF]) for _ in range(2)]
        w2 = [sb("w2", [128, FC, D]) for _ in range(2)]
        hidden = sb("hidden", [128, FC, N])
        loaded = [load_sem("loaded") for _ in range(2)]
        hidden_psum, bank_read, hidden_ready, y_psum, y_added = (
            sem(n) for n in ("hidden_psum", "bank_read", "hidden_ready", "y_psum", "y_added"))
        if second:
            parts1 = [sb("parts1", [C, 2 * FF]) for _ in range(3)]
            parts2 = [sb("parts2", [128, FC * D]) for _ in range(3)]
            mix = [sb("mix", [128, 2]) for _ in range(2)]
            b1 = [sb("b1", [128, FC]) for _ in range(2)]
            relu = sb("relu", [128, FC, N])
            parts_read = sem("parts_read")
            mixed = sem("mixed")
            added = sem("added")
            scaled = sem("scaled")
            b1_loaded = [load_sem("b1_loaded") for _ in range(2)]

        with nc.Block() as block:
            @block.sync
            def _(sp):
                raise_to_start(sp, raised)
                with sp.Fori(0, EXPERTS // 2) as pair:
                    for k in range(2):
                        e = pair * 2 + k
                        if not second:
                            sp.wait_ge(y_psum, turn((e - 1) * TURNS, 0))
                            sp.dma_start(w1[k][:, :, :], a["b_w1"][bass.ds(e, 1)].rearrange("e p c f -> (e p) c f")
                                         ).then_inc(loaded[k], 16)
                            sp.dma_start(w2[k][:, :, :], a["b_w2"][bass.ds(e, 1)].rearrange("e p c f -> (e p) c f")
                                         ).then_inc(loaded[k], 16)
                        else:
                            sp.wait_ge(y_psum, turn((e - 1) * TURNS, 0))
                            sp.dma_start(b1[k][:, :], a["i_b1"][bass.ds(e, 1)].rearrange("e p c -> (e p) c")
                                         ).then_inc(b1_loaded[k], 16)
                            sp.wait_ge(parts_read, turn(e, 0))
                            for n in range(3):
                                sp.dma_start(parts1[n][:, :], a[f"i_w1_{n}"][bass.ds(e, 1)].rearrange("e p f -> (e p) f")
                                             ).then_inc(loaded[k], 16)
                                sp.dma_start(parts2[n][:, :], a[f"i_w2_{n}"][bass.ds(e, 1)].rearrange("e p f -> (e p) f")
                                             ).then_inc(loaded[k], 16)
                            sp.dma_start(mix[k][:, :], a["i_mix"][bass.ds(e, 1), :].to_broadcast([128, 2])
                                         ).then_inc(loaded[k], 16)

            if second:
                @block.gpsimd
                def _(pool):
                    with pool.Fori(0, EXPERTS // 2) as pair:
                        for k in range(2):
                            e = pair * 2 + k
                            pool.wait_ge(loaded[k], pair * (16 * 7) + 16 * 7)
                            pool.wait_ge(y_psum, turn((e - 1) * TURNS, 0))
                            out1 = w1[k][:, :, :].rearrange("p c f -> p (c f)")
                            out2 = w2[k][:, :, :].rearrange("p c f -> p (c f)")
                            pool.tensor_tensor(out1, parts1[1][:, :], mix[k][0:C, 0:1].to_broadcast([C, 2 * FF]),
                                               ALU.mult)
                            pool.tensor_tensor(out2, parts2[1][:, :], mix[k][:, 1:2].to_broadcast([128, FC * D]),
                                               ALU.mult).then_inc(scaled, 1)
                            pool.wait_ge(scaled, turn(e))
                            pool.tensor_tensor(out1, parts1[0][:, :], out1, ALU.add)
                            pool.tensor_tensor(out2, parts2[0][:, :], out2, ALU.add).then_inc(added, 1)
                            pool.wait_ge(added, turn(e))
                            pool.tensor_tensor(out1, out1, parts1[2][:, :], ALU.add)
                            pool.tensor_tensor(out2, out2, parts2[2][:, :], ALU.add).then_inc(mixed, 1)
                            pool.wait_ge(mixed, turn(e))
                            pool.nop().then_inc(parts_read, 1)

            @block.tensor
            def _(pe):
                with pe.Fori(0, EXPERTS // 2) as pair:
                    for k in range(2):
                        e = pair * 2 + k
                        with pe.Fori(0, TURNS) as i:
                            t = e * TURNS + i
                            if second:
                                pe.wait_ge(mixed, turn(e))
                            else:
                                pe.wait_ge(loaded[k], pair * 32 + 32)
                            for m in range(FC):
                                pe.wait_ge(bank_read, turn(t, m + 1 - RING, FC))
                                for c in range(2):
                                    mm = pe.matmul(bank[m % RING][:, 0:N], w1[k][:, c, m * 128:(m + 1) * 128],
                                                   core.zT_all[:, c, bass.ds(i * N, N)],
                                                   start=(c == 0), stop=(c == 1))
                                mm.then_inc(hidden_psum, 1)
                            pe.wait_ge(y_added, turn(t, 0))
                            for m in range(FC):
                                pe.wait_ge(hidden_ready, turn(t, m + 1, FC))
                                for b in range(GROUP):
                                    mm = pe.matmul(bank[4 + b][0:T, 0:D], hidden[:, m, cols(b)], w2[k][:, m, :],
                                                   start=(m == 0), stop=(m == FC - 1))
                            mm.then_inc(y_psum, 1)

            @block.scalar
            def _(act):
                with act.Fori(0, EXPERTS // 2) as pair:
                    for k in range(2):
                        with act.Fori(0, TURNS) as i:
                            t = (pair * 2 + k) * TURNS + i
                            if second:
                                act.wait_ge(b1_loaded[k], pair * 16 + 16)
                                act.wait_ge(hidden_ready, turn(t, 0, FC))
                                for m in range(FC):
                                    act.wait_ge(hidden_psum, turn(t, m + 1, FC))
                                    act.activation(relu[:, m, :], bank[m % RING][:, 0:N], ACT.Relu,
                                                   bias=b1[k][:, m:m + 1]).then_inc(bank_read, 1)
                            else:
                                act.wait_ge(y_psum, turn(t, 0))
                                for m in range(FC):
                                    act.wait_ge(hidden_psum, turn(t, m + 1, FC))
                                    act.activation(hidden[:, m, :], bank[m % RING][:, 0:N], ACT.Gelu
                                                   ).then_inc(hidden_ready, 1)
                                    act.wait_ge(hidden_ready, turn(t, m + 1, FC))
                                    act.sem_inc(bank_read, 1)

            @block.vector
            def _(v):
                with v.Fori(0, EXPERTS // 2) as pair:
                    for k in range(2):
                        with v.Fori(0, TURNS) as i:
                            e = pair * 2 + k
                            t = e * TURNS + i
                            if second:
                                v.wait_ge(y_psum, turn(t, 0))
                                for m in range(FC):
                                    v.wait_ge(bank_read, turn(t, m + 1, FC))
                                    v.tensor_tensor(hidden[:, m, :], relu[:, m, :], relu[:, m, :], ALU.mult
                                                    ).then_inc(hidden_ready, 1)
                            v.wait_ge(y_psum, turn(t))
                            for b in range(GROUP):
                                gate = core.gates[:, bass.ds(i * (GROUP * EXPERTS) + b * EXPERTS + e, 1)]
                                ins = v.scalar_tensor_tensor(out=sample_of(h, i, b), in0=bank[4 + b][0:T, 0:D],
                                                             scalar=gate, in1=sample_of(h, i, b),
                                                             op0=ALU.mult, op1=ALU.add)
                            ins.then_inc(y_added, 1)



def ssm_stage(core, a):
    nc, bank, h = core.nc, core.bank, core.h
    STATES = 16
    PER = 128 // STATES
    TILES = D // PER
    HALF = TILES // 2
    TAPS = 4
    PAD = TAPS - 1
    with ExitStack() as ctx:
        sb, sem, load_sem, raised = stage_tools(core, ctx)
        norm = Norm(sb, sem, "norm")
        w_in = sb("w_in", [C, 2, 2 * D])
        w_dt = sb("w_dt", [C, 2, D])
        w_b = sb("w_b", [C, 2, D * STATES])
        w_c = sb("w_c", [C, 2, D * STATES])
        w_out = sb("w_out", [C, 2, D])
        b_out = sb("b_out", [1, D])
        spread = sb("spread", [C, HALF, 128])
        gather = sb("gather", [128, HALF, C])
        per_channel = sb("per_channel", [C, 2, 5 + TAPS])
        neg_bv = sb("neg_bv", [C, 2])
        row_consts = sb("row_consts", [128, 3, TILES])
        decay_rate = sb("decay_rate", [128, TILES])
        xn = sb("xn", [T, GROUP, D])
        xT = sb("xT", [C, 2, N])
        u = sb("u", [C, 2, GROUP, PAD + T])
        gate = sb("gate", [C, 2, N])
        conv = sb("conv", [C, 2, N])
        dt = sb("dt", [C, 2, N])
        dtu = sb("dtu", [C, 2, N])
        z = sb("z", [C, 2, N])
        soft = sb("soft", [C, 2, N])
        decay = sb("decay", [128, 2, N])
        dtu_rows = sb("dtu_rows", [128, 2, N])
        drive = sb("drive", [128, 2, N])
        state = sb("state", [128, 2, N])
        product = sb("product", [128, 2, N])
        y = sb("y", [C, 2, N])
        w_loaded, rate_exp, consts_ready = (load_sem(n) for n in ("w_loaded", "rate_exp", "consts_ready"))
        names = ("xn_ready", "xT_psum", "xT_ready", "uv_psum", "u_ready", "gate_exp", "conv_ready", "dt_psum",
                 "z_ready", "log_ready", "dt_ready", "b_psum", "spread_psum", "c_psum", "spread_read", "b_read",
                 "product_ready", "gathered", "y_ready", "out_psum", "h_done")
        s = {n: sem(n) for n in names}
        loads = [(w_in, "c_wi"), (w_dt, "c_wdt"), (per_channel, "c_channel"), (row_consts, "c_rows"),
                 (spread, "spread"), (gather, "gather"), (w_b, "c_wb"), (w_c, "c_wc"), (w_out, "c_wo"),
                 (b_out, "c_bo")]

        with nc.Block() as block:
            @block.sync
            def _(sp):
                raise_to_start(sp, raised)
                for tile, name in loads:
                    sp.dma_start(tile[tuple(slice(None) for _ in tile.shape)], a[name]).then_inc(w_loaded, 16)

            @block.gpsimd
            def _(pool):
                with pool.Fori(0, TURNS) as i:
                    norm_rstd(pool, core, norm, i)

            @block.tensor
            def _(pe):
                pe.wait_ge(w_loaded, 16 * len(loads))

                def gather_tile(i, j):
                    c = j // HALF
                    if j == 0:
                        pe.wait_ge(s["y_ready"], turn(i, 0))
                    pe.wait_ge(s["product_ready"], turn(i, j + 1, TILES))
                    pe.matmul(bank[6 + c][0:C, 0:N], gather[:, j % HALF, :], product[:, j % 2, :],
                              start=(j % HALF == 0), stop=(j % HALF == HALF - 1)).then_inc(s["gathered"], 1)

                with pe.Fori(0, TURNS) as i:
                    pe.wait_ge(s["h_done"], turn(i, 0))
                    pe.wait_ge(s["xn_ready"], turn(i))
                    transpose_group(pe, core, bank[0:2], xn, s["xT_psum"])
                    pe.wait_ge(s["xT_ready"], turn(i))
                    for j in range(4):
                        for c in range(2):
                            mm = pe.matmul(bank[2 + j][0:C, 0:N], w_in[:, c, j * C:(j + 1) * C], xT[:, c, :],
                                           start=(c == 0), stop=(c == 1))
                    mm.then_inc(s["uv_psum"], 1)
                    pe.wait_ge(s["conv_ready"], turn(i))
                    for j in range(2):
                        for c in range(2):
                            mm = pe.matmul(bank[j][0:C, 0:N], w_dt[:, c, j * C:(j + 1) * C], conv[:, c, :],
                                           start=(c == 0), stop=(c == 1))
                    mm.then_inc(s["dt_psum"], 1)
                    pe.wait_ge(s["gate_exp"], turn(i))
                    pe.wait_ge(s["dt_ready"], turn(i))
                    for j in range(TILES):
                        c = j // HALF
                        pe.wait_ge(s["spread_read"], turn(i, j, TILES))
                        pe.matmul(bank[4][:, 0:N], spread[:, j % HALF, :], dt[:, c, :], start=True, stop=True)
                        pe.matmul(bank[5][:, 0:N], spread[:, j % HALF, :], dtu[:, c, :], start=True, stop=True
                                  ).then_inc(s["spread_psum"], 1)
                        pe.wait_ge(s["b_read"], turn(i, j - 1, TILES))
                        for c in range(2):
                            mm = pe.matmul(bank[j % 2][:, 0:N], w_b[:, c, j * 128:(j + 1) * 128], conv[:, c, :],
                                           start=(c == 0), stop=(c == 1))
                        mm.then_inc(s["b_psum"], 1)
                        pe.wait_ge(s["product_ready"], turn(i, j - 1, TILES))
                        for c in range(2):
                            mm = pe.matmul(bank[2 + j % 2][:, 0:N], w_c[:, c, j * 128:(j + 1) * 128], conv[:, c, :],
                                           start=(c == 0), stop=(c == 1))
                        mm.then_inc(s["c_psum"], 1)
                        if j:
                            gather_tile(i, j - 1)
                    gather_tile(i, TILES - 1)
                    pe.wait_ge(s["y_ready"], turn(i))
                    for b in range(GROUP):
                        out = bank[b // 2][0:T, cols(b % 2, D)]
                        for c in range(2):
                            pe.matmul(out, y[:, c, cols(b)], w_out[:, c, :], start=(c == 0), stop=False)
                        mm = pe.matmul(out, core.ones[0:1, 0:T], b_out[:, :], start=False, stop=True)
                    mm.then_inc(s["out_psum"], 1)

            @block.scalar
            def _(act):
                act.wait_ge(w_loaded, 16 * len(loads))
                act.activation(decay_rate[:, :], row_consts[:, 0, :], ACT.Exp).then_inc(rate_exp, 1)
                act.wait_ge(consts_ready, 1)
                with act.Fori(0, TURNS) as i:
                    act.wait_ge(s["xT_psum"], turn(i))
                    for c in range(2):
                        ins = act.activation(xT[:, c, :], bank[c][0:C, 0:N], ACT.Copy)
                    ins.then_inc(s["xT_ready"], 1)
                    act.wait_ge(s["y_ready"], turn(i, 0))
                    act.wait_ge(s["uv_psum"], turn(i))
                    for c in range(2):
                        ins = act.activation(u[:, c, :, PAD:PAD + T],
                                             bank[2 + c][0:C, 0:N].rearrange("d (b t) -> d b t", b=GROUP),
                                             ACT.Identity, bias=per_channel[:, c, 0:1])
                    ins.then_inc(s["u_ready"], 1)
                    for c in range(2):
                        ins = act.activation(gate[:, c, :], bank[4 + c][0:C, 0:N], ACT.Exp,
                                             bias=neg_bv[:, c:c + 1], scale=-1.0)
                    ins.then_inc(s["gate_exp"], 1)
                    act.wait_ge(s["z_ready"], turn(i))
                    act.activation(soft[:, :, :], soft[:, :, :], ACT.Exp)
                    act.drain()
                    act.activation(soft[:, :, :], soft[:, :, :], ACT.Ln, bias=1.0).then_inc(s["log_ready"], 1)
                    for j in range(TILES):
                        act.wait_ge(s["product_ready"], turn(i, j - 1, TILES))
                        act.wait_ge(s["spread_psum"], turn(i, j + 1, TILES))
                        act.activation(decay[:, j % 2, :].rearrange("r (b t) -> r b t", b=GROUP)[:, :, 1:T],
                                       bank[4][:, 0:N].rearrange("r (b t) -> r b t", b=GROUP)[:, :, 1:T],
                                       ACT.Exp, scale=decay_rate[:, j:j + 1])
                        act.activation(dtu_rows[:, j % 2, :], bank[5][:, 0:N], ACT.Copy
                                       ).then_inc(s["spread_read"], 1)

            @block.vector
            def _(v):
                v.memset(decay[:, :, :], 0.0)
                v.memset(u[:, :, :, :], 0.0)
                v.wait_ge(w_loaded, 16 * len(loads))
                v.tensor_scalar(neg_bv[:, :], per_channel[:, :, 1], -1.0, None, ALU.mult)
                v.wait_ge(rate_exp, 1)
                v.tensor_scalar(decay_rate[:, :], decay_rate[:, :], -1.0, None, ALU.mult).then_inc(consts_ready, 1)
                with v.Fori(0, TURNS) as i:
                    norm_statistics(v, norm, lambda b: sample_of(h, i, b))
                    v.wait_ge(norm.rstd_ready, turn(i))
                    for b in range(GROUP):
                        ins = norm_apply(v, norm, lambda b: sample_of(h, i, b), lambda b: xn[:, b, :], b)
                    ins.then_inc(s["xn_ready"], 1)
                    v.wait_ge(s["u_ready"], turn(i))
                    by_sample = [conv[:, c, :].rearrange("d (b t) -> d b t", b=GROUP) for c in range(2)]
                    for c in range(2):
                        v.tensor_scalar(by_sample[c], u[:, c, :, 0:T], per_channel[:, c, 5:6],
                                        per_channel[:, c, 2:3], ALU.mult, ALU.add)
                    for k in range(1, TAPS):
                        v.drain()
                        for c in range(2):
                            ins = v.scalar_tensor_tensor(out=by_sample[c], in0=u[:, c, :, k:k + T],
                                                         scalar=per_channel[:, c, 5 + k:6 + k], in1=by_sample[c],
                                                         op0=ALU.mult, op1=ALU.add)
                    ins.then_inc(s["conv_ready"], 1)
                    v.wait_ge(s["gate_exp"], turn(i))
                    v.tensor_scalar(gate[:, :, :], gate[:, :, :], 1.0, None, ALU.add)
                    v.drain()
                    v.reciprocal(gate[:, :, :], gate[:, :, :])
                    v.wait_ge(s["dt_psum"], turn(i))
                    for c in range(2):
                        v.tensor_scalar(z[:, c, :], bank[c][0:C, 0:N], per_channel[:, c, 3:4], None, ALU.add)
                    v.drain()
                    v.scalar_tensor_tensor(out=soft[:, :, :], in0=z[:, :, :], scalar=-1.0, in1=z[:, :, :],
                                           op0=ALU.mult, op1=ALU.min).then_inc(s["z_ready"], 1)
                    v.wait_ge(s["log_ready"], turn(i))
                    v.scalar_tensor_tensor(out=dt[:, :, :], in0=z[:, :, :], scalar=0.0, in1=soft[:, :, :],
                                           op0=ALU.max, op1=ALU.add)
                    v.drain()
                    v.tensor_tensor(dtu[:, :, :], dt[:, :, :], conv[:, :, :], ALU.mult).then_inc(s["dt_ready"], 1)
                    for j in range(TILES):
                        k = j % 2
                        v.wait_ge(s["spread_read"], turn(i, j + 1, TILES))
                        v.wait_ge(s["b_psum"], turn(i, j + 1, TILES))
                        v.scalar_tensor_tensor(out=drive[:, k, :], in0=bank[k][:, 0:N],
                                               scalar=row_consts[:, 1, j:j + 1], in1=dtu_rows[:, k, :],
                                               op0=ALU.add, op1=ALU.mult).then_inc(s["b_read"], 1)
                        v.drain()
                        v.tensor_tensor_scan(state[:, k, :], decay[:, k, :], drive[:, k, :], 0.0, ALU.mult, ALU.add)
                        v.drain()
                        v.wait_ge(s["gathered"], turn(i, j - 1, TILES))
                        v.wait_ge(s["c_psum"], turn(i, j + 1, TILES))
                        v.scalar_tensor_tensor(out=product[:, k, :], in0=bank[2 + k][:, 0:N],
                                               scalar=row_consts[:, 2, j:j + 1], in1=state[:, k, :],
                                               op0=ALU.add, op1=ALU.mult).then_inc(s["product_ready"], 1)
                    v.wait_ge(s["gathered"], turn(i, TILES, TILES))
                    for c in range(2):
                        v.scalar_tensor_tensor(out=y[:, c, :], in0=conv[:, c, :], scalar=per_channel[:, c, 4:5],
                                               in1=bank[6 + c][0:C, 0:N], op0=ALU.mult, op1=ALU.add)
                    v.drain()
                    v.tensor_tensor(y[:, :, :], y[:, :, :], gate[:, :, :], ALU.mult).then_inc(s["y_ready"], 1)
                    v.wait_ge(s["out_psum"], turn(i))
                    for p in range(2):
                        rows = h[:, bass.ds(i * (GROUP * D) + p * (2 * D), 2 * D)]
                        ins = v.tensor_tensor(rows, bank[p][0:T, 0:2 * D], rows, ALU.add)
                    ins.then_inc(s["h_done"], 1)



def gated_heads_stage(core, a):
    nc, bank, h = core.nc, core.bank, core.h
    HD = 64
    WIDE = HEADS * HD
    QK = 2 * WIDE // 128
    SHARED, ROUTED = 2, 10
    GATES = ROUTED + 2 + SHARED
    with ExitStack() as ctx:
        sb, sem, load_sem, raised = stage_tools(core, ctx)
        norm = Norm(sb, sem, "norm")
        w = sb("w_qkv", [C, 2, 3 * WIDE])
        w_gate = sb("w_gate", [C, 2, GATES])
        w_out = sb("w_out", [128, WIDE // 128, D])
        b_v = sb("b_v", [1, WIDE])
        b_out = sb("b_out", [1, D])
        b_qk = sb("b_qk", [128, QK])
        b_centered = sb("b_centered", [128, QK])
        affine = sb("affine", [128, 4])
        affine_in = sb("affine_in", [128, 4])
        head_sum = sb("head_sum", [C, 2, 2 * HEADS])
        average = sb("average", [128, 128])
        eps = sb("eps", [128, 1])
        xn = sb("xn", [T, GROUP, D])
        xT = sb("xT", [C, 2, N])
        centered = sb("centered", [128, 2, N])
        square = sb("square", [128, 2, N])
        rstd = sb("rstd", [128, 2, N])
        qkT = sb("qkT", [128, QK, N])
        vals = sb("vals", [T, GROUP, WIDE])
        o = sb("o", [T, GROUP, WIDE])
        oT = sb("oT", [128, WIDE // 128, N])
        att = Heads(core, sb, sem, HD, core.mask64)
        qT, kT = qkT[:, 0:QK // 2, :], qkT[:, QK // 2:QK, :]
        glog = sb("glog", [T, GROUP, GATES])
        gpeak = sb("gpeak", [T, 3, GROUP])
        gsum = sb("gsum", [T, 3, GROUP])
        top = TopTwo(sb, ROUTED, "top")
        gates = sb("gates_12", [T, GROUP, HEADS])
        weight = sb("weight", [T, 2, HEADS])
        w_loaded, bias_mean, bias_ready, centered_ready = (
            load_sem(n) for n in ("w_loaded", "bias_mean", "bias_ready", "centered_ready"))
        names = ("xn_ready", "xT_psum", "xT_ready", "gate_psum", "gate_read", "gshift_ready", "gexp_ready",
                 "qk_psum", "square_ready", "centered_done", "var_psum", "rstd_q_ready", "qk_ready",
                 "v_psum", "v_ready", "oT_psum", "oT_act", "oT_dve", "out_psum", "h_done")
        s = {n: sem(n) for n in names}
        loads = [(w, "e_wqkv"), (w_gate, "e_wg"), (w_out, "e_wproj"), (b_v, "e_bv"), (b_out, "e_bproj"),
                 (b_qk, "e_bqk"), (affine_in, "e_affine"), (average, "average")]
        parts = ((0, ROUTED), (ROUTED, ROUTED + 2), (ROUTED + 2, GATES))

        with nc.Block() as block:
            @block.sync
            def _(sp):
                raise_to_start(sp, raised)
                for tile, name in loads:
                    sp.dma_start(tile[tuple(slice(None) for _ in tile.shape)], a[name]).then_inc(w_loaded, 16)

            @block.gpsimd
            def _(pool):
                with pool.Fori(0, TURNS) as i:
                    norm_rstd(pool, core, norm, i)
                    pool.wait_ge(att.scores_psum, turn(i, 0, GROUP))
                    pool.wait_ge(s["qk_ready"], turn(i, QK, QK))
                    for b in range(GROUP):
                        heads_pool(pool, att, i, kT, b)

            @block.tensor
            def _(pe):
                pe.wait_ge(w_loaded, 16 * len(loads))
                pe.matmul(bank[7][:, 0:QK], average[:, :], b_qk[:, :], start=True, stop=True).then_inc(bias_mean, 1)
                pe.wait_ge(centered_ready, 1)
                pe.wait_ge(bias_ready, 1)

                def variance(i, j):
                    pe.wait_ge(s["rstd_q_ready"], turn(i, j - 1, QK))
                    pe.wait_ge(s["square_ready"], turn(i, j + 1, QK))
                    pe.matmul(bank[4 + j % 2][:, 0:N], average[:, :], square[:, j % 2, :], start=True, stop=True
                              ).then_inc(s["var_psum"], 1)

                with pe.Fori(0, TURNS) as i:
                    pe.wait_ge(s["oT_dve"], turn(i, 0))
                    pe.wait_ge(s["xn_ready"], turn(i))
                    transpose_group(pe, core, bank[0:2], xn, s["xT_psum"])
                    pe.wait_ge(s["h_done"], turn(i, 0))
                    pe.wait_ge(s["xT_ready"], turn(i))
                    for b in range(GROUP):
                        for c in range(2):
                            mm = pe.matmul(bank[6][0:T, cols(b, GATES)], xT[:, c, cols(b)], w_gate[:, c, :],
                                           start=(c == 0), stop=(c == 1))
                    mm.then_inc(s["gate_psum"], 1)
                    pe.wait_ge(s["oT_act"], turn(i, 0))
                    for j in range(QK):
                        pe.wait_ge(s["centered_done"], turn(i, j - 1, QK))
                        for c in range(2):
                            mm = pe.matmul(bank[2 + j % 2][:, 0:N], w[:, c, j * 128:(j + 1) * 128], xT[:, c, :],
                                           start=(c == 0), stop=(c == 1))
                        mm.then_inc(s["qk_psum"], 1)
                        if j:
                            variance(i, j - 1)
                    variance(i, QK - 1)
                    for b in range(GROUP):
                        if b < 2:
                            pe.wait_ge(s["centered_done"], turn(i, QK, QK))
                        pe.wait_ge(s["v_ready"], turn(i, b - 1, GROUP))
                        for p in range(2):
                            out = bank[b % 2 * 2 + p][0:T, 0:WIDE // 2]
                            part = slice(p * WIDE // 2, (p + 1) * WIDE // 2)
                            for c in range(2):
                                pe.matmul(out, xT[:, c, cols(b)], w[:, c, 2 * WIDE:3 * WIDE][:, part],
                                          start=(c == 0), stop=False)
                            mm = pe.matmul(out, core.ones[0:1, 0:T], b_v[:, part], start=False, stop=True)
                        mm.then_inc(s["v_psum"], 1)
                    pe.wait_ge(s["v_ready"], turn(i, GROUP, GROUP))
                    pe.wait_ge(s["gate_read"], turn(i))
                    pe.wait_ge(s["rstd_q_ready"], turn(i, QK, QK))
                    pe.wait_ge(s["qk_ready"], turn(i, QK, QK))
                    heads_tensor(pe, att, i, qT, vals)
                    pe.wait_ge(att.context_done, turn(i, GROUP, GROUP))
                    for j in range(WIDE // 128):
                        for b in range(GROUP):
                            mm = pe.transpose(bank[j][:, cols(b)], o[:, b, j * 128:(j + 1) * 128],
                                              core.ident[0:T, 0:T])
                    mm.then_inc(s["oT_psum"], 1)
                    pe.wait_ge(s["oT_act"], turn(i))
                    pe.wait_ge(s["oT_dve"], turn(i))
                    for b in range(GROUP):
                        out = bank[6 + b // 2][0:T, cols(b % 2, D)]
                        for j in range(WIDE // 128):
                            pe.matmul(out, oT[:, j, cols(b)], w_out[:, j, :], start=(j == 0), stop=False)
                        mm = pe.matmul(out, core.ones[0:1, 0:T], b_out[:, :], start=False, stop=True)
                    mm.then_inc(s["out_psum"], 1)

            @block.scalar
            def _(act):
                act.wait_ge(bias_ready, 1)
                with act.Fori(0, TURNS) as i:
                    act.wait_ge(s["xT_psum"], turn(i))
                    for c in range(2):
                        ins = act.activation(xT[:, c, :], bank[c][0:C, 0:N], ACT.Copy)
                    ins.then_inc(s["xT_ready"], 1)
                    act.wait_ge(s["gshift_ready"], turn(i))
                    act.activation(glog[:, :, :], glog[:, :, :], ACT.Exp).then_inc(s["gexp_ready"], 1)

                    def inverse_root(j):
                        act.wait_ge(s["qk_ready"], turn(i, j - 1, QK))
                        act.wait_ge(s["var_psum"], turn(i, j + 1, QK))
                        act.activation(rstd[:, j % 2, :], bank[4 + j % 2][:, 0:N], ACT.Ln, bias=eps[:, 0:1])
                        act.drain()
                        act.activation(rstd[:, j % 2, :], rstd[:, j % 2, :], ACT.Exp, scale=-0.5
                                       ).then_inc(s["rstd_q_ready"], 1)

                    for j in range(QK):
                        act.wait_ge(s["var_psum"], turn(i, j - 1, QK))
                        act.wait_ge(s["qk_psum"], turn(i, j + 1, QK))
                        act.activation(square[:, j % 2, :], bank[2 + j % 2][:, 0:N], ACT.Square,
                                       bias=b_centered[:, j:j + 1]).then_inc(s["square_ready"], 1)
                        if j:
                            inverse_root(j - 1)
                    inverse_root(QK - 1)
                    for b in range(GROUP):
                        act.wait_ge(s["v_psum"], turn(i, b + 1, GROUP))
                        for p in range(2):
                            ins = act.activation(vals[:, b, p * WIDE // 2:(p + 1) * WIDE // 2],
                                                 bank[b % 2 * 2 + p][0:T, 0:WIDE // 2], ACT.Copy)
                        ins.then_inc(s["v_ready"], 1)
                    heads_scalar(act, att, i)
                    act.wait_ge(s["oT_psum"], turn(i))
                    for j in range(3, 6):
                        ins = act.activation(oT[:, j, :], bank[j][:, 0:N], ACT.Copy)
                    ins.then_inc(s["oT_act"], 1)

            @block.vector
            def _(v):
                v.memset(eps[:, :], EPS)
                v.wait_ge(w_loaded, 16 * len(loads))
                heads_of = [w[:, c, 0:2 * WIDE].rearrange("p (n d) -> p n d", d=HD) for c in range(2)]
                for c in range(2):
                    v.tensor_reduce(head_sum[:, c, :], heads_of[c], AX.X, ALU.add)
                v.drain()
                v.tensor_scalar(head_sum[:, :, :], head_sum[:, :, :], 1.0 / HD, None, ALU.mult)
                v.drain()
                for c in range(2):
                    ins = v.tensor_tensor(heads_of[c], heads_of[c],
                                          head_sum[:, c, :].unsqueeze(2).to_broadcast([C, 2 * HEADS, HD]),
                                          ALU.subtract)
                ins.then_inc(centered_ready, 1)
                v.tensor_scalar(affine[:, 0:2], affine_in[:, 0:2], HD ** -0.5, None, ALU.mult)
                v.tensor_copy(affine[:, 2:4], affine_in[:, 2:4])
                v.wait_ge(bias_mean, 1)
                v.tensor_tensor(b_centered[:, :], b_qk[:, :], bank[7][:, 0:QK], ALU.subtract).then_inc(bias_ready, 1)
                v.drain()
                with v.Fori(0, TURNS) as i:
                    norm_statistics(v, norm, lambda b: sample_of(h, i, b))
                    v.wait_ge(norm.rstd_ready, turn(i))
                    for b in range(GROUP):
                        ins = norm_apply(v, norm, lambda b: sample_of(h, i, b), lambda b: xn[:, b, :], b)
                    ins.then_inc(s["xn_ready"], 1)
                    v.wait_ge(s["gate_psum"], turn(i))
                    v.tensor_copy(glog[:, :, :], bank[6][0:T, 0:GROUP * GATES]).then_inc(s["gate_read"], 1)
                    v.drain()
                    for n, (lo, hi) in enumerate(parts):
                        v.tensor_reduce(gpeak[:, n, :], glog[:, :, lo:hi], AX.X, ALU.max)
                    v.drain()
                    for n, (lo, hi) in enumerate(parts):
                        ins = v.tensor_tensor(glog[:, :, lo:hi], glog[:, :, lo:hi],
                                              gpeak[:, n, :].unsqueeze(2).to_broadcast([T, GROUP, hi - lo]),
                                              ALU.subtract)
                    ins.then_inc(s["gshift_ready"], 1)
                    v.wait_ge(s["gexp_ready"], turn(i))
                    for n, (lo, hi) in enumerate(parts):
                        v.tensor_reduce(gsum[:, n, :], glog[:, :, lo:hi], AX.X, ALU.add)
                    v.drain()
                    v.reciprocal(gsum[:, :, :], gsum[:, :, :])
                    v.drain()
                    for n, (lo, hi) in enumerate(parts):
                        v.tensor_tensor(glog[:, :, lo:hi], glog[:, :, lo:hi],
                                        gsum[:, n, :].unsqueeze(2).to_broadcast([T, GROUP, hi - lo]), ALU.mult)
                    v.drain()
                    top_two_hot(v, core, top, glog[:, :, 0:ROUTED])
                    v.tensor_tensor(top.hot[:, 0, :, :], top.hot[:, 0, :, :], top.hot[:, 1, :, :], ALU.add)
                    v.drain()
                    v.tensor_tensor(glog[:, :, 0:ROUTED], glog[:, :, 0:ROUTED], top.hot[:, 0, :, :], ALU.mult)
                    v.drain()
                    v.tensor_reduce(gsum[:, 0, :], glog[:, :, 0:ROUTED], AX.X, ALU.add)
                    v.drain()
                    v.tensor_scalar(gsum[:, 0, :], gsum[:, 0, :], 2.0 ** -23, None, ALU.max)
                    v.drain()
                    v.reciprocal(gsum[:, 0, :], gsum[:, 0, :])
                    v.drain()
                    v.scalar_tensor_tensor(out=gsum[:, 0, :], in0=gsum[:, 0, :], scalar=4.0,
                                           in1=glog[:, :, ROUTED + 1], op0=ALU.mult, op1=ALU.mult)
                    v.tensor_scalar(gsum[:, 1, :], glog[:, :, ROUTED], 4.0, None, ALU.mult)
                    v.drain()
                    v.tensor_tensor(gates[:, :, SHARED:HEADS], glog[:, :, 0:ROUTED],
                                    gsum[:, 0, :].unsqueeze(2).to_broadcast([T, GROUP, ROUTED]), ALU.mult)
                    v.tensor_tensor(gates[:, :, 0:SHARED], glog[:, :, ROUTED + 2:GATES],
                                    gsum[:, 1, :].unsqueeze(2).to_broadcast([T, GROUP, SHARED]), ALU.mult)

                    def normed(j):
                        kind = 0 if j < QK // 2 else 2
                        if j == 0:
                            v.wait_ge(att.scores_psum, turn(i, 0, GROUP))
                            v.wait_ge(att.kblock_ready, turn(i, 0, GROUP))
                        v.wait_ge(s["centered_done"], turn(i, j + 1, QK))
                        v.wait_ge(s["rstd_q_ready"], turn(i, j + 1, QK))
                        v.tensor_tensor(qkT[:, j, :], centered[:, j % 2, :], rstd[:, j % 2, :], ALU.mult)
                        v.drain()
                        v.tensor_scalar(qkT[:, j, :], qkT[:, j, :], affine[:, kind:kind + 1],
                                        affine[:, kind + 1:kind + 2], ALU.mult, ALU.add).then_inc(s["qk_ready"], 1)

                    for j in range(QK):
                        v.wait_ge(s["square_ready"], turn(i, j + 1, QK))
                        v.tensor_scalar(centered[:, j % 2, :], bank[2 + j % 2][:, 0:N], b_centered[:, j:j + 1], None,
                                        ALU.add).then_inc(s["centered_done"], 1)
                        if j:
                            normed(j - 1)
                    normed(QK - 1)

                    def rescale(b, inv):
                        v.tensor_tensor(weight[:, b % 2, :], inv, gates[:, b, :], ALU.mult)
                        v.drain()
                        for p in range(2):
                            ins = v.tensor_tensor(o[:, b, p * WIDE // 2:(p + 1) * WIDE // 2]
                                                  .rearrange("t (n d) -> t n d", d=HD),
                                                  bank[6 + p][0:T, 0:WIDE // 2].rearrange("t (n d) -> t n d", d=HD),
                                                  weight[:, b % 2, 6 * p:6 * p + 6].unsqueeze(2)
                                                  .to_broadcast([T, 6, HD]), ALU.mult)
                        return ins
                    heads_vector(v, att, i, rescale)
                    v.wait_ge(s["oT_psum"], turn(i))
                    for j in range(3):
                        ins = v.tensor_copy(oT[:, j, :], bank[j][:, 0:N])
                    ins.then_inc(s["oT_dve"], 1)
                    v.wait_ge(s["out_psum"], turn(i))
                    for p in range(2):
                        rows = h[:, bass.ds(i * (GROUP * D) + p * (2 * D), 2 * D)]
                        ins = v.tensor_tensor(rows, bank[6 + p][0:T, 0:2 * D], rows, ALU.add)
                    ins.then_inc(s["h_done"], 1)



def position_attention_stage(core, a):
    nc, bank, h = core.nc, core.bank, core.h
    KV = D // 3
    with ExitStack() as ctx:
        sb, sem, load_sem, raised = stage_tools(core, ctx)
        norm = Norm(sb, sem, "norm")
        table = sb("table", [C, 2, T])
        w_v = sb("w_v", [C, 2, KV])
        w_out = sb("w_out", [KV, D])
        peak = sb("peak", [T, 1])
        total = sb("total", [T, 1])
        probs = sb("probs", [T, T])
        probsT = sb("probsT", [T, T])
        xn = sb("xn", [T, GROUP, D])
        xT = sb("xT", [C, 2, N])
        vals = sb("vals", [T, GROUP, KV])
        contextT = sb("contextT", [KV, N])
        w_loaded, scores_psum, peak_ready, exp_ready, probs_ready, probsT_psum, probsT_ready = (
            load_sem(n) for n in ("w_loaded", "scores_psum", "peak_ready", "exp_ready", "probs_ready",
                                  "probsT_psum", "probsT_ready"))
        names = ("xn_ready", "xT_psum", "xT_ready", "v_psum", "v_ready", "context_psum", "context_ready",
                 "out_psum", "h_done")
        s = {n: sem(n) for n in names}

        with nc.Block() as block:
            @block.sync
            def _(sp):
                raise_to_start(sp, raised)
                sp.dma_start(table[:, :, :], a["f_table"]).then_inc(w_loaded, 16)
                sp.dma_start(w_v[:, :, :], a["f_wv"]).then_inc(w_loaded, 16)
                sp.dma_start(w_out[:, :], a["f_wo"]).then_inc(w_loaded, 16)

            @block.gpsimd
            def _(pool):
                with pool.Fori(0, TURNS) as i:
                    norm_rstd(pool, core, norm, i)

            @block.tensor
            def _(pe):
                pe.wait_ge(w_loaded, 48)
                for c in range(2):
                    mm = pe.matmul(bank[6][0:T, 0:T], table[:, c, :], table[:, c, :], start=(c == 0), stop=(c == 1))
                mm.then_inc(scores_psum, 1)
                pe.wait_ge(probs_ready, 1)
                pe.transpose(bank[7][0:T, 0:T], probs[:, :], core.ident[0:T, 0:T]).then_inc(probsT_psum, 1)
                pe.wait_ge(probsT_ready, 1)
                with pe.Fori(0, TURNS) as i:
                    pe.wait_ge(s["xn_ready"], turn(i))
                    pe.wait_ge(s["xT_ready"], turn(i, 0))
                    transpose_group(pe, core, bank[0:2], xn, s["xT_psum"])
                    pe.wait_ge(s["v_ready"], turn(i, 0))
                    pe.wait_ge(s["xT_ready"], turn(i))
                    for b in range(GROUP):
                        for c in range(2):
                            mm = pe.matmul(bank[2][0:T, cols(b, KV)], xT[:, c, cols(b)], w_v[:, c, :],
                                           start=(c == 0), stop=(c == 1))
                    mm.then_inc(s["v_psum"], 1)
                    pe.wait_ge(s["context_ready"], turn(i, 0))
                    pe.wait_ge(s["v_ready"], turn(i))
                    for b in range(GROUP):
                        mm = pe.matmul(bank[3][0:KV, cols(b)], vals[:, b, :], probsT[:, :], start=True, stop=True)
                    mm.then_inc(s["context_psum"], 1)
                    pe.wait_ge(s["h_done"], turn(i, 0))
                    pe.wait_ge(s["context_ready"], turn(i))
                    for b in range(GROUP):
                        mm = pe.matmul(bank[4 + b // 2][0:T, cols(b % 2, D)], contextT[:, cols(b)], w_out[:, :],
                                       start=True, stop=True)
                    mm.then_inc(s["out_psum"], 1)

            @block.scalar
            def _(act):
                act.wait_ge(peak_ready, 1)
                act.activation(probs[:, :], bank[6][0:T, 0:T], ACT.Exp, bias=peak[:, 0:1],
                               accum_out=total[:, 0:1]).then_inc(exp_ready, 1)
                act.wait_ge(probsT_psum, 1)
                act.activation(probsT[:, :], bank[7][0:T, 0:T], ACT.Copy).then_inc(probsT_ready, 1)
                with act.Fori(0, TURNS) as i:
                    act.wait_ge(s["v_psum"], turn(i, 0))
                    act.wait_ge(s["xT_psum"], turn(i))
                    for c in range(2):
                        ins = act.activation(xT[:, c, :], bank[c][0:C, 0:N], ACT.Copy)
                    ins.then_inc(s["xT_ready"], 1)
                    act.wait_ge(s["context_psum"], turn(i, 0))
                    act.wait_ge(s["v_psum"], turn(i))
                    act.activation(vals[:, :, :], bank[2][0:T, 0:GROUP * KV], ACT.Copy).then_inc(s["v_ready"], 1)
                    act.wait_ge(s["out_psum"], turn(i, 0))
                    act.wait_ge(s["context_psum"], turn(i))
                    act.activation(contextT[:, :], bank[3][0:KV, 0:N], ACT.Copy).then_inc(s["context_ready"], 1)

            @block.vector
            def _(v):
                v.wait_ge(scores_psum, 1)
                v.tensor_reduce(peak[:, :], bank[6][0:T, 0:T], AX.X, ALU.max, negate=True).then_inc(peak_ready, 1)
                v.wait_ge(exp_ready, 1)
                v.reciprocal(total[:, :], total[:, :])
                v.drain()
                v.tensor_scalar(probs[:, :], probs[:, :], total[:, 0:1], None, ALU.mult).then_inc(probs_ready, 1)
                with v.Fori(0, TURNS) as i:
                    norm_statistics(v, norm, lambda b: sample_of(h, i, b))
                    v.wait_ge(s["xT_psum"], turn(i, 0))
                    v.wait_ge(norm.rstd_ready, turn(i))
                    for b in range(GROUP):
                        ins = norm_apply(v, norm, lambda b: sample_of(h, i, b), lambda b: xn[:, b, :], b)
                    ins.then_inc(s["xn_ready"], 1)
                    v.wait_ge(s["out_psum"], turn(i))
                    for p in range(2):
                        rows = h[:, bass.ds(i * (GROUP * D) + p * (2 * D), 2 * D)]
                        ins = v.tensor_tensor(rows, bank[4 + p][0:T, 0:2 * D], rows, ALU.add)
                    ins.then_inc(s["h_done"], 1)



def int8_stage(core, a):
    nc, bank, h = core.nc, core.bank, core.h
    ROUND = 1.5 * 2.0 ** 23
    ACT_SCALE, W_SCALE = 0.02, 0.01
    with ExitStack() as ctx:
        sb, sem, load_sem, raised = stage_tools(core, ctx)
        norm = Norm(sb, sem, "norm")
        w_words = sb("w_words", [C, 2 * D // 4], I32)
        w8 = w_words[:, :].bitcast(I8).rearrange("p (c n) -> p c n", c=2)
        w = sb("w", [C, 2, D], BF16)
        ident = sb("ident16", [128, 128], BF16)
        bias = sb("bias", [T, D])
        xn = sb("xn", [T, GROUP, D])
        quant = sb("quant", [T, GROUP, D], BF16)
        quantT = sb("quantT", [C, 2, N], BF16)
        scaled = sb("scaled", [T, GROUP, D])
        w_loaded, consts_ready = load_sem("w_loaded"), load_sem("consts_ready")
        names = ("quant_ready", "quantT_psum", "quantT_ready", "out_psum", "h_done")
        s = {n: sem(n) for n in names}
        turned = [bank[c][0:C, 0:N // 2].bitcast(BF16) for c in range(2)]

        with nc.Block() as block:
            @block.sync
            def _(sp):
                raise_to_start(sp, raised)
                sp.dma_start(w_words[:, :], a["g_w"]).then_inc(w_loaded, 16)
                sp.dma_start(bias[:, :], a["g_bias"].to_broadcast([T, D])).then_inc(w_loaded, 16)

            @block.gpsimd
            def _(pool):
                with pool.Fori(0, TURNS) as i:
                    norm_rstd(pool, core, norm, i)

            @block.tensor
            def _(pe):
                pe.wait_ge(consts_ready, 1)
                with pe.Fori(0, TURNS) as i:
                    pe.wait_ge(s["quantT_ready"], turn(i, 0))
                    pe.wait_ge(s["quant_ready"], turn(i))
                    for c in range(2):
                        for b in range(GROUP):
                            mm = pe.transpose(turned[c][:, cols(b)], quant[:, b, c * C:(c + 1) * C],
                                              ident[0:T, 0:T])
                    mm.then_inc(s["quantT_psum"], 1)
                    pe.wait_ge(s["h_done"], turn(i, 0))
                    pe.wait_ge(s["quantT_ready"], turn(i))
                    for b in range(GROUP):
                        for c in range(2):
                            mm = pe.matmul(bank[4 + b // 2][0:T, cols(b % 2, D)], quantT[:, c, cols(b)], w[:, c, :],
                                           start=(c == 0), stop=(c == 1))
                    mm.then_inc(s["out_psum"], 1)

            @block.scalar
            def _(act):
                with act.Fori(0, TURNS) as i:
                    act.wait_ge(s["out_psum"], turn(i, 0))
                    act.wait_ge(s["quantT_psum"], turn(i))
                    for c in range(2):
                        ins = act.activation(quantT[:, c, :], turned[c], ACT.Copy)
                    ins.then_inc(s["quantT_ready"], 1)

            @block.vector
            def _(v):
                v.wait_ge(w_loaded, 32)
                v.tensor_copy(w[:, :, :], w8)
                v.tensor_copy(ident[:, :], core.ident[:, :]).then_inc(consts_ready, 1)
                with v.Fori(0, TURNS) as i:
                    norm_statistics(v, norm, lambda b: sample_of(h, i, b))
                    v.wait_ge(norm.rstd_ready, turn(i))
                    for b in range(GROUP):
                        norm_apply(v, norm, lambda b: sample_of(h, i, b), lambda b: xn[:, b, :], b)
                    v.drain()
                    v.tensor_scalar(xn[:, :, :], xn[:, :, :], 1.0 / ACT_SCALE, ROUND, ALU.mult, ALU.add)
                    v.drain()
                    v.tensor_scalar(xn[:, :, :], xn[:, :, :], ROUND, 127.0, ALU.subtract, ALU.min)
                    v.drain()
                    v.wait_ge(s["quantT_psum"], turn(i, 0))
                    v.tensor_scalar(quant[:, :, :], xn[:, :, :], -128.0, None, ALU.max).then_inc(s["quant_ready"], 1)
                    v.wait_ge(s["out_psum"], turn(i))
                    for p in range(2):
                        v.scalar_tensor_tensor(out=scaled[:, 2 * p:2 * p + 2, :],
                                               in0=bank[4 + p][0:T, 0:2 * D].rearrange("t (b d) -> t b d", b=2),
                                               scalar=ACT_SCALE * W_SCALE,
                                               in1=bias[:, :].unsqueeze(1).to_broadcast([T, 2, D]),
                                               op0=ALU.mult, op1=ALU.add)
                    v.drain()
                    rows = h[:, bass.ds(i * (GROUP * D), GROUP * D)]
                    v.tensor_tensor(rows, rows, scaled[:, :, :].rearrange("t b d -> t (b d)"), ALU.add
                                    ).then_inc(s["h_done"], 1)



def rotary_heads_stage(core, a):
    nc, bank, h = core.nc, core.bank, core.h
    with ExitStack() as ctx:
        sb, sem, load_sem, raised = stage_tools(core, ctx)
        norm = Norm(sb, sem, "norm")
        w = sb("w", [C, 2, 5 * D])
        b_qk = sb("b_qk", [C, 8])
        b_v = sb("b_v", [1, D])
        w_out = sb("w_out", [C, 2, D])
        b_out = sb("b_out", [1, D])
        angles = sb("angles", [C, 4, T])
        xn = sb("xn", [T, GROUP, D])
        xT = sb("xT", [C, 2, N])
        cos_part = sb("cos_part", [C, 2, N])
        sin_part = sb("sin_part", [C, 2, N])
        qkT = sb("qkT", [C, 4, N])
        qT, kT = qkT[:, 0:2, :], qkT[:, 2:4, :]
        vals = sb("vals", [T, GROUP, D])
        o = sb("o", [T, GROUP, D])
        oT = sb("oT", [C, 2, N])
        att = Heads(core, sb, sem, 16, core.mask16)
        w_loaded = load_sem("w_loaded")
        names = ("xn_ready", "xT_psum", "xT_ready", "qk_psum", "parts_ready", "qk_ready", "v_psum", "v_ready",
                 "oT_psum", "oT_ready", "out_psum", "h_done")
        s = {n: sem(n) for n in names}
        loads = [(w, "h_w"), (b_qk, "h_bqk"), (b_v, "h_bv"), (w_out, "h_wo"), (b_out, "h_bo"), (angles, "h_angles")]

        with nc.Block() as block:
            @block.sync
            def _(sp):
                raise_to_start(sp, raised)
                for tile, name in loads:
                    sp.dma_start(tile[tuple(slice(None) for _ in tile.shape)], a[name]).then_inc(w_loaded, 16)

            @block.gpsimd
            def _(pool):
                with pool.Fori(0, TURNS) as i:
                    norm_rstd(pool, core, norm, i)
                    pool.wait_ge(att.scores_psum, turn(i, 0, GROUP))
                    pool.wait_ge(s["qk_ready"], turn(i, 4, 4))
                    for b in range(GROUP):
                        heads_pool(pool, att, i, kT, b)

            @block.tensor
            def _(pe):
                pe.wait_ge(w_loaded, 16 * len(loads))
                with pe.Fori(0, TURNS) as i:
                    pe.wait_ge(s["xn_ready"], turn(i))
                    transpose_group(pe, core, bank[0:2], xn, s["xT_psum"])
                    pe.wait_ge(s["h_done"], turn(i, 0))
                    pe.wait_ge(s["xT_ready"], turn(i))
                    for j in range(4):
                        pe.wait_ge(s["parts_ready"], turn(i, j - 1, 4))
                        for r in range(2):
                            at = (2 * (j // 2) + r) * D + j % 2 * C
                            for c in range(2):
                                mm = pe.matmul(bank[2 + j % 2 * 2 + r][0:C, 0:N], w[:, c, at:at + C], xT[:, c, :],
                                               start=(c == 0), stop=(c == 1))
                        mm.then_inc(s["qk_psum"], 1)
                    for b in range(GROUP):
                        out = bank[6 + b // 2][0:T, cols(b % 2, D)]
                        for c in range(2):
                            pe.matmul(out, xT[:, c, cols(b)], w[:, c, 4 * D:5 * D], start=(c == 0), stop=False)
                        mm = pe.matmul(out, core.ones[0:1, 0:T], b_v[:, :], start=False, stop=True)
                    mm.then_inc(s["v_psum"], 1)
                    pe.wait_ge(s["qk_ready"], turn(i, 4, 4))
                    pe.wait_ge(s["v_ready"], turn(i))
                    heads_tensor(pe, att, i, qT, vals)
                    pe.wait_ge(att.context_done, turn(i, GROUP, GROUP))
                    transpose_group(pe, core, bank[0:2], o, s["oT_psum"])
                    pe.wait_ge(s["oT_ready"], turn(i))
                    for b in range(GROUP):
                        out = bank[2 + b // 2][0:T, cols(b % 2, D)]
                        for c in range(2):
                            pe.matmul(out, oT[:, c, cols(b)], w_out[:, c, :], start=(c == 0), stop=False)
                        mm = pe.matmul(out, core.ones[0:1, 0:T], b_out[:, :], start=False, stop=True)
                    mm.then_inc(s["out_psum"], 1)

            @block.scalar
            def _(act):
                with act.Fori(0, TURNS) as i:
                    act.wait_ge(s["xT_psum"], turn(i))
                    for c in range(2):
                        ins = act.activation(xT[:, c, :], bank[c][0:C, 0:N], ACT.Copy)
                    ins.then_inc(s["xT_ready"], 1)
                    act.wait_ge(s["v_psum"], turn(i))
                    for p in range(2):
                        ins = act.activation(vals[:, 2 * p:2 * p + 2, :], bank[6 + p][0:T, 0:2 * D], ACT.Copy)
                    ins.then_inc(s["v_ready"], 1)
                    heads_scalar(act, att, i)
                    act.wait_ge(s["oT_psum"], turn(i))
                    for c in range(2):
                        ins = act.activation(oT[:, c, :], bank[c][0:C, 0:N], ACT.Copy)
                    ins.then_inc(s["oT_ready"], 1)

            @block.vector
            def _(v):
                v.wait_ge(w_loaded, 16 * len(loads))
                with v.Fori(0, TURNS) as i:
                    norm_statistics(v, norm, lambda b: sample_of(h, i, b))
                    v.wait_ge(norm.rstd_ready, turn(i))
                    for b in range(GROUP):
                        ins = norm_apply(v, norm, lambda b: sample_of(h, i, b), lambda b: xn[:, b, :], b)
                    ins.then_inc(s["xn_ready"], 1)
                    for j in range(4):
                        k, kind = j % 2, j // 2
                        v.wait_ge(s["qk_psum"], turn(i, j + 1, 4))
                        for part, r in ((cos_part, 0), (sin_part, 1)):
                            at = 4 * kind + 2 * r + k
                            ins = v.scalar_tensor_tensor(
                                out=part[:, k, :].rearrange("d (b t) -> d b t", b=GROUP),
                                in0=bank[2 + 2 * k + r][0:C, 0:N].rearrange("d (b t) -> d b t", b=GROUP),
                                scalar=b_qk[:, at:at + 1],
                                in1=angles[:, 2 * kind + r, :].unsqueeze(1).to_broadcast([C, GROUP, T]),
                                op0=ALU.add, op1=ALU.mult)
                        ins.then_inc(s["parts_ready"], 1)
                        v.drain()
                        v.tensor_tensor(qkT[:, j, :], cos_part[:, k, :], sin_part[:, k, :], ALU.add
                                        ).then_inc(s["qk_ready"], 1)

                    def rescale(b, inv):
                        return v.tensor_tensor(o[:, b, :].rearrange("t (n d) -> t n d", n=HEADS),
                                               bank[6][0:T, 0:D].rearrange("t (n d) -> t n d", n=HEADS),
                                               inv.unsqueeze(2).to_broadcast([T, HEADS, 16]), ALU.mult)
                    heads_vector(v, att, i, rescale)
                    v.wait_ge(s["out_psum"], turn(i))
                    for p in range(2):
                        rows = h[:, bass.ds(i * (GROUP * D) + p * (2 * D), 2 * D)]
                        ins = v.tensor_tensor(rows, bank[2 + p][0:T, 0:2 * D], rows, ALU.add)
                    ins.then_inc(s["h_done"], 1)



def second_router_stage(core, a):
    nc, bank, h = core.nc, core.bank, core.h
    PROBE = 24
    COLS = EXPERTS + PROBE + 1
    with ExitStack() as ctx:
        sb, sem, load_sem, raised = stage_tools(core, ctx)
        norm = Norm(sb, sem, "norm")
        w = sb("w", [C, 2, COLS])
        emb = sb("emb", [T, EXPERTS, PROBE])
        emb_square = sb("emb_square", [T, EXPERTS, PROBE])
        emb_norm = sb("emb_norm", [T, EXPERTS])
        emb_sum = sb("emb_sum", [T, EXPERTS])
        emb_inv = sb("emb_inv", [T, EXPERTS])
        mean_factor = sb("mean_factor", [T, EXPERTS])
        fatigue_energy = sb("fatigue_energy", [T, 2, EXPERTS])
        constant_bias = sb("constant_bias", [T, EXPERTS])
        b2 = sb("b2", [EXPERTS, D])
        xn = sb("xn", [T, GROUP, D])
        xT = sb("xT", [C, 2, N])
        raw = sb("raw", [T, GROUP, COLS])
        probe_square = sb("probe_square", [T, GROUP, PROBE])
        probe_sum = sb("probe_sum", [T, GROUP])
        probe_norm = sb("probe_norm", [T, GROUP])
        probe_inv = sb("probe_inv", [T, GROUP])
        aligned = sb("aligned", [T, GROUP, EXPERTS, PROBE])
        align = sb("align", [T, GROUP, EXPERTS])
        term = sb("term", [T, GROUP, EXPERTS])
        gatesT = sb("gatesT", [EXPERTS, N])
        router = Router(sb, sem, "router")
        w_loaded, emb_sum_ready, emb_norm_ready = (load_sem(n) for n in ("w_loaded", "emb_sum_ready", "emb_norm_ready"))
        names = ("xn_ready", "xT_psum", "xT_ready", "xT_kept", "raw_psum", "raw_read", "probe_sum_ready",
                 "probe_norm_ready", "gates_ready", "gatesT_psum", "gatesT_ready", "bias_psum", "h_done")
        s = {n: sem(n) for n in names}

        with nc.Block() as block:
            @block.sync
            def _(sp):
                raise_to_start(sp, raised)
                sp.dma_start(w[:, :, :], a["i_router"]).then_inc(w_loaded, 16)
                sp.dma_start(b2[:, :], a["i_b2"]).then_inc(w_loaded, 16)
                sp.dma_start(emb[:, :, :].rearrange("t e r -> t (e r)"),
                             a["i_emb"].to_broadcast([T, EXPERTS * PROBE])).then_inc(w_loaded, 16)
                sp.dma_start(fatigue_energy[:, :, :].rearrange("t a e -> t (a e)"),
                             a["i_fe"].to_broadcast([T, 2 * EXPERTS])).then_inc(w_loaded, 16)

            @block.gpsimd
            def _(pool):
                pool.wait_ge(emb_sum_ready, 1)
                pool.tensor_tensor(emb_norm[:, :], emb_sum[:, :], core.plus_half[0:T, 0:EXPERTS], ALU.pow
                                   ).then_inc(emb_norm_ready, 1)
                with pool.Fori(0, TURNS) as i:
                    norm_rstd(pool, core, norm, i)
                    pool.wait_ge(s["probe_sum_ready"], turn(i))
                    pool.tensor_tensor(probe_norm[:, :], probe_sum[:, :], core.plus_half[0:T, 0:GROUP], ALU.pow
                                       ).then_inc(s["probe_norm_ready"], 1)

            @block.tensor
            def _(pe):
                pe.wait_ge(w_loaded, 64)
                with pe.Fori(0, TURNS) as i:
                    pe.wait_ge(s["xn_ready"], turn(i))
                    transpose_group(pe, core, bank[0:2], xn, s["xT_psum"])
                    pe.wait_ge(s["xT_ready"], turn(i))
                    pe.wait_ge(s["raw_read"], turn(i, 0))
                    for b in range(GROUP):
                        for c in range(2):
                            mm = pe.matmul(bank[2][0:T, cols(b, COLS)], xT[:, c, cols(b)], w[:, c, :],
                                           start=(c == 0), stop=(c == 1))
                    mm.then_inc(s["raw_psum"], 1)
                    pe.wait_ge(s["gates_ready"], turn(i))
                    for b in range(GROUP):
                        mm = pe.transpose(bank[3][0:EXPERTS, cols(b)], router.gates[:, b, :], core.ident[0:T, 0:T])
                    mm.then_inc(s["gatesT_psum"], 1)
                    pe.wait_ge(s["gatesT_ready"], turn(i))
                    pe.wait_ge(s["h_done"], turn(i, 0))
                    for b in range(GROUP):
                        mm = pe.matmul(bank[4 + b // 2][0:T, cols(b % 2, D)], gatesT[:, cols(b)], b2[:, :],
                                       start=True, stop=True)
                    mm.then_inc(s["bias_psum"], 1)

            @block.scalar
            def _(act):
                with act.Fori(0, TURNS) as i:
                    act.wait_ge(s["raw_psum"], turn(i, 0))
                    act.wait_ge(s["xT_kept"], turn(i, 0))
                    act.wait_ge(s["xT_psum"], turn(i))
                    for c in range(2):
                        ins = act.activation(xT[:, c, :], bank[c][0:C, 0:N], ACT.Copy)
                    ins.then_inc(s["xT_ready"], 1)
                    router_scalar(act, router, i)
                    act.wait_ge(s["gatesT_psum"], turn(i))
                    act.activation(gatesT[:, :], bank[3][0:EXPERTS, 0:N], ACT.Copy).then_inc(s["gatesT_ready"], 1)

            @block.vector
            def _(v):
                v.wait_ge(w_loaded, 64)
                v.tensor_tensor(emb_square[:, :, :], emb[:, :, :], emb[:, :, :], ALU.mult)
                v.drain()
                v.tensor_reduce(emb_sum[:, :], emb_square[:, :, :], AX.X, ALU.add).then_inc(emb_sum_ready, 1)
                v.tensor_tensor(constant_bias[:, :], fatigue_energy[:, 1, :], fatigue_energy[:, 0, :], ALU.subtract)
                v.drain()
                v.tensor_scalar(constant_bias[:, :], constant_bias[:, :], 0.1, None, ALU.mult)
                v.wait_ge(emb_norm_ready, 1)
                v.tensor_scalar(mean_factor[:, :], emb_norm[:, :], 0.02, 0.02, ALU.mult, ALU.add)
                v.tensor_scalar(emb_inv[:, :], emb_norm[:, :], 1e-12, None, ALU.max)
                v.drain()
                v.reciprocal(emb_inv[:, :], emb_inv[:, :])
                v.drain()
                v.tensor_tensor(emb[:, :, :], emb[:, :, :],
                                emb_inv[:, :].unsqueeze(2).to_broadcast([T, EXPERTS, PROBE]), ALU.mult)
                v.drain()
                wide = [T, GROUP, EXPERTS]
                with v.Fori(0, TURNS) as i:
                    norm_statistics(v, norm, lambda b: sample_of(h, i, b))
                    v.wait_ge(norm.rstd_ready, turn(i))
                    for b in range(GROUP):
                        ins = norm_apply(v, norm, lambda b: sample_of(h, i, b), lambda b: xn[:, b, :], b)
                    ins.then_inc(s["xn_ready"], 1)
                    v.wait_ge(s["xT_ready"], turn(i))
                    for c in range(2):
                        ins = v.tensor_scalar(core.zT_all[:, c, bass.ds(i * N, N)], xT[:, c, :], 1.0, None, ALU.mult)
                    ins.then_inc(s["xT_kept"], 1)
                    v.wait_ge(s["raw_psum"], turn(i))
                    v.tensor_copy(raw[:, :, :], bank[2][0:T, 0:GROUP * COLS]).then_inc(s["raw_read"], 1)
                    v.drain()
                    probe = raw[:, :, EXPERTS:EXPERTS + PROBE]
                    v.tensor_tensor(probe_square[:, :, :], probe, probe, ALU.mult)
                    v.drain()
                    v.tensor_reduce(probe_sum[:, :], probe_square[:, :, :], AX.X, ALU.add
                                    ).then_inc(s["probe_sum_ready"], 1)
                    for b in range(GROUP):
                        v.tensor_tensor(aligned[:, b, :, :],
                                        raw[:, b, EXPERTS:EXPERTS + PROBE].unsqueeze(1)
                                        .to_broadcast([T, EXPERTS, PROBE]), emb[:, :, :], ALU.mult)
                    v.drain()
                    for b in range(GROUP):
                        v.tensor_reduce(align[:, b, :], aligned[:, b, :, :], AX.X, ALU.add)
                    v.wait_ge(s["probe_norm_ready"], turn(i))
                    v.tensor_scalar(probe_inv[:, :], probe_norm[:, :], 1e-12, None, ALU.max)
                    v.drain()
                    v.reciprocal(probe_inv[:, :], probe_inv[:, :])
                    v.tensor_tensor(term[:, :, :], raw[:, :, COLS - 1:COLS].to_broadcast(wide),
                                    mean_factor[:, :].unsqueeze(1).to_broadcast(wide), ALU.mult)
                    v.drain()
                    v.tensor_tensor(router.logits[:, :, :], raw[:, :, 0:EXPERTS], term[:, :, :], ALU.add)
                    v.tensor_tensor(align[:, :, :], align[:, :, :],
                                    probe_inv[:, :].unsqueeze(2).to_broadcast(wide), ALU.mult)
                    v.drain()
                    v.scalar_tensor_tensor(out=router.logits[:, :, :], in0=align[:, :, :], scalar=0.02,
                                           in1=router.logits[:, :, :], op0=ALU.mult, op1=ALU.add)
                    v.drain()
                    v.tensor_tensor(router.logits[:, :, :], router.logits[:, :, :],
                                    constant_bias[:, :].unsqueeze(1).to_broadcast(wide), ALU.add)
                    v.drain()
                    router_vector(v, core, router, i).then_inc(s["gates_ready"], 1)
                    v.wait_ge(s["bias_psum"], turn(i))
                    for p in range(2):
                        rows = h[:, bass.ds(i * (GROUP * D) + p * (2 * D), 2 * D)]
                        ins = v.tensor_tensor(rows, bank[4 + p][0:T, 0:2 * D], rows, ALU.add)
                    ins.then_inc(s["h_done"], 1)


def store_stage(core, a):
    nc = core.nc
    with ExitStack() as ctx:
        _, _, load_sem, _ = stage_tools(core, ctx)
        stored = load_sem("stored")
        with nc.Block() as block:
            @block.sync
            def _(sp):
                sp.dma_start(a["out"].rearrange("s t d -> t s d"),
                             core.h[:, :].rearrange("t (s d) -> t s d", d=D)).then_inc(stored, 16)
                sp.wait_ge(stored, 16)


def build(nc, a):
    with ExitStack() as ctx:
        core = Core()
        core.nc, core.made = nc, 0
        core.h = ctx.enter_context(nc.sbuf_tensor("h", [T, SAMPLES * D], F32))
        core.minus_half = ctx.enter_context(nc.sbuf_tensor("minus_half", [128, 48], F32))
        core.plus_half = ctx.enter_context(nc.sbuf_tensor("plus_half", [128, 48], F32))
        core.ones = ctx.enter_context(nc.sbuf_tensor("ones", [128, 128], F32))
        core.constants = {}
        core.zT_all = ctx.enter_context(nc.sbuf_tensor("zT_all", [C, 2, SAMPLES * T], F32))
        core.gates = ctx.enter_context(nc.sbuf_tensor("gates", [T, SAMPLES * EXPERTS], F32))
        for name, shape in (("ident", [128, 128]), ("mask16", [C, 6]), ("mask64", [128, 2]), ("iota", [128, 16])):
            core.constants[name] = ctx.enter_context(nc.sbuf_tensor("c_" + name, shape, F32))
        core.ident, core.iota = core.constants["ident"], core.constants["iota"]
        core.mask16, core.mask64 = core.constants["mask16"], core.constants["mask64"]
        core.bank = [ctx.enter_context(nc.psum_tensor(f"bank{i}", [128, 512], F32)) for i in range(8)]
        stages = [
            lambda: tokens_stage(core, a),
            lambda: wide_attention_stage(core, a),
            lambda: (first_heads_stage(core, a), experts_stage(core, a, False)),
            lambda: ssm_stage(core, a),
            lambda: gated_heads_stage(core, a),
            lambda: position_attention_stage(core, a),
            lambda: int8_stage(core, a),
            lambda: rotary_heads_stage(core, a),
            lambda: (second_router_stage(core, a), experts_stage(core, a, True)),
        ]
        for stage in stages:
            stage()
        store_stage(core, a)



def shape_constants(np):
    ident = np.eye(128, dtype=np.float32)
    mask16 = (np.arange(C)[:, None] // 16 == np.arange(6)[None, :]).astype(np.float32)
    mask64 = (np.arange(128)[:, None] // 64 == np.arange(2)[None, :]).astype(np.float32)
    iota = np.tile(np.arange(16, dtype=np.float32), (128, 1))
    spread = (np.arange(C)[:, None, None] == (np.arange(12)[:, None] * 8 + np.arange(128)[None, :] // 16)[None])
    gather = spread.transpose(2, 1, 0)
    average = (mask64 @ mask64.T) / np.float32(64)
    pos = np.arange(T, dtype=np.float32)[:, None]
    freqs = np.float32(10000.0) ** (-np.arange(0, D, 2, dtype=np.float32) / D)
    table = np.concatenate([np.sin(pos * freqs), np.cos(pos * freqs)], axis=1).astype(np.float32).T
    half, turned = 8, 4
    scale = np.float32(10000.0) ** (np.float32(2) * np.arange(turned, dtype=np.float32) / np.float32(16))
    angle = np.zeros((T, half), np.float32)
    angle[:, :turned] = pos / scale
    cos = np.tile(np.cos(angle).T, (2 * 6, 1))
    sin = np.tile(np.concatenate([-np.sin(angle).T, np.sin(angle).T]), (6, 1))
    angles = np.stack([cos / 4, sin / 4, cos, sin], axis=1).astype(np.float32)
    return {"f_table": table.reshape(2, C, T).swapaxes(0, 1), "h_angles": angles, "ident": ident, "mask16": mask16, "mask64": mask64, "iota": iota, "average": average,
            "spread": spread.astype(np.float32), "gather": gather.astype(np.float32)}


def kernel(**inputs):
    import numpy as np
    import concourse.bacc as bacc
    from concourse.bass_utils import run_bass_kernel_spmd as run

    x = {k: np.asarray(v) for k, v in inputs.items()}

    def chunks(w, k):
        return w.reshape(k, w.shape[0] // k, *w.shape[1:]).swapaxes(0, 1)

    def per_partition(b, k):
        return b.reshape(k, -1).T

    arrays = shape_constants(np)
    image = x["x"].reshape(SAMPLES, 3, 6, 16, 6, 16).transpose(0, 1, 2, 4, 3, 5).reshape(SAMPLES, IMG, 768)
    image = image.transpose(2, 0, 1)
    arrays["patches"] = chunks(image, PATCH_K)
    arrays["tok_w"] = chunks(x["L0_tok_W"].T, PATCH_K)
    arrays["tok_b"] = x["L0_tok_b"].reshape(1, D)
    arrays["cls"] = x["L0_tok_class_token"]
    arrays["pos"] = x["L0_tok_pos_embedding"]
    arrays["txt"] = x["txt"]
    arrays["a_wqkv"] = chunks(x["L0_attn_W_qkv"], 2)
    arrays["a_bqk"] = per_partition(x["L0_attn_b_qkv"][0:2 * D], 4)
    arrays["a_bv"] = x["L0_attn_b_qkv"][2 * D:].reshape(1, D)
    arrays["b_wqkv"] = chunks(x["L0_ffn_Wqkv"], 2)
    arrays["b_wproj"] = chunks(x["L0_ffn_Wproj"], 2)
    arrays["b_wrouter"] = chunks(x["L0_ffn_Wrouter"], 2)
    arrays["b_affine"] = np.concatenate([per_partition(x["L0_ffn_" + n], 2)
                                         for n in ("ln1_g", "ln1_b", "ln2_g", "ln2_b")], axis=1)
    arrays["b_w1"] = x["L0_ffn_W1"].reshape(EXPERTS, 2, C, FF).transpose(0, 2, 1, 3)
    arrays["b_w2"] = x["L0_ffn_W2"].reshape(EXPERTS, FC, 128, D).transpose(0, 2, 1, 3)
    ssm = {k[8:]: v for k, v in x.items() if k.startswith("L1_attn_")}
    arrays["c_wi"] = chunks(ssm["Wi"], 2)
    arrays["c_wdt"] = chunks(ssm["Wdt"], 2)
    arrays["c_wb"] = chunks(ssm["WB"], 2)
    arrays["c_wc"] = chunks(ssm["WC"], 2)
    arrays["c_wo"] = chunks(ssm["Wo"], 2)
    arrays["c_bo"] = ssm["bo"].reshape(1, D)
    arrays["c_channel"] = np.concatenate(
        [v.reshape(2, C, -1).swapaxes(0, 1) for v in (ssm["bi"][:D], ssm["bi"][D:], ssm["bconv"], ssm["bdt"], ssm["D"],
                                                      ssm["Wconv"])], axis=2)
    arrays["c_rows"] = np.stack([v.reshape(24, 128).T for v in (ssm["A_log"], ssm["bB"], ssm["bC"])], axis=1)
    gh = {k[7:]: v for k, v in x.items() if k.startswith("L1_ffn_")}
    arrays["e_wqkv"] = chunks(gh["qkv_w"], 2)
    arrays["e_wg"] = chunks(np.concatenate([gh["wg_w"], gh["wg0_w"], gh["wg1_w"]], axis=1), 2)
    arrays["e_wproj"] = chunks(gh["proj_w"], 6)
    arrays["e_bv"] = gh["qkv_b"][1536:].reshape(1, 768)
    arrays["e_bqk"] = gh["qkv_b"][:1536].reshape(12, 128).T
    arrays["e_bproj"] = gh["proj_b"].reshape(1, D)
    arrays["e_affine"] = np.stack([np.tile(gh[n], 2) for n in ("q_norm_w", "q_norm_b", "k_norm_w", "k_norm_b")], axis=1)
    arrays["f_wv"] = chunks(x["L2_attn_Wv"].T, 2)
    arrays["f_wo"] = x["L2_attn_Wo"].T
    arrays["g_w"] = np.ascontiguousarray(chunks(x["L2_ffn_weight_t"], 2)).reshape(C, 2 * D).view(np.int32)
    arrays["g_bias"] = x["L2_ffn_bias"].reshape(1, D)
    rh = {k[8:]: v for k, v in x.items() if k.startswith("L3_attn_")}
    exchange = (np.arange(D) // 16) * 16 + (np.arange(D) + 8) % 16
    arrays["h_w"] = chunks(np.concatenate([rh["wq"].T, rh["wq"].T[:, exchange], rh["wk"].T, rh["wk"].T[:, exchange],
                                           rh["wv"].T], axis=1), 2)
    arrays["h_bqk"] = np.concatenate([per_partition(b, 2) for b in (rh["bq"], rh["bq"][exchange], rh["bk"],
                                                                    rh["bk"][exchange])], axis=1)
    arrays["h_bv"] = rh["bv"].reshape(1, D)
    arrays["h_wo"] = chunks(rh["wo"].T, 2)
    arrays["h_bo"] = rh["bo"].reshape(1, D)
    ex = {k[7:]: v for k, v in x.items() if k.startswith("L3_ffn_")}
    arrays["i_router"] = chunks(np.concatenate([ex["router_w"].T, ex["probe_w"].T,
                                                np.full((D, 1), 1.0 / D, np.float32)], axis=1), 2)
    arrays["i_emb"] = ex["router_emb"].reshape(1, -1)
    arrays["i_fe"] = np.concatenate([ex["fatigue"], ex["energy"]]).reshape(1, -1)
    arrays["i_b2"] = ex["b2"]
    arrays["i_b1"] = ex["b1"].reshape(EXPERTS, FC, 128).transpose(0, 2, 1)
    arrays["i_mix"] = np.stack([ex["m_gate1"], ex["m_gate2"]], axis=1)
    for n, part in enumerate(("w_fast", "w_slow", "h_fast")):
        arrays[f"i_w1_{n}"] = ex[part + "1"].reshape(EXPERTS, 2, C, FF).transpose(0, 2, 1, 3).reshape(EXPERTS, C, -1)
        arrays[f"i_w2_{n}"] = ex[part + "2"].reshape(EXPERTS, FC, 128, D).transpose(0, 2, 1, 3).reshape(EXPERTS, 128, -1)
    arrays = {k: np.ascontiguousarray(v) for k, v in arrays.items()}

    nc = bacc.Bacc("TRN2", target_bir_lowering=False, num_devices=1)
    args = {k: nc.dram_tensor(k + "_dram", v.shape, mybir.dt.from_np(v.dtype), kind="ExternalInput").ap()
            for k, v in arrays.items()}
    args["out"] = nc.dram_tensor("out_dram", (SAMPLES, T, D), F32, kind="ExternalOutput").ap()
    build(nc, args)
    r = run(nc, [{k + "_dram": v for k, v in arrays.items()}], core_ids=[0])
    return r.results[0]["out_dram"]
```

```python
from contextlib import ExitStack

import concourse.bass as bass
from concourse import mybir

F32 = mybir.dt.float32
F32R = mybir.dt.float32r
BF16 = mybir.dt.bfloat16
U32 = mybir.dt.uint32
I8 = mybir.dt.int8
I32 = mybir.dt.int32
ALU = mybir.AluOpType
ACT = mybir.ActivationFunctionType
AX = mybir.AxisListType

SAMPLES = 16
IMG = 36
FRONT = IMG + 1
TXT = 77
T = FRONT + TXT
D = 192
C = D // 2
GROUP = 4
TURNS = SAMPLES // GROUP
N = GROUP * T
PATCH_K = 768 // 128
EPS = 1e-5
HEADS = 12
EXPERTS = 8
FF = 768
FC = FF // 128


START = 5


def turn(i, n=1, per=1):
    return i * per + n + START


def cols(b, width=T):
    return slice(b * width, (b + 1) * width)


class Core:
    pass


def stage_tools(core, ctx):
    nc = core.nc

    def sb(name, shape, dtype=F32):
        core.made += 1
        return ctx.enter_context(nc.sbuf_tensor(f"{name}_{core.made}", shape, dtype))

    raised, every = [], []
    ctx.callback(lambda: (nc.clear_and_free_semaphores(every), nc.all_engine_barrier()))

    def load_sem(name):
        core.made += 1
        every.append(nc.alloc_semaphore(f"{name}_{core.made}"))
        return every[-1]

    def sem(name):
        raised.append(load_sem(name))
        return raised[-1]

    return sb, sem, load_sem, raised


def raise_to_start(sp, raised):
    for s in raised:
        sp.sem_inc(s, START)


def sample_of(h, i, b):
    return h[:, bass.ds(i * (GROUP * D) + b * D, D)]



class Norm:

    def __init__(self, sb, sem, tag):
        self.stats = sb(f"{tag}_stats", [T, GROUP, 6])
        self.mean_var = sb(f"{tag}_mean_var", [T, GROUP, 2])
        self.var_eps = sb(f"{tag}_var_eps", [T, GROUP])
        self.rstd = sb(f"{tag}_rstd", [T, GROUP])
        self.var_ready = sem(f"{tag}_var_ready")
        self.rstd_ready = sem(f"{tag}_rstd_ready")


def norm_statistics(v, norm, source):
    for b in range(GROUP):
        v.bn_stats(norm.stats[:, b, :], source(b))
    v.drain()
    for b in range(GROUP):
        v.bn_aggr(norm.mean_var[:, b, :], norm.stats[:, b, :])
    v.drain()
    v.tensor_scalar(norm.var_eps[:, :], norm.mean_var[:, :, 1], EPS, None, ALU.add).then_inc(norm.var_ready, 1)


def norm_rstd(pool, core, norm, i):
    pool.wait_ge(norm.var_ready, turn(i))
    pool.tensor_tensor(norm.rstd[:, :], norm.var_eps[:, :], core.minus_half[0:T, 0:GROUP],
                       ALU.pow).then_inc(norm.rstd_ready, 1)


def norm_apply(v, norm, source, target, b):
    return v.tensor_scalar(target(b), source(b), norm.mean_var[:, b, 0:1], norm.rstd[:, b:b + 1],
                           ALU.subtract, ALU.mult)


def transpose_group(pe, core, banks, source, done):
    for c in range(2):
        for b in range(GROUP):
            mm = pe.transpose(banks[c][0:C, cols(b)], source[:, b, c * C:(c + 1) * C], core.ident[0:T, 0:T])
    mm.then_inc(done, 1)



HIGH = 128
REST = D - HIGH


def duplicate_rest(v, source):
    v.drain()
    return v.tensor_copy(source[:, :, D:D + REST], source[:, :, HIGH:D])


def transpose_for_experts(pe, core, banks, source, done):
    for c in range(2):
        for b in range(GROUP):
            mm = pe.transpose(banks[c][:, cols(b)], source[:, b, c * HIGH:(c + 1) * HIGH], core.ident[0:T, 0:T])
    mm.then_inc(done, 1)


def keep_for_experts(v, core, zT, i):
    at = bass.ds(i * N, N)
    v.tensor_scalar(core.z_hi[:, at], zT[:, 0, :], 1.0, None, ALU.mult)
    v.tensor_scalar(core.z_rest[:, at], zT[:, 1, :], 1.0, None, ALU.mult)
    v.drain()
    v.tensor_tensor(core.z_lo[:, at], zT[:, 0, :], core.z_hi[:, at].bitcast(F32), ALU.subtract)
    return v.tensor_tensor(core.z_rest[REST:128, at], zT[REST:128, 1, :], core.z_rest[REST:128, at].bitcast(F32),
                           ALU.subtract)


class SplitWeights:

    def __init__(self, sb, name, columns):
        self.raw = sb(f"{name}_raw", [128, 2, columns])
        self.hi = sb(f"{name}_hi", [128, 2, columns], F32R)
        self.lo = sb(f"{name}_lo", [128, columns], F32R)
        self.lo_rest = sb(f"{name}_lo_rest", [REST, columns], F32R)

    def load(self, sp, source, loaded):
        columns = source.shape[-1]
        sp.dma_start(self.raw[:, 0, :], source[0:HIGH, :]).then_inc(loaded, 16)
        sp.dma_start(self.raw[:, 1, :], source[HIGH:D, :].unsqueeze(0).to_broadcast([2, REST, columns])
                     ).then_inc(loaded, 16)

    def high(self, act):
        return act.activation(self.hi[:, :, :], self.raw[:, :, :], ACT.Copy)

    def low(self, v):
        v.tensor_tensor(self.lo[:, :], self.raw[:, 0, :], self.hi[:, 0, :].bitcast(F32), ALU.subtract)
        return v.tensor_tensor(self.lo_rest[:, :], self.raw[0:REST, 1, :], self.hi[0:REST, 1, :].bitcast(F32),
                               ALU.subtract)


class SplitColumns:

    def __init__(self, core):
        self.hi, self.lo, self.rest = (core.z_hi[:, k * N:(k + 1) * N] for k in range(3))

    def high(self, act, banks):
        act.activation(self.hi[:, :], banks[0][:, 0:N], ACT.Copy)
        return act.activation(self.rest[:, :], banks[1][:, 0:N], ACT.Copy)

    def low(self, v, banks):
        v.tensor_tensor(self.lo[:, :], banks[0][:, 0:N], self.hi[:, :].bitcast(F32), ALU.subtract)
        return v.tensor_tensor(self.rest[REST:128, :], banks[1][REST:128, 0:N], self.rest[REST:128, :].bitcast(F32),
                               ALU.subtract)


def product_by_columns(pe, out, w, m, x):
    pe.matmul(out, w.hi[:, 0, m], x.hi[:, :], start=True, stop=False)
    pe.matmul(out, w.hi[:, 0, m], x.lo[:, :], start=False, stop=False)
    pe.matmul(out, w.lo[:, m], x.hi[:, :], start=False, stop=False)
    pe.matmul(out, w.hi[:, 1, m], x.rest[:, :], start=False, stop=False)
    return pe.matmul(out, w.lo_rest[:, m], x.rest[0:REST, :], start=False, stop=True)


def product_by_rows(pe, out, x, t, w, m, more=False):
    pe.matmul(out, x.hi[:, t], w.hi[:, 0, m], start=True, stop=False)
    pe.matmul(out, x.hi[:, t], w.lo[:, m], start=False, stop=False)
    pe.matmul(out, x.lo[:, t], w.hi[:, 0, m], start=False, stop=False)
    pe.matmul(out, x.rest[:, t], w.hi[:, 1, m], start=False, stop=False)
    return pe.matmul(out, x.rest[0:REST, t], w.lo_rest[:, m], start=False, stop=not more)



def tokens_stage(core, a):
    nc = core.nc
    with ExitStack() as ctx:
        sb, sem, load_sem, raised = stage_tools(core, ctx)
        patches = sb("patches", [128, PATCH_K, GROUP, FRONT])
        w = sb("w_patch", [128, PATCH_K, D])
        front = sb("front", [FRONT, D])
        pos = sb("pos", [FRONT, D])
        front_pos = sb("front_pos", [FRONT, D])
        const_loaded, text_loaded, w_loaded, patch_loaded = (
            load_sem(n) for n in ("const_loaded", "text_loaded", "w_loaded", "patch_loaded"))
        cleared = load_sem("cleared")
        tokens_psum, tokens_added = sem("tokens_psum"), sem("tokens_added")

        with nc.Block() as block:
            @block.sync
            def _(sp):
                raise_to_start(sp, raised)
                sp.dma_start(w[:, :, :], a["tok_w"]).then_inc(w_loaded, 16)
                sp.dma_start(front[1:FRONT, :], a["tok_b"].to_broadcast([IMG, D])).then_inc(w_loaded, 16)
                sp.dma_start(front[0:1, :], a["cls"]).then_inc(w_loaded, 16)
                sp.dma_start(pos[:, :], a["pos"]).then_inc(w_loaded, 16)
                sp.wait_ge(cleared, 1)
                with sp.Fori(0, TURNS) as i:
                    sp.wait_ge(tokens_psum, turn(i, 0))
                    for k in range(PATCH_K):
                        sp.dma_start(patches[:, k, :, 1:FRONT],
                                     a["patches"][:, k, bass.ds(i * GROUP, GROUP), :]).then_inc(patch_loaded, 16)

            @block.scalar
            def _(act):
                act.dma_start(core.h[FRONT:T, 0:SAMPLES * D].rearrange("t (s d) -> t s d", d=D),
                              a["txt"].rearrange("s t d -> t s d")).then_inc(text_loaded, 16)
                for name, tile in core.constants.items():
                    act.dma_start(tile[tuple(slice(None) for _ in tile.shape)], a[name]).then_inc(const_loaded, 16)
                act.wait_ge(text_loaded, 16)
                act.wait_ge(const_loaded, 16 * len(core.constants))

            @block.gpsimd
            def _(pool):
                pool.memset(core.minus_half[:, :], -0.5)
                pool.memset(core.plus_half[:, :], 0.5)
                pool.memset(core.ones[:, :], 1.0)
                pool.memset(core.h[:, SAMPLES * D:(SAMPLES + GROUP) * D], 0.0)
                pool.memset(patches[:, :, :, 0:1], 0.0).then_inc(cleared, 1)

            @block.tensor
            def _(pe):
                pe.wait_ge(w_loaded, 64)
                pe.wait_ge(cleared, 1)
                with pe.Fori(0, TURNS) as i:
                    pe.wait_ge(patch_loaded, i * (16 * PATCH_K) + 16 * PATCH_K)
                    pe.wait_ge(tokens_added, turn(i, 0))
                    for b in range(GROUP):
                        for k in range(PATCH_K):
                            mm = pe.matmul(core.bank[b][0:FRONT, 0:D], patches[:, k, b, :], w[:, k, :],
                                           start=(k == 0), stop=(k == PATCH_K - 1))
                    mm.then_inc(tokens_psum, 1)

            @block.vector
            def _(v):
                v.wait_ge(w_loaded, 64)
                v.tensor_tensor(front_pos[:, :], front[:, :], pos[:, :], ALU.add)
                v.drain()
                with v.Fori(0, TURNS) as i:
                    v.wait_ge(tokens_psum, turn(i))
                    for b in range(GROUP):
                        add = v.tensor_tensor(core.h[0:FRONT, bass.ds(i * (GROUP * D) + b * D, D)],
                                              core.bank[b][0:FRONT, 0:D], front_pos[:, :], ALU.add)
                    add.then_inc(tokens_added, 1)



def wide_attention_stage(core, a):
    nc, bank, h = core.nc, core.bank, core.h
    scale = D ** -0.5
    with ExitStack() as ctx:
        sb, sem, load_sem, raised = stage_tools(core, ctx)
        norm = Norm(sb, sem, "norm")
        w = sb("w_qkv", [C, 2, 3 * D])
        bqk = sb("b_qk", [C, 4])
        bqk_s = sb("b_qk_scaled", [C, 4])
        bv = sb("b_v", [1, D])
        xn = sb("xn", [T, GROUP, D])
        xT = sb("xT", [C, 2, N])
        qkT = sb("qkT", [C, 4, N])
        vals = sb("vals", [T, GROUP, D])
        probs = sb("probs", [T, GROUP, T])
        probsT = sb("probsT", [T, GROUP, T])
        negmax = sb("negmax", [T, GROUP])
        total = sb("total", [T, GROUP])
        inv = sb("inv", [T, GROUP])
        w_loaded = load_sem("w_loaded")
        bias_scaled = load_sem("bias_scaled")
        names = ("xn_ready", "xT_psum", "xT_ready", "qk_psum", "qk_ready", "v_psum", "v_ready", "scores_psum",
                 "max_ready", "probs_ready", "probsT_psum", "probsT_ready", "context_psum", "h_done")
        s = {n: sem(n) for n in names}

        with nc.Block() as block:
            @block.sync
            def _(sp):
                raise_to_start(sp, raised)
                sp.dma_start(w[:, :, :], a["a_wqkv"]).then_inc(w_loaded, 16)
                sp.dma_start(bqk[:, :], a["a_bqk"]).then_inc(w_loaded, 16)
                sp.dma_start(bv[:, :], a["a_bv"]).then_inc(w_loaded, 16)

            @block.gpsimd
            def _(pool):
                norm_rstd(pool, core, norm, 0)
                with pool.Fori(0, TURNS) as i:
                    norm_rstd(pool, core, norm, i + 1)

            @block.tensor
            def _(pe):
                pe.wait_ge(w_loaded, 48)
                with pe.Fori(0, TURNS) as i:
                    pe.wait_ge(s["probs_ready"], turn(i, 0))
                    pe.wait_ge(s["probsT_ready"], turn(i, 0))
                    pe.wait_ge(s["xn_ready"], turn(i))
                    transpose_group(pe, core, bank[0:2], xn, s["xT_psum"])
                    pe.wait_ge(s["h_done"], turn(i, 0))
                    pe.wait_ge(s["xT_ready"], turn(i))
                    for j in range(4):
                        for c in range(2):
                            mm = pe.matmul(bank[2 + j][0:C, 0:N], w[:, c, j * C:(j + 1) * C], xT[:, c, :],
                                           start=(c == 0), stop=(c == 1))
                    mm.then_inc(s["qk_psum"], 1)
                    pe.wait_ge(s["v_ready"], turn(i, 0))
                    for b in range(GROUP):
                        out = bank[6 + b // 2][0:T, (b % 2) * D:(b % 2 + 1) * D]
                        for c in range(2):
                            pe.matmul(out, xT[:, c, cols(b)], w[:, c, 2 * D:3 * D], start=(c == 0), stop=False)
                        mm = pe.matmul(out, core.ones[0:1, 0:T], bv[:, :], start=False, stop=True)
                    mm.then_inc(s["v_psum"], 1)
                    pe.wait_ge(s["qk_ready"], turn(i))
                    for b in range(GROUP):
                        for c in range(2):
                            mm = pe.matmul(bank[0][0:T, cols(b)], qkT[:, c, cols(b)], qkT[:, 2 + c, cols(b)],
                                           start=(c == 0), stop=(c == 1))
                    mm.then_inc(s["scores_psum"], 1)
                    pe.wait_ge(s["probs_ready"], turn(i))
                    for b in range(GROUP):
                        mm = pe.transpose(bank[1][0:T, cols(b)], probs[:, b, :], core.ident[0:T, 0:T])
                    mm.then_inc(s["probsT_psum"], 1)
                    pe.wait_ge(s["v_ready"], turn(i))
                    pe.wait_ge(s["probsT_ready"], turn(i))
                    for b in range(GROUP):
                        mm = pe.matmul(bank[2 + b // 2][0:T, (b % 2) * D:(b % 2 + 1) * D], probsT[:, b, :],
                                       vals[:, b, :], start=True, stop=True)
                    mm.then_inc(s["context_psum"], 1)

            @block.scalar
            def _(act):
                act.wait_ge(w_loaded, 48)
                act.wait_ge(bias_scaled, 1)
                with act.Fori(0, TURNS) as i:
                    act.wait_ge(s["v_psum"], turn(i, 0))
                    act.wait_ge(s["xT_psum"], turn(i))
                    for c in range(2):
                        ins = act.activation(xT[:, c, :], bank[c][0:C, 0:N], ACT.Copy)
                    ins.then_inc(s["xT_ready"], 1)
                    act.wait_ge(s["scores_psum"], turn(i, 0))
                    act.wait_ge(s["qk_psum"], turn(i))
                    for j in range(4):
                        ins = act.activation(qkT[:, j, :], bank[2 + j][0:C, 0:N], ACT.Identity,
                                             bias=bqk_s[:, j:j + 1], scale=scale if j < 2 else 1.0)
                    ins.then_inc(s["qk_ready"], 1)
                    act.wait_ge(s["probsT_psum"], turn(i, 0))
                    act.wait_ge(s["h_done"], turn(i, 0))
                    act.wait_ge(s["max_ready"], turn(i))
                    for b in range(GROUP):
                        ins = act.activation(probs[:, b, :], bank[0][0:T, cols(b)], ACT.Exp,
                                             bias=negmax[:, b:b + 1], accum_out=total[:, b:b + 1])
                    ins.then_inc(s["probs_ready"], 1)
                    act.wait_ge(s["context_psum"], turn(i, 0))
                    act.wait_ge(s["probsT_psum"], turn(i))
                    act.activation(probsT[:, :, :], bank[1][0:T, 0:N], ACT.Copy).then_inc(s["probsT_ready"], 1)

            @block.vector
            def _(v):
                v.wait_ge(w_loaded, 48)
                v.tensor_scalar(bqk_s[:, 0:2], bqk[:, 0:2], scale, None, ALU.mult)
                v.tensor_copy(bqk_s[:, 2:4], bqk[:, 2:4]).then_inc(bias_scaled, 1)
                def normed(i):
                    norm_statistics(v, norm, lambda b: sample_of(h, i, b))
                    v.wait_ge(s["xT_psum"], turn(i, 0))
                    v.wait_ge(norm.rstd_ready, turn(i))
                    for b in range(GROUP):
                        ins = norm_apply(v, norm, lambda b: sample_of(h, i, b), lambda b: xn[:, b, :], b)
                    ins.then_inc(s["xn_ready"], 1)

                normed(0)
                with v.Fori(0, TURNS) as i:
                    v.wait_ge(s["context_psum"], turn(i, 0))
                    v.wait_ge(s["v_psum"], turn(i))
                    for p in range(2):
                        ins = v.tensor_copy(vals[:, 2 * p:2 * p + 2, :], bank[6 + p][0:T, 0:2 * D])
                    ins.then_inc(s["v_ready"], 1)
                    v.wait_ge(s["probs_ready"], turn(i, 0))
                    v.wait_ge(s["scores_psum"], turn(i))
                    v.tensor_reduce(negmax[:, :], bank[0][0:T, 0:N].rearrange("q (b k) -> q b k", b=GROUP),
                                    AX.X, ALU.max, negate=True).then_inc(s["max_ready"], 1)
                    normed(i + 1)
                    v.wait_ge(s["probs_ready"], turn(i))
                    v.reciprocal(inv[:, :], total[:, :])
                    v.drain()
                    v.wait_ge(s["context_psum"], turn(i))
                    for b in range(GROUP):
                        ins = v.scalar_tensor_tensor(out=sample_of(h, i, b),
                                                     in0=bank[2 + b // 2][0:T, (b % 2) * D:(b % 2 + 1) * D],
                                                     scalar=inv[:, b:b + 1], in1=sample_of(h, i, b),
                                                     op0=ALU.mult, op1=ALU.add)
                    ins.then_inc(s["h_done"], 1)



UNITS = 2 * GROUP
UNIT_HEADS = HEADS // 2


class Heads:

    def __init__(self, core, sb, sem, head_dim, mask):
        self.core, self.head_dim, self.mask = core, head_dim, mask
        self.rows = mask.shape[0]
        self.per_chunk = self.rows // head_dim
        self.chunks = HEADS // self.per_chunk
        self.kblock = sb("kblock", [self.rows, GROUP, self.chunks, self.per_chunk, T])
        self.vals = sb("vals", [T, GROUP, HEADS, head_dim + 1])
        self.negmax = sb("negmax", [T, 2, UNIT_HEADS])
        self.probs = sb("probs", [T, 2, UNIT_HEADS, T])
        self.probsT = sb("probsT", [T, 2, UNIT_HEADS, T])
        self.inv = sb("inv", [T, 2, UNIT_HEADS])
        self.kblock_ready = sem("kblock_ready")
        self.scores_psum = sem("scores_psum")
        self.shifted_ready = sem("shifted_ready")
        self.probs_ready = sem("probs_ready")
        self.probsT_psum = sem("probsT_psum")
        self.probsT_ready = sem("probsT_ready")
        self.context_psum = sem("context_psum")
        self.context_done = sem("context_done")

    def pair(self, first):
        return self.core.psum[0:T, first:first + 2, 0:3 * T].rearrange("t a (n k) -> t a n k", n=3)

    def context(self, u):
        width = self.head_dim + 1
        return self.core.bank[6 + u % 2][0:T, 0:UNIT_HEADS * width].rearrange("t (n d) -> t n d", d=width)


def paired(buffer):
    return buffer.rearrange("t (a n) k -> t a n k", a=2)


def heads_pool(pool, att, i, kT, b):
    for c in range(att.chunks):
        shape = [att.rows, att.per_chunk, T]
        ins = pool.tensor_tensor(att.kblock[:, b, c, :, :],
                                 kT[:, c, cols(b)].unsqueeze(1).to_broadcast(shape),
                                 att.mask[:, :].unsqueeze(2).to_broadcast(shape), ALU.mult)
    ins.then_inc(att.kblock_ready, 1)


def heads_tensor(pe, att, i, qT):
    core, per = att.core, att.per_chunk

    def scores(u):
        b, half = u // 2, u % 2
        pe.wait_ge(att.kblock_ready, turn(i, b + 1, GROUP))
        pe.wait_ge(att.shifted_ready, turn(i, u - 1, UNITS))
        first = half * UNIT_HEADS
        while first < (half + 1) * UNIT_HEADS:
            c = first // per
            last = min((c + 1) * per, (first // 3 + 1) * 3)
            mm = pe.matmul(core.bank[2 * (u % 2) + first // 3 % 2][0:T, first % 3 * T:((last - 1) % 3 + 1) * T],
                           qT[:, c, cols(b)], att.kblock[:, b, c, first - c * per:last - c * per, :],
                           start=True, stop=True)
            first = last
        mm.then_inc(att.scores_psum, 1)

    def transposes(u):
        pe.wait_ge(att.probsT_ready, turn(i, u, UNITS))
        pe.wait_ge(att.probs_ready, turn(i, u + 1, UNITS))
        for n in range(UNIT_HEADS):
            mm = pe.transpose(core.bank[4 + n // 3][0:T, cols(n % 3)], att.probs[:, u % 2, n, :],
                              core.ident[0:T, 0:T])
        mm.then_inc(att.probsT_psum, 1)

    def context(u):
        pe.wait_ge(att.context_done, turn(i, u - 1, UNITS))
        pe.wait_ge(att.probsT_ready, turn(i, u + 1, UNITS))
        for n in range(UNIT_HEADS):
            mm = pe.matmul(att.context(u)[:, n, :], att.probsT[:, u % 2, n, :],
                           att.vals[:, u // 2, u % 2 * UNIT_HEADS + n, :], start=True, stop=True)
        mm.then_inc(att.context_psum, 1)

    scores(0)
    scores(1)
    transposes(0)
    for u in range(UNITS):
        if u + 2 < UNITS:
            scores(u + 2)
        if u + 1 < UNITS:
            transposes(u + 1)
        context(u)


def heads_scalar(act, att, i):
    def exponentials(u):
        act.wait_ge(att.shifted_ready, turn(i, u + 1, UNITS))
        act.activation(att.probs[:, u % 2, :, :], att.probs[:, u % 2, :, :], ACT.Exp).then_inc(att.probs_ready, 1)

    exponentials(0)
    exponentials(1)
    for u in range(UNITS):
        act.wait_ge(att.context_psum, turn(i, u - 1, UNITS))
        act.wait_ge(att.probsT_psum, turn(i, u + 1, UNITS))
        act.activation(paired(att.probsT[:, u % 2, :, :]), att.pair(4), ACT.Copy).then_inc(att.probsT_ready, 1)
        if u + 2 < UNITS:
            exponentials(u + 2)


def heads_vector(v, att, i, rescale):
    def shift(u):
        v.wait_ge(att.scores_psum, turn(i, u + 1, UNITS))
        v.tensor_reduce(att.negmax[:, u % 2, :].rearrange("t (a n) -> t a n", a=2), att.pair(2 * (u % 2)),
                        AX.X, ALU.max, negate=True)
        v.drain()
        v.wait_ge(att.probsT_psum, turn(i, u - 1, UNITS))
        v.tensor_tensor(paired(att.probs[:, u % 2, :, :]), att.pair(2 * (u % 2)),
                        att.negmax[:, u % 2, :].rearrange("t (a n) -> t a n", a=2).unsqueeze(3)
                        .to_broadcast([T, 2, 3, T]), ALU.add).then_inc(att.shifted_ready, 1)

    shift(0)
    shift(1)
    for u in range(UNITS):
        if u + 2 < UNITS:
            shift(u + 2)
        v.wait_ge(att.context_psum, turn(i, u + 1, UNITS))
        v.reciprocal(att.inv[:, u % 2, :], att.context(u)[:, :, att.head_dim])
        v.drain()
        rescale(u, att.inv[:, u % 2, :]).then_inc(att.context_done, 1)



class TopTwo:
    def __init__(self, sb, width, tag):
        self.width = width
        self.best = sb(f"{tag}_best", [T, GROUP, 8])
        self.where = sb(f"{tag}_where", [T, GROUP, 8], U32)
        self.index = sb(f"{tag}_index", [T, GROUP, 8])
        self.hot = sb(f"{tag}_hot", [T, 2, GROUP, width])


def top_two_hot(v, core, top, logits):
    shape = [T, GROUP, top.width]
    for b in range(GROUP):
        v.max(top.best[:, b, :], logits[:, b, :])
    v.drain()
    for b in range(GROUP):
        v.max_index(top.where[:, b, :], top.best[:, b, :], logits[:, b, :])
    v.drain()
    v.tensor_copy(top.index[:, :, :], top.where[:, :, :])
    v.drain()
    for k in range(2):
        v.tensor_tensor(top.hot[:, k, :, :],
                        core.iota[0:T, 0:top.width].unsqueeze(1).to_broadcast(shape),
                        top.index[:, :, k:k + 1].to_broadcast(shape), ALU.is_equal)
    v.drain()


class Router:
    def __init__(self, sb, sem, tag):
        self.top = TopTwo(sb, EXPERTS, tag)
        self.logits = sb(f"{tag}_logits", [T, GROUP, EXPERTS])
        self.gap = sb(f"{tag}_gap", [T, GROUP])
        self.ratio = sb(f"{tag}_ratio", [T, GROUP])
        self.weight = sb(f"{tag}_weight", [T, 2, GROUP])
        self.gates = sb(f"{tag}_gates", [T, GROUP, EXPERTS])
        self.gap_ready = sem(f"{tag}_gap_ready")
        self.ratio_ready = sem(f"{tag}_ratio_ready")


def router_vector(v, core, r, i):
    shape = [T, GROUP, EXPERTS]
    top_two_hot(v, core, r.top, r.logits)
    v.tensor_tensor(r.gap[:, :], r.top.best[:, :, 1], r.top.best[:, :, 0], ALU.subtract).then_inc(r.gap_ready, 1)
    v.wait_ge(r.ratio_ready, turn(i))
    v.tensor_scalar(r.gap[:, :], r.ratio[:, :], 1.0, None, ALU.add)
    v.drain()
    v.reciprocal(r.weight[:, 0, :], r.gap[:, :])
    v.drain()
    v.tensor_tensor(r.weight[:, 1, :], r.weight[:, 0, :], r.ratio[:, :], ALU.mult)
    v.drain()
    for k in range(2):
        v.tensor_tensor(r.top.hot[:, k, :, :], r.top.hot[:, k, :, :],
                        r.weight[:, k, :].unsqueeze(2).to_broadcast(shape), ALU.mult)
    v.drain()
    v.tensor_tensor(core.gates[:, bass.ds(i * (GROUP * EXPERTS), GROUP * EXPERTS)],
                    r.top.hot[:, 0, :, :].rearrange("t b e -> t (b e)"),
                    r.top.hot[:, 1, :, :].rearrange("t b e -> t (b e)"), ALU.add)
    return v.tensor_tensor(r.gates[:, :, :], r.top.hot[:, 0, :, :], r.top.hot[:, 1, :, :], ALU.add)


def router_scalar(act, r, i):
    act.wait_ge(r.gap_ready, turn(i))
    act.activation(r.ratio[:, :], r.gap[:, :], ACT.Exp).then_inc(r.ratio_ready, 1)



def first_heads_stage(core, a, weights):
    nc, bank, h = core.nc, core.bank, core.h
    with ExitStack() as ctx:
        sb, sem, load_sem, raised = stage_tools(core, ctx)
        outer, inner, second = (Norm(sb, sem, n) for n in ("outer", "inner", "second"))
        w = sb("w_qkv", [C, 2, 3 * D])
        w_out = sb("w_out", [C, 2, D])
        w_router = sb("w_router", [128, 2, EXPERTS])
        affine = sb("affine", [C, 4])
        affine2 = sb("affine2", [128, 4])
        xn = sb("xn", [T, GROUP, D])
        xnn = sb("xnn", [T, GROUP, D])
        xT = sb("xT", [C, 2, N])
        qT = sb("qT", [C, 2, N])
        kT = sb("kT", [C, 2, N])
        o = sb("o", [T, GROUP, D])
        oT = sb("oT", [C, 2, N])
        zn = sb("zn", [T, GROUP, D + REST])
        zT = sb("zT", [128, 2, N])
        att = Heads(core, sb, sem, 16, core.mask16)
        router = Router(sb, sem, "router")
        w_loaded, ones_ready = load_sem("w_loaded"), load_sem("ones_ready")
        names = ("xnn_ready", "xT_psum", "xT_ready", "q_psum", "k_psum", "v_psum", "q_ready", "k_ready", "v_ready",
                 "oT_psum", "oT_ready", "out_psum", "zn_ready", "zT_psum", "zT_ready", "zT_kept", "logits_psum",
                 "logits_read", "gates_done")
        s = {n: sem(n) for n in names}

        with nc.Block() as block:
            @block.sync
            def _(sp):
                raise_to_start(sp, raised)
                raise_to_start(sp, weights.raised)
                sp.dma_start(w[:, :, :], a["b_wqkv"]).then_inc(w_loaded, 16)
                sp.dma_start(w_out[:, :, :], a["b_wproj"]).then_inc(w_loaded, 16)
                sp.dma_start(w_router[:, 0, :], a["b_wrouter"][0:HIGH, :]).then_inc(w_loaded, 16)
                sp.dma_start(w_router[0:REST, 1, :], a["b_wrouter"][HIGH:D, :]).then_inc(w_loaded, 16)
                sp.dma_start(affine[:, :], a["b_affine"]).then_inc(w_loaded, 16)
                sp.dma_start(affine2[:, :], a["b_affine2"]).then_inc(w_loaded, 16)
                weights.load(sp, a, (0, 0))

            @block.gpsimd
            def _(pool):
                pool.memset(att.vals[:, :, :, 16:17], 1.0).then_inc(ones_ready, 1)
                norm_rstd(pool, core, outer, 0)
                norm_rstd(pool, core, inner, 0)
                with pool.Fori(0, TURNS) as i:
                    pool.wait_ge(att.scores_psum, turn(i, 0, UNITS))
                    pool.wait_ge(s["k_ready"], turn(i))
                    for b in range(GROUP):
                        heads_pool(pool, att, i, kT, b)
                    norm_rstd(pool, core, second, i)
                    norm_rstd(pool, core, outer, i + 1)
                    norm_rstd(pool, core, inner, i + 1)
                for _ in weights.steps(pool, (0, 0)):
                    pass

            @block.tensor
            def _(pe):
                pe.wait_ge(w_loaded, 96)
                pe.wait_ge(ones_ready, 1)
                with pe.Fori(0, TURNS) as i:
                    pe.wait_ge(s["oT_ready"], turn(i, 0))
                    pe.wait_ge(s["xnn_ready"], turn(i))
                    transpose_group(pe, core, bank[0:2], xnn, s["xT_psum"])
                    pe.wait_ge(s["zn_ready"], turn(i, 0))
                    pe.wait_ge(s["zT_ready"], turn(i, 0))
                    pe.wait_ge(s["logits_read"], turn(i, 0))
                    pe.wait_ge(s["xT_ready"], turn(i))
                    for j, done in enumerate(("q_psum", "q_psum", "k_psum", "k_psum")):
                        for c in range(2):
                            mm = pe.matmul(bank[2 + j][0:C, 0:N], w[:, c, j * C:(j + 1) * C], xT[:, c, :],
                                           start=(c == 0), stop=(c == 1))
                        if j % 2:
                            mm.then_inc(s[done], 1)
                    for b in range(GROUP):
                        for c in range(2):
                            mm = pe.matmul(bank[6 + b // 2][0:T, cols(b % 2, D)], xT[:, c, cols(b)],
                                           w[:, c, 2 * D:3 * D], start=(c == 0), stop=(c == 1))
                    mm.then_inc(s["v_psum"], 1)
                    pe.wait_ge(s["q_ready"], turn(i))
                    pe.wait_ge(s["k_ready"], turn(i))
                    pe.wait_ge(s["v_ready"], turn(i))
                    heads_tensor(pe, att, i, qT)
                    pe.wait_ge(att.context_done, turn(i, UNITS, UNITS))
                    transpose_group(pe, core, bank[0:2], o, s["oT_psum"])
                    pe.wait_ge(s["oT_ready"], turn(i))
                    for b in range(GROUP):
                        for c in range(2):
                            mm = pe.matmul(bank[2 + b // 2][0:T, cols(b % 2, D)], oT[:, c, cols(b)], w_out[:, c, :],
                                           start=(c == 0), stop=(c == 1))
                    mm.then_inc(s["out_psum"], 1)
                    pe.wait_ge(s["zn_ready"], turn(i))
                    transpose_for_experts(pe, core, bank[4:6], zn, s["zT_psum"])
                    pe.wait_ge(s["zT_ready"], turn(i))
                    for b in range(GROUP):
                        for c in range(2):
                            rows = slice(0, (HIGH, REST)[c])
                            mm = pe.matmul(bank[6][0:T, cols(b, EXPERTS)], zT[rows, c, cols(b)], w_router[rows, c, :],
                                           start=(c == 0), stop=(c == 1))
                    mm.then_inc(s["logits_psum"], 1)

            @block.scalar
            def _(act):
                act.wait_ge(w_loaded, 96)
                with act.Fori(0, TURNS) as i:
                    act.wait_ge(s["v_psum"], turn(i, 0))
                    act.wait_ge(s["xT_psum"], turn(i))
                    for c in range(2):
                        ins = act.activation(xT[:, c, :], bank[c][0:C, 0:N], ACT.Identity,
                                             bias=affine[:, 2 + c:3 + c], scale=affine[:, c:c + 1])
                    ins.then_inc(s["xT_ready"], 1)
                    act.wait_ge(att.kblock_ready, turn(i, 0, GROUP))
                    act.wait_ge(s["k_psum"], turn(i))
                    for c in range(2):
                        ins = act.activation(kT[:, c, :], bank[4 + c][0:C, 0:N], ACT.Copy)
                    ins.then_inc(s["k_ready"], 1)
                    act.wait_ge(att.scores_psum, turn(i, 0, UNITS))
                    for c in range(2):
                        ins = act.activation(qT[:, c, :], bank[2 + c][0:C, 0:N], ACT.Copy, scale=0.25)
                    ins.then_inc(s["q_ready"], 1)
                    heads_scalar(act, att, i)
                    act.wait_ge(s["logits_psum"], turn(i, 0))
                    act.wait_ge(s["zT_kept"], turn(i, 0))
                    act.wait_ge(s["zT_psum"], turn(i))
                    for c in range(2):
                        ins = act.activation(zT[:, c, :], bank[4 + c][:, 0:N], ACT.Identity,
                                             bias=affine2[:, 2 + c:3 + c], scale=affine2[:, c:c + 1])
                    ins.then_inc(s["zT_ready"], 1)
                    router_scalar(act, router, i)

            @block.vector
            def _(v):
                v.wait_ge(w_loaded, 96)
                def normed(i):
                    norm_statistics(v, outer, lambda b: sample_of(h, i, b))
                    v.wait_ge(outer.rstd_ready, turn(i))
                    for b in range(GROUP):
                        norm_apply(v, outer, lambda b: sample_of(h, i, b), lambda b: xn[:, b, :], b)
                    v.drain()
                    norm_statistics(v, inner, lambda b: xn[:, b, :])
                    v.wait_ge(inner.rstd_ready, turn(i))
                    for b in range(GROUP):
                        ins = norm_apply(v, inner, lambda b: xn[:, b, :], lambda b: xnn[:, b, :], b)
                    ins.then_inc(s["xnn_ready"], 1)

                normed(0)
                with v.Fori(0, TURNS) as i:
                    v.wait_ge(s["v_psum"], turn(i))
                    for b in range(GROUP):
                        ins = v.tensor_copy(att.vals[:, b, :, 0:16], bank[6 + b // 2][0:T, cols(b % 2, D)]
                                            .rearrange("t (n d) -> t n d", d=16))
                    ins.then_inc(s["v_ready"], 1)

                    def rescale(u, inv):
                        return v.tensor_tensor(o[:, u // 2, cols(u % 2, C)].rearrange("t (n d) -> t n d", d=16),
                                               att.context(u)[:, :, 0:16],
                                               inv.unsqueeze(2).to_broadcast([T, UNIT_HEADS, 16]), ALU.mult)
                    heads_vector(v, att, i, rescale)
                    v.wait_ge(s["oT_psum"], turn(i))
                    for c in range(2):
                        ins = v.tensor_copy(oT[:, c, :], bank[c][0:C, 0:N])
                    ins.then_inc(s["oT_ready"], 1)
                    v.wait_ge(s["out_psum"], turn(i))
                    for p in range(2):
                        v.tensor_tensor(xn[:, 2 * p:2 * p + 2, :], xn[:, 2 * p:2 * p + 2, :],
                                        bank[2 + p][0:T, 0:2 * D].rearrange("t (b d) -> t b d", b=2), ALU.add)
                    v.drain()
                    rows = h[:, bass.ds(i * (GROUP * D), GROUP * D)]
                    v.tensor_tensor(rows, rows, xn[:, :, :].rearrange("t b d -> t (b d)"), ALU.add)
                    norm_statistics(v, second, lambda b: xn[:, b, :])
                    v.wait_ge(second.rstd_ready, turn(i))
                    for b in range(GROUP):
                        norm_apply(v, second, lambda b: xn[:, b, :], lambda b: zn[:, b, 0:D], b)
                    duplicate_rest(v, zn).then_inc(s["zn_ready"], 1)
                    normed(i + 1)
                    v.wait_ge(s["zT_ready"], turn(i))
                    keep_for_experts(v, core, zT, i).then_inc(s["zT_kept"], 1)
                    v.wait_ge(s["logits_psum"], turn(i))
                    v.tensor_copy(router.logits[:, :, :], bank[6][0:T, 0:GROUP * EXPERTS]).then_inc(s["logits_read"], 1)
                    v.drain()
                    router_vector(v, core, router, i).then_inc(s["gates_done"], 1)



class ExpertWeights:

    def __init__(self, core, ctx, second):
        sb, sem, load_sem, self.raised = stage_tools(core, ctx)
        self.core, self.second = core, second
        parts = 3 if second else 1
        self.raw1 = [sb("raw1", [128, 2, FF]) for _ in range(parts)]
        self.raw2 = [sb("raw2", [128, FC, D]) for _ in range(parts)]
        self.w1_hi = [sb("w1_hi", [128, 2, FF], F32R) for _ in range(2)]
        self.w1_lo = [sb("w1_lo", [128, FF], F32R) for _ in range(2)]
        self.w1_lo_rest = [sb("w1_lo_rest", [REST, FF], F32R) for _ in range(2)]
        self.w2 = [sb("w2", [128, FC, 2, D], F32R) for _ in range(2)]
        self.loads = 3 * parts + second
        if second:
            self.mix = sb("mix", [128, 2])
            self.b1 = [sb("b1", [128, FC]) for _ in range(2)]
            self.b1_loaded = [load_sem("b1_loaded") for _ in range(2)]
        self.loaded = load_sem("loaded")
        self.raw_read, self.scaled, self.added, self.mixed, self.high_ready, self.split_ready, self.y_psum = (
            sem(n) for n in ("raw_read", "scaled", "added", "mixed", "high_ready", "split_ready", "y_psum"))

    def load(self, sp, a, e):
        e, k = e
        row = bass.ds(e, 1)
        if self.second:
            sp.wait_ge(self.y_psum, turn((e - 1) * TURNS, 0))
            sp.dma_start(self.b1[k][:, :], a["i_b1"][row].rearrange("e p c -> (e p) c")
                         ).then_inc(self.b1_loaded[k], 16)
        sp.wait_ge(self.raw_read, turn(e, 0))
        if self.second:
            sp.dma_start(self.mix[:, :], a["i_mix"][row, :].to_broadcast([128, 2])).then_inc(self.loaded, 16)
        for n in range(len(self.raw1)):
            w1 = a[f"i_w1_{n}" if self.second else "b_w1"][row].rearrange("e k f -> (e k) f")
            w2 = a[f"i_w2_{n}" if self.second else "b_w2"][row].rearrange("e p c f -> (e p) c f")
            sp.dma_start(self.raw1[n][:, 0, :], w1[0:HIGH, :]).then_inc(self.loaded, 16)
            sp.dma_start(self.raw1[n][:, 1, :], w1[HIGH:D, :].unsqueeze(0).to_broadcast([2, REST, FF])
                         ).then_inc(self.loaded, 16)
            sp.dma_start(self.raw2[n][:, :, :], w2).then_inc(self.loaded, 16)

    def steps(self, pool, e):
        e, k = e
        raw1, raw2, w1_hi, w1_lo, w1_lo_rest, w2 = (
            self.raw1, self.raw2, self.w1_hi[k], self.w1_lo[k], self.w1_lo_rest[k], self.w2[k])
        pool.wait_ge(self.loaded, e * (16 * self.loads) + 16 * self.loads)
        both = [(raw1[n][:, :, :].rearrange("p c f -> p (c f)"),
                 raw2[n][:, :, :].rearrange("p c f -> p (c f)")) for n in range(len(raw1))]
        if self.second:
            for m in range(2):
                ins = pool.tensor_tensor(both[1][m], both[1][m],
                                         self.mix[:, m:m + 1].to_broadcast(list(both[1][m].shape)), ALU.mult)
            ins.then_inc(self.scaled, 1)
            yield
            pool.wait_ge(self.scaled, turn(e))
            for m in range(2):
                ins = pool.tensor_tensor(both[0][m], both[0][m], both[1][m], ALU.add)
            ins.then_inc(self.added, 1)
            yield
            pool.wait_ge(self.added, turn(e))
            for m in range(2):
                ins = pool.tensor_tensor(both[0][m], both[0][m], both[2][m], ALU.add)
            ins.then_inc(self.mixed, 1)
            yield
            pool.wait_ge(self.mixed, turn(e))
        pool.wait_ge(self.y_psum, turn((e - 1) * TURNS, 0))
        one = self.core.ones[:, 0:1]
        pool.tensor_tensor(w1_hi[:, :, :].rearrange("p c f -> p (c f)"), both[0][0],
                           one.to_broadcast([128, 2 * FF]), ALU.mult)
        pool.tensor_tensor(w2[:, :, 0, :], raw2[0][:, :, :], one.unsqueeze(2).to_broadcast([128, FC, D]), ALU.mult
                           ).then_inc(self.high_ready, 1)
        pool.wait_ge(self.high_ready, turn(e))
        pool.tensor_tensor(w1_lo[:, :], raw1[0][:, 0, :], w1_hi[:, 0, :].bitcast(F32), ALU.subtract)
        pool.tensor_tensor(w1_lo_rest[:, :], raw1[0][0:REST, 1, :], w1_hi[0:REST, 1, :].bitcast(F32), ALU.subtract)
        pool.tensor_tensor(w2[:, :, 1, :], raw2[0][:, :, :], w2[:, :, 0, :].bitcast(F32), ALU.subtract
                           ).then_inc(self.split_ready, 1)
        yield
        pool.wait_ge(self.split_ready, turn(e))
        pool.sem_inc(self.raw_read, 1)

    def rest_of_the_experts(self, engine, each):
        with engine.Fori(0, EXPERTS // 2 - 1) as pair:
            each((pair * 2 + 1, 1))
            each((pair * 2 + 2, 0))
        each((EXPERTS - 1, 1))


def experts_stage(core, a, weights):
    nc, bank, h = core.nc, core.bank, core.h
    RING = 3
    second = weights.second
    w1_hi, w1_lo, w1_lo_rest, w2 = weights.w1_hi, weights.w1_lo, weights.w1_lo_rest, weights.w2
    y_psum, split_ready = weights.y_psum, weights.split_ready
    with ExitStack() as ctx:
        sb, sem, load_sem, raised = stage_tools(core, ctx)
        hidden = sb("hidden", [128, FC, N])
        hidden_hi = sb("hidden_hi", [128, FC, N], F32R)
        hidden_lo = sb("hidden_lo", [128, FC, N], F32R)
        names = ("hidden_psum", "bank_read", "hidden_ready", "hi_ready", "lo_ready", "y_half", "y_added")
        s = {n: sem(n) for n in names}
        if second:
            relu = sb("relu", [128, 2, N])
            b1, b1_loaded = weights.b1, weights.b1_loaded

        with nc.Block() as block:
            @block.sync
            def _(sp):
                raise_to_start(sp, raised)
                weights.rest_of_the_experts(sp, lambda e: weights.load(sp, a, e))

            @block.gpsimd
            def _(pool):
                def split(e):
                    for _ in weights.steps(pool, e):
                        pass

                weights.rest_of_the_experts(pool, split)

            @block.tensor
            def _(pe):
                with pe.Fori(0, EXPERTS // 2) as pair:
                    for k in range(2):
                        e = pair * 2 + k
                        with pe.Fori(0, TURNS) as i:
                            t = e * TURNS + i
                            at = bass.ds(i * N, N)
                            pe.wait_ge(split_ready, turn(e))
                            for m in range(FC):
                                f = slice(m * 128, (m + 1) * 128)
                                out = bank[m % RING][:, 0:N]
                                pe.wait_ge(s["bank_read"], turn(t, m + 1 - RING, FC))
                                pe.matmul(out, w1_hi[k][:, 0, f], core.z_hi[:, at], start=True, stop=False)
                                pe.matmul(out, w1_hi[k][:, 0, f], core.z_lo[:, at], start=False, stop=False)
                                pe.matmul(out, w1_lo[k][:, f], core.z_hi[:, at], start=False, stop=False)
                                pe.matmul(out, w1_hi[k][:, 1, f], core.z_rest[:, at], start=False, stop=False)
                                pe.matmul(out, w1_lo_rest[k][:, f], core.z_rest[0:REST, at], start=False, stop=True
                                          ).then_inc(s["hidden_psum"], 1)
                            pe.wait_ge(s["y_added"], turn(t, 0))
                            for m in range(FC):
                                first, last = m == 0, m == FC - 1
                                pe.wait_ge(s["lo_ready"], turn(t, m + 1, FC))
                                for b in range(GROUP):
                                    pe.matmul(bank[4 + b][0:T, 0:2 * D], hidden_hi[:, m, cols(b)],
                                              w2[k][:, m, :, :].rearrange("p a d -> p (a d)"),
                                              start=first, stop=last)
                                    mm = pe.matmul(bank[4 + b][0:T, 0:D], hidden_lo[:, m, cols(b)], w2[k][:, m, 0, :],
                                                   start=False, stop=last, skip_group_check=True)
                            mm.then_inc(y_psum, 1)

            @block.scalar
            def _(act):
                with act.Fori(0, EXPERTS // 2) as pair:
                    for k in range(2):
                        with act.Fori(0, TURNS) as i:
                            e = pair * 2 + k
                            t = e * TURNS + i
                            if second:
                                act.wait_ge(b1_loaded[k], pair * 16 + 16)
                            act.wait_ge(s["lo_ready"], turn(t, 0, FC))
                            for m in range(FC):
                                act.wait_ge(s["hidden_psum"], turn(t, m + 1, FC))
                                if second:
                                    act.activation(relu[:, m % 2, :], bank[m % RING][:, 0:N], ACT.Relu,
                                                   bias=b1[k][:, m:m + 1]).then_inc(s["bank_read"], 1)
                                    act.wait_ge(s["bank_read"], turn(t, m + 1, FC))
                                    act.activation(hidden[:, m, :], relu[:, m % 2, :], ACT.Square
                                                   ).then_inc(s["hidden_ready"], 1)
                                else:
                                    act.activation(hidden[:, m, :], bank[m % RING][:, 0:N], ACT.Gelu
                                                   ).then_inc(s["bank_read"], 1)

            @block.vector
            def _(v):
                written = s["hidden_ready"] if second else s["bank_read"]
                with v.Fori(0, EXPERTS // 2) as pair:
                    for k in range(2):
                        with v.Fori(0, TURNS) as i:
                            e = pair * 2 + k
                            t = e * TURNS + i
                            v.wait_ge(y_psum, turn(t, 0))
                            for m in range(FC):
                                v.wait_ge(written, turn(t, m + 1, FC))
                                v.tensor_copy(hidden_hi[:, m, :], hidden[:, m, :]).then_inc(s["hi_ready"], 1)
                                v.wait_ge(s["hi_ready"], turn(t, m + 1, FC))
                                v.tensor_tensor(hidden_lo[:, m, :], hidden[:, m, :], hidden_hi[:, m, :].bitcast(F32),
                                                ALU.subtract).then_inc(s["lo_ready"], 1)
                            v.wait_ge(y_psum, turn(t))
                            for part, done in ((0, s["y_half"]), (1, s["y_added"])):
                                for b in range(GROUP):
                                    gate = core.gates[:, bass.ds(i * (GROUP * EXPERTS) + b * EXPERTS + e, 1)]
                                    ins = v.scalar_tensor_tensor(out=sample_of(h, i, b),
                                                                 in0=bank[4 + b][0:T, cols(part, D)],
                                                                 scalar=gate, in1=sample_of(h, i, b),
                                                                 op0=ALU.mult, op1=ALU.add)
                                ins.then_inc(done, 1)
                                if part == 0:
                                    v.wait_ge(s["y_half"], turn(t))



def ssm_stage(core, a):
    nc, bank, h = core.nc, core.bank, core.h
    STATES = 16
    PER = 128 // STATES
    TILES = D // PER
    HALF = TILES // 2
    TAPS = 4
    PAD = TAPS - 1
    PIECES = 8
    PIECE = D * STATES // PIECES
    PIECE_TILES = TILES // PIECES
    SELECTIONS = 4
    with ExitStack() as ctx:
        sb, sem, load_sem, raised = stage_tools(core, ctx)
        norm = Norm(sb, sem, "norm")
        w_in = sb("w_in", [C, 2, 2 * D])
        w_dt = sb("w_dt", [C, 2, D])
        w_out = sb("w_out", [C, 2, D])
        b_out = sb("b_out", [1, D])
        raw = [sb("raw", [128, 2 * PIECE]) for _ in range(2)]
        w_hi = [sb(n, [C, 2, D * STATES], F32R) for n in ("w_b_hi", "w_c_hi")]
        w_lo = [sb(n, [C, 2, D * STATES], F32R) for n in ("w_b_lo", "w_c_lo")]
        spread = sb("spread", [C, HALF, 128], F32R)
        gather = sb("gather", [128, HALF, C], F32R)
        per_channel = sb("per_channel", [C, 2, 5 + TAPS])
        neg_bv = sb("neg_bv", [C, 2])
        row_consts = sb("row_consts", [128, 3, TILES])
        decay_rate = sb("decay_rate", [128, TILES])
        xn = sb("xn", [T, GROUP, D])
        xT = sb("xT", [C, 2, N])
        u = sb("u", [C, 2, GROUP, PAD + T])
        gate = sb("gate", [C, 2, N])
        conv = sb("conv", [C, 2, N])
        dt = sb("dt", [C, 2, N])
        dtu = sb("dtu", [C, 2, N])
        z = sb("z", [C, 2, N])
        soft, y = xT, z
        (conv_hi, conv_lo), (dt_hi, dt_lo), (dtu_hi, dtu_lo) = (
            [buffer[0:C, k * 2 * N:(k + 1) * 2 * N].rearrange("d (c t) -> d c t", c=2) for k in range(2)]
            for buffer in (core.z_hi, core.z_lo, core.z_rest))
        decay = sb("decay", [128, 2, N])
        dtu_rows = sb("dtu_rows", [128, 2, N])
        drive = sb("drive", [128, N])
        state = sb("state", [128, N])
        product = sb("product", [128, 2, N])
        product_hi = sb("product_hi", [128, 2, N], F32R)
        product_lo = sb("product_lo", [128, 2, N], F32R)
        w_loaded, rate_exp, consts_ready, selection_ready, piece_high, piece_ready = (
            load_sem(n) for n in ("w_loaded", "rate_exp", "consts_ready", "selection_ready", "piece_high",
                                  "piece_ready"))
        raw_loaded = [load_sem("raw_loaded") for _ in range(2)]
        names = ("xn_ready", "xT_psum", "xT_ready", "u_psum", "v_psum", "u_ready", "gate_exp", "conv_ready",
                 "conv_high", "conv_split", "dt_psum", "z_ready", "log_ready", "dt_done", "dt_high", "dtu_done",
                 "dtu_high", "dt_split", "b_psum", "spread_psum", "c_psum", "spread_read", "b_read",
                 "product_ready", "product_high", "product_split", "gathered", "y_ready", "out_psum", "h_done")
        s = {n: sem(n) for n in names}
        loads = [(w_in, "c_wi"), (w_dt, "c_wdt"), (per_channel, "c_channel"), (row_consts, "c_rows"),
                 (w_out, "c_wo"), (b_out, "c_bo")]

        def selection(matrix, k):
            part = slice(k % 2 * HALF // 2, (k % 2 + 1) * HALF // 2)
            return matrix[:, part, :].rearrange("p j r -> p (j r)")

        selections = [(spread, "spread"), (spread, "spread"), (gather, "gather"), (gather, "gather")]

        with nc.Block() as block:
            @block.sync
            def _(sp):
                raise_to_start(sp, raised)
                for tile, name in loads:
                    sp.dma_start(tile[tuple(slice(None) for _ in tile.shape)], a[name]).then_inc(w_loaded, 16)
                for n in range(SELECTIONS + 2 * PIECES):
                    if 2 <= n < SELECTIONS + 2:
                        sp.wait_ge(selection_ready, n - 1)
                    elif n >= SELECTIONS + 2:
                        sp.wait_ge(piece_ready, n - 1 - SELECTIONS)
                    if n < SELECTIONS:
                        source = selection(a[selections[n][1]], n)
                        target = raw[n % 2][0:source.shape[0], 0:source.shape[1]]
                    else:
                        p = n - SELECTIONS
                        source = a[("c_wb", "c_wc")[p % 2]][:, :, p // 2 * PIECE:(p // 2 + 1) * PIECE]
                        target = raw[n % 2][0:C, :].rearrange("d (c f) -> d c f", c=2)
                    sp.dma_start(target, source).then_inc(raw_loaded[n % 2], 16)

            @block.gpsimd
            def _(pool):
                norm_rstd(pool, core, norm, 0)
                for p in range(2 * PIECES):
                    n = SELECTIONS + p
                    source = raw[n % 2][0:C, :].rearrange("d (c f) -> d c f", c=2)
                    high, low = (part[p % 2][:, :, p // 2 * PIECE:(p // 2 + 1) * PIECE] for part in (w_hi, w_lo))
                    pool.wait_ge(raw_loaded[n % 2], 16 * (n // 2 + 1))
                    pool.tensor_tensor(high, source, core.ones[0:C, 0:1].unsqueeze(2).to_broadcast([C, 2, PIECE]),
                                       ALU.mult).then_inc(piece_high, 1)
                    pool.wait_ge(piece_high, p + 1)
                    pool.tensor_tensor(low, source, high.bitcast(F32), ALU.subtract).then_inc(piece_ready, 1)
                with pool.Fori(0, TURNS) as i:
                    pool.wait_ge(s["conv_high"], turn(i))
                    pool.tensor_tensor(conv_lo, conv[:, :, :], conv_hi.bitcast(F32), ALU.subtract
                                       ).then_inc(s["conv_split"], 1)
                    for j in range(TILES):
                        pool.wait_ge(s["product_high"], turn(i, j + 1, TILES))
                        pool.tensor_tensor(product_lo[:, j % 2, :], product[:, j % 2, :],
                                           product_hi[:, j % 2, :].bitcast(F32), ALU.subtract
                                           ).then_inc(s["product_split"], 1)
                    norm_rstd(pool, core, norm, i + 1)

            @block.tensor
            def _(pe):
                pe.wait_ge(w_loaded, 16 * len(loads))
                pe.wait_ge(selection_ready, SELECTIONS)

                def projected(kind, i, j):
                    pe.wait_ge(piece_ready, 2 * (j // PIECE_TILES) + kind + 1)
                    pe.wait_ge(s[("b_read", "product_ready")[kind]], turn(i, j - 1, TILES))
                    out = bank[2 * kind + j % 2][:, 0:N]
                    rows = slice(j * 128, (j + 1) * 128)
                    for c in range(2):
                        pe.matmul(out, w_hi[kind][:, c, rows], conv_hi[:, c, :], start=(c == 0), stop=False)
                        pe.matmul(out, w_hi[kind][:, c, rows], conv_lo[:, c, :], start=False, stop=False)
                        mm = pe.matmul(out, w_lo[kind][:, c, rows], conv_hi[:, c, :], start=False, stop=(c == 1))
                    mm.then_inc(s[("b_psum", "c_psum")[kind]], 1)

                def gather_tile(i, j):
                    pe.wait_ge(s["product_split"], turn(i, j + 1, TILES))
                    for part, operand in enumerate((product_hi, product_lo)):
                        mm = pe.matmul(bank[6 + j // HALF][0:C, 0:N], gather[:, j % HALF, :], operand[:, j % 2, :],
                                       start=(j % HALF == 0 and part == 0), stop=(j % HALF == HALF - 1 and part == 1))
                    mm.then_inc(s["gathered"], 1)

                with pe.Fori(0, TURNS) as i:
                    pe.wait_ge(s["h_done"], turn(i, 0))
                    pe.wait_ge(s["xn_ready"], turn(i))
                    transpose_group(pe, core, bank[0:2], xn, s["xT_psum"])
                    pe.wait_ge(s["xT_ready"], turn(i))
                    for j in range(4):
                        for c in range(2):
                            mm = pe.matmul(bank[2 + j][0:C, 0:N], w_in[:, c, j * C:(j + 1) * C], xT[:, c, :],
                                           start=(c == 0), stop=(c == 1))
                        if j % 2:
                            mm.then_inc(s[("u_psum", "v_psum")[j // 2]], 1)
                    pe.wait_ge(s["conv_ready"], turn(i))
                    for j in range(2):
                        for c in range(2):
                            mm = pe.matmul(bank[6 + j][0:C, 0:N], w_dt[:, c, j * C:(j + 1) * C], conv[:, c, :],
                                           start=(c == 0), stop=(c == 1))
                    mm.then_inc(s["dt_psum"], 1)
                    pe.wait_ge(s["conv_split"], turn(i))
                    for j in range(2):
                        projected(0, i, j)
                        projected(1, i, j)
                    pe.wait_ge(s["dt_split"], turn(i))
                    for j in range(TILES):
                        c = j // HALF
                        pe.wait_ge(s["spread_read"], turn(i, j, TILES))
                        for part, (of_dt, of_dtu) in enumerate(((dt_hi, dtu_hi), (dt_lo, dtu_lo))):
                            for first, operand in ((4, of_dt), (5, of_dtu)):
                                mm = pe.matmul(bank[first][:, 0:N], spread[:, j % HALF, :], operand[:, c, :],
                                               start=(part == 0), stop=(part == 1))
                        mm.then_inc(s["spread_psum"], 1)
                        if j >= 2:
                            gather_tile(i, j - 2)
                        if 1 <= j < TILES - 1:
                            projected(0, i, j + 1)
                            projected(1, i, j + 1)
                    gather_tile(i, TILES - 2)
                    gather_tile(i, TILES - 1)
                    pe.wait_ge(s["y_ready"], turn(i))
                    for b in range(GROUP):
                        out = bank[b // 2][0:T, cols(b % 2, D)]
                        for c in range(2):
                            pe.matmul(out, y[:, c, cols(b)], w_out[:, c, :], start=(c == 0), stop=False)
                        mm = pe.matmul(out, core.ones[0:1, 0:T], b_out[:, :], start=False, stop=True)
                    mm.then_inc(s["out_psum"], 1)

            @block.scalar
            def _(act):
                act.wait_ge(w_loaded, 16 * len(loads))
                act.activation(decay_rate[:, :], row_consts[:, 0, :], ACT.Exp).then_inc(rate_exp, 1)
                act.wait_ge(consts_ready, 1)
                with act.Fori(0, TURNS) as i:
                    act.wait_ge(s["xT_psum"], turn(i))
                    for c in range(2):
                        ins = act.activation(xT[:, c, :], bank[c][0:C, 0:N], ACT.Copy)
                    ins.then_inc(s["xT_ready"], 1)
                    act.wait_ge(s["u_psum"], turn(i))
                    for c in range(2):
                        ins = act.activation(u[:, c, :, PAD:PAD + T],
                                             bank[2 + c][0:C, 0:N].rearrange("d (b t) -> d b t", b=GROUP),
                                             ACT.Identity, bias=per_channel[:, c, 0:1])
                    ins.then_inc(s["u_ready"], 1)
                    act.wait_ge(s["y_ready"], turn(i, 0))
                    act.wait_ge(s["v_psum"], turn(i))
                    for c in range(2):
                        ins = act.activation(gate[:, c, :], bank[4 + c][0:C, 0:N], ACT.Exp,
                                             bias=neg_bv[:, c:c + 1], scale=-1.0)
                    ins.then_inc(s["gate_exp"], 1)
                    act.wait_ge(s["conv_ready"], turn(i))
                    act.activation(conv_hi, conv[:, :, :], ACT.Copy).then_inc(s["conv_high"], 1)
                    act.wait_ge(s["z_ready"], turn(i))
                    act.activation(soft[:, :, :], soft[:, :, :], ACT.Exp)
                    act.drain()
                    act.activation(soft[:, :, :], soft[:, :, :], ACT.Ln, bias=1.0).then_inc(s["log_ready"], 1)
                    act.wait_ge(s["dt_done"], turn(i))
                    act.activation(dt_hi, dt[:, :, :], ACT.Copy).then_inc(s["dt_high"], 1)
                    act.wait_ge(s["dtu_done"], turn(i))
                    act.activation(dtu_hi, dtu[:, :, :], ACT.Copy).then_inc(s["dtu_high"], 1)

                    def product_high(j):
                        act.wait_ge(s["gathered"], turn(i, j - 1, TILES))
                        act.wait_ge(s["product_ready"], turn(i, j + 1, TILES))
                        act.activation(product_hi[:, j % 2, :], product[:, j % 2, :], ACT.Copy
                                       ).then_inc(s["product_high"], 1)

                    for j in range(TILES):
                        act.wait_ge(s["product_ready"], turn(i, j - 1, TILES))
                        act.wait_ge(s["spread_psum"], turn(i, j + 1, TILES))
                        act.activation(decay[:, j % 2, :].rearrange("r (b t) -> r b t", b=GROUP)[:, :, 1:T],
                                       bank[4][:, 0:N].rearrange("r (b t) -> r b t", b=GROUP)[:, :, 1:T],
                                       ACT.Exp, scale=decay_rate[:, j:j + 1])
                        act.activation(dtu_rows[:, j % 2, :], bank[5][:, 0:N], ACT.Copy
                                       ).then_inc(s["spread_read"], 1)
                        if j:
                            product_high(j - 1)
                    product_high(TILES - 1)

            @block.vector
            def _(v):
                def normed(i):
                    norm_statistics(v, norm, lambda b: sample_of(h, i, b))
                    v.wait_ge(norm.rstd_ready, turn(i))
                    for b in range(GROUP):
                        ins = norm_apply(v, norm, lambda b: sample_of(h, i, b), lambda b: xn[:, b, :], b)
                    ins.then_inc(s["xn_ready"], 1)

                normed(0)
                v.memset(decay[:, :, :], 0.0)
                v.memset(u[:, :, :, :], 0.0)
                v.wait_ge(w_loaded, 16 * len(loads))
                v.tensor_scalar(neg_bv[:, :], per_channel[:, :, 1], -1.0, None, ALU.mult)
                v.wait_ge(rate_exp, 1)
                v.tensor_scalar(decay_rate[:, :], decay_rate[:, :], -1.0, None, ALU.mult).then_inc(consts_ready, 1)
                for n, (matrix, _) in enumerate(selections):
                    target = selection(matrix, n)
                    v.wait_ge(raw_loaded[n % 2], 16 * (n // 2 + 1))
                    v.tensor_copy(target, raw[n % 2][0:target.shape[0], 0:target.shape[1]]
                                  ).then_inc(selection_ready, 1)
                with v.Fori(0, TURNS) as i:
                    v.wait_ge(s["u_ready"], turn(i))
                    by_sample = [conv[:, c, :].rearrange("d (b t) -> d b t", b=GROUP) for c in range(2)]
                    for c in range(2):
                        v.tensor_scalar(by_sample[c], u[:, c, :, 0:T], per_channel[:, c, 5:6],
                                        per_channel[:, c, 2:3], ALU.mult, ALU.add)
                    for k in range(1, TAPS):
                        v.drain()
                        for c in range(2):
                            ins = v.scalar_tensor_tensor(out=by_sample[c], in0=u[:, c, :, k:k + T],
                                                         scalar=per_channel[:, c, 5 + k:6 + k], in1=by_sample[c],
                                                         op0=ALU.mult, op1=ALU.add)
                    ins.then_inc(s["conv_ready"], 1)
                    v.wait_ge(s["gate_exp"], turn(i))
                    v.tensor_scalar(gate[:, :, :], gate[:, :, :], 1.0, None, ALU.add)
                    v.wait_ge(s["dt_psum"], turn(i))
                    for c in range(2):
                        v.tensor_scalar(z[:, c, :], bank[6 + c][0:C, 0:N], per_channel[:, c, 3:4], None, ALU.add)
                    v.drain()
                    v.scalar_tensor_tensor(out=soft[:, :, :], in0=z[:, :, :], scalar=-1.0, in1=z[:, :, :],
                                           op0=ALU.mult, op1=ALU.min).then_inc(s["z_ready"], 1)
                    v.wait_ge(s["log_ready"], turn(i))
                    v.scalar_tensor_tensor(out=dt[:, :, :], in0=z[:, :, :], scalar=0.0, in1=soft[:, :, :],
                                           op0=ALU.max, op1=ALU.add).then_inc(s["dt_done"], 1)
                    v.wait_ge(s["dt_done"], turn(i))
                    v.tensor_tensor(dtu[:, :, :], dt[:, :, :], conv[:, :, :], ALU.mult).then_inc(s["dtu_done"], 1)
                    v.wait_ge(s["dt_high"], turn(i))
                    v.tensor_tensor(dt_lo, dt[:, :, :], dt_hi.bitcast(F32), ALU.subtract)
                    v.wait_ge(s["dtu_high"], turn(i))
                    v.tensor_tensor(dtu_lo, dtu[:, :, :], dtu_hi.bitcast(F32), ALU.subtract
                                    ).then_inc(s["dt_split"], 1)
                    for j in range(TILES):
                        k = j % 2
                        v.wait_ge(s["spread_read"], turn(i, j + 1, TILES))
                        v.wait_ge(s["b_psum"], turn(i, j + 1, TILES))
                        v.scalar_tensor_tensor(out=drive[:, :], in0=bank[k][:, 0:N],
                                               scalar=row_consts[:, 1, j:j + 1], in1=dtu_rows[:, k, :],
                                               op0=ALU.add, op1=ALU.mult).then_inc(s["b_read"], 1)
                        v.drain()
                        v.tensor_tensor_scan(state[:, :], decay[:, k, :], drive[:, :], 0.0, ALU.mult, ALU.add)
                        v.drain()
                        v.wait_ge(s["product_split"], turn(i, j - 1, TILES))
                        v.wait_ge(s["c_psum"], turn(i, j + 1, TILES))
                        v.scalar_tensor_tensor(out=product[:, k, :], in0=bank[2 + k][:, 0:N],
                                               scalar=row_consts[:, 2, j:j + 1], in1=state[:, :],
                                               op0=ALU.add, op1=ALU.mult).then_inc(s["product_ready"], 1)
                        if j < 2 * GROUP:
                            part = gate[:, j // GROUP, cols(j % GROUP)]
                            v.reciprocal(part, part)
                    v.wait_ge(s["gathered"], turn(i, TILES, TILES))
                    for c in range(2):
                        v.scalar_tensor_tensor(out=y[:, c, :], in0=conv[:, c, :], scalar=per_channel[:, c, 4:5],
                                               in1=bank[6 + c][0:C, 0:N], op0=ALU.mult, op1=ALU.add)
                    v.drain()
                    v.tensor_tensor(y[:, :, :], y[:, :, :], gate[:, :, :], ALU.mult).then_inc(s["y_ready"], 1)
                    normed(i + 1)
                    v.wait_ge(s["out_psum"], turn(i))
                    for p in range(2):
                        rows = h[:, bass.ds(i * (GROUP * D) + p * (2 * D), 2 * D)]
                        ins = v.tensor_tensor(rows, bank[p][0:T, 0:2 * D], rows, ALU.add)
                    ins.then_inc(s["h_done"], 1)



def gated_heads_stage(core, a):
    nc, bank, h = core.nc, core.bank, core.h
    HD = 64
    WIDE = HEADS * HD
    QK = 2 * WIDE // 128
    SHARED, ROUTED = 2, 10
    GATES = ROUTED + 2 + SHARED
    RING = 4
    SQUARES = 3
    with ExitStack() as ctx:
        sb, sem, load_sem, raised = stage_tools(core, ctx)
        norm = Norm(sb, sem, "norm")
        w = SplitWeights(sb, "w_qkv_gate", 3 * WIDE + GATES)
        w_out = sb("w_out", [128, WIDE // 128, D])
        b_v = sb("b_v", [1, WIDE])
        b_v_hi, b_v_lo, ones_row = (sb(n, [1, m], F32R) for n, m in (("b_v_hi", WIDE), ("b_v_lo", WIDE), ("ones", T)))
        b_out = sb("b_out", [1, D])
        b_qk = sb("b_qk", [128, QK])
        b_centered = sb("b_centered", [128, QK])
        affine = sb("affine", [128, 4])
        affine_in = sb("affine_in", [128, 4])
        head_sum = sb("head_sum", [128, 2, 2 * HEADS])
        average = sb("average", [128, 128])
        eps = sb("eps", [128, 1])
        xn = sb("xn", [T, GROUP, D + REST])
        xT = SplitColumns(core)
        rstd = sb("rstd", [128, QK, N])
        qkT = sb("qkT", [128, QK, N])
        spare = w.raw[:, :, :].rearrange("p a m -> p (a m)")
        square = spare[:, 0:SQUARES * N].rearrange("p (k t) -> p k t", k=SQUARES)
        oT = spare[:, SQUARES * N:(SQUARES + WIDE // 128) * N].rearrange("p (j t) -> p j t", t=N)
        o = (rstd[0:T, :, :].rearrange("t j n -> t (j n)")[:, 0:GROUP * WIDE]
             .rearrange("t (b m) -> t b m", b=GROUP))
        att = Heads(core, sb, sem, HD, core.mask64)
        qT, kT = qkT[:, 0:QK // 2, :], qkT[:, QK // 2:QK, :]
        glog = sb("glog", [T, GROUP, GATES])
        gpeak = sb("gpeak", [T, 3, GROUP])
        gsum = sb("gsum", [T, 3, GROUP])
        top = TopTwo(sb, ROUTED, "top")
        gates = sb("gates_12", [T, GROUP, HEADS])
        weight = sb("weight", [T, 2, 6])
        w_loaded, ones_ready, bias_mean, bias_ready, w_centered, w_high, w_split = (
            load_sem(n) for n in ("w_loaded", "ones_ready", "bias_mean", "bias_ready", "w_centered", "w_high",
                                  "w_split"))
        names = ("xn_ready", "xT_psum", "xT_high", "xT_split", "gate_psum", "gate_read", "gshift_ready", "gexp_ready",
                 "qk_psum", "square_ready", "centered_done", "var_psum", "log_done", "half_rstd", "half_ready",
                 "v_psum", "v_ready", "oT_psum", "oT_act", "oT_dve", "out_psum", "h_done")
        s = {n: sem(n) for n in names}
        loads = [(w_out, "e_wproj"), (b_v, "e_bv"), (b_out, "e_bproj"),
                 (b_qk, "e_bqk"), (affine_in, "e_affine"), (average, "average")]
        HALF = QK // 2
        chunk = list(range(HALF, QK)) + list(range(HALF))
        parts = ((0, ROUTED), (ROUTED, ROUTED + 2), (ROUTED + 2, GATES))

        with nc.Block() as block:
            @block.sync
            def _(sp):
                raise_to_start(sp, raised)
                w.load(sp, a["e_wqkvg"], w_loaded)
                for tile, name in loads:
                    sp.dma_start(tile[tuple(slice(None) for _ in tile.shape)], a[name]).then_inc(w_loaded, 16)

            @block.gpsimd
            def _(pool):
                pool.memset(att.vals[:, :, :, HD:HD + 1], 1.0).then_inc(ones_ready, 1)
                norm_rstd(pool, core, norm, 0)
                with pool.Fori(0, TURNS) as i:
                    pool.wait_ge(att.scores_psum, turn(i, 0, UNITS))
                    pool.wait_ge(s["half_ready"], turn(i, 1, 2))
                    for b in range(GROUP):
                        heads_pool(pool, att, i, kT, b)
                    norm_rstd(pool, core, norm, i + 1)

            @block.tensor
            def _(pe):
                pe.wait_ge(w_loaded, 16 * (2 + len(loads)))
                pe.matmul(bank[7][:, 0:QK], average[:, :], b_qk[:, :], start=True, stop=True).then_inc(bias_mean, 1)
                pe.wait_ge(ones_ready, 1)
                pe.wait_ge(w_split, 1)
                pe.wait_ge(bias_ready, 1)

                def variance(i, j):
                    pe.wait_ge(s["log_done"], turn(i, j - 1, QK))
                    pe.wait_ge(s["square_ready"], turn(i, j + 1, QK))
                    pe.matmul(bank[4 + j % 2][:, 0:N], average[:, :], square[:, j % SQUARES, :], start=True, stop=True
                              ).then_inc(s["var_psum"], 1)

                with pe.Fori(0, TURNS) as i:
                    pe.wait_ge(s["oT_dve"], turn(i, 0))
                    pe.wait_ge(s["xn_ready"], turn(i))
                    transpose_for_experts(pe, core, bank[0:2], xn, s["xT_psum"])
                    pe.wait_ge(s["h_done"], turn(i, 0))
                    pe.wait_ge(s["xT_split"], turn(i))
                    for b in range(GROUP):
                        mm = product_by_rows(pe, bank[6][0:T, cols(b, GATES)], xT, cols(b), w,
                                             slice(3 * WIDE, 3 * WIDE + GATES))
                    mm.then_inc(s["gate_psum"], 1)
                    pe.wait_ge(s["oT_act"], turn(i, 0))
                    for j in range(QK):
                        if j >= RING:
                            pe.wait_ge(s["centered_done"], turn(i, j + 1 - RING, QK))
                        mm = product_by_columns(pe, bank[j % RING][:, 0:N], w,
                                                slice(chunk[j] * 128, (chunk[j] + 1) * 128), xT)
                        mm.then_inc(s["qk_psum"], 1)
                        if j >= 2:
                            variance(i, j - 2)
                    variance(i, QK - 2)
                    variance(i, QK - 1)
                    for b in range(GROUP):
                        if b < 2:
                            pe.wait_ge(s["centered_done"], turn(i, QK, QK))
                        pe.wait_ge(s["v_ready"], turn(i, b - 1, GROUP))
                        for p in range(2):
                            out = bank[b % 2 * 2 + p][0:T, 0:WIDE // 2]
                            part = slice(p * WIDE // 2, (p + 1) * WIDE // 2)
                            product_by_rows(pe, out, xT, cols(b), w,
                                            slice(2 * WIDE + part.start, 2 * WIDE + part.stop), more=True)
                            pe.matmul(out, ones_row[:, :], b_v_hi[:, part], start=False, stop=False)
                            mm = pe.matmul(out, ones_row[:, :], b_v_lo[:, part], start=False, stop=True)
                        mm.then_inc(s["v_psum"], 1)
                    pe.wait_ge(s["v_ready"], turn(i, GROUP, GROUP))
                    pe.wait_ge(s["gate_read"], turn(i))
                    pe.wait_ge(s["log_done"], turn(i, QK, QK))
                    pe.wait_ge(s["half_ready"], turn(i, 2, 2))
                    heads_tensor(pe, att, i, qT)
                    pe.wait_ge(att.context_done, turn(i, UNITS, UNITS))
                    for j in range(WIDE // 128):
                        for b in range(GROUP):
                            mm = pe.transpose(bank[j][:, cols(b)], o[:, b, j * 128:(j + 1) * 128],
                                              core.ident[0:T, 0:T])
                    mm.then_inc(s["oT_psum"], 1)
                    pe.wait_ge(s["oT_act"], turn(i))
                    pe.wait_ge(s["oT_dve"], turn(i))
                    for b in range(GROUP):
                        out = bank[6 + b // 2][0:T, cols(b % 2, D)]
                        for j in range(WIDE // 128):
                            pe.matmul(out, oT[:, j, cols(b)], w_out[:, j, :], start=(j == 0), stop=False)
                        mm = pe.matmul(out, core.ones[0:1, 0:T], b_out[:, :], start=False, stop=True)
                    mm.then_inc(s["out_psum"], 1)

            @block.scalar
            def _(act):
                act.wait_ge(w_centered, 1)
                w.high(act).then_inc(w_high, 1)
                act.wait_ge(bias_ready, 1)
                with act.Fori(0, TURNS) as i:
                    act.wait_ge(s["xT_psum"], turn(i))
                    xT.high(act, bank[0:2]).then_inc(s["xT_high"], 1)

                    def logarithm(j):
                        act.wait_ge(s["var_psum"], turn(i, j + 1, QK))
                        act.activation(rstd[:, chunk[j], :], bank[4 + j % 2][:, 0:N], ACT.Ln, bias=eps[:, 0:1]
                                       ).then_inc(s["log_done"], 1)

                    def inverse_roots(half):
                        act.wait_ge(s["log_done"], turn(i, (half + 1) * HALF, QK))
                        of_half = rstd[:, chunk[half * HALF]:chunk[half * HALF] + HALF, :]
                        act.activation(of_half, of_half, ACT.Exp, scale=-0.5).then_inc(s["half_rstd"], 1)

                    for j in range(QK):
                        if j % HALF == 2:
                            act.wait_ge(s["half_ready"], turn(i, j // HALF - 1, 2))
                        act.wait_ge(s["var_psum"], turn(i, j + 1 - SQUARES, QK))
                        act.wait_ge(s["qk_psum"], turn(i, j + 1, QK))
                        act.activation(square[:, j % SQUARES, :], bank[j % RING][:, 0:N], ACT.Square,
                                       bias=b_centered[:, chunk[j]:chunk[j] + 1]).then_inc(s["square_ready"], 1)
                        if j >= 2:
                            logarithm(j - 2)
                        if j == HALF + 1:
                            inverse_roots(0)
                    logarithm(QK - 2)
                    logarithm(QK - 1)
                    inverse_roots(1)
                    act.wait_ge(s["gshift_ready"], turn(i))
                    act.activation(glog[:, :, :], glog[:, :, :], ACT.Exp).then_inc(s["gexp_ready"], 1)
                    for b in range(GROUP):
                        act.wait_ge(s["v_psum"], turn(i, b + 1, GROUP))
                        for p in range(2):
                            ins = act.activation(att.vals[:, b, 6 * p:6 * p + 6, 0:HD],
                                                 bank[b % 2 * 2 + p][0:T, 0:WIDE // 2]
                                                 .rearrange("t (n d) -> t n d", d=HD), ACT.Copy)
                        ins.then_inc(s["v_ready"], 1)
                    heads_scalar(act, att, i)
                    act.wait_ge(s["oT_psum"], turn(i))
                    for j in range(3, 6):
                        ins = act.activation(oT[:, j, :], bank[j][:, 0:N], ACT.Copy)
                    ins.then_inc(s["oT_act"], 1)

            @block.vector
            def _(v):
                v.memset(eps[:, :], EPS)
                v.wait_ge(w_loaded, 16 * (2 + len(loads)))
                heads_of = [w.raw[:, c, 0:2 * WIDE].rearrange("p (n d) -> p n d", d=HD) for c in range(2)]
                for c in range(2):
                    v.tensor_reduce(head_sum[:, c, :], heads_of[c], AX.X, ALU.add)
                v.drain()
                v.tensor_scalar(head_sum[:, :, :], head_sum[:, :, :], 1.0 / HD, None, ALU.mult)
                v.drain()
                for c in range(2):
                    ins = v.tensor_tensor(heads_of[c], heads_of[c],
                                          head_sum[:, c, :].unsqueeze(2).to_broadcast([128, 2 * HEADS, HD]),
                                          ALU.subtract)
                ins.then_inc(w_centered, 1)
                v.memset(ones_row[:, :].bitcast(F32), 1.0)
                v.tensor_copy(b_v_hi[:, :], b_v[:, :])
                v.drain()
                v.tensor_tensor(b_v_lo[:, :], b_v[:, :], b_v_hi[:, :].bitcast(F32), ALU.subtract)
                v.tensor_scalar(affine[:, 0:2], affine_in[:, 0:2], HD ** -0.5, None, ALU.mult)
                v.tensor_copy(affine[:, 2:4], affine_in[:, 2:4])
                v.wait_ge(bias_mean, 1)
                v.tensor_tensor(b_centered[:, :], b_qk[:, :], bank[7][:, 0:QK], ALU.subtract).then_inc(bias_ready, 1)
                v.wait_ge(w_high, 1)
                w.low(v).then_inc(w_split, 1)

                def normed(i):
                    norm_statistics(v, norm, lambda b: sample_of(h, i, b))
                    v.wait_ge(norm.rstd_ready, turn(i))
                    for b in range(GROUP):
                        norm_apply(v, norm, lambda b: sample_of(h, i, b), lambda b: xn[:, b, 0:D], b)
                    duplicate_rest(v, xn).then_inc(s["xn_ready"], 1)

                normed(0)
                with v.Fori(0, TURNS) as i:
                    v.wait_ge(s["xT_high"], turn(i))
                    xT.low(v, bank[0:2]).then_inc(s["xT_split"], 1)
                    v.wait_ge(s["gate_psum"], turn(i))
                    v.tensor_copy(glog[:, :, :], bank[6][0:T, 0:GROUP * GATES]).then_inc(s["gate_read"], 1)
                    v.drain()
                    for n, (lo, hi) in enumerate(parts):
                        v.tensor_reduce(gpeak[:, n, :], glog[:, :, lo:hi], AX.X, ALU.max)
                    v.drain()
                    for n, (lo, hi) in enumerate(parts):
                        ins = v.tensor_tensor(glog[:, :, lo:hi], glog[:, :, lo:hi],
                                              gpeak[:, n, :].unsqueeze(2).to_broadcast([T, GROUP, hi - lo]),
                                              ALU.subtract)
                    ins.then_inc(s["gshift_ready"], 1)

                    def scaled(half, first, count):
                        lo = chunk[half * HALF] + first
                        kind = 2 if half == 0 else 0
                        v.wait_ge(s["centered_done"], turn(i, (half + 1) * HALF, QK))
                        v.wait_ge(s["half_rstd"], turn(i, half + 1, 2))
                        v.tensor_tensor(qkT[:, lo:lo + count, :], qkT[:, lo:lo + count, :], rstd[:, lo:lo + count, :],
                                        ALU.mult)
                        v.drain()
                        ins = v.tensor_scalar(qkT[:, lo:lo + count, :], qkT[:, lo:lo + count, :],
                                              affine[:, kind:kind + 1], affine[:, kind + 1:kind + 2],
                                              ALU.mult, ALU.add)
                        if first + count == HALF:
                            ins.then_inc(s["half_ready"], 1)

                    for j in range(QK):
                        if j == 0:
                            v.wait_ge(att.kblock_ready, turn(i, 0, GROUP))
                        elif j == HALF:
                            v.wait_ge(att.scores_psum, turn(i, 0, UNITS))
                        v.wait_ge(s["square_ready"], turn(i, j + 1, QK))
                        v.tensor_scalar(qkT[:, chunk[j], :], bank[j % RING][:, 0:N],
                                        b_centered[:, chunk[j]:chunk[j] + 1], None,
                                        ALU.add).then_inc(s["centered_done"], 1)
                        if j >= HALF + 3:
                            scaled(0, 2 * (j - HALF - 3), 2)
                    scaled(1, 0, HALF)
                    v.wait_ge(s["gexp_ready"], turn(i))
                    for n, (lo, hi) in enumerate(parts):
                        v.tensor_reduce(gsum[:, n, :], glog[:, :, lo:hi], AX.X, ALU.add)
                    v.drain()
                    v.reciprocal(gsum[:, :, :], gsum[:, :, :])
                    v.drain()
                    for n, (lo, hi) in enumerate(parts):
                        v.tensor_tensor(glog[:, :, lo:hi], glog[:, :, lo:hi],
                                        gsum[:, n, :].unsqueeze(2).to_broadcast([T, GROUP, hi - lo]), ALU.mult)
                    v.drain()
                    top_two_hot(v, core, top, glog[:, :, 0:ROUTED])
                    v.tensor_tensor(top.hot[:, 0, :, :], top.hot[:, 0, :, :], top.hot[:, 1, :, :], ALU.add)
                    v.drain()
                    v.tensor_tensor(glog[:, :, 0:ROUTED], glog[:, :, 0:ROUTED], top.hot[:, 0, :, :], ALU.mult)
                    v.drain()
                    v.tensor_reduce(gsum[:, 0, :], glog[:, :, 0:ROUTED], AX.X, ALU.add)
                    v.drain()
                    v.tensor_scalar(gsum[:, 0, :], gsum[:, 0, :], 2.0 ** -23, None, ALU.max)
                    v.drain()
                    v.reciprocal(gsum[:, 0, :], gsum[:, 0, :])
                    v.drain()
                    v.scalar_tensor_tensor(out=gsum[:, 0, :], in0=gsum[:, 0, :], scalar=4.0,
                                           in1=glog[:, :, ROUTED + 1], op0=ALU.mult, op1=ALU.mult)
                    v.tensor_scalar(gsum[:, 1, :], glog[:, :, ROUTED], 4.0, None, ALU.mult)
                    v.drain()
                    v.tensor_tensor(gates[:, :, SHARED:HEADS], glog[:, :, 0:ROUTED],
                                    gsum[:, 0, :].unsqueeze(2).to_broadcast([T, GROUP, ROUTED]), ALU.mult)
                    v.tensor_tensor(gates[:, :, 0:SHARED], glog[:, :, ROUTED + 2:GATES],
                                    gsum[:, 1, :].unsqueeze(2).to_broadcast([T, GROUP, SHARED]), ALU.mult)

                    def rescale(u, inv):
                        v.tensor_tensor(weight[:, u % 2, :], inv, gates[:, u // 2, cols(u % 2, 6)], ALU.mult)
                        v.drain()
                        return v.tensor_tensor(o[:, u // 2, cols(u % 2, 6 * HD)].rearrange("t (n d) -> t n d", d=HD),
                                               att.context(u)[:, :, 0:HD],
                                               weight[:, u % 2, :].unsqueeze(2).to_broadcast([T, 6, HD]), ALU.mult)
                    heads_vector(v, att, i, rescale)
                    v.wait_ge(s["oT_psum"], turn(i))
                    for j in range(3):
                        ins = v.tensor_copy(oT[:, j, :], bank[j][:, 0:N])
                    ins.then_inc(s["oT_dve"], 1)
                    normed(i + 1)
                    v.wait_ge(s["out_psum"], turn(i))
                    for p in range(2):
                        rows = h[:, bass.ds(i * (GROUP * D) + p * (2 * D), 2 * D)]
                        ins = v.tensor_tensor(rows, bank[6 + p][0:T, 0:2 * D], rows, ALU.add)
                    ins.then_inc(s["h_done"], 1)



def position_attention_stage(core, a):
    nc, bank, h = core.nc, core.bank, core.h
    KV = D // 3
    with ExitStack() as ctx:
        sb, sem, load_sem, raised = stage_tools(core, ctx)
        norm = Norm(sb, sem, "norm")
        table = sb("table", [C, 2, T])
        w_v = sb("w_v", [C, 2, KV])
        w_out = sb("w_out", [KV, D])
        peak = sb("peak", [T, 1])
        total = sb("total", [T, 1])
        probs = sb("probs", [T, T])
        probsT = sb("probsT", [T, T])
        xn = sb("xn", [T, GROUP, D])
        xT = sb("xT", [C, 2, N])
        vals = sb("vals", [T, GROUP, KV])
        contextT = sb("contextT", [KV, N])
        w_loaded, scores_psum, peak_ready, exp_ready, probs_ready, probsT_psum, probsT_ready = (
            load_sem(n) for n in ("w_loaded", "scores_psum", "peak_ready", "exp_ready", "probs_ready",
                                  "probsT_psum", "probsT_ready"))
        names = ("xn_ready", "xT_psum", "xT_ready", "v_psum", "v_ready", "context_psum", "context_ready",
                 "out_psum", "h_done")
        s = {n: sem(n) for n in names}

        with nc.Block() as block:
            @block.sync
            def _(sp):
                raise_to_start(sp, raised)
                sp.dma_start(table[:, :, :], a["f_table"]).then_inc(w_loaded, 16)
                sp.dma_start(w_v[:, :, :], a["f_wv"]).then_inc(w_loaded, 16)
                sp.dma_start(w_out[:, :], a["f_wo"]).then_inc(w_loaded, 16)

            @block.gpsimd
            def _(pool):
                norm_rstd(pool, core, norm, 0)
                with pool.Fori(0, TURNS) as i:
                    norm_rstd(pool, core, norm, i + 1)

            @block.tensor
            def _(pe):
                pe.wait_ge(w_loaded, 48)
                for c in range(2):
                    mm = pe.matmul(bank[6][0:T, 0:T], table[:, c, :], table[:, c, :], start=(c == 0), stop=(c == 1))
                mm.then_inc(scores_psum, 1)
                pe.wait_ge(probs_ready, 1)
                pe.transpose(bank[7][0:T, 0:T], probs[:, :], core.ident[0:T, 0:T]).then_inc(probsT_psum, 1)
                pe.wait_ge(probsT_ready, 1)
                with pe.Fori(0, TURNS) as i:
                    pe.wait_ge(s["xn_ready"], turn(i))
                    pe.wait_ge(s["xT_ready"], turn(i, 0))
                    transpose_group(pe, core, bank[0:2], xn, s["xT_psum"])
                    pe.wait_ge(s["v_ready"], turn(i, 0))
                    pe.wait_ge(s["xT_ready"], turn(i))
                    for b in range(GROUP):
                        for c in range(2):
                            mm = pe.matmul(bank[2][0:T, cols(b, KV)], xT[:, c, cols(b)], w_v[:, c, :],
                                           start=(c == 0), stop=(c == 1))
                    mm.then_inc(s["v_psum"], 1)
                    pe.wait_ge(s["context_ready"], turn(i, 0))
                    pe.wait_ge(s["v_ready"], turn(i))
                    for b in range(GROUP):
                        mm = pe.matmul(bank[3][0:KV, cols(b)], vals[:, b, :], probsT[:, :], start=True, stop=True)
                    mm.then_inc(s["context_psum"], 1)
                    pe.wait_ge(s["h_done"], turn(i, 0))
                    pe.wait_ge(s["context_ready"], turn(i))
                    for b in range(GROUP):
                        mm = pe.matmul(bank[4 + b // 2][0:T, cols(b % 2, D)], contextT[:, cols(b)], w_out[:, :],
                                       start=True, stop=True)
                    mm.then_inc(s["out_psum"], 1)

            @block.scalar
            def _(act):
                act.wait_ge(peak_ready, 1)
                act.activation(probs[:, :], bank[6][0:T, 0:T], ACT.Exp, bias=peak[:, 0:1],
                               accum_out=total[:, 0:1]).then_inc(exp_ready, 1)
                act.wait_ge(probsT_psum, 1)
                act.activation(probsT[:, :], bank[7][0:T, 0:T], ACT.Copy).then_inc(probsT_ready, 1)
                with act.Fori(0, TURNS) as i:
                    act.wait_ge(s["v_psum"], turn(i, 0))
                    act.wait_ge(s["xT_psum"], turn(i))
                    for c in range(2):
                        ins = act.activation(xT[:, c, :], bank[c][0:C, 0:N], ACT.Copy)
                    ins.then_inc(s["xT_ready"], 1)
                    act.wait_ge(s["context_psum"], turn(i, 0))
                    act.wait_ge(s["v_psum"], turn(i))
                    act.activation(vals[:, :, :], bank[2][0:T, 0:GROUP * KV], ACT.Copy).then_inc(s["v_ready"], 1)
                    act.wait_ge(s["out_psum"], turn(i, 0))
                    act.wait_ge(s["context_psum"], turn(i))
                    act.activation(contextT[:, :], bank[3][0:KV, 0:N], ACT.Copy).then_inc(s["context_ready"], 1)

            @block.vector
            def _(v):
                v.wait_ge(scores_psum, 1)
                v.tensor_reduce(peak[:, :], bank[6][0:T, 0:T], AX.X, ALU.max, negate=True).then_inc(peak_ready, 1)
                v.wait_ge(exp_ready, 1)
                v.reciprocal(total[:, :], total[:, :])
                v.drain()
                v.tensor_scalar(probs[:, :], probs[:, :], total[:, 0:1], None, ALU.mult).then_inc(probs_ready, 1)
                def normed(i):
                    norm_statistics(v, norm, lambda b: sample_of(h, i, b))
                    v.wait_ge(s["xT_psum"], turn(i, 0))
                    v.wait_ge(norm.rstd_ready, turn(i))
                    for b in range(GROUP):
                        ins = norm_apply(v, norm, lambda b: sample_of(h, i, b), lambda b: xn[:, b, :], b)
                    ins.then_inc(s["xn_ready"], 1)

                normed(0)
                with v.Fori(0, TURNS) as i:
                    normed(i + 1)
                    v.wait_ge(s["out_psum"], turn(i))
                    for p in range(2):
                        rows = h[:, bass.ds(i * (GROUP * D) + p * (2 * D), 2 * D)]
                        ins = v.tensor_tensor(rows, bank[4 + p][0:T, 0:2 * D], rows, ALU.add)
                    ins.then_inc(s["h_done"], 1)



def int8_stage(core, a):
    nc, bank, h = core.nc, core.bank, core.h
    ROUND = 1.5 * 2.0 ** 23
    ACT_SCALE, W_SCALE = 0.02, 0.01
    with ExitStack() as ctx:
        sb, sem, load_sem, raised = stage_tools(core, ctx)
        norm = Norm(sb, sem, "norm")
        w_words = sb("w_words", [C, 2 * D // 4], I32)
        w8 = w_words[:, :].bitcast(I8).rearrange("p (c n) -> p c n", c=2)
        w = sb("w", [C, 2, D], BF16)
        ident = sb("ident16", [128, 128], BF16)
        bias = sb("bias", [T, D])
        xn = sb("xn", [T, GROUP, D])
        quant = sb("quant", [T, GROUP, D], BF16)
        quantT = sb("quantT", [C, 2, N], BF16)
        scaled = sb("scaled", [T, GROUP, D])
        w_loaded, consts_ready = load_sem("w_loaded"), load_sem("consts_ready")
        names = ("quant_ready", "quantT_psum", "quantT_ready", "out_psum", "h_done")
        s = {n: sem(n) for n in names}
        turned = [bank[c][0:C, 0:N // 2].bitcast(BF16) for c in range(2)]

        with nc.Block() as block:
            @block.sync
            def _(sp):
                raise_to_start(sp, raised)
                sp.dma_start(w_words[:, :], a["g_w"]).then_inc(w_loaded, 16)
                sp.dma_start(bias[:, :], a["g_bias"].to_broadcast([T, D])).then_inc(w_loaded, 16)

            @block.gpsimd
            def _(pool):
                norm_rstd(pool, core, norm, 0)
                with pool.Fori(0, TURNS) as i:
                    norm_rstd(pool, core, norm, i + 1)

            @block.tensor
            def _(pe):
                pe.wait_ge(consts_ready, 1)
                with pe.Fori(0, TURNS) as i:
                    pe.wait_ge(s["quantT_ready"], turn(i, 0))
                    pe.wait_ge(s["quant_ready"], turn(i))
                    for c in range(2):
                        for b in range(GROUP):
                            mm = pe.transpose(turned[c][:, cols(b)], quant[:, b, c * C:(c + 1) * C],
                                              ident[0:T, 0:T])
                    mm.then_inc(s["quantT_psum"], 1)
                    pe.wait_ge(s["h_done"], turn(i, 0))
                    pe.wait_ge(s["quantT_ready"], turn(i))
                    for b in range(GROUP):
                        for c in range(2):
                            mm = pe.matmul(bank[4 + b // 2][0:T, cols(b % 2, D)], quantT[:, c, cols(b)], w[:, c, :],
                                           start=(c == 0), stop=(c == 1))
                    mm.then_inc(s["out_psum"], 1)

            @block.scalar
            def _(act):
                with act.Fori(0, TURNS) as i:
                    act.wait_ge(s["out_psum"], turn(i, 0))
                    act.wait_ge(s["quantT_psum"], turn(i))
                    for c in range(2):
                        ins = act.activation(quantT[:, c, :], turned[c], ACT.Copy)
                    ins.then_inc(s["quantT_ready"], 1)

            @block.vector
            def _(v):
                v.wait_ge(w_loaded, 32)
                v.tensor_copy(w[:, :, :], w8)
                v.tensor_copy(ident[:, :], core.ident[:, :]).then_inc(consts_ready, 1)
                def quantized(i):
                    norm_statistics(v, norm, lambda b: sample_of(h, i, b))
                    v.wait_ge(norm.rstd_ready, turn(i))
                    for b in range(GROUP):
                        norm_apply(v, norm, lambda b: sample_of(h, i, b), lambda b: xn[:, b, :], b)
                    v.drain()
                    v.tensor_scalar(xn[:, :, :], xn[:, :, :], 1.0 / ACT_SCALE, ROUND, ALU.mult, ALU.add)
                    v.drain()
                    v.tensor_scalar(xn[:, :, :], xn[:, :, :], ROUND, 127.0, ALU.subtract, ALU.min)
                    v.drain()
                    v.wait_ge(s["quantT_psum"], turn(i, 0))
                    v.tensor_scalar(quant[:, :, :], xn[:, :, :], -128.0, None, ALU.max).then_inc(s["quant_ready"], 1)

                quantized(0)
                with v.Fori(0, TURNS) as i:
                    quantized(i + 1)
                    v.wait_ge(s["out_psum"], turn(i))
                    for p in range(2):
                        v.scalar_tensor_tensor(out=scaled[:, 2 * p:2 * p + 2, :],
                                               in0=bank[4 + p][0:T, 0:2 * D].rearrange("t (b d) -> t b d", b=2),
                                               scalar=ACT_SCALE * W_SCALE,
                                               in1=bias[:, :].unsqueeze(1).to_broadcast([T, 2, D]),
                                               op0=ALU.mult, op1=ALU.add)
                    v.drain()
                    rows = h[:, bass.ds(i * (GROUP * D), GROUP * D)]
                    v.tensor_tensor(rows, rows, scaled[:, :, :].rearrange("t b d -> t (b d)"), ALU.add
                                    ).then_inc(s["h_done"], 1)



def rotary_heads_stage(core, a):
    nc, bank, h = core.nc, core.bank, core.h
    with ExitStack() as ctx:
        sb, sem, load_sem, raised = stage_tools(core, ctx)
        norm = Norm(sb, sem, "norm")
        w = sb("w", [C, 2, 5 * D])
        b_qk = sb("b_qk", [C, 8])
        b_v = sb("b_v", [1, D])
        w_out = sb("w_out", [C, 2, D])
        b_out = sb("b_out", [1, D])
        angles = sb("angles", [C, 4, T])
        xn = sb("xn", [T, GROUP, D])
        xT = sb("xT", [C, 2, N])
        cos_part = sb("cos_part", [C, 2, N])
        sin_part = sb("sin_part", [C, 2, N])
        qkT = sb("qkT", [C, 4, N])
        qT, kT = qkT[:, 0:2, :], qkT[:, 2:4, :]
        o = sb("o", [T, GROUP, D])
        oT = sb("oT", [C, 2, N])
        att = Heads(core, sb, sem, 16, core.mask16)
        w_loaded, ones_ready = load_sem("w_loaded"), load_sem("ones_ready")
        names = ("xn_ready", "xT_psum", "xT_ready", "qk_psum", "parts_ready", "qk_ready", "v_psum", "v_ready",
                 "oT_psum", "oT_ready", "out_psum", "h_done")
        s = {n: sem(n) for n in names}
        loads = [(w, "h_w"), (b_qk, "h_bqk"), (b_v, "h_bv"), (w_out, "h_wo"), (b_out, "h_bo"), (angles, "h_angles")]

        with nc.Block() as block:
            @block.sync
            def _(sp):
                raise_to_start(sp, raised)
                for tile, name in loads:
                    sp.dma_start(tile[tuple(slice(None) for _ in tile.shape)], a[name]).then_inc(w_loaded, 16)

            @block.gpsimd
            def _(pool):
                pool.memset(att.vals[:, :, :, 16:17], 1.0).then_inc(ones_ready, 1)
                norm_rstd(pool, core, norm, 0)
                with pool.Fori(0, TURNS) as i:
                    pool.wait_ge(att.scores_psum, turn(i, 0, UNITS))
                    pool.wait_ge(s["qk_ready"], turn(i, 4, 4))
                    for b in range(GROUP):
                        heads_pool(pool, att, i, kT, b)
                    norm_rstd(pool, core, norm, i + 1)

            @block.tensor
            def _(pe):
                pe.wait_ge(w_loaded, 16 * len(loads))
                pe.wait_ge(ones_ready, 1)
                with pe.Fori(0, TURNS) as i:
                    pe.wait_ge(s["xn_ready"], turn(i))
                    transpose_group(pe, core, bank[0:2], xn, s["xT_psum"])
                    pe.wait_ge(s["h_done"], turn(i, 0))
                    pe.wait_ge(s["xT_ready"], turn(i))
                    for j in range(4):
                        pe.wait_ge(s["parts_ready"], turn(i, j - 1, 4))
                        for r in range(2):
                            at = (2 * (j // 2) + r) * D + j % 2 * C
                            for c in range(2):
                                mm = pe.matmul(bank[2 + j % 2 * 2 + r][0:C, 0:N], w[:, c, at:at + C], xT[:, c, :],
                                               start=(c == 0), stop=(c == 1))
                        mm.then_inc(s["qk_psum"], 1)
                    for b in range(GROUP):
                        out = bank[6 + b // 2][0:T, cols(b % 2, D)]
                        for c in range(2):
                            pe.matmul(out, xT[:, c, cols(b)], w[:, c, 4 * D:5 * D], start=(c == 0), stop=False)
                        mm = pe.matmul(out, core.ones[0:1, 0:T], b_v[:, :], start=False, stop=True)
                    mm.then_inc(s["v_psum"], 1)
                    pe.wait_ge(s["qk_ready"], turn(i, 4, 4))
                    pe.wait_ge(s["v_ready"], turn(i))
                    heads_tensor(pe, att, i, qT)
                    pe.wait_ge(att.context_done, turn(i, UNITS, UNITS))
                    transpose_group(pe, core, bank[0:2], o, s["oT_psum"])
                    pe.wait_ge(s["oT_ready"], turn(i))
                    for b in range(GROUP):
                        out = bank[2 + b // 2][0:T, cols(b % 2, D)]
                        for c in range(2):
                            pe.matmul(out, oT[:, c, cols(b)], w_out[:, c, :], start=(c == 0), stop=False)
                        mm = pe.matmul(out, core.ones[0:1, 0:T], b_out[:, :], start=False, stop=True)
                    mm.then_inc(s["out_psum"], 1)

            @block.scalar
            def _(act):
                with act.Fori(0, TURNS) as i:
                    act.wait_ge(s["xT_psum"], turn(i))
                    for c in range(2):
                        ins = act.activation(xT[:, c, :], bank[c][0:C, 0:N], ACT.Copy)
                    ins.then_inc(s["xT_ready"], 1)
                    act.wait_ge(s["v_psum"], turn(i))
                    for b in range(GROUP):
                        ins = act.activation(att.vals[:, b, :, 0:16], bank[6 + b // 2][0:T, cols(b % 2, D)]
                                             .rearrange("t (n d) -> t n d", d=16), ACT.Copy)
                    ins.then_inc(s["v_ready"], 1)
                    heads_scalar(act, att, i)
                    act.wait_ge(s["oT_psum"], turn(i))
                    for c in range(2):
                        ins = act.activation(oT[:, c, :], bank[c][0:C, 0:N], ACT.Copy)
                    ins.then_inc(s["oT_ready"], 1)

            @block.vector
            def _(v):
                v.wait_ge(w_loaded, 16 * len(loads))
                def normed(i):
                    norm_statistics(v, norm, lambda b: sample_of(h, i, b))
                    v.wait_ge(norm.rstd_ready, turn(i))
                    for b in range(GROUP):
                        ins = norm_apply(v, norm, lambda b: sample_of(h, i, b), lambda b: xn[:, b, :], b)
                    ins.then_inc(s["xn_ready"], 1)

                normed(0)
                with v.Fori(0, TURNS) as i:
                    for j in range(4):
                        k, kind = j % 2, j // 2
                        v.wait_ge(s["qk_psum"], turn(i, j + 1, 4))
                        for part, r in ((cos_part, 0), (sin_part, 1)):
                            at = 4 * kind + 2 * r + k
                            ins = v.scalar_tensor_tensor(
                                out=part[:, k, :].rearrange("d (b t) -> d b t", b=GROUP),
                                in0=bank[2 + 2 * k + r][0:C, 0:N].rearrange("d (b t) -> d b t", b=GROUP),
                                scalar=b_qk[:, at:at + 1],
                                in1=angles[:, 2 * kind + r, :].unsqueeze(1).to_broadcast([C, GROUP, T]),
                                op0=ALU.add, op1=ALU.mult)
                        ins.then_inc(s["parts_ready"], 1)
                        v.drain()
                        v.tensor_tensor(qkT[:, j, :], cos_part[:, k, :], sin_part[:, k, :], ALU.add
                                        ).then_inc(s["qk_ready"], 1)

                    def rescale(u, inv):
                        return v.tensor_tensor(o[:, u // 2, cols(u % 2, C)].rearrange("t (n d) -> t n d", d=16),
                                               att.context(u)[:, :, 0:16],
                                               inv.unsqueeze(2).to_broadcast([T, UNIT_HEADS, 16]), ALU.mult)
                    heads_vector(v, att, i, rescale)
                    normed(i + 1)
                    v.wait_ge(s["out_psum"], turn(i))
                    for p in range(2):
                        rows = h[:, bass.ds(i * (GROUP * D) + p * (2 * D), 2 * D)]
                        ins = v.tensor_tensor(rows, bank[2 + p][0:T, 0:2 * D], rows, ALU.add)
                    ins.then_inc(s["h_done"], 1)



def second_router_stage(core, a, weights):
    nc, bank, h = core.nc, core.bank, core.h
    PROBE = 24
    COLS = EXPERTS + PROBE + 1
    with ExitStack() as ctx:
        sb, sem, load_sem, raised = stage_tools(core, ctx)
        norm = Norm(sb, sem, "norm")
        w = sb("w", [128, 2, COLS])
        emb = sb("emb", [T, EXPERTS, PROBE])
        emb_square = sb("emb_square", [T, EXPERTS, PROBE])
        emb_norm = sb("emb_norm", [T, EXPERTS])
        emb_sum = sb("emb_sum", [T, EXPERTS])
        emb_inv = sb("emb_inv", [T, EXPERTS])
        mean_factor = sb("mean_factor", [T, EXPERTS])
        fatigue_energy = sb("fatigue_energy", [T, 2, EXPERTS])
        constant_bias = sb("constant_bias", [T, EXPERTS])
        b2 = sb("b2", [EXPERTS, D])
        xn = sb("xn", [T, GROUP, D + REST])
        xT = sb("xT", [128, 2, N])
        raw = sb("raw", [T, GROUP, COLS])
        probe_square = sb("probe_square", [T, GROUP, PROBE])
        probe_sum = sb("probe_sum", [T, GROUP])
        probe_norm = sb("probe_norm", [T, GROUP])
        probe_inv = sb("probe_inv", [T, GROUP])
        aligned = sb("aligned", [T, GROUP, EXPERTS, PROBE])
        align = sb("align", [T, GROUP, EXPERTS])
        term = sb("term", [T, GROUP, EXPERTS])
        gatesT = sb("gatesT", [EXPERTS, N])
        router = Router(sb, sem, "router")
        w_loaded, emb_sum_ready, emb_norm_ready = (load_sem(n) for n in ("w_loaded", "emb_sum_ready", "emb_norm_ready"))
        names = ("xn_ready", "xT_psum", "xT_ready", "xT_kept", "raw_psum", "raw_read", "probe_sum_ready",
                 "probe_norm_ready", "gates_ready", "gatesT_psum", "gatesT_ready", "bias_psum", "h_done")
        s = {n: sem(n) for n in names}

        with nc.Block() as block:
            @block.sync
            def _(sp):
                raise_to_start(sp, raised)
                raise_to_start(sp, weights.raised)
                sp.dma_start(w[:, 0, :], a["i_router"][0:HIGH, :]).then_inc(w_loaded, 16)
                sp.dma_start(w[0:REST, 1, :], a["i_router"][HIGH:D, :]).then_inc(w_loaded, 16)
                sp.dma_start(b2[:, :], a["i_b2"]).then_inc(w_loaded, 16)
                sp.dma_start(emb[:, :, :].rearrange("t e r -> t (e r)"),
                             a["i_emb"].to_broadcast([T, EXPERTS * PROBE])).then_inc(w_loaded, 16)
                sp.dma_start(fatigue_energy[:, :, :].rearrange("t a e -> t (a e)"),
                             a["i_fe"].to_broadcast([T, 2 * EXPERTS])).then_inc(w_loaded, 16)
                weights.load(sp, a, (0, 0))

            @block.gpsimd
            def _(pool):
                pool.wait_ge(emb_sum_ready, 1)
                pool.tensor_tensor(emb_norm[:, :], emb_sum[:, :], core.plus_half[0:T, 0:EXPERTS], ALU.pow
                                   ).then_inc(emb_norm_ready, 1)
                steps = weights.steps(pool, (0, 0))
                for i in range(TURNS):
                    norm_rstd(pool, core, norm, i)
                    pool.wait_ge(s["probe_sum_ready"], turn(i))
                    pool.tensor_tensor(probe_norm[:, :], probe_sum[:, :], core.plus_half[0:T, 0:GROUP], ALU.pow
                                       ).then_inc(s["probe_norm_ready"], 1)
                    next(steps)
                for _ in steps:
                    pass

            @block.tensor
            def _(pe):
                pe.wait_ge(w_loaded, 80)
                with pe.Fori(0, TURNS) as i:
                    pe.wait_ge(s["xn_ready"], turn(i))
                    transpose_for_experts(pe, core, bank[0:2], xn, s["xT_psum"])
                    pe.wait_ge(s["xT_ready"], turn(i))
                    pe.wait_ge(s["raw_read"], turn(i, 0))
                    for b in range(GROUP):
                        for c in range(2):
                            rows = slice(0, (HIGH, REST)[c])
                            mm = pe.matmul(bank[2][0:T, cols(b, COLS)], xT[rows, c, cols(b)], w[rows, c, :],
                                           start=(c == 0), stop=(c == 1))
                    mm.then_inc(s["raw_psum"], 1)
                    pe.wait_ge(s["gates_ready"], turn(i))
                    for b in range(GROUP):
                        mm = pe.transpose(bank[3][0:EXPERTS, cols(b)], router.gates[:, b, :], core.ident[0:T, 0:T])
                    mm.then_inc(s["gatesT_psum"], 1)
                    pe.wait_ge(s["gatesT_ready"], turn(i))
                    pe.wait_ge(s["h_done"], turn(i, 0))
                    for b in range(GROUP):
                        mm = pe.matmul(bank[4 + b // 2][0:T, cols(b % 2, D)], gatesT[:, cols(b)], b2[:, :],
                                       start=True, stop=True)
                    mm.then_inc(s["bias_psum"], 1)

            @block.scalar
            def _(act):
                with act.Fori(0, TURNS) as i:
                    act.wait_ge(s["raw_psum"], turn(i, 0))
                    act.wait_ge(s["xT_kept"], turn(i, 0))
                    act.wait_ge(s["xT_psum"], turn(i))
                    for c in range(2):
                        ins = act.activation(xT[:, c, :], bank[c][:, 0:N], ACT.Copy)
                    ins.then_inc(s["xT_ready"], 1)
                    router_scalar(act, router, i)
                    act.wait_ge(s["gatesT_psum"], turn(i))
                    act.activation(gatesT[:, :], bank[3][0:EXPERTS, 0:N], ACT.Copy).then_inc(s["gatesT_ready"], 1)

            @block.vector
            def _(v):
                v.wait_ge(w_loaded, 80)
                v.tensor_tensor(emb_square[:, :, :], emb[:, :, :], emb[:, :, :], ALU.mult)
                v.drain()
                v.tensor_reduce(emb_sum[:, :], emb_square[:, :, :], AX.X, ALU.add).then_inc(emb_sum_ready, 1)
                v.tensor_tensor(constant_bias[:, :], fatigue_energy[:, 1, :], fatigue_energy[:, 0, :], ALU.subtract)
                v.drain()
                v.tensor_scalar(constant_bias[:, :], constant_bias[:, :], 0.1, None, ALU.mult)
                v.wait_ge(emb_norm_ready, 1)
                v.tensor_scalar(mean_factor[:, :], emb_norm[:, :], 0.02, 0.02, ALU.mult, ALU.add)
                v.tensor_scalar(emb_inv[:, :], emb_norm[:, :], 1e-12, None, ALU.max)
                v.drain()
                v.reciprocal(emb_inv[:, :], emb_inv[:, :])
                v.drain()
                v.tensor_tensor(emb[:, :, :], emb[:, :, :],
                                emb_inv[:, :].unsqueeze(2).to_broadcast([T, EXPERTS, PROBE]), ALU.mult)
                v.drain()
                wide = [T, GROUP, EXPERTS]
                with v.Fori(0, TURNS) as i:
                    norm_statistics(v, norm, lambda b: sample_of(h, i, b))
                    v.wait_ge(norm.rstd_ready, turn(i))
                    for b in range(GROUP):
                        norm_apply(v, norm, lambda b: sample_of(h, i, b), lambda b: xn[:, b, 0:D], b)
                    duplicate_rest(v, xn).then_inc(s["xn_ready"], 1)
                    v.wait_ge(s["xT_ready"], turn(i))
                    keep_for_experts(v, core, xT, i).then_inc(s["xT_kept"], 1)
                    v.wait_ge(s["raw_psum"], turn(i))
                    v.tensor_copy(raw[:, :, :], bank[2][0:T, 0:GROUP * COLS]).then_inc(s["raw_read"], 1)
                    v.drain()
                    probe = raw[:, :, EXPERTS:EXPERTS + PROBE]
                    v.tensor_tensor(probe_square[:, :, :], probe, probe, ALU.mult)
                    v.drain()
                    v.tensor_reduce(probe_sum[:, :], probe_square[:, :, :], AX.X, ALU.add
                                    ).then_inc(s["probe_sum_ready"], 1)
                    for b in range(GROUP):
                        v.tensor_tensor(aligned[:, b, :, :],
                                        raw[:, b, EXPERTS:EXPERTS + PROBE].unsqueeze(1)
                                        .to_broadcast([T, EXPERTS, PROBE]), emb[:, :, :], ALU.mult)
                    v.drain()
                    for b in range(GROUP):
                        v.tensor_reduce(align[:, b, :], aligned[:, b, :, :], AX.X, ALU.add)
                    v.wait_ge(s["probe_norm_ready"], turn(i))
                    v.tensor_scalar(probe_inv[:, :], probe_norm[:, :], 1e-12, None, ALU.max)
                    v.drain()
                    v.reciprocal(probe_inv[:, :], probe_inv[:, :])
                    v.tensor_tensor(term[:, :, :], raw[:, :, COLS - 1:COLS].to_broadcast(wide),
                                    mean_factor[:, :].unsqueeze(1).to_broadcast(wide), ALU.mult)
                    v.drain()
                    v.tensor_tensor(router.logits[:, :, :], raw[:, :, 0:EXPERTS], term[:, :, :], ALU.add)
                    v.tensor_tensor(align[:, :, :], align[:, :, :],
                                    probe_inv[:, :].unsqueeze(2).to_broadcast(wide), ALU.mult)
                    v.drain()
                    v.scalar_tensor_tensor(out=router.logits[:, :, :], in0=align[:, :, :], scalar=0.02,
                                           in1=router.logits[:, :, :], op0=ALU.mult, op1=ALU.add)
                    v.drain()
                    v.tensor_tensor(router.logits[:, :, :], router.logits[:, :, :],
                                    constant_bias[:, :].unsqueeze(1).to_broadcast(wide), ALU.add)
                    v.drain()
                    router_vector(v, core, router, i).then_inc(s["gates_ready"], 1)
                    v.wait_ge(s["bias_psum"], turn(i))
                    for p in range(2):
                        rows = h[:, bass.ds(i * (GROUP * D) + p * (2 * D), 2 * D)]
                        ins = v.tensor_tensor(rows, bank[4 + p][0:T, 0:2 * D], rows, ALU.add)
                    ins.then_inc(s["h_done"], 1)


def store_stage(core, a):
    nc = core.nc
    with ExitStack() as ctx:
        _, _, load_sem, _ = stage_tools(core, ctx)
        stored = load_sem("stored")
        with nc.Block() as block:
            @block.sync
            def _(sp):
                sp.dma_start(a["out"].rearrange("s t d -> t s d"),
                             core.h[:, 0:SAMPLES * D].rearrange("t (s d) -> t s d", d=D)).then_inc(stored, 16)
                sp.wait_ge(stored, 16)


def build(nc, a):
    with ExitStack() as ctx:
        core = Core()
        core.nc, core.made = nc, 0
        core.h = ctx.enter_context(nc.sbuf_tensor("h", [T, (SAMPLES + GROUP) * D], F32))
        core.minus_half = ctx.enter_context(nc.sbuf_tensor("minus_half", [128, 48], F32))
        core.plus_half = ctx.enter_context(nc.sbuf_tensor("plus_half", [128, 48], F32))
        core.ones = ctx.enter_context(nc.sbuf_tensor("ones", [128, 128], F32))
        core.constants = {}
        core.z_hi, core.z_lo, core.z_rest = (
            ctx.enter_context(nc.sbuf_tensor(n, [128, SAMPLES * T], F32R)) for n in ("z_hi", "z_lo", "z_rest"))
        core.gates = ctx.enter_context(nc.sbuf_tensor("gates", [T, SAMPLES * EXPERTS], F32))
        for name, shape in (("ident", [128, 128]), ("mask16", [C, 6]), ("mask64", [128, 2]), ("iota", [128, 16])):
            core.constants[name] = ctx.enter_context(nc.sbuf_tensor("c_" + name, shape, F32))
        core.ident, core.iota = core.constants["ident"], core.constants["iota"]
        core.mask16, core.mask64 = core.constants["mask16"], core.constants["mask64"]
        core.psum = ctx.enter_context(nc.psum_tensor("psum", [128, 8, 512], F32))
        core.bank = [core.psum[:, i, :] for i in range(8)]

        def routed(second, router_stage):
            with ExitStack() as weights_ctx:
                weights = ExpertWeights(core, weights_ctx, second)
                router_stage(core, a, weights)
                experts_stage(core, a, weights)

        stages = [
            lambda: tokens_stage(core, a),
            lambda: wide_attention_stage(core, a),
            lambda: routed(False, first_heads_stage),
            lambda: ssm_stage(core, a),
            lambda: gated_heads_stage(core, a),
            lambda: position_attention_stage(core, a),
            lambda: int8_stage(core, a),
            lambda: rotary_heads_stage(core, a),
            lambda: routed(True, second_router_stage),
        ]
        for stage in stages:
            stage()
        store_stage(core, a)



def shape_constants(np):
    ident = np.eye(128, dtype=np.float32)
    mask16 = (np.arange(C)[:, None] // 16 == np.arange(6)[None, :]).astype(np.float32)
    mask64 = (np.arange(128)[:, None] // 64 == np.arange(2)[None, :]).astype(np.float32)
    iota = np.tile(np.arange(16, dtype=np.float32), (128, 1))
    spread = (np.arange(C)[:, None, None] == (np.arange(12)[:, None] * 8 + np.arange(128)[None, :] // 16)[None])
    gather = spread.transpose(2, 1, 0)
    average = (mask64 @ mask64.T) / np.float32(64)
    pos = np.arange(T, dtype=np.float32)[:, None]
    freqs = np.float32(10000.0) ** (-np.arange(0, D, 2, dtype=np.float32) / D)
    table = np.concatenate([np.sin(pos * freqs), np.cos(pos * freqs)], axis=1).astype(np.float32).T
    half, turned = 8, 4
    scale = np.float32(10000.0) ** (np.float32(2) * np.arange(turned, dtype=np.float32) / np.float32(16))
    angle = np.zeros((T, half), np.float32)
    angle[:, :turned] = pos / scale
    cos = np.tile(np.cos(angle).T, (2 * 6, 1))
    sin = np.tile(np.concatenate([-np.sin(angle).T, np.sin(angle).T]), (6, 1))
    angles = np.stack([cos / 4, sin / 4, cos, sin], axis=1).astype(np.float32)
    return {"f_table": table.reshape(2, C, T).swapaxes(0, 1), "h_angles": angles, "ident": ident, "mask16": mask16, "mask64": mask64, "iota": iota, "average": average,
            "spread": spread.astype(np.float32), "gather": gather.astype(np.float32)}


def kernel(**inputs):
    import numpy as np
    import concourse.bacc as bacc
    from concourse.bass_utils import run_bass_kernel_spmd as run

    x = {k: np.asarray(v) for k, v in inputs.items()}

    def chunks(w, k):
        return w.reshape(k, w.shape[0] // k, *w.shape[1:]).swapaxes(0, 1)

    def per_partition(b, k):
        return b.reshape(k, -1).T

    arrays = shape_constants(np)
    image = x["x"].reshape(SAMPLES, 3, 6, 16, 6, 16).transpose(0, 1, 2, 4, 3, 5).reshape(SAMPLES, IMG, 768)
    image = image.transpose(2, 0, 1)
    arrays["patches"] = chunks(image, PATCH_K)
    arrays["tok_w"] = chunks(x["L0_tok_W"].T, PATCH_K)
    arrays["tok_b"] = x["L0_tok_b"].reshape(1, D)
    arrays["cls"] = x["L0_tok_class_token"]
    arrays["pos"] = x["L0_tok_pos_embedding"]
    arrays["txt"] = x["txt"]
    arrays["a_wqkv"] = chunks(x["L0_attn_W_qkv"], 2)
    arrays["a_bqk"] = per_partition(x["L0_attn_b_qkv"][0:2 * D], 4)
    arrays["a_bv"] = x["L0_attn_b_qkv"][2 * D:].reshape(1, D)
    arrays["b_wqkv"] = chunks(x["L0_ffn_Wqkv"], 2)
    arrays["b_wproj"] = chunks(x["L0_ffn_Wproj"], 2)
    arrays["b_wrouter"] = x["L0_ffn_Wrouter"]
    arrays["b_affine"] = np.concatenate([per_partition(x["L0_ffn_" + n], 2) for n in ("ln1_g", "ln1_b")], axis=1)
    arrays["b_affine2"] = np.stack([part for v in (x["L0_ffn_ln2_g"], x["L0_ffn_ln2_b"])
                                    for part in (v[:HIGH], np.tile(v[HIGH:], 2))], axis=1)
    arrays["b_w1"] = x["L0_ffn_W1"]
    arrays["b_w2"] = x["L0_ffn_W2"].reshape(EXPERTS, FC, 128, D).transpose(0, 2, 1, 3)
    ssm = {k[8:]: v for k, v in x.items() if k.startswith("L1_attn_")}
    arrays["c_wi"] = chunks(ssm["Wi"], 2)
    arrays["c_wdt"] = chunks(ssm["Wdt"], 2)
    arrays["c_wb"] = chunks(ssm["WB"], 2)
    arrays["c_wc"] = chunks(ssm["WC"], 2)
    arrays["c_wo"] = chunks(ssm["Wo"], 2)
    arrays["c_bo"] = ssm["bo"].reshape(1, D)
    arrays["c_channel"] = np.concatenate(
        [v.reshape(2, C, -1).swapaxes(0, 1) for v in (ssm["bi"][:D], ssm["bi"][D:], ssm["bconv"], ssm["bdt"], ssm["D"],
                                                      ssm["Wconv"])], axis=2)
    arrays["c_rows"] = np.stack([v.reshape(24, 128).T for v in (ssm["A_log"], ssm["bB"], ssm["bC"])], axis=1)
    gh = {k[7:]: v for k, v in x.items() if k.startswith("L1_ffn_")}
    arrays["e_wqkvg"] = np.concatenate([gh["qkv_w"], gh["wg_w"], gh["wg0_w"], gh["wg1_w"]], axis=1)
    arrays["e_wproj"] = chunks(gh["proj_w"], 6)
    arrays["e_bv"] = gh["qkv_b"][1536:].reshape(1, 768)
    arrays["e_bqk"] = gh["qkv_b"][:1536].reshape(12, 128).T
    arrays["e_bproj"] = gh["proj_b"].reshape(1, D)
    arrays["e_affine"] = np.stack([np.tile(gh[n], 2) for n in ("q_norm_w", "q_norm_b", "k_norm_w", "k_norm_b")], axis=1)
    arrays["f_wv"] = chunks(x["L2_attn_Wv"].T, 2)
    arrays["f_wo"] = x["L2_attn_Wo"].T
    arrays["g_w"] = np.ascontiguousarray(chunks(x["L2_ffn_weight_t"], 2)).reshape(C, 2 * D).view(np.int32)
    arrays["g_bias"] = x["L2_ffn_bias"].reshape(1, D)
    rh = {k[8:]: v for k, v in x.items() if k.startswith("L3_attn_")}
    exchange = (np.arange(D) // 16) * 16 + (np.arange(D) + 8) % 16
    arrays["h_w"] = chunks(np.concatenate([rh["wq"].T, rh["wq"].T[:, exchange], rh["wk"].T, rh["wk"].T[:, exchange],
                                           rh["wv"].T], axis=1), 2)
    arrays["h_bqk"] = np.concatenate([per_partition(b, 2) for b in (rh["bq"], rh["bq"][exchange], rh["bk"],
                                                                    rh["bk"][exchange])], axis=1)
    arrays["h_bv"] = rh["bv"].reshape(1, D)
    arrays["h_wo"] = chunks(rh["wo"].T, 2)
    arrays["h_bo"] = rh["bo"].reshape(1, D)
    ex = {k[7:]: v for k, v in x.items() if k.startswith("L3_ffn_")}
    arrays["i_router"] = np.concatenate([ex["router_w"].T, ex["probe_w"].T,
                                         np.full((D, 1), 1.0 / D, np.float32)], axis=1)
    arrays["i_emb"] = ex["router_emb"].reshape(1, -1)
    arrays["i_fe"] = np.concatenate([ex["fatigue"], ex["energy"]]).reshape(1, -1)
    arrays["i_b2"] = ex["b2"]
    arrays["i_b1"] = ex["b1"].reshape(EXPERTS, FC, 128).transpose(0, 2, 1)
    arrays["i_mix"] = np.stack([ex["m_gate1"], ex["m_gate2"]], axis=1)
    for n, part in enumerate(("w_fast", "w_slow", "h_fast")):
        arrays[f"i_w1_{n}"] = ex[part + "1"]
        arrays[f"i_w2_{n}"] = ex[part + "2"].reshape(EXPERTS, FC, 128, D).transpose(0, 2, 1, 3)
    arrays = {k: np.ascontiguousarray(v) for k, v in arrays.items()}

    nc = bacc.Bacc("TRN2", target_bir_lowering=False, num_devices=1)
    args = {k: nc.dram_tensor(k + "_dram", v.shape, mybir.dt.from_np(v.dtype), kind="ExternalInput").ap()
            for k, v in arrays.items()}
    args["out"] = nc.dram_tensor("out_dram", (SAMPLES, T, D), F32, kind="ExternalOutput").ap()
    build(nc, args)
    r = run(nc, [{k + "_dram": v for k, v in arrays.items()}], core_ids=[0])
    return r.results[0]["out_dram"]
```

```python
from contextlib import ExitStack

import concourse.bass as bass
from concourse import mybir

F32 = mybir.dt.float32
F32R = mybir.dt.float32r
BF16 = mybir.dt.bfloat16
U32 = mybir.dt.uint32
I8 = mybir.dt.int8
I32 = mybir.dt.int32
ALU = mybir.AluOpType
ACT = mybir.ActivationFunctionType
AX = mybir.AxisListType

SAMPLES = 16
IMG = 36
FRONT = IMG + 1
TXT = 77
T = FRONT + TXT
D = 192
C = D // 2
GROUP = 4
TURNS = SAMPLES // GROUP
N = GROUP * T
PATCH_K = 768 // 128
EPS = 1e-5
HEADS = 12
EXPERTS = 8
FF = 768
FC = FF // 128


START = 5


def turn(i, n=1, per=1):
    return i * per + n + START


def cols(b, width=T):
    return slice(b * width, (b + 1) * width)


class Core:
    pass


def stage_tools(core, ctx):
    nc = core.nc

    def sb(name, shape, dtype=F32):
        core.made += 1
        return ctx.enter_context(nc.sbuf_tensor(f"{name}_{core.made}", shape, dtype))

    raised, every = [], []
    ctx.callback(lambda: (nc.clear_and_free_semaphores(every), nc.all_engine_barrier()))

    def load_sem(name):
        core.made += 1
        every.append(nc.alloc_semaphore(f"{name}_{core.made}"))
        return every[-1]

    def sem(name):
        raised.append(load_sem(name))
        return raised[-1]

    return sb, sem, load_sem, raised


def raise_to_start(sp, raised):
    for s in raised:
        sp.sem_inc(s, START)


def sample_of(h, i, b):
    return h[:, bass.ds(i * (GROUP * D) + b * D, D)]



class Norm:

    def __init__(self, sb, sem, tag):
        self.stats = sb(f"{tag}_stats", [T, GROUP, 6])
        self.mean_var = sb(f"{tag}_mean_var", [T, GROUP, 2])
        self.var_eps = sb(f"{tag}_var_eps", [T, GROUP])
        self.rstd = sb(f"{tag}_rstd", [T, GROUP])
        self.var_ready = sem(f"{tag}_var_ready")
        self.rstd_ready = sem(f"{tag}_rstd_ready")


def norm_statistics(v, norm, source):
    for b in range(GROUP):
        v.bn_stats(norm.stats[:, b, :], source(b))
    v.drain()
    for b in range(GROUP):
        v.bn_aggr(norm.mean_var[:, b, :], norm.stats[:, b, :])
    v.drain()
    v.tensor_scalar(norm.var_eps[:, :], norm.mean_var[:, :, 1], EPS, None, ALU.add).then_inc(norm.var_ready, 1)


def add_bias(v, h, i, bias):
    rows = h[:, bass.ds(i * (GROUP * D), GROUP * D)].rearrange("t (b d) -> t b d", b=GROUP)
    v.tensor_tensor(rows, rows, bias[:, :].unsqueeze(1).to_broadcast([T, GROUP, D]), ALU.add)
    v.drain()


def norm_rstd(pool, core, norm, i):
    pool.wait_ge(norm.var_ready, turn(i))
    pool.tensor_tensor(norm.rstd[:, :], norm.var_eps[:, :], core.minus_half[0:T, 0:GROUP],
                       ALU.pow).then_inc(norm.rstd_ready, 1)


def norm_apply(v, norm, source, target, b):
    return v.tensor_scalar(target(b), source(b), norm.mean_var[:, b, 0:1], norm.rstd[:, b:b + 1],
                           ALU.subtract, ALU.mult)


def transpose_group(pe, core, banks, source, done):
    for c in range(2):
        for b in range(GROUP):
            mm = pe.transpose(banks[c][0:C, cols(b)], source[:, b, c * C:(c + 1) * C], core.ident[0:T, 0:T])
    mm.then_inc(done, 1)



HIGH = 128
REST = D - HIGH


def duplicate_rest(v, source):
    v.drain()
    return v.tensor_copy(source[:, :, D:D + REST], source[:, :, HIGH:D])


def transpose_for_experts(pe, core, banks, source, done):
    for c in range(2):
        for b in range(GROUP):
            mm = pe.transpose(banks[c][:, cols(b)], source[:, b, c * HIGH:(c + 1) * HIGH], core.ident[0:T, 0:T])
    mm.then_inc(done, 1)


def keep_for_experts(v, core, zT, i):
    at = bass.ds(i * N, N)
    v.tensor_scalar(core.z_hi[:, at], zT[:, 0, :], 1.0, None, ALU.mult)
    v.tensor_scalar(core.z_rest[:, at], zT[:, 1, :], 1.0, None, ALU.mult)
    v.drain()
    v.tensor_tensor(core.z_lo[:, at], zT[:, 0, :], core.z_hi[:, at].bitcast(F32), ALU.subtract)
    return v.tensor_tensor(core.z_rest[REST:128, at], zT[REST:128, 1, :], core.z_rest[REST:128, at].bitcast(F32),
                           ALU.subtract)


class SplitWeights:

    def __init__(self, sb, name, columns):
        self.raw = sb(f"{name}_raw", [128, 2, columns])
        self.hi = sb(f"{name}_hi", [128, 2, columns], F32R)
        self.lo = sb(f"{name}_lo", [128, columns], F32R)
        self.lo_rest = sb(f"{name}_lo_rest", [REST, columns], F32R)

    def load(self, sp, source, loaded):
        columns = source.shape[-1]
        sp.dma_start(self.raw[:, 0, :], source[0:HIGH, :]).then_inc(loaded, 16)
        sp.dma_start(self.raw[:, 1, :], source[HIGH:D, :].unsqueeze(0).to_broadcast([2, REST, columns])
                     ).then_inc(loaded, 16)

    def high(self, act):
        return act.activation(self.hi[:, :, :], self.raw[:, :, :], ACT.Copy)

    def low(self, v):
        v.tensor_tensor(self.lo[:, :], self.raw[:, 0, :], self.hi[:, 0, :].bitcast(F32), ALU.subtract)
        return v.tensor_tensor(self.lo_rest[:, :], self.raw[0:REST, 1, :], self.hi[0:REST, 1, :].bitcast(F32),
                               ALU.subtract)


class SplitColumns:

    def __init__(self, core):
        self.hi, self.lo, self.rest = (core.z_hi[:, k * N:(k + 1) * N] for k in range(3))

    def high(self, act, banks):
        act.activation(self.hi[:, :], banks[0][:, 0:N], ACT.Copy)
        return act.activation(self.rest[:, :], banks[1][:, 0:N], ACT.Copy)

    def low(self, v, banks):
        v.tensor_tensor(self.lo[:, :], banks[0][:, 0:N], self.hi[:, :].bitcast(F32), ALU.subtract)
        return v.tensor_tensor(self.rest[REST:128, :], banks[1][REST:128, 0:N], self.rest[REST:128, :].bitcast(F32),
                               ALU.subtract)


def product_by_columns(pe, out, w, m, x):
    pe.matmul(out, w.hi[:, 0, m], x.hi[:, :], start=True, stop=False)
    pe.matmul(out, w.hi[:, 0, m], x.lo[:, :], start=False, stop=False)
    pe.matmul(out, w.lo[:, m], x.hi[:, :], start=False, stop=False)
    pe.matmul(out, w.hi[:, 1, m], x.rest[:, :], start=False, stop=False)
    return pe.matmul(out, w.lo_rest[:, m], x.rest[0:REST, :], start=False, stop=True)


def product_by_rows(pe, out, x, t, w, m, more=False):
    pe.matmul(out, x.hi[:, t], w.hi[:, 0, m], start=True, stop=False)
    pe.matmul(out, x.hi[:, t], w.lo[:, m], start=False, stop=False)
    pe.matmul(out, x.lo[:, t], w.hi[:, 0, m], start=False, stop=False)
    pe.matmul(out, x.rest[:, t], w.hi[:, 1, m], start=False, stop=False)
    return pe.matmul(out, x.rest[0:REST, t], w.lo_rest[:, m], start=False, stop=not more)



def tokens_stage(core, a):
    nc = core.nc
    with ExitStack() as ctx:
        sb, sem, load_sem, raised = stage_tools(core, ctx)
        patches = [sb("patches", [128, PATCH_K, GROUP, FRONT]) for _ in range(2)]
        w = sb("w_patch", [128, PATCH_K, D])
        front = sb("front", [FRONT, D])
        pos = sb("pos", [FRONT, D])
        front_pos = sb("front_pos", [FRONT, D])
        const_loaded, text_loaded, w_loaded = (load_sem(n) for n in ("const_loaded", "text_loaded", "w_loaded"))
        patch_loaded = [load_sem("patch_loaded") for _ in range(2)]
        cleared = load_sem("cleared")
        tokens_psum, tokens_added = sem("tokens_psum"), sem("tokens_added")

        with nc.Block() as block:
            @block.sync
            def _(sp):
                raise_to_start(sp, raised)
                sp.dma_start(w[:, :, :], a["tok_w"]).then_inc(w_loaded, 16)
                sp.dma_start(front[1:FRONT, :], a["tok_b"].to_broadcast([IMG, D])).then_inc(w_loaded, 16)
                sp.dma_start(front[0:1, :], a["cls"]).then_inc(w_loaded, 16)
                sp.dma_start(pos[:, :], a["pos"]).then_inc(w_loaded, 16)
                sp.wait_ge(cleared, 1)
                with sp.Fori(0, TURNS // 2) as pair:
                    for n in range(2):
                        i = pair * 2 + n
                        sp.wait_ge(tokens_psum, turn(i, -1))
                        for k in range(PATCH_K):
                            sp.dma_start(patches[n][:, k, :, 1:FRONT],
                                         a["patches"][:, k, bass.ds(i * GROUP, GROUP), :]
                                         ).then_inc(patch_loaded[n], 16)

            @block.scalar
            def _(act):
                act.dma_start(core.h[FRONT:T, 0:SAMPLES * D].rearrange("t (s d) -> t s d", d=D),
                              a["txt"].rearrange("s t d -> t s d")).then_inc(text_loaded, 16)
                for name, tile in core.constants.items():
                    act.dma_start(tile[tuple(slice(None) for _ in tile.shape)], a[name]).then_inc(const_loaded, 16)
                act.wait_ge(text_loaded, 16)
                act.wait_ge(const_loaded, 16 * len(core.constants))

            @block.gpsimd
            def _(pool):
                pool.memset(core.minus_half[:, :], -0.5)
                pool.memset(core.plus_half[:, :], 0.5)
                pool.memset(core.ones[:, :], 1.0)
                pool.memset(core.h[:, SAMPLES * D:(SAMPLES + GROUP) * D], 0.0)
                pool.memset(patches[0][:, :, :, 0:1], 0.0)
                pool.memset(patches[1][:, :, :, 0:1], 0.0).then_inc(cleared, 1)

            @block.tensor
            def _(pe):
                pe.wait_ge(w_loaded, 64)
                pe.wait_ge(cleared, 1)
                with pe.Fori(0, TURNS // 2) as pair:
                    for n in range(2):
                        i = pair * 2 + n
                        pe.wait_ge(patch_loaded[n], pair * (16 * PATCH_K) + 16 * PATCH_K)
                        pe.wait_ge(tokens_added, turn(i, -1))
                        for b in range(GROUP):
                            for k in range(PATCH_K):
                                mm = pe.matmul(core.bank[n * GROUP + b][0:FRONT, 0:D], patches[n][:, k, b, :],
                                               w[:, k, :], start=(k == 0), stop=(k == PATCH_K - 1))
                        mm.then_inc(tokens_psum, 1)

            @block.vector
            def _(v):
                v.wait_ge(w_loaded, 64)
                v.tensor_tensor(front_pos[:, :], front[:, :], pos[:, :], ALU.add)
                v.drain()
                with v.Fori(0, TURNS // 2) as pair:
                    for n in range(2):
                        i = pair * 2 + n
                        v.wait_ge(tokens_psum, turn(i))
                        for b in range(GROUP):
                            add = v.tensor_tensor(core.h[0:FRONT, bass.ds(i * (GROUP * D) + b * D, D)],
                                                  core.bank[n * GROUP + b][0:FRONT, 0:D], front_pos[:, :], ALU.add)
                        add.then_inc(tokens_added, 1)



def wide_attention_stage(core, a):
    nc, bank, h = core.nc, core.bank, core.h
    scale = D ** -0.5
    with ExitStack() as ctx:
        sb, sem, load_sem, raised = stage_tools(core, ctx)
        norm = Norm(sb, sem, "norm")
        w = SplitWeights(sb, "w_qkv", 3 * D)
        bqk = sb("b_qk", [C, 4])
        bqk_s = sb("b_qk_scaled", [C, 4])
        bv = sb("b_v", [1, D])
        xn = sb("xn", [T, GROUP, D + REST])
        xT = SplitColumns(core)
        qkT = sb("qkT", [C, 4, N])
        vals = sb("vals", [T, GROUP, D])
        probs = sb("probs", [T, GROUP, T])
        probsT = sb("probsT", [T, GROUP, T])
        negmax = sb("negmax", [T, GROUP])
        total = sb("total", [T, GROUP])
        inv = sb("inv", [T, GROUP])
        w_loaded, w_high, w_split = (load_sem(n) for n in ("w_loaded", "w_high", "w_split"))
        bias_scaled = load_sem("bias_scaled")
        names = ("xn_ready", "xT_psum", "xT_high", "xT_split", "qk_psum", "qk_ready", "v_psum", "v_ready", "scores_psum",
                 "max_ready", "probs_ready", "probsT_psum", "probsT_ready", "context_psum", "h_done")
        s = {n: sem(n) for n in names}

        with nc.Block() as block:
            @block.sync
            def _(sp):
                raise_to_start(sp, raised)
                w.load(sp, a["a_wqkv"], w_loaded)
                sp.dma_start(bqk[:, :], a["a_bqk"]).then_inc(w_loaded, 16)
                sp.dma_start(bv[:, :], a["a_bv"]).then_inc(w_loaded, 16)

            @block.gpsimd
            def _(pool):
                norm_rstd(pool, core, norm, 0)
                with pool.Fori(0, TURNS) as i:
                    norm_rstd(pool, core, norm, i + 1)

            @block.tensor
            def _(pe):
                pe.wait_ge(w_loaded, 64)
                pe.wait_ge(w_split, 1)
                with pe.Fori(0, TURNS) as i:
                    pe.wait_ge(s["probs_ready"], turn(i, 0))
                    pe.wait_ge(s["probsT_ready"], turn(i, 0))
                    pe.wait_ge(s["xn_ready"], turn(i))
                    transpose_for_experts(pe, core, bank[0:2], xn, s["xT_psum"])
                    pe.wait_ge(s["h_done"], turn(i, 0))
                    pe.wait_ge(s["xT_split"], turn(i))
                    for j in range(4):
                        mm = product_by_columns(pe, bank[2 + j][0:C, 0:N], w, slice(j * C, (j + 1) * C), xT)
                    mm.then_inc(s["qk_psum"], 1)
                    pe.wait_ge(s["v_ready"], turn(i, 0))
                    for b in range(GROUP):
                        out = bank[6 + b // 2][0:T, (b % 2) * D:(b % 2 + 1) * D]
                        product_by_rows(pe, out, xT, cols(b), w, slice(2 * D, 3 * D), more=True)
                        mm = pe.matmul(out, core.ones[0:1, 0:T], bv[:, :], start=False, stop=True)
                    mm.then_inc(s["v_psum"], 1)
                    pe.wait_ge(s["qk_ready"], turn(i))
                    for b in range(GROUP):
                        for c in range(2):
                            mm = pe.matmul(bank[0][0:T, cols(b)], qkT[:, c, cols(b)], qkT[:, 2 + c, cols(b)],
                                           start=(c == 0), stop=(c == 1))
                    mm.then_inc(s["scores_psum"], 1)
                    pe.wait_ge(s["probs_ready"], turn(i))
                    for b in range(GROUP):
                        mm = pe.transpose(bank[1][0:T, cols(b)], probs[:, b, :], core.ident[0:T, 0:T])
                    mm.then_inc(s["probsT_psum"], 1)
                    pe.wait_ge(s["v_ready"], turn(i))
                    pe.wait_ge(s["probsT_ready"], turn(i))
                    for b in range(GROUP):
                        mm = pe.matmul(bank[2 + b // 2][0:T, (b % 2) * D:(b % 2 + 1) * D], probsT[:, b, :],
                                       vals[:, b, :], start=True, stop=True)
                    mm.then_inc(s["context_psum"], 1)

            @block.scalar
            def _(act):
                act.wait_ge(w_loaded, 64)
                w.high(act).then_inc(w_high, 1)
                act.wait_ge(bias_scaled, 1)
                with act.Fori(0, TURNS) as i:
                    act.wait_ge(s["v_psum"], turn(i, 0))
                    act.wait_ge(s["xT_psum"], turn(i))
                    xT.high(act, bank[0:2]).then_inc(s["xT_high"], 1)
                    act.wait_ge(s["scores_psum"], turn(i, 0))
                    act.wait_ge(s["qk_psum"], turn(i))
                    for j in range(4):
                        ins = act.activation(qkT[:, j, :], bank[2 + j][0:C, 0:N], ACT.Identity,
                                             bias=bqk_s[:, j:j + 1], scale=scale if j < 2 else 1.0)
                    ins.then_inc(s["qk_ready"], 1)
                    act.wait_ge(s["probsT_psum"], turn(i, 0))
                    act.wait_ge(s["h_done"], turn(i, 0))
                    act.wait_ge(s["max_ready"], turn(i))
                    for b in range(GROUP):
                        ins = act.activation(probs[:, b, :], bank[0][0:T, cols(b)], ACT.Exp,
                                             bias=negmax[:, b:b + 1], accum_out=total[:, b:b + 1])
                    ins.then_inc(s["probs_ready"], 1)
                    act.wait_ge(s["context_psum"], turn(i, 0))
                    act.wait_ge(s["probsT_psum"], turn(i))
                    act.activation(probsT[:, :, :], bank[1][0:T, 0:N], ACT.Copy).then_inc(s["probsT_ready"], 1)

            @block.vector
            def _(v):
                def normed(i):
                    norm_statistics(v, norm, lambda b: sample_of(h, i, b))
                    v.wait_ge(s["xT_psum"], turn(i, 0))
                    v.wait_ge(norm.rstd_ready, turn(i))
                    for b in range(GROUP):
                        norm_apply(v, norm, lambda b: sample_of(h, i, b), lambda b: xn[:, b, 0:D], b)
                    duplicate_rest(v, xn).then_inc(s["xn_ready"], 1)

                normed(0)
                v.wait_ge(w_loaded, 64)
                v.tensor_scalar(bqk_s[:, 0:2], bqk[:, 0:2], scale, None, ALU.mult)
                v.tensor_copy(bqk_s[:, 2:4], bqk[:, 2:4]).then_inc(bias_scaled, 1)
                v.wait_ge(w_high, 1)
                w.low(v).then_inc(w_split, 1)
                with v.Fori(0, TURNS) as i:
                    v.wait_ge(s["xT_high"], turn(i))
                    xT.low(v, bank[0:2]).then_inc(s["xT_split"], 1)
                    v.wait_ge(s["context_psum"], turn(i, 0))
                    v.wait_ge(s["v_psum"], turn(i))
                    for p in range(2):
                        ins = v.tensor_copy(vals[:, 2 * p:2 * p + 2, :], bank[6 + p][0:T, 0:2 * D])
                    ins.then_inc(s["v_ready"], 1)
                    v.wait_ge(s["probs_ready"], turn(i, 0))
                    v.wait_ge(s["scores_psum"], turn(i))
                    v.tensor_reduce(negmax[:, :], bank[0][0:T, 0:N].rearrange("q (b k) -> q b k", b=GROUP),
                                    AX.X, ALU.max, negate=True).then_inc(s["max_ready"], 1)
                    normed(i + 1)
                    v.wait_ge(s["probs_ready"], turn(i))
                    v.reciprocal(inv[:, :], total[:, :])
                    v.drain()
                    v.wait_ge(s["context_psum"], turn(i))
                    for b in range(GROUP):
                        ins = v.scalar_tensor_tensor(out=sample_of(h, i, b),
                                                     in0=bank[2 + b // 2][0:T, (b % 2) * D:(b % 2 + 1) * D],
                                                     scalar=inv[:, b:b + 1], in1=sample_of(h, i, b),
                                                     op0=ALU.mult, op1=ALU.add)
                    ins.then_inc(s["h_done"], 1)



UNITS = 2 * GROUP
UNIT_HEADS = HEADS // 2


class Heads:

    def __init__(self, core, sb, sem, head_dim, mask, context_first=False):
        self.context_first = context_first
        self.core, self.head_dim, self.mask = core, head_dim, mask
        self.rows = mask.shape[0]
        self.per_chunk = self.rows // head_dim
        self.chunks = HEADS // self.per_chunk
        self.kblock = sb("kblock", [self.rows, GROUP, self.chunks, self.per_chunk, T])
        self.vals = sb("vals", [T, GROUP, HEADS, head_dim + 1])
        self.negmax = sb("negmax", [T, 2, UNIT_HEADS])
        self.probs = sb("probs", [T, 2, UNIT_HEADS, T])
        self.probsT = sb("probsT", [T, 2, UNIT_HEADS, T])
        self.inv = sb("inv", [T, 2, UNIT_HEADS])
        self.kblock_ready = sem("kblock_ready")
        self.scores_psum = sem("scores_psum")
        self.shifted_ready = sem("shifted_ready")
        self.probs_ready = sem("probs_ready")
        self.probsT_psum = sem("probsT_psum")
        self.probsT_ready = sem("probsT_ready")
        self.context_psum = sem("context_psum")
        self.context_done = sem("context_done")

    def pair(self, first):
        return self.core.psum[0:T, first:first + 2, 0:3 * T].rearrange("t a (n k) -> t a n k", n=3)

    def context(self, u):
        width = self.head_dim + 1
        return self.core.bank[6 + u % 2][0:T, 0:UNIT_HEADS * width].rearrange("t (n d) -> t n d", d=width)


def paired(buffer):
    return buffer.rearrange("t (a n) k -> t a n k", a=2)


def heads_pool(pool, att, i, kT, b):
    for c in range(att.chunks):
        shape = [att.rows, att.per_chunk, T]
        ins = pool.tensor_tensor(att.kblock[:, b, c, :, :],
                                 kT[:, c, cols(b)].unsqueeze(1).to_broadcast(shape),
                                 att.mask[:, :].unsqueeze(2).to_broadcast(shape), ALU.mult)
    ins.then_inc(att.kblock_ready, 1)


def heads_tensor(pe, att, i, qT):
    core, per = att.core, att.per_chunk

    def scores(u):
        b, half = u // 2, u % 2
        pe.wait_ge(att.kblock_ready, turn(i, b + 1, GROUP))
        pe.wait_ge(att.shifted_ready, turn(i, u - 1, UNITS))
        first = half * UNIT_HEADS
        while first < (half + 1) * UNIT_HEADS:
            c = first // per
            last = min((c + 1) * per, (first // 3 + 1) * 3)
            mm = pe.matmul(core.bank[2 * (u % 2) + first // 3 % 2][0:T, first % 3 * T:((last - 1) % 3 + 1) * T],
                           qT[:, c, cols(b)], att.kblock[:, b, c, first - c * per:last - c * per, :],
                           start=True, stop=True)
            first = last
        mm.then_inc(att.scores_psum, 1)

    def transposes(u):
        pe.wait_ge(att.probsT_ready, turn(i, u, UNITS))
        pe.wait_ge(att.probs_ready, turn(i, u + 1, UNITS))
        for n in range(UNIT_HEADS):
            mm = pe.transpose(core.bank[4 + n // 3][0:T, cols(n % 3)], att.probs[:, u % 2, n, :],
                              core.ident[0:T, 0:T])
        mm.then_inc(att.probsT_psum, 1)

    def context(u):
        pe.wait_ge(att.context_done, turn(i, u - 1, UNITS))
        pe.wait_ge(att.probsT_ready, turn(i, u + 1, UNITS))
        for n in range(UNIT_HEADS):
            mm = pe.matmul(att.context(u)[:, n, :], att.probsT[:, u % 2, n, :],
                           att.vals[:, u // 2, u % 2 * UNIT_HEADS + n, :], start=True, stop=True)
        mm.then_inc(att.context_psum, 1)

    scores(0)
    scores(1)
    transposes(0)
    for u in range(UNITS):
        if u + 2 < UNITS:
            scores(u + 2)
        if att.context_first:
            context(u)
        if u + 1 < UNITS:
            transposes(u + 1)
        if not att.context_first:
            context(u)


def heads_scalar(act, att, i):
    def exponentials(u):
        act.wait_ge(att.shifted_ready, turn(i, u + 1, UNITS))
        act.activation(att.probs[:, u % 2, :, :], att.probs[:, u % 2, :, :], ACT.Exp).then_inc(att.probs_ready, 1)

    exponentials(0)
    exponentials(1)
    for u in range(UNITS):
        if att.context_first and u >= 2:
            exponentials(u)
        act.wait_ge(att.context_psum, turn(i, u - 1, UNITS))
        act.wait_ge(att.probsT_psum, turn(i, u + 1, UNITS))
        act.activation(paired(att.probsT[:, u % 2, :, :]), att.pair(4), ACT.Copy).then_inc(att.probsT_ready, 1)
        if not att.context_first and u + 2 < UNITS:
            exponentials(u + 2)


def heads_vector(v, att, i, rescale):
    def shift(u):
        v.wait_ge(att.scores_psum, turn(i, u + 1, UNITS))
        v.tensor_reduce(att.negmax[:, u % 2, :].rearrange("t (a n) -> t a n", a=2), att.pair(2 * (u % 2)),
                        AX.X, ALU.max, negate=True)
        v.drain()
        v.wait_ge(att.probsT_psum, turn(i, u - 1, UNITS))
        v.tensor_tensor(paired(att.probs[:, u % 2, :, :]), att.pair(2 * (u % 2)),
                        att.negmax[:, u % 2, :].rearrange("t (a n) -> t a n", a=2).unsqueeze(3)
                        .to_broadcast([T, 2, 3, T]), ALU.add).then_inc(att.shifted_ready, 1)

    shift(0)
    shift(1)
    for u in range(UNITS):
        if u + 2 < UNITS:
            shift(u + 2)
        v.wait_ge(att.context_psum, turn(i, u + 1, UNITS))
        v.reciprocal(att.inv[:, u % 2, :], att.context(u)[:, :, att.head_dim])
        v.drain()
        rescale(u, att.inv[:, u % 2, :]).then_inc(att.context_done, 1)



class TopTwo:
    def __init__(self, sb, width, tag, samples=GROUP):
        self.width, self.samples = width, samples
        self.best = sb(f"{tag}_best", [T, samples, 8])
        self.where = sb(f"{tag}_where", [T, samples, 8], U32)
        self.index = sb(f"{tag}_index", [T, samples, 8])
        self.hot = sb(f"{tag}_hot", [T, 2, samples, width])


def top_two_hot(v, core, top, logits):
    shape = [T, top.samples, top.width]
    for b in range(top.samples):
        v.max(top.best[:, b, :], logits[:, b, :])
    v.drain()
    for b in range(top.samples):
        v.max_index(top.where[:, b, :], top.best[:, b, :], logits[:, b, :])
    v.drain()
    v.tensor_copy(top.index[:, :, :], top.where[:, :, :])
    v.drain()
    for k in range(2):
        v.tensor_tensor(top.hot[:, k, :, :],
                        core.iota[0:T, 0:top.width].unsqueeze(1).to_broadcast(shape),
                        top.index[:, :, k:k + 1].to_broadcast(shape), ALU.is_equal)
    v.drain()


class Router:

    def __init__(self, sb, sem, tag, samples=GROUP):
        self.samples = samples
        self.top = TopTwo(sb, EXPERTS, tag, samples)
        self.logits = sb(f"{tag}_logits", [T, samples, EXPERTS])
        self.gap = sb(f"{tag}_gap", [T, samples])
        self.ratio = sb(f"{tag}_ratio", [T, samples])
        self.weight = sb(f"{tag}_weight", [T, 2, samples])
        self.gap_ready = sem(f"{tag}_gap_ready")
        self.ratio_ready = sem(f"{tag}_ratio_ready")


def router_vector(v, core, r, i):
    shape = [T, r.samples, EXPERTS]
    top_two_hot(v, core, r.top, r.logits)
    v.tensor_tensor(r.gap[:, :], r.top.best[:, :, 1], r.top.best[:, :, 0], ALU.subtract).then_inc(r.gap_ready, 1)
    v.wait_ge(r.ratio_ready, turn(i))
    v.tensor_scalar(r.gap[:, :], r.ratio[:, :], 1.0, None, ALU.add)
    v.drain()
    v.reciprocal(r.weight[:, 0, :], r.gap[:, :])
    v.drain()
    v.tensor_tensor(r.weight[:, 1, :], r.weight[:, 0, :], r.ratio[:, :], ALU.mult)
    v.drain()
    for k in range(2):
        v.tensor_tensor(r.top.hot[:, k, :, :], r.top.hot[:, k, :, :],
                        r.weight[:, k, :].unsqueeze(2).to_broadcast(shape), ALU.mult)
    v.drain()
    at = slice(None) if r.samples == SAMPLES else bass.ds(i * (GROUP * EXPERTS), GROUP * EXPERTS)
    return v.tensor_tensor(core.gates[:, at], r.top.hot[:, 0, :, :].rearrange("t b e -> t (b e)"),
                           r.top.hot[:, 1, :, :].rearrange("t b e -> t (b e)"), ALU.add)


def router_scalar(act, r, i):
    act.wait_ge(r.gap_ready, turn(i))
    act.activation(r.ratio[:, :], r.gap[:, :], ACT.Exp).then_inc(r.ratio_ready, 1)



def first_heads_stage(core, a, weights):
    nc, bank, h = core.nc, core.bank, core.h
    with ExitStack() as ctx:
        sb, sem, load_sem, raised = stage_tools(core, ctx)
        outer, inner, second = (Norm(sb, sem, n) for n in ("outer", "inner", "second"))
        w = sb("w_qkv", [C, 2, 3 * D])
        w_out = sb("w_out", [C, 2, D])
        w_router = sb("w_router", [128, 2, EXPERTS])
        affine = sb("affine", [C, 4])
        affine2 = sb("affine2", [128, 4])
        xn = sb("xn", [T, GROUP, D])
        xnn = sb("xnn", [T, GROUP, D])
        xT = sb("xT", [C, 2, N])
        qT = sb("qT", [C, 2, N])
        kT = sb("kT", [C, 2, N])
        o = sb("o", [T, GROUP, D])
        oT = sb("oT", [C, 2, N])
        zn = sb("zn", [T, GROUP, D + REST])
        zT = sb("zT", [128, 2, N])
        att = Heads(core, sb, sem, 16, core.mask16)
        router = Router(sb, sem, "router")
        w_loaded, ones_ready = load_sem("w_loaded"), load_sem("ones_ready")
        names = ("xnn_ready", "xT_psum", "xT_ready", "q_psum", "k_psum", "v_psum", "q_ready", "k_ready", "v_ready",
                 "oT_psum", "oT_ready", "out_psum", "zn_ready", "zT_psum", "zT_ready", "zT_kept", "logits_psum",
                 "logits_read", "gates_done")
        s = {n: sem(n) for n in names}

        with nc.Block() as block:
            @block.sync
            def _(sp):
                raise_to_start(sp, raised)
                raise_to_start(sp, weights.raised)
                sp.dma_start(w[:, :, :], a["b_wqkv"]).then_inc(w_loaded, 16)
                sp.dma_start(w_out[:, :, :], a["b_wproj"]).then_inc(w_loaded, 16)
                sp.dma_start(w_router[:, 0, :], a["b_wrouter"][0:HIGH, :]).then_inc(w_loaded, 16)
                sp.dma_start(w_router[0:REST, 1, :], a["b_wrouter"][HIGH:D, :]).then_inc(w_loaded, 16)
                sp.dma_start(affine[:, :], a["b_affine"]).then_inc(w_loaded, 16)
                sp.dma_start(affine2[:, :], a["b_affine2"]).then_inc(w_loaded, 16)
                weights.load(sp, a, (0, 0))

            @block.gpsimd
            def _(pool):
                pool.memset(att.vals[:, :, :, 16:17], 1.0).then_inc(ones_ready, 1)
                norm_rstd(pool, core, outer, 0)
                norm_rstd(pool, core, inner, 0)
                with pool.Fori(0, TURNS) as i:
                    pool.wait_ge(att.scores_psum, turn(i, 0, UNITS))
                    pool.wait_ge(s["k_ready"], turn(i))
                    for b in range(GROUP):
                        heads_pool(pool, att, i, kT, b)
                    norm_rstd(pool, core, second, i)
                    norm_rstd(pool, core, outer, i + 1)
                    norm_rstd(pool, core, inner, i + 1)
                for _ in weights.steps(pool, (0, 0)):
                    pass

            @block.tensor
            def _(pe):
                pe.wait_ge(w_loaded, 96)
                pe.wait_ge(ones_ready, 1)
                with pe.Fori(0, TURNS) as i:
                    pe.wait_ge(s["oT_ready"], turn(i, 0))
                    pe.wait_ge(s["xnn_ready"], turn(i))
                    transpose_group(pe, core, bank[0:2], xnn, s["xT_psum"])
                    pe.wait_ge(s["zn_ready"], turn(i, 0))
                    pe.wait_ge(s["zT_ready"], turn(i, 0))
                    pe.wait_ge(s["logits_read"], turn(i, 0))
                    pe.wait_ge(s["xT_ready"], turn(i))
                    for j, done in enumerate(("q_psum", "q_psum", "k_psum", "k_psum")):
                        for c in range(2):
                            mm = pe.matmul(bank[2 + j][0:C, 0:N], w[:, c, j * C:(j + 1) * C], xT[:, c, :],
                                           start=(c == 0), stop=(c == 1))
                        if j % 2:
                            mm.then_inc(s[done], 1)
                    for b in range(GROUP):
                        for c in range(2):
                            mm = pe.matmul(bank[6 + b // 2][0:T, cols(b % 2, D)], xT[:, c, cols(b)],
                                           w[:, c, 2 * D:3 * D], start=(c == 0), stop=(c == 1))
                    mm.then_inc(s["v_psum"], 1)
                    pe.wait_ge(s["q_ready"], turn(i))
                    pe.wait_ge(s["k_ready"], turn(i))
                    pe.wait_ge(s["v_ready"], turn(i))
                    heads_tensor(pe, att, i, qT)
                    pe.wait_ge(att.context_done, turn(i, UNITS, UNITS))
                    transpose_group(pe, core, bank[0:2], o, s["oT_psum"])
                    pe.wait_ge(s["oT_ready"], turn(i))
                    for b in range(GROUP):
                        for c in range(2):
                            mm = pe.matmul(bank[2 + b // 2][0:T, cols(b % 2, D)], oT[:, c, cols(b)], w_out[:, c, :],
                                           start=(c == 0), stop=(c == 1))
                    mm.then_inc(s["out_psum"], 1)
                    pe.wait_ge(s["zn_ready"], turn(i))
                    transpose_for_experts(pe, core, bank[4:6], zn, s["zT_psum"])
                    pe.wait_ge(s["zT_ready"], turn(i))
                    for b in range(GROUP):
                        for c in range(2):
                            rows = slice(0, (HIGH, REST)[c])
                            mm = pe.matmul(bank[6][0:T, cols(b, EXPERTS)], zT[rows, c, cols(b)], w_router[rows, c, :],
                                           start=(c == 0), stop=(c == 1))
                    mm.then_inc(s["logits_psum"], 1)

            @block.scalar
            def _(act):
                act.wait_ge(w_loaded, 96)
                with act.Fori(0, TURNS) as i:
                    act.wait_ge(s["v_psum"], turn(i, 0))
                    act.wait_ge(s["xT_psum"], turn(i))
                    for c in range(2):
                        ins = act.activation(xT[:, c, :], bank[c][0:C, 0:N], ACT.Identity,
                                             bias=affine[:, 2 + c:3 + c], scale=affine[:, c:c + 1])
                    ins.then_inc(s["xT_ready"], 1)
                    act.wait_ge(att.kblock_ready, turn(i, 0, GROUP))
                    act.wait_ge(s["k_psum"], turn(i))
                    for c in range(2):
                        ins = act.activation(kT[:, c, :], bank[4 + c][0:C, 0:N], ACT.Copy)
                    ins.then_inc(s["k_ready"], 1)
                    act.wait_ge(att.scores_psum, turn(i, 0, UNITS))
                    for c in range(2):
                        ins = act.activation(qT[:, c, :], bank[2 + c][0:C, 0:N], ACT.Copy, scale=0.25)
                    ins.then_inc(s["q_ready"], 1)
                    heads_scalar(act, att, i)
                    act.wait_ge(s["logits_psum"], turn(i, 0))
                    act.wait_ge(s["zT_kept"], turn(i, 0))
                    act.wait_ge(s["zT_psum"], turn(i))
                    for c in range(2):
                        ins = act.activation(zT[:, c, :], bank[4 + c][:, 0:N], ACT.Identity,
                                             bias=affine2[:, 2 + c:3 + c], scale=affine2[:, c:c + 1])
                    ins.then_inc(s["zT_ready"], 1)
                    router_scalar(act, router, i)

            @block.vector
            def _(v):
                def normed(i):
                    norm_statistics(v, outer, lambda b: sample_of(h, i, b))
                    v.wait_ge(outer.rstd_ready, turn(i))
                    for b in range(GROUP):
                        norm_apply(v, outer, lambda b: sample_of(h, i, b), lambda b: xn[:, b, :], b)
                    v.drain()
                    norm_statistics(v, inner, lambda b: xn[:, b, :])
                    v.wait_ge(inner.rstd_ready, turn(i))
                    for b in range(GROUP):
                        ins = norm_apply(v, inner, lambda b: xn[:, b, :], lambda b: xnn[:, b, :], b)
                    ins.then_inc(s["xnn_ready"], 1)

                normed(0)
                v.wait_ge(w_loaded, 96)
                with v.Fori(0, TURNS) as i:
                    v.wait_ge(s["v_psum"], turn(i))
                    for b in range(GROUP):
                        ins = v.tensor_copy(att.vals[:, b, :, 0:16], bank[6 + b // 2][0:T, cols(b % 2, D)]
                                            .rearrange("t (n d) -> t n d", d=16))
                    ins.then_inc(s["v_ready"], 1)

                    def rescale(u, inv):
                        return v.tensor_tensor(o[:, u // 2, cols(u % 2, C)].rearrange("t (n d) -> t n d", d=16),
                                               att.context(u)[:, :, 0:16],
                                               inv.unsqueeze(2).to_broadcast([T, UNIT_HEADS, 16]), ALU.mult)
                    heads_vector(v, att, i, rescale)
                    v.wait_ge(s["oT_psum"], turn(i))
                    for c in range(2):
                        ins = v.tensor_copy(oT[:, c, :], bank[c][0:C, 0:N])
                    ins.then_inc(s["oT_ready"], 1)
                    v.wait_ge(s["out_psum"], turn(i))
                    for p in range(2):
                        v.tensor_tensor(xn[:, 2 * p:2 * p + 2, :], xn[:, 2 * p:2 * p + 2, :],
                                        bank[2 + p][0:T, 0:2 * D].rearrange("t (b d) -> t b d", b=2), ALU.add)
                    v.drain()
                    rows = h[:, bass.ds(i * (GROUP * D), GROUP * D)]
                    v.tensor_tensor(rows, rows, xn[:, :, :].rearrange("t b d -> t (b d)"), ALU.add)
                    norm_statistics(v, second, lambda b: xn[:, b, :])
                    v.wait_ge(second.rstd_ready, turn(i))
                    for b in range(GROUP):
                        norm_apply(v, second, lambda b: xn[:, b, :], lambda b: zn[:, b, 0:D], b)
                    duplicate_rest(v, zn).then_inc(s["zn_ready"], 1)
                    normed(i + 1)
                    v.wait_ge(s["zT_ready"], turn(i))
                    keep_for_experts(v, core, zT, i).then_inc(s["zT_kept"], 1)
                    v.wait_ge(s["logits_psum"], turn(i))
                    v.tensor_copy(router.logits[:, :, :], bank[6][0:T, 0:GROUP * EXPERTS]).then_inc(s["logits_read"], 1)
                    v.drain()
                    router_vector(v, core, router, i).then_inc(s["gates_done"], 1)



class ExpertWeights:

    def __init__(self, core, ctx, second):
        sb, sem, load_sem, self.raised = stage_tools(core, ctx)
        self.core, self.second = core, second
        parts = 3 if second else 1
        self.raw1 = [sb("raw1", [128, 2, FF]) for _ in range(parts)]
        self.raw2 = [sb("raw2", [128, FC, D]) for _ in range(parts)]
        self.w1_hi = [sb("w1_hi", [128, 2, FF], F32R) for _ in range(2)]
        self.w1_lo = [sb("w1_lo", [128, FF], F32R) for _ in range(2)]
        self.w1_lo_rest = [sb("w1_lo_rest", [REST, FF], F32R) for _ in range(2)]
        self.w2 = [sb("w2", [128, FC, 2, D], F32R) for _ in range(2)]
        self.loads = 3 * parts + second
        if second:
            self.mix = sb("mix", [128, 2])
            self.b1 = [sb("b1", [128, FC]) for _ in range(2)]
            self.b1_loaded = [load_sem("b1_loaded") for _ in range(2)]
        self.loaded = load_sem("loaded")
        self.raw_read, self.scaled, self.added, self.mixed, self.high_ready, self.split_ready, self.y_psum = (
            sem(n) for n in ("raw_read", "scaled", "added", "mixed", "high_ready", "split_ready", "y_psum"))

    def load(self, sp, a, e):
        e, k = e
        row = bass.ds(e, 1)
        if self.second:
            sp.wait_ge(self.y_psum, turn((e - 1) * TURNS, 0))
            sp.dma_start(self.b1[k][:, :], a["i_b1"][row].rearrange("e p c -> (e p) c")
                         ).then_inc(self.b1_loaded[k], 16)
        sp.wait_ge(self.raw_read, turn(e, 0))
        if self.second:
            sp.dma_start(self.mix[:, :], a["i_mix"][row, :].to_broadcast([128, 2])).then_inc(self.loaded, 16)
        for n in range(len(self.raw1)):
            w1 = a[f"i_w1_{n}" if self.second else "b_w1"][row].rearrange("e k f -> (e k) f")
            w2 = a[f"i_w2_{n}" if self.second else "b_w2"][row].rearrange("e p c f -> (e p) c f")
            sp.dma_start(self.raw1[n][:, 0, :], w1[0:HIGH, :]).then_inc(self.loaded, 16)
            sp.dma_start(self.raw1[n][:, 1, :], w1[HIGH:D, :].unsqueeze(0).to_broadcast([2, REST, FF])
                         ).then_inc(self.loaded, 16)
            sp.dma_start(self.raw2[n][:, :, :], w2).then_inc(self.loaded, 16)

    def steps(self, pool, e):
        e, k = e
        raw1, raw2, w1_hi, w1_lo, w1_lo_rest, w2 = (
            self.raw1, self.raw2, self.w1_hi[k], self.w1_lo[k], self.w1_lo_rest[k], self.w2[k])
        pool.wait_ge(self.loaded, e * (16 * self.loads) + 16 * self.loads)
        both = [(raw1[n][:, :, :].rearrange("p c f -> p (c f)"),
                 raw2[n][:, :, :].rearrange("p c f -> p (c f)")) for n in range(len(raw1))]
        if self.second:
            for m in range(2):
                ins = pool.tensor_tensor(both[1][m], both[1][m],
                                         self.mix[:, m:m + 1].to_broadcast(list(both[1][m].shape)), ALU.mult)
            ins.then_inc(self.scaled, 1)
            yield
            pool.wait_ge(self.scaled, turn(e))
            for m in range(2):
                ins = pool.tensor_tensor(both[0][m], both[0][m], both[1][m], ALU.add)
            ins.then_inc(self.added, 1)
            yield
            pool.wait_ge(self.added, turn(e))
            for m in range(2):
                ins = pool.tensor_tensor(both[0][m], both[0][m], both[2][m], ALU.add)
            ins.then_inc(self.mixed, 1)
            yield
            pool.wait_ge(self.mixed, turn(e))
        pool.wait_ge(self.y_psum, turn((e - 1) * TURNS, 0))
        one = self.core.ones[:, 0:1]
        pool.tensor_tensor(w1_hi[:, :, :].rearrange("p c f -> p (c f)"), both[0][0],
                           one.to_broadcast([128, 2 * FF]), ALU.mult)
        pool.tensor_tensor(w2[:, :, 0, :], raw2[0][:, :, :], one.unsqueeze(2).to_broadcast([128, FC, D]), ALU.mult
                           ).then_inc(self.high_ready, 1)
        pool.wait_ge(self.high_ready, turn(e))
        pool.tensor_tensor(w1_lo[:, :], raw1[0][:, 0, :], w1_hi[:, 0, :].bitcast(F32), ALU.subtract)
        pool.tensor_tensor(w1_lo_rest[:, :], raw1[0][0:REST, 1, :], w1_hi[0:REST, 1, :].bitcast(F32), ALU.subtract)
        pool.tensor_tensor(w2[:, :, 1, :], raw2[0][:, :, :], w2[:, :, 0, :].bitcast(F32), ALU.subtract
                           ).then_inc(self.split_ready, 1)
        yield
        pool.wait_ge(self.split_ready, turn(e))
        pool.sem_inc(self.raw_read, 1)

    def rest_of_the_experts(self, engine, each):
        with engine.Fori(0, EXPERTS // 2 - 1) as pair:
            each((pair * 2 + 1, 1))
            each((pair * 2 + 2, 0))
        each((EXPERTS - 1, 1))


def experts_stage(core, a, weights):
    nc, bank, h = core.nc, core.bank, core.h
    RING = 3
    second = weights.second
    w1_hi, w1_lo, w1_lo_rest, w2 = weights.w1_hi, weights.w1_lo, weights.w1_lo_rest, weights.w2
    y_psum, split_ready = weights.y_psum, weights.split_ready
    with ExitStack() as ctx:
        sb, sem, load_sem, raised = stage_tools(core, ctx)
        hidden = sb("hidden", [128, FC, N])
        hidden_hi = sb("hidden_hi", [128, FC, N], F32R)
        hidden_lo = sb("hidden_lo", [128, FC, N], F32R)
        names = ("hidden_psum", "bank_read", "hidden_ready", "hi_ready", "lo_ready", "y_half", "y_added")
        s = {n: sem(n) for n in names}
        if second:
            relu = sb("relu", [128, 2, N])
            b1, b1_loaded = weights.b1, weights.b1_loaded

        with nc.Block() as block:
            @block.sync
            def _(sp):
                raise_to_start(sp, raised)
                weights.rest_of_the_experts(sp, lambda e: weights.load(sp, a, e))

            @block.gpsimd
            def _(pool):
                def split(e):
                    for _ in weights.steps(pool, e):
                        pass

                weights.rest_of_the_experts(pool, split)

            @block.tensor
            def _(pe):
                with pe.Fori(0, EXPERTS // 2) as pair:
                    for k in range(2):
                        e = pair * 2 + k
                        with pe.Fori(0, TURNS) as i:
                            t = e * TURNS + i
                            at = bass.ds(i * N, N)
                            pe.wait_ge(split_ready, turn(e))
                            for m in range(FC):
                                f = slice(m * 128, (m + 1) * 128)
                                out = bank[m % RING][:, 0:N]
                                pe.wait_ge(s["bank_read"], turn(t, m + 1 - RING, FC))
                                pe.matmul(out, w1_hi[k][:, 0, f], core.z_hi[:, at], start=True, stop=False)
                                pe.matmul(out, w1_hi[k][:, 0, f], core.z_lo[:, at], start=False, stop=False)
                                pe.matmul(out, w1_lo[k][:, f], core.z_hi[:, at], start=False, stop=False)
                                pe.matmul(out, w1_hi[k][:, 1, f], core.z_rest[:, at], start=False, stop=False)
                                pe.matmul(out, w1_lo_rest[k][:, f], core.z_rest[0:REST, at], start=False, stop=True
                                          ).then_inc(s["hidden_psum"], 1)
                            pe.wait_ge(s["y_added"], turn(t, 0))
                            for m in range(FC):
                                first, last = m == 0, m == FC - 1
                                pe.wait_ge(s["lo_ready"], turn(t, m + 1, FC))
                                for b in range(GROUP):
                                    pe.matmul(bank[4 + b][0:T, 0:2 * D], hidden_hi[:, m, cols(b)],
                                              w2[k][:, m, :, :].rearrange("p a d -> p (a d)"),
                                              start=first, stop=last)
                                    mm = pe.matmul(bank[4 + b][0:T, 0:D], hidden_lo[:, m, cols(b)], w2[k][:, m, 0, :],
                                                   start=False, stop=last, skip_group_check=True)
                            mm.then_inc(y_psum, 1)

            @block.scalar
            def _(act):
                with act.Fori(0, EXPERTS // 2) as pair:
                    for k in range(2):
                        with act.Fori(0, TURNS) as i:
                            e = pair * 2 + k
                            t = e * TURNS + i
                            if second:
                                act.wait_ge(b1_loaded[k], pair * 16 + 16)
                            act.wait_ge(s["lo_ready"], turn(t, 0, FC))
                            for m in range(FC):
                                act.wait_ge(s["hidden_psum"], turn(t, m + 1, FC))
                                if second:
                                    act.activation(relu[:, m % 2, :], bank[m % RING][:, 0:N], ACT.Relu,
                                                   bias=b1[k][:, m:m + 1]).then_inc(s["bank_read"], 1)
                                    act.wait_ge(s["bank_read"], turn(t, m + 1, FC))
                                    act.activation(hidden[:, m, :], relu[:, m % 2, :], ACT.Square
                                                   ).then_inc(s["hidden_ready"], 1)
                                else:
                                    act.activation(hidden[:, m, :], bank[m % RING][:, 0:N], ACT.Gelu
                                                   ).then_inc(s["bank_read"], 1)

            @block.vector
            def _(v):
                written = s["hidden_ready"] if second else s["bank_read"]
                with v.Fori(0, EXPERTS // 2) as pair:
                    for k in range(2):
                        with v.Fori(0, TURNS) as i:
                            e = pair * 2 + k
                            t = e * TURNS + i
                            v.wait_ge(y_psum, turn(t, 0))
                            for m in range(FC):
                                v.wait_ge(written, turn(t, m + 1, FC))
                                v.tensor_copy(hidden_hi[:, m, :], hidden[:, m, :]).then_inc(s["hi_ready"], 1)
                                v.wait_ge(s["hi_ready"], turn(t, m + 1, FC))
                                v.tensor_tensor(hidden_lo[:, m, :], hidden[:, m, :], hidden_hi[:, m, :].bitcast(F32),
                                                ALU.subtract).then_inc(s["lo_ready"], 1)
                            v.wait_ge(y_psum, turn(t))
                            for part, done in ((0, s["y_half"]), (1, s["y_added"])):
                                for b in range(GROUP):
                                    gate = core.gates[:, bass.ds(i * (GROUP * EXPERTS) + b * EXPERTS + e, 1)]
                                    ins = v.scalar_tensor_tensor(out=sample_of(h, i, b),
                                                                 in0=bank[4 + b][0:T, cols(part, D)],
                                                                 scalar=gate, in1=sample_of(h, i, b),
                                                                 op0=ALU.mult, op1=ALU.add)
                                ins.then_inc(done, 1)
                                if part == 0:
                                    v.wait_ge(s["y_half"], turn(t))



def ssm_stage(core, a):
    nc, bank, h = core.nc, core.bank, core.h
    STATES = 16
    PER = 128 // STATES
    TILES = D // PER
    HALF = TILES // 2
    TAPS = 4
    PAD = TAPS - 1
    PIECES = 8
    PIECE = D * STATES // PIECES
    PIECE_TILES = TILES // PIECES
    STEPS, FIRST_STEP = 6, 5
    FIRST_PIECES = 6
    SELECTIONS = 4
    with ExitStack() as ctx:
        sb, sem, load_sem, raised = stage_tools(core, ctx)
        norm = Norm(sb, sem, "norm")
        w_in = sb("w_in", [C, 2, 2 * D])
        w_dt = sb("w_dt", [C, 2, D])
        w_out = sb("w_out", [C, 2, D])
        b_out = sb("b_out", [T, D])
        raw = [sb("raw", [128, 2 * PIECE]) for _ in range(2)]
        w_hi = [sb(n, [C, 2, D * STATES], F32R) for n in ("w_b_hi", "w_c_hi")]
        w_lo = [sb(n, [C, 2, D * STATES], F32R) for n in ("w_b_lo", "w_c_lo")]
        spread = sb("spread", [C, HALF, 128], F32R)
        gather = sb("gather", [128, HALF, C], F32R)
        per_channel = sb("per_channel", [C, 2, 5 + TAPS])
        neg_bv = sb("neg_bv", [C, 2])
        row_consts = sb("row_consts", [128, 3, TILES])
        decay_rate = sb("decay_rate", [128, TILES])
        xn = sb("xn", [T, GROUP, D])
        xT = sb("xT", [C, 2, N])
        u = sb("u", [C, 2, GROUP, PAD + T])
        gate = sb("gate", [C, 2, N])
        conv = sb("conv", [C, 2, N])
        dt = sb("dt", [C, 2, N])
        dtu = sb("dtu", [C, 2, N])
        z = sb("z", [C, 2, N])
        soft, y = xT, z
        exp_v = dtu
        (conv_hi, conv_lo), (dt_hi, dt_lo), (dtu_hi, dtu_lo) = (
            [buffer[0:C, k * 2 * N:(k + 1) * 2 * N].rearrange("d (c t) -> d c t", c=2) for k in range(2)]
            for buffer in (core.z_hi, core.z_lo, core.z_rest))
        decay = sb("decay", [128, 2, N])
        dtu_rows = sb("dtu_rows", [128, 2, N])
        drive = sb("drive", [128, N])
        state = sb("state", [128, N])
        product = sb("product", [128, 2, N])
        product_hi = sb("product_hi", [128, 2, N], F32R)
        product_lo = sb("product_lo", [128, 2, N], F32R)
        w_loaded, rate_exp, consts_ready, selection_ready, first_high, first_ready, piece_high, piece_ready = (
            load_sem(n) for n in ("w_loaded", "rate_exp", "consts_ready", "selection_ready", "first_high",
                                  "first_ready", "piece_high", "piece_ready"))
        raw_loaded = [load_sem("raw_loaded") for _ in range(2)]
        names = ("xn_ready", "step_psum", "step_read", "conv_ready",
                 "conv_high", "conv_split", "dt_psum", "z_ready", "log_ready", "dt_done", "dt_high", "dtu_done",
                 "dtu_high", "dt_split", "b_psum", "spread_psum", "c_psum", "spread_read", "b_read",
                 "product_ready", "product_high", "product_split", "gathered", "y_ready", "out_psum", "h_done")
        s = {n: sem(n) for n in names}
        loads = [(w_in, "c_wi"), (w_dt, "c_wdt"), (per_channel, "c_channel"), (row_consts, "c_rows"),
                 (w_out, "c_wo")]

        def selection(matrix, k):
            part = slice(k % 2 * HALF // 2, (k % 2 + 1) * HALF // 2)
            return matrix[:, part, :].rearrange("p j r -> p (j r)")

        selections = [(spread, "spread"), (spread, "spread"), (gather, "gather"), (gather, "gather")]

        def piece(p):
            at = slice(p // 2 * PIECE, (p // 2 + 1) * PIECE)
            return (raw[(SELECTIONS + p) % 2][0:C, :].rearrange("d (c f) -> d c f", c=2),
                    w_hi[p % 2][:, :, at], w_lo[p % 2][:, :, at])

        with nc.Block() as block:
            @block.sync
            def _(sp):
                raise_to_start(sp, raised)
                for tile, name in loads:
                    sp.dma_start(tile[tuple(slice(None) for _ in tile.shape)], a[name]).then_inc(w_loaded, 16)
                sp.dma_start(b_out[:, :], a["c_bo"].to_broadcast([T, D])).then_inc(w_loaded, 16)
                for n in range(SELECTIONS + 2 * PIECES):
                    before = n - 2
                    if before >= SELECTIONS + FIRST_PIECES:
                        sp.wait_ge(piece_ready, before + 1 - SELECTIONS - FIRST_PIECES)
                    elif before >= SELECTIONS:
                        sp.wait_ge(first_ready, before + 1 - SELECTIONS)
                    elif before >= 0:
                        sp.wait_ge(selection_ready, before + 1)
                    if n < SELECTIONS:
                        source = selection(a[selections[n][1]], n)
                        target = raw[n % 2][0:source.shape[0], 0:source.shape[1]]
                    else:
                        p = n - SELECTIONS
                        source = a[("c_wb", "c_wc")[p % 2]][:, :, p // 2 * PIECE:(p // 2 + 1) * PIECE]
                        target = raw[n % 2][0:C, :].rearrange("d (c f) -> d c f", c=2)
                    sp.dma_start(target, source).then_inc(raw_loaded[n % 2], 16)

            @block.gpsimd
            def _(pool):
                norm_rstd(pool, core, norm, 0)
                for p in range(FIRST_PIECES, 2 * PIECES):
                    n = SELECTIONS + p
                    source, high, low = piece(p)
                    pool.wait_ge(raw_loaded[n % 2], 16 * (n // 2 + 1))
                    pool.tensor_tensor(high, source, core.ones[0:C, 0:1].unsqueeze(2).to_broadcast([C, 2, PIECE]),
                                       ALU.mult).then_inc(piece_high, 1)
                    pool.wait_ge(piece_high, p - FIRST_PIECES + 1)
                    pool.tensor_tensor(low, source, high.bitcast(F32), ALU.subtract).then_inc(piece_ready, 1)
                with pool.Fori(0, TURNS) as i:
                    for j in range(TILES):
                        pool.wait_ge(s["product_high"], turn(i, j + 1, TILES))
                        pool.tensor_tensor(product_lo[:, j % 2, :], product[:, j % 2, :],
                                           product_hi[:, j % 2, :].bitcast(F32), ALU.subtract
                                           ).then_inc(s["product_split"], 1)
                        if j == 1:
                            norm_rstd(pool, core, norm, i + 1)

            @block.tensor
            def _(pe):
                pe.wait_ge(w_loaded, 16 * (1 + len(loads)))
                pe.wait_ge(selection_ready, SELECTIONS)

                def projected(kind, i, j):
                    p = 2 * (j // PIECE_TILES) + kind
                    if p < FIRST_PIECES:
                        pe.wait_ge(first_ready, p + 1)
                    else:
                        pe.wait_ge(piece_ready, p - FIRST_PIECES + 1)
                    pe.wait_ge(s[("b_read", "product_ready")[kind]], turn(i, j - 1, TILES))
                    out = bank[2 * kind + j % 2][:, 0:N]
                    rows = slice(j * 128, (j + 1) * 128)
                    for c in range(2):
                        pe.matmul(out, w_hi[kind][:, c, rows], conv_hi[:, c, :], start=(c == 0), stop=False)
                        pe.matmul(out, w_hi[kind][:, c, rows], conv_lo[:, c, :], start=False, stop=False)
                        mm = pe.matmul(out, w_lo[kind][:, c, rows], conv_hi[:, c, :], start=False, stop=(c == 1))
                    mm.then_inc(s[("b_psum", "c_psum")[kind]], 1)

                def gather_tile(i, j):
                    pe.wait_ge(s["product_split"], turn(i, j + 1, TILES))
                    for part, operand in enumerate((product_hi, product_lo)):
                        mm = pe.matmul(bank[6 + j // HALF][0:C, 0:N], gather[:, j % HALF, :], operand[:, j % 2, :],
                                       start=(j % HALF == 0 and part == 0), stop=(j % HALF == HALF - 1 and part == 1))
                    mm.then_inc(s["gathered"], 1)

                def step(i, k):
                    if k == 0:
                        pe.wait_ge(s["y_ready"], turn(i, -1))
                        pe.wait_ge(s["xn_ready"], turn(i))
                    pe.wait_ge(s["step_read"], turn(i, k, STEPS))
                    out = bank[7][0:C, 0:N]
                    if k < 2:
                        for b in range(GROUP):
                            mm = pe.transpose(out[:, cols(b)], xn[:, b, k * C:(k + 1) * C], core.ident[0:T, 0:T])
                    else:
                        for c in range(2):
                            mm = pe.matmul(out, w_in[:, c, (k - 2) * C:(k - 1) * C], xT[:, c, :],
                                           start=(c == 0), stop=(c == 1))
                    mm.then_inc(s["step_psum"], 1)

                for k in range(STEPS):
                    step(0, k)
                with pe.Fori(0, TURNS) as i:
                    pe.wait_ge(s["conv_ready"], turn(i))
                    for j in range(2):
                        for c in range(2):
                            mm = pe.matmul(bank[6 + j][0:C, 0:N], w_dt[:, c, j * C:(j + 1) * C], conv[:, c, :],
                                           start=(c == 0), stop=(c == 1))
                    mm.then_inc(s["dt_psum"], 1)
                    pe.wait_ge(s["h_done"], turn(i, 0))
                    pe.wait_ge(s["conv_split"], turn(i))
                    for j in range(2):
                        projected(0, i, j)
                        projected(1, i, j)
                    pe.wait_ge(s["dt_split"], turn(i))
                    for j in range(TILES):
                        c = j // HALF
                        pe.wait_ge(s["spread_read"], turn(i, j, TILES))
                        for part, (of_dt, of_dtu) in enumerate(((dt_hi, dtu_hi), (dt_lo, dtu_lo))):
                            for first, operand in ((4, of_dt), (5, of_dtu)):
                                mm = pe.matmul(bank[first][:, 0:N], spread[:, j % HALF, :], operand[:, c, :],
                                               start=(part == 0), stop=(part == 1))
                        mm.then_inc(s["spread_psum"], 1)
                        if j - 2 == HALF:
                            pe.wait_ge(s["step_read"], turn(i + 1, STEPS, STEPS))
                        if j >= 2:
                            gather_tile(i, j - 2)
                        if 0 <= j - FIRST_STEP < STEPS:
                            step(i + 1, j - FIRST_STEP)
                        if 1 <= j < TILES - 1:
                            projected(0, i, j + 1)
                            projected(1, i, j + 1)
                    gather_tile(i, TILES - 2)
                    gather_tile(i, TILES - 1)
                    pe.wait_ge(s["y_ready"], turn(i))
                    for b in range(GROUP):
                        out = bank[b // 2][0:T, cols(b % 2, D)]
                        for c in range(2):
                            mm = pe.matmul(out, y[:, c, cols(b)], w_out[:, c, :], start=(c == 0), stop=(c == 1))
                    mm.then_inc(s["out_psum"], 1)

            @block.scalar
            def _(act):
                act.wait_ge(w_loaded, 16 * (1 + len(loads)))
                act.activation(decay_rate[:, :], row_consts[:, 0, :], ACT.Exp).then_inc(rate_exp, 1)
                act.wait_ge(consts_ready, 1)

                def step(i, k):
                    act.wait_ge(s["step_psum"], turn(i, k + 1, STEPS))
                    source, c = bank[7][0:C, 0:N], k % 2
                    if k < 2:
                        ins = act.activation(xT[:, c, :], source, ACT.Copy)
                    elif k < 4:
                        ins = act.activation(u[:, c, :, PAD:PAD + T], source.rearrange("d (b t) -> d b t", b=GROUP),
                                             ACT.Identity, bias=per_channel[:, c, 0:1])
                    else:
                        ins = act.activation(exp_v[:, c, :], source, ACT.Exp, bias=neg_bv[:, c:c + 1], scale=-1.0)
                    ins.then_inc(s["step_read"], 1)

                for k in range(STEPS):
                    step(0, k)
                with act.Fori(0, TURNS) as i:
                    act.wait_ge(s["conv_ready"], turn(i))
                    act.activation(conv_hi, conv[:, :, :], ACT.Copy).then_inc(s["conv_high"], 1)
                    act.wait_ge(s["z_ready"], turn(i))
                    act.activation(soft[:, :, :], soft[:, :, :], ACT.Exp)
                    act.drain()
                    act.activation(soft[:, :, :], soft[:, :, :], ACT.Ln, bias=1.0).then_inc(s["log_ready"], 1)
                    act.wait_ge(s["dt_done"], turn(i))
                    act.activation(dt_hi, dt[:, :, :], ACT.Copy).then_inc(s["dt_high"], 1)
                    act.wait_ge(s["dtu_done"], turn(i))
                    act.activation(dtu_hi, dtu[:, :, :], ACT.Copy).then_inc(s["dtu_high"], 1)

                    def product_high(j):
                        act.wait_ge(s["gathered"], turn(i, j - 1, TILES))
                        act.wait_ge(s["product_ready"], turn(i, j + 1, TILES))
                        act.activation(product_hi[:, j % 2, :], product[:, j % 2, :], ACT.Copy
                                       ).then_inc(s["product_high"], 1)

                    for j in range(TILES):
                        act.wait_ge(s["product_ready"], turn(i, j - 1, TILES))
                        act.wait_ge(s["spread_psum"], turn(i, j + 1, TILES))
                        act.activation(decay[:, j % 2, :].rearrange("r (b t) -> r b t", b=GROUP)[:, :, 1:T],
                                       bank[4][:, 0:N].rearrange("r (b t) -> r b t", b=GROUP)[:, :, 1:T],
                                       ACT.Exp, scale=decay_rate[:, j:j + 1])
                        act.activation(dtu_rows[:, j % 2, :], bank[5][:, 0:N], ACT.Copy
                                       ).then_inc(s["spread_read"], 1)
                        if j:
                            product_high(j - 1)
                        if 0 <= j - FIRST_STEP < STEPS:
                            step(i + 1, j - FIRST_STEP)
                    product_high(TILES - 1)

            @block.vector
            def _(v):
                def apply_norm(i):
                    v.wait_ge(norm.rstd_ready, turn(i))
                    for b in range(GROUP):
                        ins = norm_apply(v, norm, lambda b: sample_of(h, i, b), lambda b: xn[:, b, :], b)
                    ins.then_inc(s["xn_ready"], 1)

                norm_statistics(v, norm, lambda b: sample_of(h, 0, b))
                apply_norm(0)
                v.memset(decay[:, :, :], 0.0)
                v.memset(u[:, :, :, :], 0.0)
                v.wait_ge(w_loaded, 16 * (1 + len(loads)))
                v.tensor_scalar(neg_bv[:, :], per_channel[:, :, 1], -1.0, None, ALU.mult)
                v.wait_ge(rate_exp, 1)
                v.tensor_scalar(decay_rate[:, :], decay_rate[:, :], -1.0, None, ALU.mult).then_inc(consts_ready, 1)
                for n, (matrix, _) in enumerate(selections):
                    target = selection(matrix, n)
                    v.wait_ge(raw_loaded[n % 2], 16 * (n // 2 + 1))
                    v.tensor_copy(target, raw[n % 2][0:target.shape[0], 0:target.shape[1]]
                                  ).then_inc(selection_ready, 1)
                for p in range(FIRST_PIECES):
                    n = SELECTIONS + p
                    source, high, low = piece(p)
                    v.wait_ge(raw_loaded[n % 2], 16 * (n // 2 + 1))
                    v.tensor_copy(high, source).then_inc(first_high, 1)
                    v.wait_ge(first_high, p + 1)
                    v.tensor_tensor(low, source, high.bitcast(F32), ALU.subtract).then_inc(first_ready, 1)

                def convolved(i):
                    v.wait_ge(s["step_read"], turn(i, STEPS, STEPS))
                    by_sample = [conv[:, c, :].rearrange("d (b t) -> d b t", b=GROUP) for c in range(2)]
                    for c in range(2):
                        v.tensor_scalar(by_sample[c], u[:, c, :, 0:T], per_channel[:, c, 5:6],
                                        per_channel[:, c, 2:3], ALU.mult, ALU.add)
                    for k in range(1, TAPS):
                        v.drain()
                        for c in range(2):
                            ins = v.scalar_tensor_tensor(out=by_sample[c], in0=u[:, c, :, k:k + T],
                                                         scalar=per_channel[:, c, 5 + k:6 + k], in1=by_sample[c],
                                                         op0=ALU.mult, op1=ALU.add)
                    ins.then_inc(s["conv_ready"], 1)
                    v.tensor_scalar(gate[:, :, :], exp_v[:, :, :], 1.0, None, ALU.add)

                convolved(0)
                with v.Fori(0, TURNS) as i:
                    v.wait_ge(s["conv_high"], turn(i))
                    v.tensor_tensor(conv_lo, conv[:, :, :], conv_hi.bitcast(F32), ALU.subtract
                                    ).then_inc(s["conv_split"], 1)
                    v.wait_ge(s["dt_psum"], turn(i))
                    for c in range(2):
                        v.tensor_scalar(z[:, c, :], bank[6 + c][0:C, 0:N], per_channel[:, c, 3:4], None, ALU.add)
                    v.drain()
                    v.scalar_tensor_tensor(out=soft[:, :, :], in0=z[:, :, :], scalar=-1.0, in1=z[:, :, :],
                                           op0=ALU.mult, op1=ALU.min).then_inc(s["z_ready"], 1)
                    v.wait_ge(s["log_ready"], turn(i))
                    v.scalar_tensor_tensor(out=dt[:, :, :], in0=z[:, :, :], scalar=0.0, in1=soft[:, :, :],
                                           op0=ALU.max, op1=ALU.add).then_inc(s["dt_done"], 1)
                    v.wait_ge(s["dt_done"], turn(i))
                    v.tensor_tensor(dtu[:, :, :], dt[:, :, :], conv[:, :, :], ALU.mult).then_inc(s["dtu_done"], 1)
                    v.wait_ge(s["dt_high"], turn(i))
                    v.tensor_tensor(dt_lo, dt[:, :, :], dt_hi.bitcast(F32), ALU.subtract)
                    v.wait_ge(s["dtu_high"], turn(i))
                    v.tensor_tensor(dtu_lo, dtu[:, :, :], dtu_hi.bitcast(F32), ALU.subtract
                                    ).then_inc(s["dt_split"], 1)
                    for j in range(TILES):
                        k = j % 2
                        v.wait_ge(s["spread_read"], turn(i, j + 1, TILES))
                        v.wait_ge(s["b_psum"], turn(i, j + 1, TILES))
                        v.scalar_tensor_tensor(out=drive[:, :], in0=bank[k][:, 0:N],
                                               scalar=row_consts[:, 1, j:j + 1], in1=dtu_rows[:, k, :],
                                               op0=ALU.add, op1=ALU.mult).then_inc(s["b_read"], 1)
                        v.drain()
                        v.tensor_tensor_scan(state[:, :], decay[:, k, :], drive[:, :], 0.0, ALU.mult, ALU.add)
                        v.drain()
                        v.wait_ge(s["product_split"], turn(i, j - 1, TILES))
                        v.wait_ge(s["c_psum"], turn(i, j + 1, TILES))
                        v.scalar_tensor_tensor(out=product[:, k, :], in0=bank[2 + k][:, 0:N],
                                               scalar=row_consts[:, 2, j:j + 1], in1=state[:, :],
                                               op0=ALU.add, op1=ALU.mult).then_inc(s["product_ready"], 1)
                        if j == 0:
                            norm_statistics(v, norm, lambda b: sample_of(h, i + 1, b))
                        if j == 2:
                            apply_norm(i + 1)
                        if 0 <= j - 2 * GROUP < 2 * GROUP:
                            part = gate[:, j // GROUP - 2, cols(j % GROUP)]
                            v.reciprocal(part, part)
                    v.wait_ge(s["gathered"], turn(i, TILES, TILES))
                    for c in range(2):
                        v.scalar_tensor_tensor(out=y[:, c, :], in0=conv[:, c, :], scalar=per_channel[:, c, 4:5],
                                               in1=bank[6 + c][0:C, 0:N], op0=ALU.mult, op1=ALU.add)
                    v.drain()
                    v.tensor_tensor(y[:, :, :], y[:, :, :], gate[:, :, :], ALU.mult).then_inc(s["y_ready"], 1)
                    convolved(i + 1)
                    add_bias(v, h, i, b_out)
                    v.wait_ge(s["out_psum"], turn(i))
                    for p in range(2):
                        rows = h[:, bass.ds(i * (GROUP * D) + p * (2 * D), 2 * D)]
                        ins = v.tensor_tensor(rows, bank[p][0:T, 0:2 * D], rows, ALU.add)
                    ins.then_inc(s["h_done"], 1)



def gated_heads_stage(core, a):
    nc, bank, h = core.nc, core.bank, core.h
    HD = 64
    WIDE = HEADS * HD
    QK = 2 * WIDE // 128
    SHARED, ROUTED = 2, 10
    GATES = ROUTED + 2 + SHARED
    RING = 4
    SQUARES = 3
    with ExitStack() as ctx:
        sb, sem, load_sem, raised = stage_tools(core, ctx)
        norm = Norm(sb, sem, "norm")
        w = SplitWeights(sb, "w_qkv_gate", 3 * WIDE + GATES)
        w_out = sb("w_out", [128, WIDE // 128, D])
        b_v = sb("b_v", [1, WIDE])
        b_v_hi, b_v_lo, ones_row = (sb(n, [1, m], F32R) for n, m in (("b_v_hi", WIDE), ("b_v_lo", WIDE), ("ones", T)))
        b_out = sb("b_out", [T, D])
        b_qk = sb("b_qk", [128, QK])
        b_centered = sb("b_centered", [128, QK])
        affine = sb("affine", [128, 4])
        affine_in = sb("affine_in", [128, 4])
        head_sum = sb("head_sum", [128, 2, 2 * HEADS])
        average = sb("average", [128, 128])
        eps = sb("eps", [128, 1])
        xn = sb("xn", [T, GROUP, D + REST])
        xT = SplitColumns(core)
        rstd = sb("rstd", [128, QK, N])
        qkT = sb("qkT", [128, QK, N])
        spare = w.raw[:, :, :].rearrange("p a m -> p (a m)")
        square = spare[:, 0:SQUARES * N].rearrange("p (k t) -> p k t", k=SQUARES)
        oT = spare[:, SQUARES * N:(SQUARES + WIDE // 128) * N].rearrange("p (j t) -> p j t", t=N)
        o = (rstd[0:T, :, :].rearrange("t j n -> t (j n)")[:, 0:GROUP * WIDE]
             .rearrange("t (b m) -> t b m", b=GROUP))
        att = Heads(core, sb, sem, HD, core.mask64, context_first=True)
        qT, kT = qkT[:, 0:QK // 2, :], qkT[:, QK // 2:QK, :]
        glog = sb("glog", [T, GROUP, GATES])
        gpeak = sb("gpeak", [T, 3, GROUP])
        gsum = sb("gsum", [T, 3, GROUP])
        top = TopTwo(sb, ROUTED, "top")
        gates = sb("gates_12", [T, GROUP, HEADS])
        weight = sb("weight", [T, 2, 6])
        w_loaded, ones_ready, bias_mean, bias_ready, w_centered, w_high, w_split = (
            load_sem(n) for n in ("w_loaded", "ones_ready", "bias_mean", "bias_ready", "w_centered", "w_high",
                                  "w_split"))
        names = ("xn_ready", "xT_psum", "xT_high", "xT_split", "gate_psum", "gate_read", "gshift_ready", "gexp_ready",
                 "qk_psum", "square_ready", "centered_done", "var_psum", "log_done", "half_rstd", "half_ready",
                 "v_psum", "v_ready", "oT_psum", "oT_act", "oT_dve", "out_psum", "h_done")
        s = {n: sem(n) for n in names}
        loads = [(w_out, "e_wproj"), (b_v, "e_bv"), (b_qk, "e_bqk"), (affine_in, "e_affine"), (average, "average")]
        HALF = QK // 2
        chunk = list(range(HALF, QK)) + list(range(HALF))
        parts = ((0, ROUTED), (ROUTED, ROUTED + 2), (ROUTED + 2, GATES))

        with nc.Block() as block:
            @block.sync
            def _(sp):
                raise_to_start(sp, raised)
                w.load(sp, a["e_wqkvg"], w_loaded)
                for tile, name in loads:
                    sp.dma_start(tile[tuple(slice(None) for _ in tile.shape)], a[name]).then_inc(w_loaded, 16)
                sp.dma_start(b_out[:, :], a["e_bproj"].to_broadcast([T, D])).then_inc(w_loaded, 16)

            @block.gpsimd
            def _(pool):
                pool.memset(att.vals[:, :, :, HD:HD + 1], 1.0).then_inc(ones_ready, 1)
                norm_rstd(pool, core, norm, 0)
                with pool.Fori(0, TURNS) as i:
                    pool.wait_ge(att.scores_psum, turn(i, 0, UNITS))
                    pool.wait_ge(s["half_ready"], turn(i, 1, 2))
                    for b in range(GROUP):
                        heads_pool(pool, att, i, kT, b)
                    norm_rstd(pool, core, norm, i + 1)

            @block.tensor
            def _(pe):
                pe.wait_ge(w_loaded, 16 * (3 + len(loads)))
                pe.matmul(bank[7][:, 0:QK], average[:, :], b_qk[:, :], start=True, stop=True).then_inc(bias_mean, 1)
                pe.wait_ge(ones_ready, 1)
                pe.wait_ge(w_split, 1)
                pe.wait_ge(bias_ready, 1)

                def variance(i, j):
                    pe.wait_ge(s["log_done"], turn(i, j - 1, QK))
                    pe.wait_ge(s["square_ready"], turn(i, j + 1, QK))
                    pe.matmul(bank[4 + j % 2][:, 0:N], average[:, :], square[:, j % SQUARES, :], start=True, stop=True
                              ).then_inc(s["var_psum"], 1)

                with pe.Fori(0, TURNS) as i:
                    pe.wait_ge(s["oT_dve"], turn(i, 0))
                    pe.wait_ge(s["xn_ready"], turn(i))
                    transpose_for_experts(pe, core, bank[0:2], xn, s["xT_psum"])
                    pe.wait_ge(s["h_done"], turn(i, 0))
                    pe.wait_ge(s["xT_split"], turn(i))
                    for b in range(GROUP):
                        mm = product_by_rows(pe, bank[6][0:T, cols(b, GATES)], xT, cols(b), w,
                                             slice(3 * WIDE, 3 * WIDE + GATES))
                    mm.then_inc(s["gate_psum"], 1)
                    pe.wait_ge(s["oT_act"], turn(i, 0))
                    for j in range(QK):
                        if j >= RING:
                            pe.wait_ge(s["centered_done"], turn(i, j + 1 - RING, QK))
                        mm = product_by_columns(pe, bank[j % RING][:, 0:N], w,
                                                slice(chunk[j] * 128, (chunk[j] + 1) * 128), xT)
                        mm.then_inc(s["qk_psum"], 1)
                        if j >= 2:
                            variance(i, j - 2)
                    variance(i, QK - 2)
                    variance(i, QK - 1)
                    for b in range(GROUP):
                        if b < 2:
                            pe.wait_ge(s["centered_done"], turn(i, QK, QK))
                        pe.wait_ge(s["v_ready"], turn(i, b - 1, GROUP))
                        for p in range(2):
                            out = bank[b % 2 * 2 + p][0:T, 0:WIDE // 2]
                            part = slice(p * WIDE // 2, (p + 1) * WIDE // 2)
                            product_by_rows(pe, out, xT, cols(b), w,
                                            slice(2 * WIDE + part.start, 2 * WIDE + part.stop), more=True)
                            pe.matmul(out, ones_row[:, :], b_v_hi[:, part], start=False, stop=False)
                            mm = pe.matmul(out, ones_row[:, :], b_v_lo[:, part], start=False, stop=True)
                        mm.then_inc(s["v_psum"], 1)
                    pe.wait_ge(s["v_ready"], turn(i, GROUP, GROUP))
                    pe.wait_ge(s["gate_read"], turn(i))
                    pe.wait_ge(s["log_done"], turn(i, QK, QK))
                    pe.wait_ge(s["half_ready"], turn(i, 2, 2))
                    heads_tensor(pe, att, i, qT)
                    pe.wait_ge(att.context_done, turn(i, UNITS, UNITS))
                    for j in range(WIDE // 128):
                        for b in range(GROUP):
                            mm = pe.transpose(bank[j][:, cols(b)], o[:, b, j * 128:(j + 1) * 128],
                                              core.ident[0:T, 0:T])
                    mm.then_inc(s["oT_psum"], 1)
                    pe.wait_ge(s["oT_act"], turn(i))
                    pe.wait_ge(s["oT_dve"], turn(i))
                    for b in range(GROUP):
                        out = bank[6 + b // 2][0:T, cols(b % 2, D)]
                        for j in range(WIDE // 128):
                            mm = pe.matmul(out, oT[:, j, cols(b)], w_out[:, j, :], start=(j == 0),
                                           stop=(j == WIDE // 128 - 1))
                    mm.then_inc(s["out_psum"], 1)

            @block.scalar
            def _(act):
                act.wait_ge(w_centered, 1)
                w.high(act).then_inc(w_high, 1)
                act.wait_ge(bias_ready, 1)
                with act.Fori(0, TURNS) as i:
                    act.wait_ge(s["xT_psum"], turn(i))
                    xT.high(act, bank[0:2]).then_inc(s["xT_high"], 1)

                    def logarithm(j):
                        act.wait_ge(s["var_psum"], turn(i, j + 1, QK))
                        act.activation(rstd[:, chunk[j], :], bank[4 + j % 2][:, 0:N], ACT.Ln, bias=eps[:, 0:1]
                                       ).then_inc(s["log_done"], 1)

                    def inverse_roots(half):
                        act.wait_ge(s["log_done"], turn(i, (half + 1) * HALF, QK))
                        of_half = rstd[:, chunk[half * HALF]:chunk[half * HALF] + HALF, :]
                        act.activation(of_half, of_half, ACT.Exp, scale=-0.5).then_inc(s["half_rstd"], 1)

                    for j in range(QK):
                        if j % HALF == 2:
                            act.wait_ge(s["half_ready"], turn(i, j // HALF - 1, 2))
                        act.wait_ge(s["var_psum"], turn(i, j + 1 - SQUARES, QK))
                        act.wait_ge(s["qk_psum"], turn(i, j + 1, QK))
                        act.activation(square[:, j % SQUARES, :], bank[j % RING][:, 0:N], ACT.Square,
                                       bias=b_centered[:, chunk[j]:chunk[j] + 1]).then_inc(s["square_ready"], 1)
                        if j >= 2:
                            logarithm(j - 2)
                        if j == HALF + 1:
                            inverse_roots(0)
                    logarithm(QK - 2)
                    logarithm(QK - 1)
                    inverse_roots(1)
                    act.wait_ge(s["gshift_ready"], turn(i))
                    act.activation(glog[:, :, :], glog[:, :, :], ACT.Exp).then_inc(s["gexp_ready"], 1)
                    for b in range(GROUP):
                        act.wait_ge(s["v_psum"], turn(i, b + 1, GROUP))
                        for p in range(2):
                            ins = act.activation(att.vals[:, b, 6 * p:6 * p + 6, 0:HD],
                                                 bank[b % 2 * 2 + p][0:T, 0:WIDE // 2]
                                                 .rearrange("t (n d) -> t n d", d=HD), ACT.Copy)
                        ins.then_inc(s["v_ready"], 1)
                    heads_scalar(act, att, i)
                    act.wait_ge(s["oT_psum"], turn(i))
                    for j in range(3, 6):
                        ins = act.activation(oT[:, j, :], bank[j][:, 0:N], ACT.Copy)
                    ins.then_inc(s["oT_act"], 1)

            @block.vector
            def _(v):
                def normed(i):
                    norm_statistics(v, norm, lambda b: sample_of(h, i, b))
                    v.wait_ge(norm.rstd_ready, turn(i))
                    for b in range(GROUP):
                        norm_apply(v, norm, lambda b: sample_of(h, i, b), lambda b: xn[:, b, 0:D], b)
                    duplicate_rest(v, xn).then_inc(s["xn_ready"], 1)

                normed(0)
                v.memset(eps[:, :], EPS)
                v.wait_ge(w_loaded, 16 * (3 + len(loads)))
                heads_of = [w.raw[:, c, 0:2 * WIDE].rearrange("p (n d) -> p n d", d=HD) for c in range(2)]
                for c in range(2):
                    v.tensor_reduce(head_sum[:, c, :], heads_of[c], AX.X, ALU.add)
                v.drain()
                v.tensor_scalar(head_sum[:, :, :], head_sum[:, :, :], 1.0 / HD, None, ALU.mult)
                v.drain()
                for c in range(2):
                    ins = v.tensor_tensor(heads_of[c], heads_of[c],
                                          head_sum[:, c, :].unsqueeze(2).to_broadcast([128, 2 * HEADS, HD]),
                                          ALU.subtract)
                ins.then_inc(w_centered, 1)
                v.memset(ones_row[:, :].bitcast(F32), 1.0)
                v.tensor_copy(b_v_hi[:, :], b_v[:, :])
                v.drain()
                v.tensor_tensor(b_v_lo[:, :], b_v[:, :], b_v_hi[:, :].bitcast(F32), ALU.subtract)
                v.tensor_scalar(affine[:, 0:2], affine_in[:, 0:2], HD ** -0.5, None, ALU.mult)
                v.tensor_copy(affine[:, 2:4], affine_in[:, 2:4])
                v.wait_ge(bias_mean, 1)
                v.tensor_tensor(b_centered[:, :], b_qk[:, :], bank[7][:, 0:QK], ALU.subtract).then_inc(bias_ready, 1)
                v.wait_ge(w_high, 1)
                w.low(v).then_inc(w_split, 1)
                with v.Fori(0, TURNS) as i:
                    v.wait_ge(s["xT_high"], turn(i))
                    xT.low(v, bank[0:2]).then_inc(s["xT_split"], 1)
                    v.wait_ge(s["gate_psum"], turn(i))
                    v.tensor_copy(glog[:, :, :], bank[6][0:T, 0:GROUP * GATES]).then_inc(s["gate_read"], 1)
                    v.drain()
                    for n, (lo, hi) in enumerate(parts):
                        v.tensor_reduce(gpeak[:, n, :], glog[:, :, lo:hi], AX.X, ALU.max)
                    v.drain()
                    for n, (lo, hi) in enumerate(parts):
                        ins = v.tensor_tensor(glog[:, :, lo:hi], glog[:, :, lo:hi],
                                              gpeak[:, n, :].unsqueeze(2).to_broadcast([T, GROUP, hi - lo]),
                                              ALU.subtract)
                    ins.then_inc(s["gshift_ready"], 1)

                    def scaled(half, first, count):
                        lo = chunk[half * HALF] + first
                        kind = 2 if half == 0 else 0
                        v.wait_ge(s["centered_done"], turn(i, (half + 1) * HALF, QK))
                        v.wait_ge(s["half_rstd"], turn(i, half + 1, 2))
                        v.tensor_tensor(qkT[:, lo:lo + count, :], qkT[:, lo:lo + count, :], rstd[:, lo:lo + count, :],
                                        ALU.mult)
                        v.drain()
                        ins = v.tensor_scalar(qkT[:, lo:lo + count, :], qkT[:, lo:lo + count, :],
                                              affine[:, kind:kind + 1], affine[:, kind + 1:kind + 2],
                                              ALU.mult, ALU.add)
                        if first + count == HALF:
                            ins.then_inc(s["half_ready"], 1)

                    for j in range(QK):
                        if j == 0:
                            v.wait_ge(att.kblock_ready, turn(i, 0, GROUP))
                        elif j == HALF:
                            v.wait_ge(att.scores_psum, turn(i, 0, UNITS))
                        v.wait_ge(s["square_ready"], turn(i, j + 1, QK))
                        v.tensor_scalar(qkT[:, chunk[j], :], bank[j % RING][:, 0:N],
                                        b_centered[:, chunk[j]:chunk[j] + 1], None,
                                        ALU.add).then_inc(s["centered_done"], 1)
                        if j >= HALF + 3:
                            scaled(0, 2 * (j - HALF - 3), 2)
                    scaled(1, 0, HALF)
                    v.wait_ge(s["gexp_ready"], turn(i))
                    for n, (lo, hi) in enumerate(parts):
                        v.tensor_reduce(gsum[:, n, :], glog[:, :, lo:hi], AX.X, ALU.add)
                    v.drain()
                    v.reciprocal(gsum[:, :, :], gsum[:, :, :])
                    v.drain()
                    for n, (lo, hi) in enumerate(parts):
                        v.tensor_tensor(glog[:, :, lo:hi], glog[:, :, lo:hi],
                                        gsum[:, n, :].unsqueeze(2).to_broadcast([T, GROUP, hi - lo]), ALU.mult)
                    v.drain()
                    top_two_hot(v, core, top, glog[:, :, 0:ROUTED])
                    v.tensor_tensor(top.hot[:, 0, :, :], top.hot[:, 0, :, :], top.hot[:, 1, :, :], ALU.add)
                    v.drain()
                    v.tensor_tensor(glog[:, :, 0:ROUTED], glog[:, :, 0:ROUTED], top.hot[:, 0, :, :], ALU.mult)
                    v.drain()
                    v.tensor_reduce(gsum[:, 0, :], glog[:, :, 0:ROUTED], AX.X, ALU.add)
                    v.drain()
                    v.tensor_scalar(gsum[:, 0, :], gsum[:, 0, :], 2.0 ** -23, None, ALU.max)
                    v.drain()
                    v.reciprocal(gsum[:, 0, :], gsum[:, 0, :])
                    v.drain()
                    v.scalar_tensor_tensor(out=gsum[:, 0, :], in0=gsum[:, 0, :], scalar=4.0,
                                           in1=glog[:, :, ROUTED + 1], op0=ALU.mult, op1=ALU.mult)
                    v.tensor_scalar(gsum[:, 1, :], glog[:, :, ROUTED], 4.0, None, ALU.mult)
                    v.drain()
                    v.tensor_tensor(gates[:, :, SHARED:HEADS], glog[:, :, 0:ROUTED],
                                    gsum[:, 0, :].unsqueeze(2).to_broadcast([T, GROUP, ROUTED]), ALU.mult)
                    v.tensor_tensor(gates[:, :, 0:SHARED], glog[:, :, ROUTED + 2:GATES],
                                    gsum[:, 1, :].unsqueeze(2).to_broadcast([T, GROUP, SHARED]), ALU.mult)

                    def rescale(u, inv):
                        v.tensor_tensor(weight[:, u % 2, :], inv, gates[:, u // 2, cols(u % 2, 6)], ALU.mult)
                        v.drain()
                        return v.tensor_tensor(o[:, u // 2, cols(u % 2, 6 * HD)].rearrange("t (n d) -> t n d", d=HD),
                                               att.context(u)[:, :, 0:HD],
                                               weight[:, u % 2, :].unsqueeze(2).to_broadcast([T, 6, HD]), ALU.mult)
                    heads_vector(v, att, i, rescale)
                    v.wait_ge(s["oT_psum"], turn(i))
                    for j in range(3):
                        ins = v.tensor_copy(oT[:, j, :], bank[j][:, 0:N])
                    ins.then_inc(s["oT_dve"], 1)
                    normed(i + 1)
                    add_bias(v, h, i, b_out)
                    v.wait_ge(s["out_psum"], turn(i))
                    for p in range(2):
                        rows = h[:, bass.ds(i * (GROUP * D) + p * (2 * D), 2 * D)]
                        ins = v.tensor_tensor(rows, bank[6 + p][0:T, 0:2 * D], rows, ALU.add)
                    ins.then_inc(s["h_done"], 1)



def position_attention_stage(core, a):
    nc, bank, h = core.nc, core.bank, core.h
    KV = D // 3
    with ExitStack() as ctx:
        sb, sem, load_sem, raised = stage_tools(core, ctx)
        norm = Norm(sb, sem, "norm")
        table = sb("table", [C, 2, T])
        w_v = sb("w_v", [C, 2, KV])
        w_out = sb("w_out", [KV, D])
        peak = sb("peak", [T, 1])
        total = sb("total", [T, 1])
        probs = sb("probs", [T, T])
        probsT = sb("probsT", [T, T])
        xn = sb("xn", [T, GROUP, D])
        xT = sb("xT", [C, 2, N])
        vals = sb("vals", [T, GROUP, KV])
        contextT = sb("contextT", [KV, N])
        w_loaded, scores_psum, peak_ready, exp_ready, probs_ready, probsT_psum, probsT_ready = (
            load_sem(n) for n in ("w_loaded", "scores_psum", "peak_ready", "exp_ready", "probs_ready",
                                  "probsT_psum", "probsT_ready"))
        names = ("xn_ready", "xT_psum", "xT_ready", "v_psum", "v_ready", "context_psum", "context_ready",
                 "out_psum", "h_done")
        s = {n: sem(n) for n in names}

        with nc.Block() as block:
            @block.sync
            def _(sp):
                raise_to_start(sp, raised)
                sp.dma_start(table[:, :, :], a["f_table"]).then_inc(w_loaded, 16)
                sp.dma_start(w_v[:, :, :], a["f_wv"]).then_inc(w_loaded, 16)
                sp.dma_start(w_out[:, :], a["f_wo"]).then_inc(w_loaded, 16)

            @block.gpsimd
            def _(pool):
                norm_rstd(pool, core, norm, 0)
                with pool.Fori(0, TURNS) as i:
                    norm_rstd(pool, core, norm, i + 1)

            @block.tensor
            def _(pe):
                pe.wait_ge(w_loaded, 48)
                for c in range(2):
                    mm = pe.matmul(bank[6][0:T, 0:T], table[:, c, :], table[:, c, :], start=(c == 0), stop=(c == 1))
                mm.then_inc(scores_psum, 1)
                pe.wait_ge(probs_ready, 1)
                pe.transpose(bank[7][0:T, 0:T], probs[:, :], core.ident[0:T, 0:T]).then_inc(probsT_psum, 1)
                pe.wait_ge(probsT_ready, 1)
                with pe.Fori(0, TURNS) as i:
                    pe.wait_ge(s["xn_ready"], turn(i))
                    pe.wait_ge(s["xT_ready"], turn(i, 0))
                    transpose_group(pe, core, bank[0:2], xn, s["xT_psum"])
                    pe.wait_ge(s["v_ready"], turn(i, 0))
                    pe.wait_ge(s["xT_ready"], turn(i))
                    for b in range(GROUP):
                        for c in range(2):
                            mm = pe.matmul(bank[2][0:T, cols(b, KV)], xT[:, c, cols(b)], w_v[:, c, :],
                                           start=(c == 0), stop=(c == 1))
                    mm.then_inc(s["v_psum"], 1)
                    pe.wait_ge(s["context_ready"], turn(i, 0))
                    pe.wait_ge(s["v_ready"], turn(i))
                    for b in range(GROUP):
                        mm = pe.matmul(bank[3][0:KV, cols(b)], vals[:, b, :], probsT[:, :], start=True, stop=True)
                    mm.then_inc(s["context_psum"], 1)
                    pe.wait_ge(s["h_done"], turn(i, 0))
                    pe.wait_ge(s["context_ready"], turn(i))
                    for b in range(GROUP):
                        mm = pe.matmul(bank[4 + b // 2][0:T, cols(b % 2, D)], contextT[:, cols(b)], w_out[:, :],
                                       start=True, stop=True)
                    mm.then_inc(s["out_psum"], 1)

            @block.scalar
            def _(act):
                act.wait_ge(peak_ready, 1)
                act.activation(probs[:, :], bank[6][0:T, 0:T], ACT.Exp, bias=peak[:, 0:1],
                               accum_out=total[:, 0:1]).then_inc(exp_ready, 1)
                act.wait_ge(probsT_psum, 1)
                act.activation(probsT[:, :], bank[7][0:T, 0:T], ACT.Copy).then_inc(probsT_ready, 1)
                with act.Fori(0, TURNS) as i:
                    act.wait_ge(s["v_psum"], turn(i, 0))
                    act.wait_ge(s["xT_psum"], turn(i))
                    for c in range(2):
                        ins = act.activation(xT[:, c, :], bank[c][0:C, 0:N], ACT.Copy)
                    ins.then_inc(s["xT_ready"], 1)
                    act.wait_ge(s["context_psum"], turn(i, 0))
                    act.wait_ge(s["v_psum"], turn(i))
                    act.activation(vals[:, :, :], bank[2][0:T, 0:GROUP * KV], ACT.Copy).then_inc(s["v_ready"], 1)
                    act.wait_ge(s["out_psum"], turn(i, 0))
                    act.wait_ge(s["context_psum"], turn(i))
                    act.activation(contextT[:, :], bank[3][0:KV, 0:N], ACT.Copy).then_inc(s["context_ready"], 1)

            @block.vector
            def _(v):
                def normed(i):
                    norm_statistics(v, norm, lambda b: sample_of(h, i, b))
                    v.wait_ge(s["xT_psum"], turn(i, 0))
                    v.wait_ge(norm.rstd_ready, turn(i))
                    for b in range(GROUP):
                        ins = norm_apply(v, norm, lambda b: sample_of(h, i, b), lambda b: xn[:, b, :], b)
                    ins.then_inc(s["xn_ready"], 1)

                normed(0)
                v.wait_ge(scores_psum, 1)
                v.tensor_reduce(peak[:, :], bank[6][0:T, 0:T], AX.X, ALU.max, negate=True).then_inc(peak_ready, 1)
                v.wait_ge(exp_ready, 1)
                v.reciprocal(total[:, :], total[:, :])
                v.drain()
                v.tensor_scalar(probs[:, :], probs[:, :], total[:, 0:1], None, ALU.mult).then_inc(probs_ready, 1)
                with v.Fori(0, TURNS) as i:
                    normed(i + 1)
                    v.wait_ge(s["out_psum"], turn(i))
                    for p in range(2):
                        rows = h[:, bass.ds(i * (GROUP * D) + p * (2 * D), 2 * D)]
                        ins = v.tensor_tensor(rows, bank[4 + p][0:T, 0:2 * D], rows, ALU.add)
                    ins.then_inc(s["h_done"], 1)



def int8_stage(core, a):
    nc, bank, h = core.nc, core.bank, core.h
    ROUND = 1.5 * 2.0 ** 23
    ACT_SCALE, W_SCALE = 0.02, 0.01
    with ExitStack() as ctx:
        sb, sem, load_sem, raised = stage_tools(core, ctx)
        norm = Norm(sb, sem, "norm")
        w_words = sb("w_words", [C, 2 * D // 4], I32)
        w8 = w_words[:, :].bitcast(I8).rearrange("p (c n) -> p c n", c=2)
        w = sb("w", [C, 2, D], BF16)
        ident = sb("ident16", [128, 128], BF16)
        bias = sb("bias", [T, D])
        xn = sb("xn", [T, GROUP, D])
        quant = sb("quant", [T, GROUP, D], BF16)
        quantT = sb("quantT", [C, 2, N], BF16)
        scaled = sb("scaled", [T, GROUP, D])
        w_loaded, consts_ready = load_sem("w_loaded"), load_sem("consts_ready")
        names = ("quant_ready", "quantT_psum", "quantT_ready", "out_psum", "h_done")
        s = {n: sem(n) for n in names}
        turned = [bank[c][0:C, 0:N // 2].bitcast(BF16) for c in range(2)]

        with nc.Block() as block:
            @block.sync
            def _(sp):
                raise_to_start(sp, raised)
                sp.dma_start(w_words[:, :], a["g_w"]).then_inc(w_loaded, 16)
                sp.dma_start(bias[:, :], a["g_bias"].to_broadcast([T, D])).then_inc(w_loaded, 16)

            @block.gpsimd
            def _(pool):
                norm_rstd(pool, core, norm, 0)
                with pool.Fori(0, TURNS) as i:
                    norm_rstd(pool, core, norm, i + 1)

            @block.tensor
            def _(pe):
                pe.wait_ge(consts_ready, 1)
                with pe.Fori(0, TURNS) as i:
                    pe.wait_ge(s["quantT_ready"], turn(i, 0))
                    pe.wait_ge(s["quant_ready"], turn(i))
                    for c in range(2):
                        for b in range(GROUP):
                            mm = pe.transpose(turned[c][:, cols(b)], quant[:, b, c * C:(c + 1) * C],
                                              ident[0:T, 0:T])
                    mm.then_inc(s["quantT_psum"], 1)
                    pe.wait_ge(s["h_done"], turn(i, 0))
                    pe.wait_ge(s["quantT_ready"], turn(i))
                    for b in range(GROUP):
                        for c in range(2):
                            mm = pe.matmul(bank[4 + b // 2][0:T, cols(b % 2, D)], quantT[:, c, cols(b)], w[:, c, :],
                                           start=(c == 0), stop=(c == 1))
                    mm.then_inc(s["out_psum"], 1)

            @block.scalar
            def _(act):
                with act.Fori(0, TURNS) as i:
                    act.wait_ge(s["out_psum"], turn(i, 0))
                    act.wait_ge(s["quantT_psum"], turn(i))
                    for c in range(2):
                        ins = act.activation(quantT[:, c, :], turned[c], ACT.Copy)
                    ins.then_inc(s["quantT_ready"], 1)

            @block.vector
            def _(v):
                def quantized(i):
                    norm_statistics(v, norm, lambda b: sample_of(h, i, b))
                    v.wait_ge(norm.rstd_ready, turn(i))
                    for b in range(GROUP):
                        norm_apply(v, norm, lambda b: sample_of(h, i, b), lambda b: xn[:, b, :], b)
                    v.drain()
                    v.tensor_scalar(xn[:, :, :], xn[:, :, :], 1.0 / ACT_SCALE, ROUND, ALU.mult, ALU.add)
                    v.drain()
                    v.tensor_scalar(xn[:, :, :], xn[:, :, :], ROUND, 127.0, ALU.subtract, ALU.min)
                    v.drain()
                    v.wait_ge(s["quantT_psum"], turn(i, 0))
                    v.tensor_scalar(quant[:, :, :], xn[:, :, :], -128.0, None, ALU.max).then_inc(s["quant_ready"], 1)

                quantized(0)
                v.wait_ge(w_loaded, 32)
                v.tensor_copy(w[:, :, :], w8)
                v.tensor_copy(ident[:, :], core.ident[:, :]).then_inc(consts_ready, 1)
                with v.Fori(0, TURNS) as i:
                    quantized(i + 1)
                    v.wait_ge(s["out_psum"], turn(i))
                    for p in range(2):
                        v.scalar_tensor_tensor(out=scaled[:, 2 * p:2 * p + 2, :],
                                               in0=bank[4 + p][0:T, 0:2 * D].rearrange("t (b d) -> t b d", b=2),
                                               scalar=ACT_SCALE * W_SCALE,
                                               in1=bias[:, :].unsqueeze(1).to_broadcast([T, 2, D]),
                                               op0=ALU.mult, op1=ALU.add)
                    v.drain()
                    rows = h[:, bass.ds(i * (GROUP * D), GROUP * D)]
                    v.tensor_tensor(rows, rows, scaled[:, :, :].rearrange("t b d -> t (b d)"), ALU.add
                                    ).then_inc(s["h_done"], 1)



def rotary_heads_stage(core, a):
    nc, bank, h = core.nc, core.bank, core.h
    with ExitStack() as ctx:
        sb, sem, load_sem, raised = stage_tools(core, ctx)
        norm = Norm(sb, sem, "norm")
        w = SplitWeights(sb, "w", 5 * D)
        b_qk = sb("b_qk", [C, 8])
        b_v = sb("b_v", [1, D])
        w_out = sb("w_out", [C, 2, D])
        b_out = sb("b_out", [T, D])
        angles = sb("angles", [C, 4, T])
        xn = sb("xn", [T, GROUP, D + REST])
        xT = SplitColumns(core)
        cos_part = sb("cos_part", [C, 2, N])
        sin_part = sb("sin_part", [C, 2, N])
        qkT = sb("qkT", [C, 4, N])
        qT, kT = qkT[:, 0:2, :], qkT[:, 2:4, :]
        o = sb("o", [T, GROUP, D])
        oT = sb("oT", [C, 2, N])
        att = Heads(core, sb, sem, 16, core.mask16)
        w_loaded, w_high, w_split, ones_ready = (
            load_sem(n) for n in ("w_loaded", "w_high", "w_split", "ones_ready"))
        names = ("xn_ready", "xT_psum", "xT_high", "xT_split", "qk_psum", "parts_ready", "qk_ready", "v_psum", "v_ready",
                 "oT_psum", "oT_ready", "out_psum", "h_done")
        s = {n: sem(n) for n in names}
        loads = [(b_qk, "h_bqk"), (b_v, "h_bv"), (w_out, "h_wo"), (angles, "h_angles")]

        with nc.Block() as block:
            @block.sync
            def _(sp):
                raise_to_start(sp, raised)
                w.load(sp, a["h_w"], w_loaded)
                for tile, name in loads:
                    sp.dma_start(tile[tuple(slice(None) for _ in tile.shape)], a[name]).then_inc(w_loaded, 16)
                sp.dma_start(b_out[:, :], a["h_bo"].to_broadcast([T, D])).then_inc(w_loaded, 16)

            @block.gpsimd
            def _(pool):
                pool.memset(att.vals[:, :, :, 16:17], 1.0).then_inc(ones_ready, 1)
                norm_rstd(pool, core, norm, 0)
                with pool.Fori(0, TURNS) as i:
                    pool.wait_ge(att.scores_psum, turn(i, 0, UNITS))
                    pool.wait_ge(s["qk_ready"], turn(i, 4, 4))
                    for b in range(GROUP):
                        heads_pool(pool, att, i, kT, b)
                    norm_rstd(pool, core, norm, i + 1)

            @block.tensor
            def _(pe):
                pe.wait_ge(w_loaded, 16 * (3 + len(loads)))
                pe.wait_ge(w_split, 1)
                pe.wait_ge(ones_ready, 1)
                with pe.Fori(0, TURNS) as i:
                    pe.wait_ge(s["xn_ready"], turn(i))
                    transpose_for_experts(pe, core, bank[0:2], xn, s["xT_psum"])
                    pe.wait_ge(s["h_done"], turn(i, 0))
                    pe.wait_ge(s["xT_split"], turn(i))
                    for j in range(4):
                        pe.wait_ge(s["parts_ready"], turn(i, j - 1, 4))
                        for r in range(2):
                            at = (2 * (j // 2) + r) * D + j % 2 * C
                            mm = product_by_columns(pe, bank[2 + j % 2 * 2 + r][0:C, 0:N], w, slice(at, at + C), xT)
                        mm.then_inc(s["qk_psum"], 1)
                    for b in range(GROUP):
                        out = bank[6 + b // 2][0:T, cols(b % 2, D)]
                        product_by_rows(pe, out, xT, cols(b), w, slice(4 * D, 5 * D), more=True)
                        mm = pe.matmul(out, core.ones[0:1, 0:T], b_v[:, :], start=False, stop=True)
                    mm.then_inc(s["v_psum"], 1)
                    pe.wait_ge(s["qk_ready"], turn(i, 4, 4))
                    pe.wait_ge(s["v_ready"], turn(i))
                    heads_tensor(pe, att, i, qT)
                    pe.wait_ge(att.context_done, turn(i, UNITS, UNITS))
                    transpose_group(pe, core, bank[0:2], o, s["oT_psum"])
                    pe.wait_ge(s["oT_ready"], turn(i))
                    for b in range(GROUP):
                        out = bank[2 + b // 2][0:T, cols(b % 2, D)]
                        for c in range(2):
                            mm = pe.matmul(out, oT[:, c, cols(b)], w_out[:, c, :], start=(c == 0), stop=(c == 1))
                    mm.then_inc(s["out_psum"], 1)

            @block.scalar
            def _(act):
                act.wait_ge(w_loaded, 16 * (3 + len(loads)))
                w.high(act).then_inc(w_high, 1)
                with act.Fori(0, TURNS) as i:
                    act.wait_ge(s["xT_psum"], turn(i))
                    xT.high(act, bank[0:2]).then_inc(s["xT_high"], 1)
                    act.wait_ge(s["v_psum"], turn(i))
                    for b in range(GROUP):
                        ins = act.activation(att.vals[:, b, :, 0:16], bank[6 + b // 2][0:T, cols(b % 2, D)]
                                             .rearrange("t (n d) -> t n d", d=16), ACT.Copy)
                    ins.then_inc(s["v_ready"], 1)
                    heads_scalar(act, att, i)
                    act.wait_ge(s["oT_psum"], turn(i))
                    for c in range(2):
                        ins = act.activation(oT[:, c, :], bank[c][0:C, 0:N], ACT.Copy)
                    ins.then_inc(s["oT_ready"], 1)

            @block.vector
            def _(v):
                def normed(i):
                    norm_statistics(v, norm, lambda b: sample_of(h, i, b))
                    v.wait_ge(norm.rstd_ready, turn(i))
                    for b in range(GROUP):
                        norm_apply(v, norm, lambda b: sample_of(h, i, b), lambda b: xn[:, b, 0:D], b)
                    duplicate_rest(v, xn).then_inc(s["xn_ready"], 1)

                normed(0)
                v.wait_ge(w_loaded, 16 * (3 + len(loads)))
                v.wait_ge(w_high, 1)
                w.low(v).then_inc(w_split, 1)
                with v.Fori(0, TURNS) as i:
                    v.wait_ge(s["xT_high"], turn(i))
                    xT.low(v, bank[0:2]).then_inc(s["xT_split"], 1)
                    for j in range(4):
                        k, kind = j % 2, j // 2
                        v.wait_ge(s["qk_psum"], turn(i, j + 1, 4))
                        for part, r in ((cos_part, 0), (sin_part, 1)):
                            at = 4 * kind + 2 * r + k
                            ins = v.scalar_tensor_tensor(
                                out=part[:, k, :].rearrange("d (b t) -> d b t", b=GROUP),
                                in0=bank[2 + 2 * k + r][0:C, 0:N].rearrange("d (b t) -> d b t", b=GROUP),
                                scalar=b_qk[:, at:at + 1],
                                in1=angles[:, 2 * kind + r, :].unsqueeze(1).to_broadcast([C, GROUP, T]),
                                op0=ALU.add, op1=ALU.mult)
                        ins.then_inc(s["parts_ready"], 1)
                        v.drain()
                        v.tensor_tensor(qkT[:, j, :], cos_part[:, k, :], sin_part[:, k, :], ALU.add
                                        ).then_inc(s["qk_ready"], 1)

                    def rescale(u, inv):
                        return v.tensor_tensor(o[:, u // 2, cols(u % 2, C)].rearrange("t (n d) -> t n d", d=16),
                                               att.context(u)[:, :, 0:16],
                                               inv.unsqueeze(2).to_broadcast([T, UNIT_HEADS, 16]), ALU.mult)
                    heads_vector(v, att, i, rescale)
                    normed(i + 1)
                    add_bias(v, h, i, b_out)
                    v.wait_ge(s["out_psum"], turn(i))
                    for p in range(2):
                        rows = h[:, bass.ds(i * (GROUP * D) + p * (2 * D), 2 * D)]
                        ins = v.tensor_tensor(rows, bank[2 + p][0:T, 0:2 * D], rows, ALU.add)
                    ins.then_inc(s["h_done"], 1)



def second_router_stage(core, a, weights):
    nc, bank, h = core.nc, core.bank, core.h
    PROBE = 24
    COLS = EXPERTS + PROBE + 1
    with ExitStack() as ctx:
        sb, sem, load_sem, raised = stage_tools(core, ctx)
        norm = Norm(sb, sem, "norm")
        w = sb("w", [128, 2, COLS])
        emb = sb("emb", [T, EXPERTS, PROBE])
        emb_square = sb("emb_square", [T, EXPERTS, PROBE])
        emb_norm = sb("emb_norm", [T, EXPERTS])
        emb_sum = sb("emb_sum", [T, EXPERTS])
        emb_inv = sb("emb_inv", [T, EXPERTS])
        mean_factor = sb("mean_factor", [T, EXPERTS])
        fatigue_energy = sb("fatigue_energy", [T, 2, EXPERTS])
        constant_bias = sb("constant_bias", [T, EXPERTS])
        pairs = SAMPLES * EXPERTS
        b2 = sb("b2", [pairs, D])
        sample_mask = sb("sample_mask", [pairs, SAMPLES])
        b2_blocks = sb("b2_blocks", [pairs, SAMPLES, D])
        xn = sb("xn", [T, GROUP, D + REST])
        xT = sb("xT", [128, 2, N])
        raw_flat = sb("raw", [T, SAMPLES * COLS])
        raw = raw_flat[:, :].rearrange("t (s c) -> t s c", c=COLS)
        probe_square = sb("probe_square", [T, SAMPLES, PROBE])
        probe_sum = sb("probe_sum", [T, SAMPLES])
        probe_norm = sb("probe_norm", [T, SAMPLES])
        probe_inv = sb("probe_inv", [T, SAMPLES])
        aligned = sb("aligned", [T, SAMPLES, EXPERTS, PROBE])
        align = sb("align", [T, SAMPLES, EXPERTS])
        term = sb("term", [T, SAMPLES, EXPERTS])
        gatesT = sb("gatesT", [pairs, T])
        router = Router(sb, sem, "router", SAMPLES)
        (w_loaded, emb_sum_ready, emb_norm_ready, blocks_ready, probe_sum_ready, probe_norm_ready, gates_ready,
         gatesT_psum, gatesT_ready, bias_psum) = (
            load_sem(n) for n in ("w_loaded", "emb_sum_ready", "emb_norm_ready", "blocks_ready", "probe_sum_ready",
                                  "probe_norm_ready", "gates_ready", "gatesT_psum", "gatesT_ready", "bias_psum"))
        names = ("xn_ready", "xT_psum", "xT_ready", "xT_kept", "raw_psum", "raw_read")
        s = {n: sem(n) for n in names}

        with nc.Block() as block:
            @block.sync
            def _(sp):
                raise_to_start(sp, raised)
                raise_to_start(sp, weights.raised)
                sp.dma_start(w[:, 0, :], a["i_router"][0:HIGH, :]).then_inc(w_loaded, 16)
                sp.dma_start(w[0:REST, 1, :], a["i_router"][HIGH:D, :]).then_inc(w_loaded, 16)
                sp.dma_start(b2[:, :], a["i_b2"].unsqueeze(0).to_broadcast([SAMPLES, EXPERTS, D])
                             ).then_inc(w_loaded, 16)
                sp.dma_start(sample_mask[:, :], a["sample_mask"]).then_inc(w_loaded, 16)
                sp.dma_start(emb[:, :, :].rearrange("t e r -> t (e r)"),
                             a["i_emb"].to_broadcast([T, EXPERTS * PROBE])).then_inc(w_loaded, 16)
                sp.dma_start(fatigue_energy[:, :, :].rearrange("t a e -> t (a e)"),
                             a["i_fe"].to_broadcast([T, 2 * EXPERTS])).then_inc(w_loaded, 16)
                weights.load(sp, a, (0, 0))

            @block.gpsimd
            def _(pool):
                norm_rstd(pool, core, norm, 0)
                pool.wait_ge(emb_sum_ready, 1)
                pool.tensor_tensor(emb_norm[:, :], emb_sum[:, :], core.plus_half[0:T, 0:EXPERTS], ALU.pow
                                   ).then_inc(emb_norm_ready, 1)
                pool.wait_ge(w_loaded, 96)
                blocks = [pairs, SAMPLES, D]
                pool.tensor_tensor(b2_blocks[:, :, :], b2[:, :].unsqueeze(1).to_broadcast(blocks),
                                   sample_mask[:, :].unsqueeze(2).to_broadcast(blocks), ALU.mult
                                   ).then_inc(blocks_ready, 1)
                with pool.Fori(0, TURNS) as i:
                    norm_rstd(pool, core, norm, i + 1)
                steps = weights.steps(pool, (0, 0))
                next(steps)
                pool.wait_ge(probe_sum_ready, 1)
                pool.tensor_tensor(probe_norm[:, :], probe_sum[:, :], core.plus_half[0:T, 0:SAMPLES], ALU.pow
                                   ).then_inc(probe_norm_ready, 1)
                for _ in steps:
                    pass

            @block.tensor
            def _(pe):
                pe.wait_ge(w_loaded, 96)
                with pe.Fori(0, TURNS) as i:
                    pe.wait_ge(s["xn_ready"], turn(i))
                    transpose_for_experts(pe, core, bank[0:2], xn, s["xT_psum"])
                    pe.wait_ge(s["xT_ready"], turn(i))
                    pe.wait_ge(s["raw_read"], turn(i, 0))
                    for b in range(GROUP):
                        for c in range(2):
                            rows = slice(0, (HIGH, REST)[c])
                            mm = pe.matmul(bank[2][0:T, cols(b, COLS)], xT[rows, c, cols(b)], w[rows, c, :],
                                           start=(c == 0), stop=(c == 1))
                    mm.then_inc(s["raw_psum"], 1)
                pe.wait_ge(gates_ready, 1)
                pe.transpose(bank[3][0:pairs, 0:T], core.gates[:, :], core.ident[0:T, 0:T]).then_inc(gatesT_psum, 1)
                pe.wait_ge(blocks_ready, 1)
                pe.wait_ge(gatesT_ready, 1)
                for p in range(SAMPLES // 2):
                    pe.matmul(bank[p][0:T, 0:2 * D], gatesT[:, :],
                              b2_blocks[:, 2 * p:2 * p + 2, :].rearrange("p s d -> p (s d)"), start=True, stop=True
                              ).then_inc(bias_psum, 1)

            @block.scalar
            def _(act):
                with act.Fori(0, TURNS) as i:
                    act.wait_ge(s["raw_psum"], turn(i, 0))
                    act.wait_ge(s["xT_kept"], turn(i, 0))
                    act.wait_ge(s["xT_psum"], turn(i))
                    for c in range(2):
                        ins = act.activation(xT[:, c, :], bank[c][:, 0:N], ACT.Copy)
                    ins.then_inc(s["xT_ready"], 1)
                router_scalar(act, router, 0)
                act.wait_ge(gatesT_psum, 1)
                act.activation(gatesT[:, :], bank[3][0:pairs, 0:T], ACT.Copy).then_inc(gatesT_ready, 1)

            @block.vector
            def _(v):
                def normed(i):
                    norm_statistics(v, norm, lambda b: sample_of(h, i, b))
                    v.wait_ge(norm.rstd_ready, turn(i))
                    for b in range(GROUP):
                        norm_apply(v, norm, lambda b: sample_of(h, i, b), lambda b: xn[:, b, 0:D], b)
                    duplicate_rest(v, xn).then_inc(s["xn_ready"], 1)

                normed(0)
                v.wait_ge(w_loaded, 96)
                v.tensor_tensor(emb_square[:, :, :], emb[:, :, :], emb[:, :, :], ALU.mult)
                v.drain()
                v.tensor_reduce(emb_sum[:, :], emb_square[:, :, :], AX.X, ALU.add).then_inc(emb_sum_ready, 1)
                v.tensor_tensor(constant_bias[:, :], fatigue_energy[:, 1, :], fatigue_energy[:, 0, :], ALU.subtract)
                v.drain()
                v.tensor_scalar(constant_bias[:, :], constant_bias[:, :], 0.1, None, ALU.mult)
                v.wait_ge(emb_norm_ready, 1)
                v.tensor_scalar(mean_factor[:, :], emb_norm[:, :], 0.02, 0.02, ALU.mult, ALU.add)
                v.tensor_scalar(emb_inv[:, :], emb_norm[:, :], 1e-12, None, ALU.max)
                v.drain()
                v.reciprocal(emb_inv[:, :], emb_inv[:, :])
                v.drain()
                v.tensor_tensor(emb[:, :, :], emb[:, :, :],
                                emb_inv[:, :].unsqueeze(2).to_broadcast([T, EXPERTS, PROBE]), ALU.mult)
                v.drain()
                with v.Fori(0, TURNS) as i:
                    v.wait_ge(s["xT_ready"], turn(i))
                    keep_for_experts(v, core, xT, i).then_inc(s["xT_kept"], 1)
                    normed(i + 1)
                    v.wait_ge(s["raw_psum"], turn(i))
                    v.tensor_scalar(raw_flat[:, bass.ds(i * (GROUP * COLS), GROUP * COLS)],
                                    bank[2][0:T, 0:GROUP * COLS], 1.0, None, ALU.mult).then_inc(s["raw_read"], 1)
                wide = [T, SAMPLES, EXPERTS]
                v.wait_ge(s["raw_read"], turn(TURNS, 0))
                probe = raw[:, :, EXPERTS:EXPERTS + PROBE]
                v.tensor_tensor(probe_square[:, :, :], probe, probe, ALU.mult)
                v.drain()
                v.tensor_reduce(probe_sum[:, :], probe_square[:, :, :], AX.X, ALU.add).then_inc(probe_sum_ready, 1)
                for b in range(SAMPLES):
                    v.tensor_tensor(aligned[:, b, :, :],
                                    raw[:, b, EXPERTS:EXPERTS + PROBE].unsqueeze(1)
                                    .to_broadcast([T, EXPERTS, PROBE]), emb[:, :, :], ALU.mult)
                v.drain()
                v.tensor_reduce(align[:, :, :], aligned[:, :, :, :], AX.X, ALU.add)
                v.tensor_tensor(term[:, :, :], raw[:, :, COLS - 1:COLS].to_broadcast(wide),
                                mean_factor[:, :].unsqueeze(1).to_broadcast(wide), ALU.mult)
                v.drain()
                v.tensor_tensor(router.logits[:, :, :], raw[:, :, 0:EXPERTS], term[:, :, :], ALU.add)
                v.wait_ge(probe_norm_ready, 1)
                v.tensor_scalar(probe_inv[:, :], probe_norm[:, :], 1e-12, None, ALU.max)
                v.drain()
                v.reciprocal(probe_inv[:, :], probe_inv[:, :])
                v.drain()
                v.tensor_tensor(align[:, :, :], align[:, :, :],
                                probe_inv[:, :].unsqueeze(2).to_broadcast(wide), ALU.mult)
                v.drain()
                v.scalar_tensor_tensor(out=router.logits[:, :, :], in0=align[:, :, :], scalar=0.02,
                                       in1=router.logits[:, :, :], op0=ALU.mult, op1=ALU.add)
                v.drain()
                v.tensor_tensor(router.logits[:, :, :], router.logits[:, :, :],
                                constant_bias[:, :].unsqueeze(1).to_broadcast(wide), ALU.add)
                v.drain()
                router_vector(v, core, router, 0).then_inc(gates_ready, 1)
                for p in range(SAMPLES // 2):
                    rows = h[:, 2 * p * D:(2 * p + 2) * D]
                    v.wait_ge(bias_psum, p + 1)
                    v.tensor_tensor(rows, bank[p][0:T, 0:2 * D], rows, ALU.add)


def store_stage(core, a):
    nc = core.nc
    with ExitStack() as ctx:
        _, _, load_sem, _ = stage_tools(core, ctx)
        stored = load_sem("stored")
        with nc.Block() as block:
            @block.sync
            def _(sp):
                sp.dma_start(a["out"].rearrange("s t d -> t s d"),
                             core.h[:, 0:SAMPLES * D].rearrange("t (s d) -> t s d", d=D)).then_inc(stored, 16)
                sp.wait_ge(stored, 16)


def build(nc, a):
    with ExitStack() as ctx:
        core = Core()
        core.nc, core.made = nc, 0
        core.h = ctx.enter_context(nc.sbuf_tensor("h", [T, (SAMPLES + GROUP) * D], F32))
        core.minus_half = ctx.enter_context(nc.sbuf_tensor("minus_half", [128, 48], F32))
        core.plus_half = ctx.enter_context(nc.sbuf_tensor("plus_half", [128, 48], F32))
        core.ones = ctx.enter_context(nc.sbuf_tensor("ones", [128, 128], F32))
        core.constants = {}
        core.z_hi, core.z_lo, core.z_rest = (
            ctx.enter_context(nc.sbuf_tensor(n, [128, SAMPLES * T], F32R)) for n in ("z_hi", "z_lo", "z_rest"))
        core.gates = ctx.enter_context(nc.sbuf_tensor("gates", [T, SAMPLES * EXPERTS], F32))
        for name, shape in (("ident", [128, 128]), ("mask16", [C, 6]), ("mask64", [128, 2]), ("iota", [128, 16])):
            core.constants[name] = ctx.enter_context(nc.sbuf_tensor("c_" + name, shape, F32))
        core.ident, core.iota = core.constants["ident"], core.constants["iota"]
        core.mask16, core.mask64 = core.constants["mask16"], core.constants["mask64"]
        core.psum = ctx.enter_context(nc.psum_tensor("psum", [128, 8, 512], F32))
        core.bank = [core.psum[:, i, :] for i in range(8)]

        def routed(second, router_stage):
            with ExitStack() as weights_ctx:
                weights = ExpertWeights(core, weights_ctx, second)
                router_stage(core, a, weights)
                experts_stage(core, a, weights)

        stages = [
            lambda: tokens_stage(core, a),
            lambda: wide_attention_stage(core, a),
            lambda: routed(False, first_heads_stage),
            lambda: ssm_stage(core, a),
            lambda: gated_heads_stage(core, a),
            lambda: position_attention_stage(core, a),
            lambda: int8_stage(core, a),
            lambda: rotary_heads_stage(core, a),
            lambda: routed(True, second_router_stage),
        ]
        for stage in stages:
            stage()
        store_stage(core, a)



def shape_constants(np):
    ident = np.eye(128, dtype=np.float32)
    mask16 = (np.arange(C)[:, None] // 16 == np.arange(6)[None, :]).astype(np.float32)
    mask64 = (np.arange(128)[:, None] // 64 == np.arange(2)[None, :]).astype(np.float32)
    iota = np.tile(np.arange(16, dtype=np.float32), (128, 1))
    spread = (np.arange(C)[:, None, None] == (np.arange(12)[:, None] * 8 + np.arange(128)[None, :] // 16)[None])
    gather = spread.transpose(2, 1, 0)
    pair = np.arange(SAMPLES * EXPERTS)
    sample_mask = (pair[:, None] // EXPERTS == np.arange(SAMPLES)[None, :]).astype(np.float32)
    average = (mask64 @ mask64.T) / np.float32(64)
    pos = np.arange(T, dtype=np.float32)[:, None]
    freqs = np.float32(10000.0) ** (-np.arange(0, D, 2, dtype=np.float32) / D)
    table = np.concatenate([np.sin(pos * freqs), np.cos(pos * freqs)], axis=1).astype(np.float32).T
    half, turned = 8, 4
    scale = np.float32(10000.0) ** (np.float32(2) * np.arange(turned, dtype=np.float32) / np.float32(16))
    angle = np.zeros((T, half), np.float32)
    angle[:, :turned] = pos / scale
    cos = np.tile(np.cos(angle).T, (2 * 6, 1))
    sin = np.tile(np.concatenate([-np.sin(angle).T, np.sin(angle).T]), (6, 1))
    angles = np.stack([cos / 4, sin / 4, cos, sin], axis=1).astype(np.float32)
    return {"f_table": table.reshape(2, C, T).swapaxes(0, 1), "h_angles": angles, "ident": ident, "mask16": mask16, "mask64": mask64, "iota": iota, "average": average,
            "sample_mask": sample_mask,
            "spread": spread.astype(np.float32), "gather": gather.astype(np.float32)}


def kernel(**inputs):
    import numpy as np
    import concourse.bacc as bacc
    from concourse.bass_utils import run_bass_kernel_spmd as run

    x = {k: np.asarray(v) for k, v in inputs.items()}

    def chunks(w, k):
        return w.reshape(k, w.shape[0] // k, *w.shape[1:]).swapaxes(0, 1)

    def per_partition(b, k):
        return b.reshape(k, -1).T

    arrays = shape_constants(np)
    image = x["x"].reshape(SAMPLES, 3, 6, 16, 6, 16).transpose(0, 1, 2, 4, 3, 5).reshape(SAMPLES, IMG, 768)
    image = image.transpose(2, 0, 1)
    arrays["patches"] = chunks(image, PATCH_K)
    arrays["tok_w"] = chunks(x["L0_tok_W"].T, PATCH_K)
    arrays["tok_b"] = x["L0_tok_b"].reshape(1, D)
    arrays["cls"] = x["L0_tok_class_token"]
    arrays["pos"] = x["L0_tok_pos_embedding"]
    arrays["txt"] = x["txt"]
    arrays["a_wqkv"] = x["L0_attn_W_qkv"]
    arrays["a_bqk"] = per_partition(x["L0_attn_b_qkv"][0:2 * D], 4)
    arrays["a_bv"] = x["L0_attn_b_qkv"][2 * D:].reshape(1, D)
    arrays["b_wqkv"] = chunks(x["L0_ffn_Wqkv"], 2)
    arrays["b_wproj"] = chunks(x["L0_ffn_Wproj"], 2)
    arrays["b_wrouter"] = x["L0_ffn_Wrouter"]
    arrays["b_affine"] = np.concatenate([per_partition(x["L0_ffn_" + n], 2) for n in ("ln1_g", "ln1_b")], axis=1)
    arrays["b_affine2"] = np.stack([part for v in (x["L0_ffn_ln2_g"], x["L0_ffn_ln2_b"])
                                    for part in (v[:HIGH], np.tile(v[HIGH:], 2))], axis=1)
    arrays["b_w1"] = x["L0_ffn_W1"]
    arrays["b_w2"] = x["L0_ffn_W2"].reshape(EXPERTS, FC, 128, D).transpose(0, 2, 1, 3)
    ssm = {k[8:]: v for k, v in x.items() if k.startswith("L1_attn_")}
    arrays["c_wi"] = chunks(ssm["Wi"], 2)
    arrays["c_wdt"] = chunks(ssm["Wdt"], 2)
    arrays["c_wb"] = chunks(ssm["WB"], 2)
    arrays["c_wc"] = chunks(ssm["WC"], 2)
    arrays["c_wo"] = chunks(ssm["Wo"], 2)
    arrays["c_bo"] = ssm["bo"].reshape(1, D)
    arrays["c_channel"] = np.concatenate(
        [v.reshape(2, C, -1).swapaxes(0, 1) for v in (ssm["bi"][:D], ssm["bi"][D:], ssm["bconv"], ssm["bdt"], ssm["D"],
                                                      ssm["Wconv"])], axis=2)
    arrays["c_rows"] = np.stack([v.reshape(24, 128).T for v in (ssm["A_log"], ssm["bB"], ssm["bC"])], axis=1)
    gh = {k[7:]: v for k, v in x.items() if k.startswith("L1_ffn_")}
    arrays["e_wqkvg"] = np.concatenate([gh["qkv_w"], gh["wg_w"], gh["wg0_w"], gh["wg1_w"]], axis=1)
    arrays["e_wproj"] = chunks(gh["proj_w"], 6)
    arrays["e_bv"] = gh["qkv_b"][1536:].reshape(1, 768)
    arrays["e_bqk"] = gh["qkv_b"][:1536].reshape(12, 128).T
    arrays["e_bproj"] = gh["proj_b"].reshape(1, D)
    arrays["e_affine"] = np.stack([np.tile(gh[n], 2) for n in ("q_norm_w", "q_norm_b", "k_norm_w", "k_norm_b")], axis=1)
    arrays["f_wv"] = chunks(x["L2_attn_Wv"].T, 2)
    arrays["f_wo"] = x["L2_attn_Wo"].T
    arrays["g_w"] = np.ascontiguousarray(chunks(x["L2_ffn_weight_t"], 2)).reshape(C, 2 * D).view(np.int32)
    arrays["g_bias"] = x["L2_ffn_bias"].reshape(1, D)
    rh = {k[8:]: v for k, v in x.items() if k.startswith("L3_attn_")}
    exchange = (np.arange(D) // 16) * 16 + (np.arange(D) + 8) % 16
    arrays["h_w"] = np.concatenate([rh["wq"].T, rh["wq"].T[:, exchange], rh["wk"].T, rh["wk"].T[:, exchange],
                                    rh["wv"].T], axis=1)
    arrays["h_bqk"] = np.concatenate([per_partition(b, 2) for b in (rh["bq"], rh["bq"][exchange], rh["bk"],
                                                                    rh["bk"][exchange])], axis=1)
    arrays["h_bv"] = rh["bv"].reshape(1, D)
    arrays["h_wo"] = chunks(rh["wo"].T, 2)
    arrays["h_bo"] = rh["bo"].reshape(1, D)
    ex = {k[7:]: v for k, v in x.items() if k.startswith("L3_ffn_")}
    arrays["i_router"] = np.concatenate([ex["router_w"].T, ex["probe_w"].T,
                                         np.full((D, 1), 1.0 / D, np.float32)], axis=1)
    arrays["i_emb"] = ex["router_emb"].reshape(1, -1)
    arrays["i_fe"] = np.concatenate([ex["fatigue"], ex["energy"]]).reshape(1, -1)
    arrays["i_b2"] = ex["b2"]
    arrays["i_b1"] = ex["b1"].reshape(EXPERTS, FC, 128).transpose(0, 2, 1)
    arrays["i_mix"] = np.stack([ex["m_gate1"], ex["m_gate2"]], axis=1)
    for n, part in enumerate(("w_fast", "w_slow", "h_fast")):
        arrays[f"i_w1_{n}"] = ex[part + "1"]
        arrays[f"i_w2_{n}"] = ex[part + "2"].reshape(EXPERTS, FC, 128, D).transpose(0, 2, 1, 3)
    arrays = {k: np.ascontiguousarray(v) for k, v in arrays.items()}

    nc = bacc.Bacc("TRN2", target_bir_lowering=False, num_devices=1)
    args = {k: nc.dram_tensor(k + "_dram", v.shape, mybir.dt.from_np(v.dtype), kind="ExternalInput").ap()
            for k, v in arrays.items()}
    args["out"] = nc.dram_tensor("out_dram", (SAMPLES, T, D), F32, kind="ExternalOutput").ap()
    build(nc, args)
    r = run(nc, [{k + "_dram": v for k, v in arrays.items()}], core_ids=[0])
    return r.results[0]["out_dram"]
```
